# Optimizing a Trainium2 kernel written in Bass

```python
import numpy as np
import jax
import jax.numpy as jnp

def _softmax(x, axis=-1):
    return jax.nn.softmax(x, axis=axis)

def _gelu(x):
    return jax.nn.gelu(x, approximate=True)

def _silu(x):
    return jax.nn.silu(x)

def _sigmoid(x):
    return jax.nn.sigmoid(x)

def _layernorm(x, axis=-1, eps=1e-05):
    m = jnp.mean(x, axis=axis, keepdims=True)
    v = jnp.var(x, axis=axis, keepdims=True)
    return (x - m) / jnp.sqrt(v + eps)

def _scatter_add(tgt, idx, src, axis=0):
    return tgt.at[idx].add(src)

def _segment_sum(src, seg, n):
    return jax.ops.segment_sum(src, seg, n)
kernel_name = 'mk_xattn_ffn_d4_seqx_r8_b22901'

def setup_inputs(seed: int=0):
    np.random.seed(seed)
    _w = jnp.asarray

    def _rec_inputs():
        import jax
        import jax.numpy as jnp
        _rk = jax.random.key(seed)
        x = 4.136e-05 + 0.9999 * jax.random.normal(jax.random.fold_in(_rk, 1), (16, 128, 128), jnp.float32)
        _lenS = 128 - jax.random.randint(jax.random.fold_in(_rk, 7), (16,), 0, max(1, 128 // 4) + 1, jnp.int32)
        _lenS2 = 128 - jax.random.randint(jax.random.fold_in(_rk, 8), (16,), 0, max(1, 128 // 4) + 1, jnp.int32)
        _ctx_2048P = jax.random.normal(jax.random.fold_in(_rk, 11), (16, 16, 256), jnp.float32)
        _ctx_2048c = jax.random.dirichlet(jax.random.fold_in(_rk, 511), 0.3 * jnp.ones((16,), jnp.float32), (16, 128))
        _ctx_2048t = jnp.einsum('bsk,bkd->bsd', _ctx_2048c, _ctx_2048P)
        _ctx_2048t = _ctx_2048t * jax.lax.rsqrt(jnp.mean(jnp.square(_ctx_2048t)) + 1e-12) * 0.953939
        ctx_2048 = -0.000392918 + 0.999932 * (_ctx_2048t + 0.3 * jax.random.normal(jax.random.fold_in(_rk, 611), (16, 128, 256), jnp.float32))
        itok_Bx1_68_817 = jax.random.randint(jax.random.fold_in(_rk, 12), (16, 1), 68, 818, jnp.int32)
        _validS = jnp.arange(128)[None, :] < _lenS[:, None]
        _validS2 = jnp.arange(128)[None, :] < _lenS2[:, None]
        _causal = jnp.tril(jnp.ones((128, 128), dtype=bool))
        mask_BxS2_if0 = jnp.where(jnp.ones((16, 128), dtype=bool), 4, 0).astype(jnp.int32)
        return (x, ctx_2048, itok_Bx1_68_817, mask_BxS2_if0)
    x, ctx_2048, itok_Bx1_68_817, mask_BxS2_if0 = _rec_inputs()

    def _L0_xattn_setup():
        import jax, jax.numpy as jnp
        import numpy as np
        UNITS = 128
        NUM_HEADS = 16
        MASK_VALUE = -1000000000000.0

        def _split_heads(x, n):
            B, S, D = x.shape
            return x.reshape(B, S, n, D // n).transpose(0, 2, 1, 3)
        key = jax.random.key(seed)
        k1, k2, k3, k4 = jax.random.split(key, 4)
        B, S = (8, 128)
        memory = jax.random.normal(k1, (B, S, 2 * UNITS), dtype=jnp.float32)
        query = jax.random.normal(k2, (B, S, UNITS), dtype=jnp.float32)
        b = jax.random.normal(k3, (S,), dtype=jnp.float32)
        seq_len = jax.random.randint(k4, (B, 1), 0, S, dtype=jnp.int32)
        return {'memory': memory, 'query': query, 'b': b, 'seq_len': seq_len}
    _L0_xattn_all = _L0_xattn_setup()
    _L0_xattn_in = {k: v for k, v in _L0_xattn_all.items() if k in ('b',)}
    del _L0_xattn_all

    def _L0_ffn_setup():
        import math
        import jax, jax.numpy as jnp
        import numpy as np
        E = 8
        H = 128
        HP = 128
        SPARSITY = 8
        N_ROTATE = 64
        ROPE_BASE = 10000.0

        def _rope(x, pos):
            half = N_ROTATE // 2
            inv_freq = 1.0 / ROPE_BASE ** (jnp.arange(half, dtype=jnp.float32) * 2.0 / N_ROTATE)
            ang = pos.astype(jnp.float32)[..., None] * inv_freq
            sin, cos = (jnp.sin(ang), jnp.cos(ang))
            x1, x2 = (x[..., :half], x[..., half:])
            return jnp.concatenate([x1 * cos - x2 * sin, x2 * cos + x1 * sin], axis=-1)
        key = jax.random.key(seed)
        k1, k2, k3, k4 = jax.random.split(key, 4)
        B, T = (4, 1024)
        X = jax.random.normal(k1, (B, T, H), dtype=jnp.float32)
        Wr = jax.random.uniform(k2, (E, H), minval=-1 / math.sqrt(H), maxval=1 / math.sqrt(H), dtype=jnp.float32)
        bq = 1 / math.sqrt(3 * HP)
        Wqkv = jax.random.uniform(k3, (E, H, 3 * HP), minval=-bq, maxval=bq, dtype=jnp.float32)
        bo = 1 / math.sqrt(H * E)
        Wo = jax.random.uniform(k4, (E, HP, H), minval=-bo, maxval=bo, dtype=jnp.float32)
        return {'X': X, 'Wr': Wr, 'Wqkv': Wqkv, 'Wo': Wo}
    _L0_ffn_all = _L0_ffn_setup()
    _L0_ffn_in = {k: v for k, v in _L0_ffn_all.items() if k in ('Wr', 'Wqkv', 'Wo')}
    del _L0_ffn_all

    def _L1_xattn_setup():
        import jax, jax.numpy as jnp
        import numpy as np
        B, L, P = (4, 512, 128)
        D_MODEL = 128
        D_GLOBAL = 256
        HEADDIM = 32
        EPSILON = 0.001
        RMS_EPS = 1e-05

        def rmsnorm(x, g, eps=RMS_EPS):
            var = jnp.mean(jnp.square(x), axis=-1, keepdims=True)
            return x * jax.lax.rsqrt(var + eps) * g

        def _hnet_depool(h, h_patch_full, patch_lens):
            h_patch = h_patch_full[..., :D_MODEL]
            bsz, plen = (h_patch.shape[0], h_patch.shape[1])
            seqlen = h.shape[1]
            logp = jnp.full((bsz, plen), -EPSILON, dtype=jnp.float32)
            bidx = jnp.cumsum(patch_lens, axis=1) - 1
            boundary_mask = jnp.zeros((bsz, seqlen), dtype=jnp.int32)
            boundary_mask = boundary_mask.at[jnp.arange(bsz)[:, None], bidx].set(1)
            dt = (-jnp.log(-jnp.expm1(logp))).astype(h_patch.dtype)
            x = h_patch / dt[..., None]
            n_heads = D_MODEL // HEADDIM
            A = -jnp.ones((n_heads,), dtype=jnp.float32)
            bcoef = jnp.exp(logp).astype(h_patch.dtype)
            x4 = x.reshape(bsz, plen, n_heads, HEADDIM)
            a = jnp.exp(dt[:, :, None] * A[None, None, :])
            u = (dt * bcoef)[:, :, None, None] * x4
            a_b = jnp.broadcast_to(a[..., None], u.shape)

            def comb(lft, rgt):
                aL, uL = lft
                aR, uR = rgt
                return (aL * aR, uL * aR + uR)
            _, s = jax.lax.associative_scan(comb, (a_b, u), axis=1)
            depool = s.reshape(bsz, plen, D_MODEL)
            plug = jnp.clip(jnp.cumsum(boundary_mask, axis=1) - 1, 0, plen - 1)
            depool_out = depool[jnp.arange(bsz)[:, None], plug]
            return depool_out + h
        key = jax.random.key(seed)
        k1, k2, k3, k4 = jax.random.split(key, 4)
        embeds = jax.random.normal(k1, (B, L, D_MODEL), dtype=jnp.float32)
        patch_embeds = jax.random.normal(k2, (B, P, D_GLOBAL), dtype=jnp.float32)
        patch_lens = jnp.full((B, P), L // P, dtype=jnp.int64)
        W_in = jax.random.normal(k3, (D_MODEL, D_MODEL), dtype=jnp.float32) * 0.02
        b_in = jnp.zeros((D_MODEL,), dtype=jnp.float32)
        g_res = jnp.ones((D_MODEL,), dtype=jnp.float32)
        g_init = jnp.ones((D_GLOBAL,), dtype=jnp.float32)
        return {'embeds': embeds, 'patch_embeds': patch_embeds, 'patch_lens': patch_lens, 'W_in': W_in, 'b_in': b_in, 'g_res': g_res, 'g_init': g_init}
    _L1_xattn_all = _L1_xattn_setup()
    _L1_xattn_in = {k: v for k, v in _L1_xattn_all.items() if k in ('W_in', 'b_in', 'g_res', 'g_init')}
    del _L1_xattn_all

    def _L1_ffn_setup():
        import jax, jax.numpy as jnp
        import numpy as np
        D = 128
        LW = 16
        DEPTH = 8
        NN = 2 ** DEPTH - 1
        NL = 2 ** DEPTH
        B, S = (2, 128)

        def _fff(x, nw, nb, w1, b1, w2, b2, act):
            node = jnp.zeros(x.shape[:2], dtype=jnp.int32)
            for _ in range(DEPTH):
                logit = jnp.einsum('bsd,bsd->bs', x, nw[node]) + nb[node]
                node = 2 * node + 1 + (logit > 0).astype(jnp.int32)
            leaf = node - NN
            h = act(jnp.einsum('bsd,bsdl->bsl', x, w1[leaf]) + b1[leaf])
            return jnp.einsum('bsl,bsld->bsd', h, w2[leaf]) + b2[leaf]

        def _forward(x, q_nw, q_nb, q_w1, q_b1, q_w2, q_b2, k_nw, k_nb, k_w1, k_b1, k_w2, k_b2, v_nw, v_nb, v_w1, v_b1, v_w2, v_b2, f_nw, f_nb, f_w1, f_b1, f_w2, f_b2):
            mu = jnp.mean(x, -1, keepdims=True)
            sd = jnp.std(x, -1, ddof=1, keepdims=True)
            xn = (x - mu) / jnp.sqrt(sd + 1e-05)
            relu = jax.nn.relu
            q = _fff(xn, q_nw, q_nb, q_w1, q_b1, q_w2, q_b2, relu)
            k = _fff(xn, k_nw, k_nb, k_w1, k_b1, k_w2, k_b2, relu)
            v = _fff(xn, v_nw, v_nb, v_w1, v_b1, v_w2, v_b2, relu)
            att = jax.nn.softmax(jnp.einsum('bqd,bkd->bqk', q, k) / jnp.sqrt(jnp.float32(D)), axis=-1)
            y = xn + jnp.einsum('bqk,bkd->bqd', att, v)
            gelu = lambda t: jax.nn.gelu(t, approximate=False)
            return y + _fff(y, f_nw, f_nb, f_w1, f_b1, f_w2, f_b2, gelu)

        def _make_fff_params(key, scale_in, scale_leaf):
            ks = jax.random.split(key, 4)
            nw = jax.random.normal(ks[0], (NN, D), jnp.float32) * scale_in
            nb = jnp.zeros((NN,), jnp.float32)
            w1 = jax.random.normal(ks[1], (NL, D, LW), jnp.float32) * scale_in
            b1 = jax.random.normal(ks[2], (NL, LW), jnp.float32) * 0.01
            w2 = jax.random.normal(ks[3], (NL, LW, D), jnp.float32) * scale_leaf
            b2 = jnp.zeros((NL, D), jnp.float32)
            return (nw, nb, w1, b1, w2, b2)
        key = jax.random.key(seed)
        kx, kq, kk, kv, kf = jax.random.split(key, 5)
        s_in = 1.0 / np.sqrt(D)
        s_lf = 1.0 / np.sqrt(LW)
        inp = {'x': jax.random.normal(kx, (B, S, D), jnp.float32)}
        for name, kk_ in (('q', kq), ('k', kk), ('v', kv), ('f', kf)):
            nw, nb, w1, b1, w2, b2 = _make_fff_params(kk_, s_in, s_lf)
            inp.update({f'{name}_nw': nw, f'{name}_nb': nb, f'{name}_w1': w1, f'{name}_b1': b1, f'{name}_w2': w2, f'{name}_b2': b2})
        return inp
    _L1_ffn_all = _L1_ffn_setup()
    _L1_ffn_in = {k: v for k, v in _L1_ffn_all.items() if k in ('q_nw', 'q_nb', 'q_w1', 'q_b1', 'q_w2', 'q_b2', 'k_nw', 'k_nb', 'k_w1', 'k_b1', 'k_w2', 'k_b2', 'v_nw', 'v_nb', 'v_w1', 'v_b1', 'v_w2', 'v_b2', 'f_nw', 'f_nb', 'f_w1', 'f_b1', 'f_w2', 'f_b2')}
    del _L1_ffn_all

    def _L2_xattn_setup():
        import jax, jax.numpy as jnp
        import numpy as np
        B, N, DIM = (8, 512, 128)
        M, CTX = (32, 256)
        HEADS, DH = (16, 64)
        INNER = HEADS * DH
        EPS = 1e-06

        def _split_heads(t):
            b, n, _ = t.shape
            return t.reshape(b, n, HEADS, DH).transpose(0, 2, 1, 3)
        key = jax.random.key(seed)
        ks = jax.random.split(key, 6)
        x = jax.random.normal(ks[0], (B, N, DIM), dtype=jnp.float32)
        context = jax.random.normal(ks[1], (B, M, CTX), dtype=jnp.float32)
        Wq = jax.random.normal(ks[2], (DIM, INNER), dtype=jnp.float32) / np.sqrt(DIM)
        Wkv = jax.random.normal(ks[3], (CTX, 2 * INNER), dtype=jnp.float32) / np.sqrt(CTX)
        null_kv = jax.random.normal(ks[4], (2, DH), dtype=jnp.float32) / np.sqrt(2.0)
        Wout = jax.random.normal(ks[5], (INNER, DIM), dtype=jnp.float32) / np.sqrt(INNER)
        ln_scale = jnp.ones((DIM,), dtype=jnp.float32)
        ln_bias = jnp.zeros((DIM,), dtype=jnp.float32)
        return {'x': x, 'context': context, 'Wq': Wq, 'Wkv': Wkv, 'null_kv': null_kv, 'Wout': Wout, 'ln_scale': ln_scale, 'ln_bias': ln_bias}
    _L2_xattn_all = _L2_xattn_setup()
    _L2_xattn_in = {k: v for k, v in _L2_xattn_all.items() if k in ('Wq', 'Wkv', 'null_kv', 'Wout', 'ln_scale', 'ln_bias')}
    del _L2_xattn_all

    def _L2_ffn_setup():
        import jax, jax.numpy as jnp
        import numpy as np
        B, S, D = (1, 256, 128)
        E, F = (16, 128)
        NG, TKG, K = (4, 2, 4)
        NSH = 2
        SCALE = 2.5
        STD = 0.02
        EPG = E // NG

        def _route(x_flat, router_w, bias):
            logits = x_flat.astype(jnp.float32) @ router_w.T
            scores = jax.nn.sigmoid(logits)
            s = scores + bias[None, :]
            sg = s.reshape(-1, NG, EPG)
            group_score = jax.lax.top_k(sg, 2)[0].sum(-1)
            gidx = jax.lax.top_k(group_score, TKG)[1]
            gmask = jnp.sum(jax.nn.one_hot(gidx, NG, dtype=jnp.float32), axis=1) > 0
            emask = jnp.repeat(gmask, EPG, axis=1)
            masked = jnp.where(emask, s, -1.0)
            topk_idx = jax.lax.top_k(masked, K)[1]
            tw = jnp.take_along_axis(scores, topk_idx, axis=1)
            tw = tw / (tw.sum(-1, keepdims=True) + 1e-20)
            tw = tw * SCALE
            return (topk_idx, tw)
        key = jax.random.key(seed)
        ks = jax.random.split(key, 8)
        return {'hidden_states': jax.random.normal(ks[0], (B, S, D), jnp.float32), 'router_w': jax.random.normal(ks[1], (E, D), jnp.float32) * STD, 'bias': jnp.zeros((E,), jnp.float32), 'gate_w': jax.random.normal(ks[2], (E, D, F), jnp.float32) * STD, 'up_w': jax.random.normal(ks[3], (E, D, F), jnp.float32) * STD, 'down_w': jax.random.normal(ks[4], (E, F, D), jnp.float32) * STD, 'sh_gate_w': jax.random.normal(ks[5], (D, NSH * F), jnp.float32) * STD, 'sh_up_w': jax.random.normal(ks[6], (D, NSH * F), jnp.float32) * STD, 'sh_down_w': jax.random.normal(ks[7], (NSH * F, D), jnp.float32) * STD}
    _L2_ffn_all = _L2_ffn_setup()
    _L2_ffn_in = {k: v for k, v in _L2_ffn_all.items() if k in ('router_w', 'bias', 'gate_w', 'up_w', 'down_w', 'sh_gate_w', 'sh_up_w', 'sh_down_w')}
    del _L2_ffn_all

    def _L3_xattn_setup():
        import jax, jax.numpy as jnp
        import numpy as np
        NUM_HEADS = 16
        key = jax.random.key(seed)
        ks = jax.random.split(key, 5)
        dim = 128
        B, N, N_c = (4, 128, 32)
        x = jax.random.normal(ks[0], (B, N, dim), dtype=jnp.float32)
        context = jax.random.normal(ks[1], (B, N_c, 2 * dim), dtype=jnp.float32)
        w_qkv = jax.random.normal(ks[2], (3 * dim, dim), dtype=jnp.float32) * 0.02
        w_proj = jax.random.normal(ks[3], (dim, dim), dtype=jnp.float32) * 0.02
        b_proj = jax.random.normal(ks[4], (dim,), dtype=jnp.float32) * 0.02
        return {'x': x, 'context': context, 'w_qkv': w_qkv, 'w_proj': w_proj, 'b_proj': b_proj}
    _L3_xattn_all = _L3_xattn_setup()
    _L3_xattn_in = {k: v for k, v in _L3_xattn_all.items() if k in ('w_qkv', 'w_proj', 'b_proj')}
    del _L3_xattn_all

    def _L3_ffn_setup():
        import jax, jax.numpy as jnp
        import numpy as np
        D_MODEL = 128
        NUM_EXPERTS = 8
        HIDDEN = 512
        TOP_K = 2
        key = jax.random.key(seed)
        ks = jax.random.split(key, 6)
        x = jax.random.normal(ks[0], (2, 128, D_MODEL), dtype=jnp.float32)
        gate_w = jax.random.normal(ks[1], (NUM_EXPERTS, D_MODEL), dtype=jnp.float32) * (1.0 / np.sqrt(D_MODEL))
        w1 = jax.random.normal(ks[2], (NUM_EXPERTS, HIDDEN, D_MODEL), dtype=jnp.float32) * (1.0 / np.sqrt(D_MODEL))
        b1 = jax.random.normal(ks[3], (NUM_EXPERTS, HIDDEN), dtype=jnp.float32) * 0.01
        w2 = jax.random.normal(ks[4], (NUM_EXPERTS, D_MODEL, HIDDEN), dtype=jnp.float32) * (1.0 / np.sqrt(HIDDEN))
        b2 = jax.random.normal(ks[5], (NUM_EXPERTS, D_MODEL), dtype=jnp.float32) * 0.01
        return {'x': x, 'gate_w': gate_w, 'w1': w1, 'b1': b1, 'w2': w2, 'b2': b2}
    _L3_ffn_all = _L3_ffn_setup()
    _L3_ffn_in = {k: v for k, v in _L3_ffn_all.items() if k in ('gate_w', 'w1', 'b1', 'w2', 'b2')}
    del _L3_ffn_all
    return {'x': x, 'ctx_2048': ctx_2048, 'itok_Bx1_68_817': itok_Bx1_68_817, 'mask_BxS2_if0': mask_BxS2_if0, 'L0_xattn_b': _L0_xattn_in['b'], 'L0_ffn_Wr': _L0_ffn_in['Wr'], 'L0_ffn_Wqkv': _L0_ffn_in['Wqkv'], 'L0_ffn_Wo': _L0_ffn_in['Wo'], 'L1_xattn_W_in': _L1_xattn_in['W_in'], 'L1_xattn_b_in': _L1_xattn_in['b_in'], 'L1_xattn_g_res': _L1_xattn_in['g_res'], 'L1_xattn_g_init': _L1_xattn_in['g_init'], 'L1_ffn_q_nw': _L1_ffn_in['q_nw'], 'L1_ffn_q_nb': _L1_ffn_in['q_nb'], 'L1_ffn_q_w1': _L1_ffn_in['q_w1'], 'L1_ffn_q_b1': _L1_ffn_in['q_b1'], 'L1_ffn_q_w2': _L1_ffn_in['q_w2'], 'L1_ffn_q_b2': _L1_ffn_in['q_b2'], 'L1_ffn_k_nw': _L1_ffn_in['k_nw'], 'L1_ffn_k_nb': _L1_ffn_in['k_nb'], 'L1_ffn_k_w1': _L1_ffn_in['k_w1'], 'L1_ffn_k_b1': _L1_ffn_in['k_b1'], 'L1_ffn_k_w2': _L1_ffn_in['k_w2'], 'L1_ffn_k_b2': _L1_ffn_in['k_b2'], 'L1_ffn_v_nw': _L1_ffn_in['v_nw'], 'L1_ffn_v_nb': _L1_ffn_in['v_nb'], 'L1_ffn_v_w1': _L1_ffn_in['v_w1'], 'L1_ffn_v_b1': _L1_ffn_in['v_b1'], 'L1_ffn_v_w2': _L1_ffn_in['v_w2'], 'L1_ffn_v_b2': _L1_ffn_in['v_b2'], 'L1_ffn_f_nw': _L1_ffn_in['f_nw'], 'L1_ffn_f_nb': _L1_ffn_in['f_nb'], 'L1_ffn_f_w1': _L1_ffn_in['f_w1'], 'L1_ffn_f_b1': _L1_ffn_in['f_b1'], 'L1_ffn_f_w2': _L1_ffn_in['f_w2'], 'L1_ffn_f_b2': _L1_ffn_in['f_b2'], 'L2_xattn_Wq': _L2_xattn_in['Wq'], 'L2_xattn_Wkv': _L2_xattn_in['Wkv'], 'L2_xattn_null_kv': _L2_xattn_in['null_kv'], 'L2_xattn_Wout': _L2_xattn_in['Wout'], 'L2_xattn_ln_scale': _L2_xattn_in['ln_scale'], 'L2_xattn_ln_bias': _L2_xattn_in['ln_bias'], 'L2_ffn_router_w': _L2_ffn_in['router_w'], 'L2_ffn_bias': _L2_ffn_in['bias'], 'L2_ffn_gate_w': _L2_ffn_in['gate_w'], 'L2_ffn_up_w': _L2_ffn_in['up_w'], 'L2_ffn_down_w': _L2_ffn_in['down_w'], 'L2_ffn_sh_gate_w': _L2_ffn_in['sh_gate_w'], 'L2_ffn_sh_up_w': _L2_ffn_in['sh_up_w'], 'L2_ffn_sh_down_w': _L2_ffn_in['sh_down_w'], 'L3_xattn_w_qkv': _L3_xattn_in['w_qkv'], 'L3_xattn_w_proj': _L3_xattn_in['w_proj'], 'L3_xattn_b_proj': _L3_xattn_in['b_proj'], 'L3_ffn_gate_w': _L3_ffn_in['gate_w'], 'L3_ffn_w1': _L3_ffn_in['w1'], 'L3_ffn_b1': _L3_ffn_in['b1'], 'L3_ffn_w2': _L3_ffn_in['w2'], 'L3_ffn_b2': _L3_ffn_in['b2']}

def reference(x, ctx_2048, itok_Bx1_68_817, mask_BxS2_if0, L0_xattn_b, L0_ffn_Wr, L0_ffn_Wqkv, L0_ffn_Wo, L1_xattn_W_in, L1_xattn_b_in, L1_xattn_g_res, L1_xattn_g_init, L1_ffn_q_nw, L1_ffn_q_nb, L1_ffn_q_w1, L1_ffn_q_b1, L1_ffn_q_w2, L1_ffn_q_b2, L1_ffn_k_nw, L1_ffn_k_nb, L1_ffn_k_w1, L1_ffn_k_b1, L1_ffn_k_w2, L1_ffn_k_b2, L1_ffn_v_nw, L1_ffn_v_nb, L1_ffn_v_w1, L1_ffn_v_b1, L1_ffn_v_w2, L1_ffn_v_b2, L1_ffn_f_nw, L1_ffn_f_nb, L1_ffn_f_w1, L1_ffn_f_b1, L1_ffn_f_w2, L1_ffn_f_b2, L2_xattn_Wq, L2_xattn_Wkv, L2_xattn_null_kv, L2_xattn_Wout, L2_xattn_ln_scale, L2_xattn_ln_bias, L2_ffn_router_w, L2_ffn_bias, L2_ffn_gate_w, L2_ffn_up_w, L2_ffn_down_w, L2_ffn_sh_gate_w, L2_ffn_sh_up_w, L2_ffn_sh_down_w, L3_xattn_w_qkv, L3_xattn_w_proj, L3_xattn_b_proj, L3_ffn_gate_w, L3_ffn_w1, L3_ffn_b1, L3_ffn_w2, L3_ffn_b2):
    import jax
    import jax.numpy as jnp

    def _L0_xattn_ref(memory, query, b, seq_len):
        import jax, jax.numpy as jnp
        import numpy as np
        UNITS = 128
        NUM_HEADS = 16
        MASK_VALUE = -1000000000000.0

        def _split_heads(x, n):
            B, S, D = x.shape
            return x.reshape(B, S, n, D // n).transpose(0, 2, 1, 3)
        B, S, _ = query.shape
        dh = UNITS // NUM_HEADS
        k_mem, v_mem = jnp.split(memory, 2, axis=2)
        Q = _split_heads(query, NUM_HEADS) * dh ** (-0.5)
        Kh = _split_heads(k_mem, NUM_HEADS)
        Vh = _split_heads(v_mem, NUM_HEADS)
        logits = jnp.einsum('bhqd,bhkd->bhqk', Q, Kh) + b
        valid = (jnp.arange(S)[None, :] < seq_len[:, 0:1]).astype(jnp.float32)
        logits = logits + MASK_VALUE * (1.0 - valid)[:, None, None, :]
        weights = jax.nn.softmax(logits, axis=-1)
        out = jnp.einsum('bhqk,bhkd->bhqd', weights, Vh)
        return out.transpose(0, 2, 1, 3).reshape(B, S, UNITS)

    def _L0_ffn_ref(X, Wr, Wqkv, Wo):
        import math
        import jax, jax.numpy as jnp
        import numpy as np
        E = 8
        H = 128
        HP = 128
        SPARSITY = 8
        N_ROTATE = 64
        ROPE_BASE = 10000.0

        def _rope(x, pos):
            half = N_ROTATE // 2
            inv_freq = 1.0 / ROPE_BASE ** (jnp.arange(half, dtype=jnp.float32) * 2.0 / N_ROTATE)
            ang = pos.astype(jnp.float32)[..., None] * inv_freq
            sin, cos = (jnp.sin(ang), jnp.cos(ang))
            x1, x2 = (x[..., :half], x[..., half:])
            return jnp.concatenate([x1 * cos - x2 * sin, x2 * cos + x1 * sin], axis=-1)
        B, T, _ = X.shape
        k = min(max(T // SPARSITY, 2), T)
        logits = jax.nn.sigmoid(jnp.einsum('bth,eh->bte', X, Wr))
        topk_vals, topk_I = jax.lax.top_k(logits.transpose(0, 2, 1), k)
        idx_flat = topk_I.reshape(B, E * k)
        Xg = jnp.take_along_axis(X, idx_flat[:, :, None], axis=1).reshape(B, E, k, H)
        QKV = jnp.einsum('beki,eij->bekj', Xg, Wqkv)
        Q, K, V = jnp.split(QKV, 3, axis=-1)
        Q = jnp.concatenate([_rope(Q[..., :N_ROTATE], topk_I), Q[..., N_ROTATE:]], axis=-1)
        K = jnp.concatenate([_rope(K[..., :N_ROTATE], topk_I), K[..., N_ROTATE:]], axis=-1)
        M = topk_I[..., :, None] >= topk_I[..., None, :]
        scores = jnp.einsum('bekd,bemd->bekm', Q, K) / math.sqrt(HP)
        scores = jnp.where(M, scores, -jnp.inf)
        A = jax.nn.softmax(scores, axis=-1)
        AV = jnp.einsum('bekm,bemd->bekd', A, V)
        AV = AV * topk_vals[..., None]
        Xpre = jnp.einsum('bekj,eji->beki', AV, Wo)
        out = jnp.zeros((B, T, H), dtype=X.dtype)
        out = out.at[jnp.arange(B)[:, None], idx_flat].add(Xpre.reshape(B, E * k, H))
        return out

    def _L1_xattn_ref(embeds, patch_embeds, patch_lens, W_in, b_in, g_res, g_init):
        import jax, jax.numpy as jnp
        import numpy as np
        B, L, P = (4, 512, 128)
        D_MODEL = 128
        D_GLOBAL = 256
        HEADDIM = 32
        EPSILON = 0.001
        RMS_EPS = 1e-05

        def rmsnorm(x, g, eps=RMS_EPS):
            var = jnp.mean(jnp.square(x), axis=-1, keepdims=True)
            return x * jax.lax.rsqrt(var + eps) * g

        def _hnet_depool(h, h_patch_full, patch_lens):
            h_patch = h_patch_full[..., :D_MODEL]
            bsz, plen = (h_patch.shape[0], h_patch.shape[1])
            seqlen = h.shape[1]
            logp = jnp.full((bsz, plen), -EPSILON, dtype=jnp.float32)
            bidx = jnp.cumsum(patch_lens, axis=1) - 1
            boundary_mask = jnp.zeros((bsz, seqlen), dtype=jnp.int32)
            boundary_mask = boundary_mask.at[jnp.arange(bsz)[:, None], bidx].set(1)
            dt = (-jnp.log(-jnp.expm1(logp))).astype(h_patch.dtype)
            x = h_patch / dt[..., None]
            n_heads = D_MODEL // HEADDIM
            A = -jnp.ones((n_heads,), dtype=jnp.float32)
            bcoef = jnp.exp(logp).astype(h_patch.dtype)
            x4 = x.reshape(bsz, plen, n_heads, HEADDIM)
            a = jnp.exp(dt[:, :, None] * A[None, None, :])
            u = (dt * bcoef)[:, :, None, None] * x4
            a_b = jnp.broadcast_to(a[..., None], u.shape)

            def comb(lft, rgt):
                aL, uL = lft
                aR, uR = rgt
                return (aL * aR, uL * aR + uR)
            _, s = jax.lax.associative_scan(comb, (a_b, u), axis=1)
            depool = s.reshape(bsz, plen, D_MODEL)
            plug = jnp.clip(jnp.cumsum(boundary_mask, axis=1) - 1, 0, plen - 1)
            depool_out = depool[jnp.arange(bsz)[:, None], plug]
            return depool_out + h
        h = rmsnorm(embeds, g_res)
        h = jnp.einsum('bld,ed->ble', h, W_in) + b_in
        h_patch = rmsnorm(patch_embeds, g_init)
        return _hnet_depool(h, h_patch, patch_lens)

    def _L1_ffn_ref(x, q_nw, q_nb, q_w1, q_b1, q_w2, q_b2, k_nw, k_nb, k_w1, k_b1, k_w2, k_b2, v_nw, v_nb, v_w1, v_b1, v_w2, v_b2, f_nw, f_nb, f_w1, f_b1, f_w2, f_b2):
        import jax, jax.numpy as jnp
        import numpy as np
        D = 128
        LW = 16
        DEPTH = 8
        NN = 2 ** DEPTH - 1
        NL = 2 ** DEPTH
        B, S = (2, 128)

        def _fff(x, nw, nb, w1, b1, w2, b2, act):
            node = jnp.zeros(x.shape[:2], dtype=jnp.int32)
            for _ in range(DEPTH):
                logit = jnp.einsum('bsd,bsd->bs', x, nw[node]) + nb[node]
                node = 2 * node + 1 + (logit > 0).astype(jnp.int32)
            leaf = node - NN
            h = act(jnp.einsum('bsd,bsdl->bsl', x, w1[leaf]) + b1[leaf])
            return jnp.einsum('bsl,bsld->bsd', h, w2[leaf]) + b2[leaf]

        def _forward(x, q_nw, q_nb, q_w1, q_b1, q_w2, q_b2, k_nw, k_nb, k_w1, k_b1, k_w2, k_b2, v_nw, v_nb, v_w1, v_b1, v_w2, v_b2, f_nw, f_nb, f_w1, f_b1, f_w2, f_b2):
            mu = jnp.mean(x, -1, keepdims=True)
            sd = jnp.std(x, -1, ddof=1, keepdims=True)
            xn = (x - mu) / jnp.sqrt(sd + 1e-05)
            relu = jax.nn.relu
            q = _fff(xn, q_nw, q_nb, q_w1, q_b1, q_w2, q_b2, relu)
            k = _fff(xn, k_nw, k_nb, k_w1, k_b1, k_w2, k_b2, relu)
            v = _fff(xn, v_nw, v_nb, v_w1, v_b1, v_w2, v_b2, relu)
            att = jax.nn.softmax(jnp.einsum('bqd,bkd->bqk', q, k) / jnp.sqrt(jnp.float32(D)), axis=-1)
            y = xn + jnp.einsum('bqk,bkd->bqd', att, v)
            gelu = lambda t: jax.nn.gelu(t, approximate=False)
            return y + _fff(y, f_nw, f_nb, f_w1, f_b1, f_w2, f_b2, gelu)

        def _make_fff_params(key, scale_in, scale_leaf):
            ks = jax.random.split(key, 4)
            nw = jax.random.normal(ks[0], (NN, D), jnp.float32) * scale_in
            nb = jnp.zeros((NN,), jnp.float32)
            w1 = jax.random.normal(ks[1], (NL, D, LW), jnp.float32) * scale_in
            b1 = jax.random.normal(ks[2], (NL, LW), jnp.float32) * 0.01
            w2 = jax.random.normal(ks[3], (NL, LW, D), jnp.float32) * scale_leaf
            b2 = jnp.zeros((NL, D), jnp.float32)
            return (nw, nb, w1, b1, w2, b2)
        return _forward(x, q_nw, q_nb, q_w1, q_b1, q_w2, q_b2, k_nw, k_nb, k_w1, k_b1, k_w2, k_b2, v_nw, v_nb, v_w1, v_b1, v_w2, v_b2, f_nw, f_nb, f_w1, f_b1, f_w2, f_b2)

    def _L2_xattn_ref(x, context, Wq, Wkv, null_kv, Wout, ln_scale, ln_bias):
        import jax, jax.numpy as jnp
        import numpy as np
        B, N, DIM = (8, 512, 128)
        M, CTX = (32, 256)
        HEADS, DH = (16, 64)
        INNER = HEADS * DH
        EPS = 1e-06

        def _split_heads(t):
            b, n, _ = t.shape
            return t.reshape(b, n, HEADS, DH).transpose(0, 2, 1, 3)
        scale = DH ** (-0.5)
        b = x.shape[0]
        q = _split_heads(jnp.einsum('bnd,df->bnf', x, Wq))
        kv = jnp.einsum('bmc,cf->bmf', context, Wkv)
        k, v = jnp.split(kv, 2, axis=-1)
        k, v = (_split_heads(k), _split_heads(v))
        nk = jnp.broadcast_to(null_kv[0], (b, HEADS, 1, DH))
        nv = jnp.broadcast_to(null_kv[1], (b, HEADS, 1, DH))
        k = jnp.concatenate((nk, k), axis=-2)
        v = jnp.concatenate((nv, v), axis=-2)
        q = q * scale
        sim = jnp.einsum('bhid,bhjd->bhij', q, k)
        attn = jax.nn.softmax(sim, axis=-1)
        out = jnp.einsum('bhij,bhjd->bhid', attn, v)
        out = out.transpose(0, 2, 1, 3).reshape(b, -1, INNER)
        out = jnp.einsum('bnf,fd->bnd', out, Wout)
        mu = jnp.mean(out, axis=-1, keepdims=True)
        var = jnp.var(out, axis=-1, keepdims=True)
        out = (out - mu) * jax.lax.rsqrt(var + EPS) * ln_scale + ln_bias
        return out

    def _L2_ffn_ref(hidden_states, router_w, bias, gate_w, up_w, down_w, sh_gate_w, sh_up_w, sh_down_w):
        import jax, jax.numpy as jnp
        import numpy as np
        B, S, D = (1, 256, 128)
        E, F = (16, 128)
        NG, TKG, K = (4, 2, 4)
        NSH = 2
        SCALE = 2.5
        STD = 0.02
        EPG = E // NG

        def _route(x_flat, router_w, bias):
            logits = x_flat.astype(jnp.float32) @ router_w.T
            scores = jax.nn.sigmoid(logits)
            s = scores + bias[None, :]
            sg = s.reshape(-1, NG, EPG)
            group_score = jax.lax.top_k(sg, 2)[0].sum(-1)
            gidx = jax.lax.top_k(group_score, TKG)[1]
            gmask = jnp.sum(jax.nn.one_hot(gidx, NG, dtype=jnp.float32), axis=1) > 0
            emask = jnp.repeat(gmask, EPG, axis=1)
            masked = jnp.where(emask, s, -1.0)
            topk_idx = jax.lax.top_k(masked, K)[1]
            tw = jnp.take_along_axis(scores, topk_idx, axis=1)
            tw = tw / (tw.sum(-1, keepdims=True) + 1e-20)
            tw = tw * SCALE
            return (topk_idx, tw)
        x = hidden_states.reshape(-1, D)
        topk_idx, tw = _route(x, router_w, bias)
        combine = (jax.nn.one_hot(topk_idx, E, dtype=tw.dtype) * tw[..., None]).sum(1)
        h = jnp.einsum('td,edf->etf', x, gate_w)
        u = jnp.einsum('td,edf->etf', x, up_w)
        y = jnp.einsum('etf,efd->etd', jax.nn.silu(h) * u, down_w)
        routed = jnp.einsum('etd,te->td', y, combine)
        sh = jax.nn.silu(x @ sh_gate_w) * (x @ sh_up_w) @ sh_down_w
        return (routed + sh).reshape(hidden_states.shape)

    def _L3_xattn_ref(x, context, w_qkv, w_proj, b_proj):
        import jax, jax.numpy as jnp
        import numpy as np
        NUM_HEADS = 16
        B, N, C = x.shape
        H = NUM_HEADS
        D = C // H
        scale = D ** (-0.5)
        qkv = (x @ w_qkv.T).reshape(B, N, 3, H, D).transpose(2, 0, 3, 1, 4)
        q, k, v = (qkv[0], qkv[1], qkv[2])
        N_c = context.shape[1]
        kv = context.reshape(B, N_c, 2, H, D).transpose(2, 0, 3, 1, 4)
        extra_k, extra_v = (kv[0], kv[1])
        k = jnp.concatenate([extra_k, k], axis=2)
        v = jnp.concatenate([extra_v, v], axis=2)
        dtype = q.dtype
        attn = jnp.einsum('bhnd,bhmd->bhnm', q * scale, k).astype(jnp.float32)
        attn = jax.nn.softmax(attn, axis=-1).astype(dtype)
        out = jnp.einsum('bhnm,bhmd->bhnd', attn, v)
        out = out.transpose(0, 2, 1, 3).reshape(B, N, C)
        return out @ w_proj.T + b_proj

    def _L3_ffn_ref(x, gate_w, w1, b1, w2, b2):
        import jax, jax.numpy as jnp
        import numpy as np
        D_MODEL = 128
        NUM_EXPERTS = 8
        HIDDEN = 512
        TOP_K = 2
        B, S, D = x.shape
        xf = x.reshape(-1, D)
        T = xf.shape[0]
        gate_logits = xf @ gate_w.T
        gate_probs = jax.nn.softmax(gate_logits, axis=-1)
        topk_scores, topk_idx = jax.lax.top_k(gate_probs, TOP_K)
        topk_scores = topk_scores / jnp.sum(topk_scores, axis=-1, keepdims=True)
        combine = jnp.zeros((T, NUM_EXPERTS), dtype=x.dtype)
        combine = combine.at[jnp.arange(T)[:, None], topk_idx].set(topk_scores)
        h = jax.nn.relu(jnp.einsum('td,ehd->teh', xf, w1) + b1)
        expert_out = jnp.einsum('teh,edh->ted', h, w2) + b2
        out = jnp.einsum('ted,te->td', expert_out, combine)
        return out.reshape(B, S, D)
    x = x + _L0_xattn_ref(ctx_2048, _layernorm(x, axis=-1), L0_xattn_b, itok_Bx1_68_817)
    x = x + _L0_ffn_ref(_layernorm(x, axis=-1), L0_ffn_Wr, L0_ffn_Wqkv, L0_ffn_Wo)
    x = x + _L1_xattn_ref(_layernorm(x, axis=-1), ctx_2048, mask_BxS2_if0, L1_xattn_W_in, L1_xattn_b_in, L1_xattn_g_res, L1_xattn_g_init)
    x = x + _L1_ffn_ref(_layernorm(x, axis=-1), L1_ffn_q_nw, L1_ffn_q_nb, L1_ffn_q_w1, L1_ffn_q_b1, L1_ffn_q_w2, L1_ffn_q_b2, L1_ffn_k_nw, L1_ffn_k_nb, L1_ffn_k_w1, L1_ffn_k_b1, L1_ffn_k_w2, L1_ffn_k_b2, L1_ffn_v_nw, L1_ffn_v_nb, L1_ffn_v_w1, L1_ffn_v_b1, L1_ffn_v_w2, L1_ffn_v_b2, L1_ffn_f_nw, L1_ffn_f_nb, L1_ffn_f_w1, L1_ffn_f_b1, L1_ffn_f_w2, L1_ffn_f_b2)
    x = x + _L2_xattn_ref(_layernorm(x, axis=-1), ctx_2048, L2_xattn_Wq, L2_xattn_Wkv, L2_xattn_null_kv, L2_xattn_Wout, L2_xattn_ln_scale, L2_xattn_ln_bias)
    x = x + _L2_ffn_ref(_layernorm(x, axis=-1), L2_ffn_router_w, L2_ffn_bias, L2_ffn_gate_w, L2_ffn_up_w, L2_ffn_down_w, L2_ffn_sh_gate_w, L2_ffn_sh_up_w, L2_ffn_sh_down_w)
    x = x + _L3_xattn_ref(_layernorm(x, axis=-1), ctx_2048, L3_xattn_w_qkv, L3_xattn_w_proj, L3_xattn_b_proj)
    x = x + _L3_ffn_ref(_layernorm(x, axis=-1), L3_ffn_gate_w, L3_ffn_w1, L3_ffn_b1, L3_ffn_w2, L3_ffn_b2)
    return x

_drawn_inputs = setup_inputs


def setup_inputs(seed=0):
    import zlib

    import numpy as np

    out = dict(_drawn_inputs(seed))
    spreads = {'L1_xattn_b_in': (0.0, 0.1),
     'L1_xattn_g_res': (1.0, 0.2),
     'L1_xattn_g_init': (1.0, 0.2),
     'L1_ffn_q_nb': (0.0, 0.1),
     'L1_ffn_q_b2': (0.0, 0.1),
     'L1_ffn_k_nb': (0.0, 0.1),
     'L1_ffn_k_b2': (0.0, 0.1),
     'L1_ffn_v_nb': (0.0, 0.1),
     'L1_ffn_v_b2': (0.0, 0.1),
     'L1_ffn_f_nb': (0.0, 0.1),
     'L1_ffn_f_b2': (0.0, 0.1),
     'L2_xattn_ln_scale': (1.0, 0.2),
     'L2_xattn_ln_bias': (0.0, 0.1),
     'L2_ffn_bias': (0.0, 0.8)}
    factors = {'L1_ffn_q_b1': 8.0,
     'L1_ffn_k_b1': 8.0,
     'L1_ffn_v_b1': 5.941,
     'L1_ffn_f_b1': 8.0,
     'L2_xattn_null_kv': 5.526,
     'L2_ffn_router_w': 8.0,
     'L2_ffn_gate_w': 8.0,
     'L2_ffn_up_w': 8.0,
     'L2_ffn_down_w': 8.0,
     'L2_ffn_sh_gate_w': 8.0,
     'L2_ffn_sh_up_w': 8.0,
     'L2_ffn_sh_down_w': 8.0,
     'L3_xattn_w_qkv': 30.166,
     'L3_xattn_b_proj': 20.742,
     'L3_ffn_b1': 64.0,
     'L3_ffn_b2': 59.723,
     'L3_xattn_w_proj': 5.075}
    for name, (base, spread) in spreads.items():
        noise = np.random.default_rng([zlib.crc32(name.encode()), seed]).standard_normal(out[name].shape)
        drawn = base * np.exp(spread * noise) if base else spread * noise
        out[name] = jnp.asarray(drawn.astype(out[name].dtype))
    for name, factor in factors.items():
        out[name] = (out[name] * factor).astype(out[name].dtype)
    return out
```

```python
from contextlib import ExitStack, contextmanager

import numpy as np

import concourse.bass as bass
from concourse import mybir

F32 = mybir.dt.float32
I32 = mybir.dt.int32
U32 = mybir.dt.uint32
ALU = mybir.AluOpType
ACT = mybir.ActivationFunctionType
AX = mybir.AxisListType

P = 128
B = 16
T = 128
D = 128
CTX = 256
LANES = 2
LN_EPS = 1e-5
NEG = -1e30

ROPE_HALF, ROPE_N, ROPE_BASE = 32, 64, 10000.0
E0, K0 = 8, 16
NODES, LEAVES, LW = 255, 256, 16
LOGP = -0.001


def constant_columns():
    p = np.arange(P)[:, None]
    c = np.arange(P)[None, :]
    f = np.float32
    inv = (1.0 / np.power(f(ROPE_BASE), np.arange(ROPE_HALF, dtype=f) * f(2.0) / f(ROPE_N))).astype(f)
    ang = (np.arange(T, dtype=f)[:, None] * inv).astype(f)
    sin, cos = np.sin(ang), np.cos(ang)
    dt = -np.log(-np.expm1(LOGP))
    power = np.maximum(c - p, 0)
    pair = np.arange(16)
    return {
        "ident": (p == c),
        "iota_row": np.broadcast_to(c, (P, P)),
        "iota_row2": np.broadcast_to(c + P, (P, P)),
        "iota_col": p,
        "upto": (p <= c),
        "ones": np.ones((P, P)),
        "headmask": (p // 8 % 4 == np.arange(4)[None, :]),
        "cos": np.concatenate([cos, cos], 1),
        "sin": np.concatenate([-sin, sin], 1),
        "sameexpert": (p // K0 == c // K0),
        "expertmask": (p // K0 == np.arange(E0)[None, :]),
        "decay": np.where(c >= p, np.exp(-dt * power), 0.0),
        "before16": np.broadcast_to((pair[None, :] < pair[:, None]).reshape(1, 256), (P, 256)),
    }


def constant_offsets():
    at, n = {}, 0
    for name, a in constant_columns().items():
        at[name] = (n, n + a.shape[1])
        n += a.shape[1]
    return at, n


class Phase:

    def __init__(self, nc, name):
        self.nc, self.name, self.ctx, self.sems = nc, name, ExitStack(), []

    def sb(self, name, shape, dt=F32):
        return self.ctx.enter_context(self.nc.sbuf_tensor(f"{self.name}_{name}", shape, dt))

    def ps(self, name, shape):
        return self.ctx.enter_context(self.nc.psum_tensor(f"{self.name}_{name}", shape, F32))

    def sem(self, name):
        s = self.nc.alloc_semaphore(f"{self.name}_{name}")
        self.sems.append(s)
        return s

    def close(self):
        self.nc.clear_and_free_semaphores(self.sems)
        self.nc.all_engine_barrier()
        self.ctx.close()


@contextmanager
def phase(nc, name):
    ph = Phase(nc, name)
    yield ph
    ph.close()


class Steps:

    def __init__(self, eng, sem):
        self.eng, self.sem, self.n = eng, sem, 0

    def __call__(self, ins):
        self.n += 1
        ins.then_inc(self.sem, 1)
        self.eng.wait_ge(self.sem, self.n)

    def restart(self):
        self.eng.sem_clear(self.sem)
        self.n = 0


class Shared:
    pass


def layer_norm_coefficients(v, step, S, stats_done, pow_ready):
    me, mo = S.stats[:, :, 1], S.stats[:, :, 4]
    ve, vo = S.stats[:, :, 2], S.stats[:, :, 5]
    step(v.tensor_tensor(S.mean[:, :], me, mo, ALU.add))
    step(v.tensor_tensor(S.dif[:, :], me, mo, ALU.subtract))
    step(v.tensor_scalar(S.mean[:, :], S.mean[:, :], 0.5, None, ALU.mult))
    step(v.tensor_tensor(S.var[:, :], ve, vo, ALU.add))
    step(v.scalar_tensor_tensor(out=S.dif[:, :], in0=S.dif[:, :], scalar=0.25, in1=S.dif[:, :],
                                op0=ALU.mult, op1=ALU.mult))
    step(v.scalar_tensor_tensor(out=S.var[:, :], in0=S.var[:, :], scalar=1.0 / D, in1=S.dif[:, :],
                                op0=ALU.mult, op1=ALU.add))
    v.tensor_scalar(S.var[:, :], S.var[:, :], LN_EPS, None, ALU.add).then_inc(stats_done, 1)
    v.wait_ge(pow_ready, 1)


def inverse_roots(g, S, stats_done, pow_ready):
    g.wait_ge(stats_done, 1)
    g.tensor_tensor(S.rstd[:, :], S.var[:, :], S.mhalf[:, :], ALU.pow).then_inc(pow_ready, 1)


def small_head_attention(nc, S, name, own_keys, seq_len=None, bias=None, weights=None):
    HEADS, DH = 16, 8
    SETS = 2 if own_keys else 1
    HPC = 1024 // (SETS * P)
    CHUNKS = HEADS // HPC
    with phase(nc, name) as ph:
        lanes = range(LANES)
        xn = [ph.sb(f"xn{l}", [P, D]) for l in lanes]
        xnT = [ph.sb(f"xnT{l}", [P, T]) for l in lanes]
        qT = [ph.sb(f"qT{l}", [P, T]) for l in lanes]
        kmask = [ph.sb(f"kmask{l}", [P, SETS, 4, P]) for l in lanes]
        probs = [ph.sb(f"probs{l}", [P, HEADS, SETS, P]) for l in lanes]
        probsT = [ph.sb(f"probsT{l}", [P, HEADS, SETS, P]) for l in lanes]
        vals = [ph.sb(f"vals{l}", [P, SETS, HEADS, DH + 1]) for l in lanes]
        mx = [ph.sb(f"mx{l}", [P, HEADS]) for l in lanes]
        rs = [ph.sb(f"rs{l}", [P, HEADS]) for l in lanes]
        osb = [ph.sb(f"osb{l}", [P, HEADS, DH]) for l in lanes]
        psA = [ph.ps(f"psA{l}", [P, 1024]) for l in lanes]
        psB = [ph.ps(f"psB{l}", [P, 1024]) for l in lanes]

        dve_step, pool_step, act_step = ph.sem("dve_step"), ph.sem("pool_step"), ph.sem("act_step")
        stats_done, pow_ready = ph.sem("stats_done"), ph.sem("pow_ready")
        xn_ready, xnT_ready, q_ready = ph.sem("xn_ready"), ph.sem("xnT_ready"), ph.sem("q_ready")
        keys_ready, scores_ready, shifted = ph.sem("keys_ready"), ph.sem("scores_ready"), ph.sem("shifted")
        exp_ready, turned, probsT_ready = ph.sem("exp_ready"), ph.sem("turned"), ph.sem("probsT_ready")
        out_ready, vals_ready = ph.sem("out_ready"), ph.sem("vals_ready")
        if own_keys:
            xnT_sb_ready, qkv_ready, kT_ready = ph.sem("xnT_sb_ready"), ph.sem("qkv_ready"), ph.sem("kT_ready")
            o_sb_ready, oT_ready, oT_sb_ready, proj_ready = (ph.sem(x) for x in
                                                             ("o_sb_ready", "oT_ready", "oT_sb_ready", "proj_ready"))
            kT = [ph.sb(f"kT{l}", [P, P]) for l in lanes]
            oT = [ph.sb(f"oT{l}", [P, P]) for l in lanes]
        else:
            len_i = ph.sb("len_i", [P, B], I32)
            len_f = ph.sb("len_f", [P, B])
            bias_row = ph.sb("bias_row", [P, P])
            bias_row_b = [ph.sb(f"bias_row_b{l}", [P, P]) for l in lanes]
            len_loaded = ph.sem("len_loaded")

        def chunk_count(i, c, l):
            return i * (CHUNKS * LANES) + (c * LANES + l + 1)

        with nc.Block() as block:
            if not own_keys:
                @block.sync
                def _(sp):
                    sp.dma_start(len_i[:, :], seq_len.partition_broadcast(P)).then_inc(len_loaded, 16)
                    sp.dma_start(bias_row[:, :], bias.partition_broadcast(P)).then_inc(len_loaded, 16)

            @block.gpsimd
            def _(g):
                step = Steps(g, pool_step)
                for l in lanes:
                    g.memset(vals[l][:, :, :, :], 1.0).then_inc(vals_ready, 1)
                inverse_roots(g, S, stats_done, pow_ready)
                with g.Fori(0, B // LANES) as i:
                    for l in lanes:
                        g.wait_ge(scores_ready, 1 + i * (CHUNKS * LANES))
                        g.tensor_tensor(kmask[l][:, 0, :, :],
                                        S.ctxT[:, 0, bass.ds(i * LANES + l, 1), :].broadcast_to([P, 4, P]),
                                        S.headmask.unsqueeze(2).broadcast_to([P, 4, P]),
                                        ALU.mult).then_inc(keys_ready, 1)
                    for l in lanes:
                        if own_keys:
                            g.wait_ge(kT_ready, i * LANES + l + 1)
                            g.tensor_tensor(kmask[l][:, 1, :, :],
                                            kT[l][:, :].unsqueeze(1).broadcast_to([P, 4, P]),
                                            S.headmask.unsqueeze(2).broadcast_to([P, 4, P]),
                                            ALU.mult).then_inc(keys_ready, 1)

            @block.vector
            def _(v):
                step = Steps(v, dve_step)
                layer_norm_coefficients(v, step, S, stats_done, pow_ready)
                if not own_keys:
                    v.wait_ge(len_loaded, 32)
                    step(v.tensor_copy(len_f[:, :], len_i[:, :]))
                with v.Fori(0, B // LANES) as i:
                    step.restart()
                    for l in lanes:
                        b = i * LANES + l
                        v.tensor_scalar(xn[l][:, :], S.x[:, b, :], S.mean[:, bass.ds(b, 1)], S.rstd[:, bass.ds(b, 1)],
                                        ALU.subtract, ALU.mult).then_inc(xn_ready, 1)
                        if not own_keys:
                            step(v.tensor_scalar(bias_row_b[l][:, :], S.iota_row, len_f[:, bass.ds(b, 1)], -1e12,
                                                 ALU.is_ge, ALU.mult))
                            step(v.tensor_tensor(bias_row_b[l][:, :], bias_row_b[l][:, :], bias_row[:, :], ALU.add))
                    for c in range(CHUNKS):
                        for l in lanes:
                            heads = slice(c * HPC, (c + 1) * HPC)
                            pr = probs[l][:, heads, :, :]
                            ps = psA[l][:, :].rearrange("p (s j k) -> p j s k", s=SETS, j=HPC)
                            v.wait_ge(scores_ready, 1 + chunk_count(i, c, l))
                            src = ps
                            if not own_keys:
                                step(v.tensor_tensor(pr[:, :, 0, :], ps[:, :, 0, :],
                                                     bias_row_b[l][:, :].unsqueeze(1).broadcast_to([P, HPC, P]),
                                                     ALU.add))
                                src = pr
                            step(v.tensor_reduce(mx[l][:, heads], src, AX.XY, ALU.max))
                            v.tensor_tensor(pr, src, mx[l][:, heads].unsqueeze(2).unsqueeze(3)
                                            .broadcast_to([P, HPC, SETS, P]), ALU.subtract).then_inc(shifted, 1)
                    for l in lanes:
                        b = i * LANES + l
                        ov = psA[l][:, 0:HEADS * (DH + 1)].rearrange("p (h d) -> p h d", d=DH + 1)
                        v.wait_ge(out_ready, 1 + i * LANES + l + 1)
                        step(v.reciprocal(rs[l][:, :], ov[:, :, DH]))
                        ins = v.tensor_tensor(osb[l][:, :, :], ov[:, :, 0:DH],
                                              rs[l][:, :].unsqueeze(2).broadcast_to([P, HEADS, DH]), ALU.mult)
                        if own_keys:
                            ins.then_inc(o_sb_ready, 1)
                        else:
                            step(ins)
                            step(v.tensor_tensor(S.x[:, b, :], S.x[:, b, :],
                                                 osb[l][:, :, :].rearrange("p h d -> p (h d)"), ALU.add))
                            step(v.bn_stats(S.stats[:, b, :], S.x[:, b, :]))
                    if own_keys:
                        for l in lanes:
                            b = i * LANES + l
                            ob = xn[l]
                            v.wait_ge(proj_ready, i * LANES + l + 1)
                            step(v.tensor_tensor(ob[:, :], psB[l][:, 0:D], weights["b_proj"], ALU.add))
                            step(v.tensor_tensor(S.x[:, b, :], S.x[:, b, :], ob[:, :], ALU.add))
                            step(v.bn_stats(S.stats[:, b, :], S.x[:, b, :]))

            @block.scalar
            def _(a):
                with a.Fori(0, B // LANES) as i:
                    for l in lanes:
                        b = i * LANES + l
                        if l == 0:
                            a.wait_ge(vals_ready, 2)
                        a.wait_ge(out_ready, 1 + i * LANES)
                        a.activation(vals[l][:, 0, :, 0:DH],
                                     S.ctx[:, bass.ds(b, 1), P:2 * P].rearrange("p o (h d) -> p (o h) d", d=DH), ACT.Copy)
                        a.wait_ge(xnT_ready, b + 1)
                        if not own_keys:
                            a.activation(qT[l][:, :], psB[l][:, 0:T], ACT.Copy, scale=DH ** -0.5).then_inc(q_ready, 1)
                        else:
                            a.activation(xnT[l][:, :], psB[l][:, 0:T], ACT.Copy).then_inc(xnT_sb_ready, 1)
                    if own_keys:
                        for l in lanes:
                            a.wait_ge(qkv_ready, i * LANES + l + 1)
                            a.activation(qT[l][:, :], psA[l][:, 0:T], ACT.Copy, scale=DH ** -0.5)
                            a.activation(kT[l][:, :], psA[l][:, T:2 * T], ACT.Copy).then_inc(kT_ready, 1)
                            a.activation(vals[l][:, 1, :, 0:DH],
                                         psA[l][:, 2 * T:3 * T].rearrange("p (h d) -> p h d", d=DH),
                                         ACT.Copy).then_inc(q_ready, 1)
                    for c in range(CHUNKS):
                        for l in lanes:
                            pr = probs[l][:, c * HPC:(c + 1) * HPC, :, :]
                            a.wait_ge(shifted, chunk_count(i, c, l))
                            a.activation(pr, pr, ACT.Exp).then_inc(exp_ready, 1)
                        for l in lanes:
                            a.wait_ge(turned, chunk_count(i, c, l))
                            a.activation(probsT[l][:, c * HPC:(c + 1) * HPC, :, :].rearrange("p j s k -> p (j s k)"),
                                         psB[l][:, :], ACT.Copy).then_inc(probsT_ready, 1)
                    if own_keys:
                        for l in lanes:
                            a.wait_ge(oT_ready, i * LANES + l + 1)
                            a.activation(oT[l][:, :], psB[l][:, 512:512 + T], ACT.Copy).then_inc(oT_sb_ready, 1)

            @block.tensor
            def _(t):
                t.sem_inc(out_ready, 1)
                t.sem_inc(scores_ready, 1)
                with t.Fori(0, B // LANES) as i:
                    for l in lanes:
                        t.wait_ge(xn_ready, i * LANES + l + 1)
                        t.transpose(psB[l][:, 0:T], xn[l][:, :], S.ident).then_inc(xnT_ready, 1)
                    if own_keys:
                        for l in lanes:
                            t.wait_ge(xnT_sb_ready, i * LANES + l + 1)
                            t.matmul(psA[l][:, 0:T], weights["wqT"], xnT[l][:, :], start=True, stop=True)
                            t.matmul(psA[l][:, T:2 * T], weights["wkT"], xnT[l][:, :], start=True, stop=True)
                            t.matmul(psA[l][:, 2 * T:3 * T], xnT[l][:, :], weights["wvT"], start=True,
                                     stop=True).then_inc(qkv_ready, 1)

                    def scores(c, l):
                        if c == 0:
                            t.wait_ge(q_ready, i * LANES + l + 1)
                            t.wait_ge(keys_ready, i * (LANES * SETS) + (l + 1 + LANES * (SETS - 1)))
                        else:
                            t.wait_ge(shifted, chunk_count(i, c - 1, l))
                        for n in range(2):
                            g4, s = (c, n) if own_keys else (2 * c + n, 0)
                            rows = slice(32 * g4, 32 * g4 + 32)
                            mm = t.matmul(psA[l][:, n * 512:(n + 1) * 512], qT[l][rows, :],
                                          kmask[l][rows, s, :, :], start=True, stop=True)
                        mm.then_inc(scores_ready, 1)

                    for l in lanes:
                        scores(0, l)
                    for c in range(CHUNKS):
                        if c + 1 < CHUNKS:
                            for l in lanes:
                                scores(c + 1, l)
                        for l in lanes:
                            t.wait_ge(exp_ready, chunk_count(i, c, l))
                            if c:
                                t.wait_ge(probsT_ready, chunk_count(i, c - 1, l))
                            for n in range(8):
                                h, s = c * HPC + n // SETS, n % SETS
                                mm = t.transpose(psB[l][:, n * P:(n + 1) * P], probs[l][:, h, s, :], S.ident)
                            mm.then_inc(turned, 1)
                    for l in lanes:
                        t.wait_ge(probsT_ready, chunk_count(i, CHUNKS - 1, l))
                        for h in range(HEADS):
                            for s in range(SETS):
                                mm = t.matmul(psA[l][:, h * (DH + 1):(h + 1) * (DH + 1)], probsT[l][:, h, s, :],
                                              vals[l][:, s, h, :], start=(s == 0), stop=(s == SETS - 1))
                        mm.then_inc(out_ready, 1)
                    if own_keys:
                        for l in lanes:
                            t.wait_ge(o_sb_ready, i * LANES + l + 1)
                            t.transpose(psB[l][:, 512:512 + T], osb[l][:, :, :].rearrange("p h d -> p (h d)"),
                                        S.ident).then_inc(oT_ready, 1)
                        for l in lanes:
                            t.wait_ge(oT_sb_ready, i * LANES + l + 1)
                            t.matmul(psB[l][:, 0:D], oT[l][:, :], weights["wprojT"], start=True,
                                     stop=True).then_inc(proj_ready, 1)


def expert_choice_attention(nc, S, name, ins):
    W3 = 3 * D
    G = B * E0 * K0
    with phase(nc, name) as ph:
        lanes = range(LANES)
        wr = ph.sb("wr", [P, E0])
        wqkv = ph.sb("wqkv", [P, E0, W3])
        wswap = ph.sb("wswap", [P, E0, 2, ROPE_N])
        wo = ph.sb("wo", [P, E0, D])
        n1 = ph.sb("n1", [P, B, D])
        gates = ph.sb("gates", [P, B, 1 + E0])
        gatesT = ph.sb("gatesT", [P, T])
        left = ph.sb("left", [P, T])
        top = ph.sb("top", [P, K0])
        top_i = ph.sb("top_i", [P, K0], U32)
        top_f = ph.sb("top_f", [P, K0])
        spread = ph.sb("spread", [P, G])
        taken = ph.sb("taken", [P, G])
        pick = [ph.sb(f"pick{l}", [P, P]) for l in lanes]
        pickT = [ph.sb(f"pickT{l}", [P, P]) for l in lanes]
        xn = [ph.sb(f"xn{l}", [P, D]) for l in lanes]
        cols = ph.sb("cols", [P, B, 1 + E0])
        gathT = ph.sb("gathT", [P, E0, B, K0])
        cosg = ph.sb("cosg", [ROPE_N, E0, B, K0])
        sing = ph.sb("sing", [ROPE_N, E0, B, K0])
        QT = ph.sb("QT", [P, E0, B, K0])
        KT = ph.sb("KT", [P, E0, B, K0])
        VT = ph.sb("VT", [P, E0, B, K0])
        QS = ph.sb("QS", [ROPE_N, E0, B, K0])
        KS = ph.sb("KS", [ROPE_N, E0, B, K0])
        AVT = ph.sb("AVT", [P, E0, B, K0])
        OUTT = ph.sb("OUTT", [P, E0, B, K0])
        q1 = [ph.sb(f"q1{l}", [P, P]) for l in lanes]
        v1 = [ph.sb(f"v1{l}", [P, P]) for l in lanes]
        vv = [ph.sb(f"vv{l}", [P, P]) for l in lanes]
        sc = [ph.sb(f"sc{l}", [P, P]) for l in lanes]
        mk = [ph.sb(f"mk{l}", [P, P]) for l in lanes]
        pT = [ph.sb(f"pT{l}", [P, P]) for l in lanes]
        st = [ph.sb(f"st{l}", [P, 4]) for l in lanes]
        ps = [ph.ps(f"ps{n}", [P, 512]) for n in range(8)]

        dve_step, act_step = ph.sem("dve_step"), ph.sem("act_step")
        stats_done, pow_ready, w_loaded = ph.sem("stats_done"), ph.sem("pow_ready"), ph.sem("w_loaded")
        xn_ready, xnT_ready, xnT_sb, logits_ready = (ph.sem(n) for n in ("xn_ready", "xnT_ready", "xnT_sb", "logits_ready"))
        logits_sb, gates_ready, gatesT_ready = ph.sem("logits_sb"), ph.sem("gates_ready"), ph.sem("gatesT_ready")
        spread_ready, taken_ready = ph.sem("spread_ready"), ph.sem("taken_ready")

        def stage_block(fn):
            with nc.Block() as block:
                fn(block)

        with nc.Block() as block:
            @block.sync
            def _(sp):
                sp.dma_start(wr[:, :], ins["L0_ffn_WrT"]).then_inc(w_loaded, 16)
                sp.dma_start(wqkv[:, :, :], ins["L0_ffn_Wqkv"].rearrange("e i j -> i e j")).then_inc(w_loaded, 16)
                sp.dma_start(wswap[:, :, :, :], ins["L0_ffn_Wswap"].rearrange("e i n j -> i e n j")).then_inc(w_loaded, 16)
                sp.dma_start(wo[:, :, :], ins["L0_ffn_Wo"].rearrange("e i j -> i e j")).then_inc(w_loaded, 16)

            @block.gpsimd
            def _(g):
                inverse_roots(g, S, stats_done, pow_ready)

            @block.vector
            def _(v):
                step = Steps(v, dve_step)
                layer_norm_coefficients(v, step, S, stats_done, pow_ready)
                step(v.tensor_copy(gates[:, :, 0], S.iota_col.broadcast_to([P, B])))
                with v.Fori(0, B // LANES) as i:
                    step.restart()
                    for l in lanes:
                        b = i * LANES + l
                        step(v.tensor_scalar(xn[l][:, :], S.x[:, b, :], S.mean[:, bass.ds(b, 1)],
                                             S.rstd[:, bass.ds(b, 1)], ALU.subtract, ALU.mult))
                        v.tensor_copy(n1[:, b, :], xn[l][:, :]).then_inc(xn_ready, 1)
                    for l in lanes:
                        b = i * LANES + l
                        v.wait_ge(xnT_ready, b + 1)
                        v.tensor_copy(pT[l][:, :], ps[l][:, 0:T]).then_inc(xnT_sb, 1)
                    for l in lanes:
                        b = i * LANES + l
                        v.wait_ge(logits_ready, b + 1)
                        v.tensor_copy(gates[:, b, 1:1 + E0], ps[2 + l][:, 0:E0]).then_inc(logits_sb, 1)
                v.wait_ge(gates_ready, 1)
                gv = gates[:, :, 1:1 + E0]
                step(v.tensor_scalar(gv, gv, 1.0, None, ALU.add))
                step(v.reciprocal(gv, gv))
                v.tensor_copy(left[:, :].rearrange("p (b e) -> p b e", e=E0), gv).then_inc(gates_ready, 1)
                v.wait_ge(gatesT_ready, 1)
                step(v.tensor_copy(gatesT[:, :], ps[4][:, 0:T]))
                step(v.max(top[:, 0:8], gatesT[:, :]))
                step(v.max_index(out=top_i[:, 0:8], in_max=top[:, 0:8], in_values=gatesT[:, :]))
                step(v.match_replace(out=left[:, :], in_to_replace=top[:, 0:8], in_values=gatesT[:, :], imm_value=-1.0))
                step(v.max(top[:, 8:16], left[:, :]))
                step(v.max_index(out=top_i[:, 8:16], in_max=top[:, 8:16], in_values=left[:, :]))
                step(v.tensor_copy(top_f[:, :], top_i[:, :]))
                v.tensor_tensor(spread[:, :].rearrange("p (c k) -> p c k", k=K0),
                                top_f[:, :].unsqueeze(1).broadcast_to([P, P, K0]),
                                S.ident.unsqueeze(2).broadcast_to([P, P, K0]), ALU.mult).then_inc(spread_ready, 1)
                for n in range(4):
                    v.wait_ge(taken_ready, n + 1)
                    step(v.tensor_copy(taken[:, n * 512:(n + 1) * 512], ps[4 + n][:, :]))

            @block.scalar
            def _(a):
                a.wait_ge(logits_sb, B)
                gv = gates[:, :, 1:1 + E0]
                a.activation(gv, gv, ACT.Exp, scale=-1.0).then_inc(gates_ready, 1)

            @block.tensor
            def _(t):
                t.wait_ge(w_loaded, 64)
                with t.Fori(0, B // LANES) as i:
                    for l in lanes:
                        t.wait_ge(xn_ready, i * LANES + l + 1)
                        t.transpose(ps[l][:, 0:T], xn[l][:, :], S.ident).then_inc(xnT_ready, 1)
                    for l in lanes:
                        t.wait_ge(xnT_sb, i * LANES + l + 1)
                        t.matmul(ps[2 + l][:, 0:E0], pT[l][:, :], wr[:, :], start=True, stop=True).then_inc(logits_ready, 1)
                t.wait_ge(gates_ready, 2)
                t.transpose(ps[4][:, 0:T], left[:, :], S.ident).then_inc(gatesT_ready, 1)
                t.wait_ge(spread_ready, 1)
                for n in range(4):
                    t.matmul(ps[4 + n][:, :], S.ones, spread[:, n * 512:(n + 1) * 512], start=True,
                             stop=True).then_inc(taken_ready, 1)

        pick_ready, gath_ready, gath_free = ph.sem("pick_ready"), ph.sem("gath_ready"), ph.sem("gath_free")
        qkv_mm, qkv_sb, rope_done = ph.sem("qkv_mm"), ph.sem("qkv_sb"), ph.sem("rope_done")
        dve_step2 = ph.sem("dve_step2")
        with nc.Block() as block:
            @block.vector
            def _(v):
                v.sem_inc(gath_free, 1)
                step = Steps(v, dve_step2)
                with v.Fori(0, B // LANES) as i:
                    step.restart()
                    for l in lanes:
                        b = i * LANES + l
                        step(v.tensor_copy(xn[l][:, :], n1[:, b, :]))
                        v.tensor_scalar(pick[l][:, :], taken[:, bass.ds(b * P, P)], S.iota_col, None,
                                        ALU.is_equal).then_inc(pick_ready, 1)
                    for l in lanes:
                        b = i * LANES + l
                        v.wait_ge(gath_ready, b + 1)
                        step(v.tensor_copy(cols[:, b, :], ps[4 * l][:, 0:1 + E0]))
                        step(v.tensor_copy(gathT[:, :, b, :], ps[4 * l + 1][:, 0:P].rearrange("p (e k) -> p e k", k=K0)))
                        step(v.tensor_copy(cosg[:, :, b, :], ps[4 * l + 2][0:ROPE_N, 0:P].rearrange("p (e k) -> p e k", k=K0)))
                        v.tensor_copy(sing[:, :, b, :], ps[4 * l + 3][0:ROPE_N, 0:P]
                                      .rearrange("p (e k) -> p e k", k=K0)).then_inc(gath_free, 1)
                step = Steps(v, dve_step2)
                step.restart()
                v.wait_ge(qkv_sb, 2 * E0)
                for x, xs in ((QT, QS), (KT, KS)):
                    r = x[0:ROPE_N, :, :, :]
                    step(v.tensor_tensor(r, r, cosg[:, :, :, :], ALU.mult))
                    step(v.tensor_tensor(xs[:, :, :, :], xs[:, :, :, :], sing[:, :, :, :], ALU.mult))
                    step(v.tensor_tensor(r, r, xs[:, :, :, :], ALU.add))

            @block.scalar
            def _(a):
                for e in range(E0):
                    p4 = ps[4 * (e % 2):4 * (e % 2) + 4]
                    a.wait_ge(qkv_mm, 2 * e + 1)
                    a.activation(QT[:, e, :, :].rearrange("p b k -> p (b k)"), p4[0][:, 0:256], ACT.Copy)
                    a.activation(KT[:, e, :, :].rearrange("p b k -> p (b k)"), p4[0][:, 256:512], ACT.Copy)
                    a.activation(VT[:, e, :, :].rearrange("p b k -> p (b k)"), p4[1][:, 0:256], ACT.Copy).then_inc(qkv_sb, 1)
                    a.wait_ge(qkv_mm, 2 * e + 2)
                    a.activation(QS[:, e, :, :].rearrange("p b k -> p (b k)"), p4[2][0:ROPE_N, 0:256], ACT.Copy)
                    a.activation(KS[:, e, :, :].rearrange("p b k -> p (b k)"), p4[2][0:ROPE_N, 256:512],
                                 ACT.Copy).then_inc(qkv_sb, 1)

            @block.tensor
            def _(t):
                with t.Fori(0, B // LANES) as i:
                    for l in lanes:
                        b = i * LANES + l
                        t.wait_ge(pick_ready, b + 1)
                        t.wait_ge(gath_free, 1 + i * LANES)
                        t.matmul(ps[4 * l][:, 0:1 + E0], pick[l][:, :], gates[:, b, :], start=True, stop=True)
                        t.matmul(ps[4 * l + 1][:, 0:P], xn[l][:, :], pick[l][:, :], start=True, stop=True)
                        t.matmul(ps[4 * l + 2][0:ROPE_N, 0:P], S.cos, pick[l][:, :], start=True, stop=True)
                        t.matmul(ps[4 * l + 3][0:ROPE_N, 0:P], S.sin, pick[l][:, :], start=True,
                                 stop=True).then_inc(gath_ready, 1)
                t.wait_ge(gath_free, 1 + B)
                for e in range(E0):
                    p4 = ps[4 * (e % 2):4 * (e % 2) + 4]
                    if e >= 2:
                        t.wait_ge(qkv_sb, 2 * (e - 1))
                    rows = gathT[:, e, :, :].rearrange("p b k -> p (b k)")
                    t.matmul(p4[0][:, 0:256], wqkv[:, e, 0:D], rows, start=True, stop=True)
                    t.matmul(p4[0][:, 256:512], wqkv[:, e, D:2 * D], rows, start=True, stop=True)
                    t.matmul(p4[1][:, 0:256], wqkv[:, e, 2 * D:3 * D], rows, start=True, stop=True).then_inc(qkv_mm, 1)
                    t.matmul(p4[2][0:ROPE_N, 0:256], wswap[:, e, 0, :], rows, start=True, stop=True)
                    t.matmul(p4[2][0:ROPE_N, 256:512], wswap[:, e, 1, :], rows, start=True, stop=True).then_inc(qkv_mm, 1)

        q1_ready, s_ready, p_shift, p_exp, p_ready, p_turned, pT_ready, av_ready, av_sb = (
            ph.sem(n) for n in ("q1_ready", "s_ready", "p_shift", "p_exp", "p_ready", "p_turned", "pT_ready", "av_ready", "av_sb"))
        v_turned, vv_ready, out_mm, out_sb = ph.sem("v_turned"), ph.sem("vv_ready"), ph.sem("out_mm"), ph.sem("out_sb")
        o1_ready, o_turned, o2_ready, scat_ready = (ph.sem(n) for n in ("o1_ready", "o_turned", "o2_ready", "scat_ready"))
        dve_step3 = ph.sem("dve_step3")
        with nc.Block() as block:
            def rows_of(X, b):
                return X[:, :, b, :]

            @block.vector
            def _(v):
                step = Steps(v, dve_step3)
                with v.Fori(0, B // LANES) as i:
                    step.restart()
                    for l in lanes:
                        b = i * LANES + l
                        step(v.tensor_copy(v1[l][:, :].rearrange("p (e k) -> p e k", k=K0), rows_of(VT, b)))
                        v.tensor_copy(q1[l][:, :].rearrange("p (e k) -> p e k", k=K0), rows_of(QT, b)).then_inc(q1_ready, 1)
                        step(v.scalar_tensor_tensor(out=mk[l][:, :], in0=taken[:, bass.ds(b * P, P)],
                                                    scalar=cols[:, b, 0:1], in1=S.sameexpert,
                                                    op0=ALU.is_le, op1=ALU.mult))
                        step(v.tensor_scalar(mk[l][:, :], mk[l][:, :], -1.0, -NEG, ALU.add, ALU.mult))
                        step(v.tensor_tensor(pick[l][:, 0:E0], cols[:, b, 1:1 + E0], S.expertmask, ALU.mult))
                        step(v.tensor_reduce(st[l][:, 3:4], pick[l][:, 0:E0], AX.X, ALU.add))
                    for l in lanes:
                        b = i * LANES + l
                        v.wait_ge(s_ready, b + 1)
                        step(v.scalar_tensor_tensor(out=sc[l][:, :], in0=ps[l][:, 0:P], scalar=float(D) ** -0.5,
                                                    in1=mk[l][:, :], op0=ALU.mult, op1=ALU.add))
                        step(v.tensor_reduce(st[l][:, 0:1], sc[l][:, :], AX.X, ALU.max))
                        v.tensor_scalar(st[l][:, 1:2], st[l][:, 0:1], -1.0, None, ALU.mult).then_inc(p_shift, 1)
                        v.wait_ge(v_turned, b + 1)
                        v.tensor_copy(vv[l][:, :], ps[4 + l][:, 0:P]).then_inc(vv_ready, 1)
                    for l in lanes:
                        b = i * LANES + l
                        v.wait_ge(p_exp, b + 1)
                        step(v.reciprocal(st[l][:, 0:1], st[l][:, 2:3]))
                        v.tensor_scalar(sc[l][:, :], sc[l][:, :], st[l][:, 0:1], st[l][:, 3:4],
                                        ALU.mult, ALU.mult).then_inc(p_ready, 1)
                    for l in lanes:
                        b = i * LANES + l
                        v.wait_ge(p_turned, b + 1)
                        v.tensor_copy(pT[l][:, :], ps[2 + l][:, 0:P]).then_inc(pT_ready, 1)
                    for l in lanes:
                        b = i * LANES + l
                        v.wait_ge(av_ready, b + 1)
                        v.tensor_copy(rows_of(AVT, b), ps[6 + l][:, 0:P].rearrange("p (e k) -> p e k", k=K0)).then_inc(av_sb, 1)
                step.restart()
                for e in range(E0):
                    v.wait_ge(out_mm, e + 1)
                    v.tensor_copy(OUTT[:, e, :, :].rearrange("p b k -> p (b k)"), ps[e][:, 0:256]).then_inc(out_sb, 1)
                v.wait_ge(out_sb, E0)
                with v.Fori(0, B // LANES) as i:
                    step.restart()
                    for l in lanes:
                        b = i * LANES + l
                        step(v.tensor_copy(v1[l][:, :].rearrange("p (e k) -> p e k", k=K0), rows_of(OUTT, b)))
                        v.tensor_scalar(pickT[l][:, :], S.iota_row, cols[:, b, 0:1], None, ALU.is_equal).then_inc(o1_ready, 1)
                    for l in lanes:
                        b = i * LANES + l
                        v.wait_ge(o_turned, b + 1)
                        v.tensor_copy(vv[l][:, :], ps[l][:, 0:P]).then_inc(o2_ready, 1)
                    for l in lanes:
                        b = i * LANES + l
                        v.wait_ge(scat_ready, b + 1)
                        step(v.tensor_tensor(S.x[:, b, :], S.x[:, b, :], ps[2 + l][:, 0:D], ALU.add))
                        step(v.bn_stats(S.stats[:, b, :], S.x[:, b, :]))

            @block.scalar
            def _(a):
                with a.Fori(0, B // LANES) as i:
                    for l in lanes:
                        b = i * LANES + l
                        a.wait_ge(p_shift, b + 1)
                        a.activation(sc[l][:, :], sc[l][:, :], ACT.Exp, bias=st[l][:, 1:2],
                                     accum_out=st[l][:, 2:3]).then_inc(p_exp, 1)

            @block.tensor
            def _(t):
                with t.Fori(0, B // LANES) as i:
                    for l in lanes:
                        b = i * LANES + l
                        t.wait_ge(q1_ready, b + 1)
                        t.matmul(ps[l][:, 0:P], q1[l][:, :], rows_of(KT, b), start=True, stop=True).then_inc(s_ready, 1)
                        t.transpose(ps[4 + l][:, 0:P], v1[l][:, :], S.ident).then_inc(v_turned, 1)
                    for l in lanes:
                        t.wait_ge(p_ready, i * LANES + l + 1)
                        t.transpose(ps[2 + l][:, 0:P], sc[l][:, :], S.ident).then_inc(p_turned, 1)
                    for l in lanes:
                        t.wait_ge(pT_ready, i * LANES + l + 1)
                        t.wait_ge(vv_ready, i * LANES + l + 1)
                        t.matmul(ps[6 + l][:, 0:P], vv[l][:, :], pT[l][:, :], start=True, stop=True).then_inc(av_ready, 1)
                t.wait_ge(av_sb, B)
                for e in range(E0):
                    t.matmul(ps[e][:, 0:256], wo[:, e, :], AVT[:, e, :, :].rearrange("p b k -> p (b k)"),
                             start=True, stop=True).then_inc(out_mm, 1)
                t.wait_ge(out_sb, E0)
                with t.Fori(0, B // LANES) as i:
                    for l in lanes:
                        t.wait_ge(o1_ready, i * LANES + l + 1)
                        t.transpose(ps[l][:, 0:P], v1[l][:, :], S.ident).then_inc(o_turned, 1)
                    for l in lanes:
                        t.wait_ge(o2_ready, i * LANES + l + 1)
                        t.matmul(ps[2 + l][:, 0:D], pickT[l][:, :], vv[l][:, :], start=True, stop=True).then_inc(scat_ready, 1)


def patch_depool(nc, S, name, ins):
    RMS_EPS = 1e-5
    dt = float(-np.log(-np.expm1(LOGP)))
    with phase(nc, name) as ph:
        lanes = range(LANES)
        w_in = ph.sb("w_in", [P, D])
        b_in, g_res, g_init = ph.sb("b_in", [P, D]), ph.sb("g_res", [P, D]), ph.sb("g_init", [P, D])
        len_i = ph.sb("len_i", [P, B], I32)
        len_f = ph.sb("len_f", [P, B])
        ends = ph.sb("ends", [P, B])
        ends_neg = ph.sb("ends_neg", [P, B])
        squares = ph.sb("squares", [P, B, CTX])
        ctx_ms = ph.sb("ctx_ms", [P, B])
        ctx_rms = ph.sb("ctx_rms", [P, B])
        xn = [ph.sb(f"xn{l}", [P, D]) for l in lanes]
        xsq = [ph.sb(f"xsq{l}", [P, D]) for l in lanes]
        hT = [ph.sb(f"hT{l}", [P, T]) for l in lanes]
        ms = [ph.sb(f"ms{l}", [P, 2]) for l in lanes]
        hit = [ph.sb(f"hit{l}", [P, T]) for l in lanes]
        marked = [ph.sb(f"marked{l}", [P, P]) for l in lanes]
        mark = [ph.sb(f"mark{l}", [P, 1]) for l in lanes]
        plug = [ph.sb(f"plug{l}", [P, T]) for l in lanes]
        u = [ph.sb(f"u{l}", [P, D]) for l in lanes]
        s = [ph.sb(f"s{l}", [P, D]) for l in lanes]
        ps = [ph.ps(f"ps{n}", [P, 512]) for n in range(8)]
        dve_step, act_step, stats_done, pow_ready, loaded, lens_mm, sq_done, ctx_pow, ms_ready, rms_ready = (
            ph.sem(n) for n in ("dve_step", "act_step", "stats_done", "pow_ready", "loaded", "lens_mm", "sq_done",
                                "ctx_pow", "ms_ready", "rms_ready"))
        hit_ready, mark_ready, marked_ready, plug_mm, plug_ready, u_ready, s_mm, s_ready, h_ready, h_turned, hT_ready, sum_ready = (
            ph.sem(n) for n in ("hit_ready", "mark_ready", "marked_ready", "plug_mm", "plug_ready", "u_ready", "s_mm",
                                "s_ready", "h_ready", "h_turned", "hT_ready", "sum_ready"))
        lens_ready, ctx_ms_ready = ph.sem("lens_ready"), ph.sem("ctx_ms_ready")
        with nc.Block() as block:
            @block.sync
            def _(sp):
                sp.dma_start(w_in[:, :], ins["L1_W_inT"]).then_inc(loaded, 16)
                sp.dma_start(b_in[:, :], ins["L1_xattn_b_in"].partition_broadcast(P)).then_inc(loaded, 16)
                sp.dma_start(g_res[:, :], ins["L1_xattn_g_res"].partition_broadcast(P)).then_inc(loaded, 16)
                sp.dma_start(g_init[:, :], ins["L1_xattn_g_init"][0:D].partition_broadcast(P)).then_inc(loaded, 16)
                sp.dma_start(len_i[:, :], ins["patch_lensT"]).then_inc(loaded, 16)

            @block.gpsimd
            def _(g):
                inverse_roots(g, S, stats_done, pow_ready)
                g.wait_ge(ctx_ms_ready, 1)
                g.tensor_tensor(ctx_rms[:, :], ctx_ms[:, :], S.mhalf[:, :], ALU.pow).then_inc(ctx_pow, 1)
                with g.Fori(0, B // LANES) as i:
                    for l in lanes:
                        g.wait_ge(ms_ready, i * LANES + l + 1)
                        g.tensor_tensor(ms[l][:, 1:2], ms[l][:, 0:1], S.mhalf[:, 0:1], ALU.pow).then_inc(rms_ready, 1)

            @block.scalar
            def _(a):
                a.activation(squares[:, :, :], S.ctx[:, :, :], ACT.Square).then_inc(sq_done, 1)

            @block.vector
            def _(v):
                step = Steps(v, dve_step)
                layer_norm_coefficients(v, step, S, stats_done, pow_ready)
                v.wait_ge(sq_done, 1)
                step(v.tensor_reduce(ctx_ms[:, :], squares[:, :, :], AX.X, ALU.add))
                v.tensor_scalar(ctx_ms[:, :], ctx_ms[:, :], 1.0 / CTX, RMS_EPS, ALU.mult, ALU.add).then_inc(ctx_ms_ready, 1)
                v.wait_ge(loaded, 80)
                v.tensor_copy(len_f[:, :], len_i[:, :]).then_inc(lens_ready, 1)
                v.wait_ge(lens_mm, 1)
                step(v.tensor_scalar(ends[:, :], ps[0][:, 0:B], -1.0, None, ALU.add))
                step(v.tensor_scalar(ends_neg[:, :], ends[:, :], 0.0, float(T), ALU.is_lt, ALU.mult))
                step(v.tensor_tensor(ends[:, :], ends[:, :], ends_neg[:, :], ALU.add))
                v.wait_ge(ctx_pow, 1)
                with v.Fori(0, B // LANES) as i:
                    step.restart()
                    for l in lanes:
                        b = i * LANES + l
                        v.tensor_scalar(hit[l][:, :], S.iota_row, ends[:, bass.ds(b, 1)], None, ALU.is_equal).then_inc(hit_ready, 1)
                        step(v.tensor_scalar(xn[l][:, :], S.x[:, b, :], S.mean[:, bass.ds(b, 1)],
                                             S.rstd[:, bass.ds(b, 1)], ALU.subtract, ALU.mult))
                        step(v.tensor_tensor(xsq[l][:, :], xn[l][:, :], xn[l][:, :], ALU.mult))
                        step(v.tensor_reduce(ms[l][:, 0:1], xsq[l][:, :], AX.X, ALU.add))
                        v.tensor_scalar(ms[l][:, 0:1], ms[l][:, 0:1], 1.0 / D, RMS_EPS, ALU.mult, ALU.add).then_inc(ms_ready, 1)
                        step(v.tensor_scalar(u[l][:, :], S.ctx[:, b, 0:D], ctx_rms[:, bass.ds(b, 1)], 1.0 / dt,
                                             ALU.mult, ALU.mult))
                        v.scalar_tensor_tensor(out=u[l][:, :], in0=u[l][:, :], scalar=float(dt * np.exp(LOGP)),
                                               in1=g_init[:, :], op0=ALU.mult, op1=ALU.mult).then_inc(u_ready, 1)
                    for l in lanes:
                        b = i * LANES + l
                        v.wait_ge(rms_ready, b + 1)
                        v.scalar_tensor_tensor(out=xsq[l][:, :], in0=xn[l][:, :], scalar=ms[l][:, 1:2],
                                               in1=g_res[:, :], op0=ALU.mult, op1=ALU.mult).then_inc(h_ready, 1)
                        v.wait_ge(mark_ready, b + 1)
                        step(v.tensor_scalar(mark[l][:, :], ps[l][:, 0:1], 1.0, None, ALU.min))
                        v.tensor_scalar(marked[l][:, :], S.ones, mark[l][:, 0:1], None, ALU.mult).then_inc(marked_ready, 1)
                        v.wait_ge(s_mm, b + 1)
                        v.tensor_copy(s[l][:, :], ps[6 + l][:, 0:D]).then_inc(s_ready, 1)
                    for l in lanes:
                        b = i * LANES + l
                        v.wait_ge(h_turned, b + 1)
                        v.tensor_copy(hT[l][:, :], ps[4 + l][:, 0:T]).then_inc(hT_ready, 1)
                        v.wait_ge(plug_mm, b + 1)
                        step(v.tensor_scalar(plug[l][:, :], ps[2 + l][:, 0:T], -1.0, 0.0, ALU.add, ALU.max))
                        v.tensor_scalar(plug[l][:, :], plug[l][:, :], S.iota_col, None, ALU.is_equal).then_inc(plug_ready, 1)
                        step(v.tensor_tensor(xn[l][:, :], S.x[:, b, :], b_in[:, :], ALU.add))
                    for l in lanes:
                        b = i * LANES + l
                        v.wait_ge(sum_ready, b + 1)
                        step(v.tensor_tensor(S.x[:, b, :], xn[l][:, :], ps[l][:, 0:D], ALU.add))
                        step(v.bn_stats(S.stats[:, b, :], S.x[:, b, :]))

            @block.tensor
            def _(t):
                t.wait_ge(lens_ready, 1)
                t.matmul(ps[0][:, 0:B], S.upto, len_f[:, :], start=True, stop=True).then_inc(lens_mm, 1)
                with t.Fori(0, B // LANES) as i:
                    for l in lanes:
                        b = i * LANES + l
                        t.wait_ge(hit_ready, b + 1)
                        t.matmul(ps[l][:, 0:1], hit[l][:, :], S.ones[:, 0:1], start=True, stop=True).then_inc(mark_ready, 1)
                        t.wait_ge(u_ready, b + 1)
                        t.matmul(ps[6 + l][:, 0:D], S.decay, u[l][:, :], start=True, stop=True).then_inc(s_mm, 1)
                    for l in lanes:
                        b = i * LANES + l
                        t.wait_ge(h_ready, b + 1)
                        t.transpose(ps[4 + l][:, 0:T], xsq[l][:, :], S.ident).then_inc(h_turned, 1)
                        t.wait_ge(marked_ready, b + 1)
                        t.matmul(ps[2 + l][:, 0:T], marked[l][:, :], S.upto, start=True, stop=True).then_inc(plug_mm, 1)
                    for l in lanes:
                        b = i * LANES + l
                        t.wait_ge(hT_ready, b + 1)
                        t.wait_ge(plug_ready, b + 1)
                        t.wait_ge(s_ready, b + 1)
                        t.matmul(ps[l][:, 0:D], hT[l][:, :], w_in[:, :], start=True, stop=False)
                        t.matmul(ps[l][:, 0:D], plug[l][:, :], s[l][:, :], start=False, stop=True).then_inc(sum_ready, 1)


ROW = LW * D + LW + LW * D + D
W1, B1, W2, B2 = 0, LW * D, LW * D + LW, LW * D + LW + LW * D
DEPTH = 8


def tree_routes(nc, S, name, nets, first_net, stream, leaves, node_w, node_b):
    G = 4
    with phase(nc, name) as ph:
        w = ph.sb("w", [P, nets * NODES])
        nb = ph.sb("nb", [P, nets * NODES])
        xn = [ph.sb(f"xn{k}", [P, D]) for k in range(G)]
        xT = [ph.sb(f"xT{k}", [P, T]) for k in range(G)]
        right = ph.sb("right", [P, G, nets, NODES])
        path = [ph.sb(f"path{k}", [P, G * nets, LEAVES]) for k in range(2)]
        leaf_f = ph.sb("leaf_f", [P, G, nets])
        ps = [ph.ps(f"ps{k}", [P, 1024]) for k in range(G)]
        dve_step, loaded, x_ready, turned, xT_ready, logits_ready = (
            ph.sem(n) for n in ("dve_step", "loaded", "x_ready", "turned", "xT_ready", "logits_ready"))
        with nc.Block() as block:
            @block.sync
            def _(sp):
                sp.dma_start(w[:, :], node_w).then_inc(loaded, 16)
                sp.dma_start(nb[:, :], node_b.partition_broadcast(P)).then_inc(loaded, 16)

            @block.vector
            def _(v):
                step = Steps(v, dve_step)
                v.wait_ge(loaded, 32)
                step(v.tensor_scalar(nb[:, :], nb[:, :], -1.0, None, ALU.mult))
                with v.Fori(0, B // G) as i:
                    step.restart()
                    for k in range(G):
                        v.tensor_copy(xn[k][:, :], stream[:, i * G + k, :]).then_inc(x_ready, 1)
                    for k in range(G):
                        v.wait_ge(turned, i * G + k + 1)
                        v.tensor_copy(xT[k][:, :], ps[k][:, 0:T]).then_inc(xT_ready, 1)
                    for k in range(G):
                        v.wait_ge(logits_ready, i * G + k + 1)
                        for n0 in range(0, nets, 2):
                            m = min(2, nets - n0)
                            at = 512 * (n0 // 2)
                            step(v.tensor_tensor(right[:, k, n0:n0 + m, :].rearrange("p n c -> p (n c)"),
                                                 ps[k][:, at:at + m * NODES],
                                                 nb[:, n0 * NODES:(n0 + m) * NODES], ALU.is_gt))
                    rt = right[:, :, :, :].rearrange("p k n c -> p (k n) c")
                    step(v.tensor_copy(path[0][:, :, 1:2], rt[:, :, 0:1]))
                    step(v.tensor_scalar(path[0][:, :, 0:1], rt[:, :, 0:1], -1.0, 1.0, ALU.mult, ALU.add))
                    for level in range(1, DEPTH):
                        width = 2 ** level
                        a, b = path[(level + 1) % 2], path[level % 2]
                        pair = b[:, :, 0:2 * width].rearrange("p g (c two) -> p g c two", two=2)
                        step(v.tensor_tensor(pair[:, :, :, 1], a[:, :, 0:width], rt[:, :, width - 1:2 * width - 1], ALU.mult))
                        step(v.tensor_tensor(pair[:, :, :, 0], a[:, :, 0:width], pair[:, :, :, 1], ALU.subtract))
                    last = path[(DEPTH - 1) % 2]
                    step(v.tensor_tensor(last[:, :, :], last[:, :, :],
                                         S.iota256.unsqueeze(1).broadcast_to([P, G * nets, LEAVES]), ALU.mult))
                    step(v.tensor_reduce(leaf_f[:, :, :].rearrange("p k n -> p (k n)"), last[:, :, :], AX.X, ALU.add))
                    for n in range(nets):
                        step(v.tensor_scalar(leaf_f[:, :, n], leaf_f[:, :, n], float(LEAVES * (first_net + n)), None, ALU.add))
                    step(v.tensor_copy(leaves[:, bass.ds(i * G, G), :], leaf_f[:, :, :]))

            @block.tensor
            def _(t):
                t.wait_ge(loaded, 32)
                with t.Fori(0, B // G) as i:
                    for k in range(G):
                        t.wait_ge(x_ready, i * G + k + 1)
                        t.transpose(ps[k][:, 0:T], xn[k][:, :], S.ident).then_inc(turned, 1)
                    for k in range(G):
                        t.wait_ge(xT_ready, i * G + k + 1)
                        for n0 in range(0, nets, 2):
                            m = min(2, nets - n0)
                            at = 512 * (n0 // 2)
                            mm = t.matmul(ps[k][:, at:at + m * NODES], xT[k][:, :],
                                          w[:, n0 * NODES:(n0 + m) * NODES], start=True, stop=True)
                        mm.then_inc(logits_ready, 1)


def leaf_gathers(g, step, leaves, picks, slots, table, gathered, used, slot_of):
    n = len(slots)
    per = n // slot_of

    def gather(i, m):
        k, net = m % slot_of, m // slot_of
        step(g.tensor_copy(picks[m][:, :], leaves[:, i * slot_of + k, net:net + 1]))
        g.indirect_dma_start(out=slots[m][:, :], out_offset=None, in_=table,
                             in_offset=bass.IndirectOffsetOnAxis(ap=picks[m][:, 0:1], axis=0)).then_inc(gathered[m], 16)
    for m in range(n):
        gather(0, m)
    with g.Fori(0, B // slot_of - 1) as i:
        step.restart()
        for m in range(n):
            g.wait_ge(used, 1 + i * n + m + 1)
            gather(i + 1, m)


def routed_trees(nc, S, name, ins):
    with phase(nc, name) as ph:
        xn3 = ph.sb("xn3", [P, B, D])
        leaves = ph.sb("leaves", [P, B, 3], U32)
        leaves_f = ph.sb("leaves_f", [P, B, 1], U32)
        table = ins["leaf_table"]

        with phase(nc, name + "_norm") as pn:
            stats = pn.sb("stats", [P, B, 6])
            mu, dif, var = pn.sb("mu", [P, B]), pn.sb("dif", [P, B]), pn.sb("var", [P, B])
            half = pn.sb("half", [P, B])
            dve_step, stats_done, pow_ready, var_ready, sd_ready, den_ready, inv_ready = (
                pn.sem(n) for n in ("dve_step", "stats_done", "pow_ready", "var_ready", "sd_ready", "den_ready", "inv_ready"))
            with nc.Block() as block:
                @block.gpsimd
                def _(g):
                    g.memset(half[:, :], 0.5).then_inc(sd_ready, 1)
                    inverse_roots(g, S, stats_done, pow_ready)
                    g.wait_ge(sd_ready, 1)
                    g.wait_ge(var_ready, 1)
                    g.tensor_tensor(var[:, :], var[:, :], half[:, :], ALU.pow).then_inc(sd_ready, 1)
                    g.wait_ge(den_ready, 1)
                    g.tensor_tensor(var[:, :], var[:, :], S.mhalf[:, :], ALU.pow).then_inc(inv_ready, 1)

                @block.vector
                def _(v):
                    step = Steps(v, dve_step)
                    layer_norm_coefficients(v, step, S, stats_done, pow_ready)
                    with v.Fori(0, B) as b:
                        step.restart()
                        step(v.tensor_scalar(xn3[:, b, :], S.x[:, b, :], S.mean[:, bass.ds(b, 1)],
                                             S.rstd[:, bass.ds(b, 1)], ALU.subtract, ALU.mult))
                        step(v.bn_stats(stats[:, b, :], xn3[:, b, :]))
                    step.restart()
                    step(v.tensor_tensor(mu[:, :], stats[:, :, 1], stats[:, :, 4], ALU.add))
                    step(v.tensor_tensor(dif[:, :], stats[:, :, 1], stats[:, :, 4], ALU.subtract))
                    step(v.tensor_scalar(mu[:, :], mu[:, :], 0.5, None, ALU.mult))
                    step(v.tensor_tensor(var[:, :], stats[:, :, 2], stats[:, :, 5], ALU.add))
                    step(v.scalar_tensor_tensor(out=dif[:, :], in0=dif[:, :], scalar=0.25 * D, in1=dif[:, :],
                                                op0=ALU.mult, op1=ALU.mult))
                    step(v.tensor_tensor(var[:, :], var[:, :], dif[:, :], ALU.add))
                    v.tensor_scalar(var[:, :], var[:, :], 1.0 / (D - 1), None, ALU.mult).then_inc(var_ready, 1)
                    v.wait_ge(sd_ready, 2)
                    v.tensor_scalar(var[:, :], var[:, :], 1e-5, None, ALU.add).then_inc(den_ready, 1)
                    v.wait_ge(inv_ready, 1)
                    with v.Fori(0, B) as b:
                        step.restart()
                        step(v.tensor_scalar(xn3[:, b, :], xn3[:, b, :], mu[:, bass.ds(b, 1)], var[:, bass.ds(b, 1)],
                                             ALU.subtract, ALU.mult))

        tree_routes(nc, S, name + "_r3", 3, 0, xn3, leaves, ins["L1_ffn_nw3"], ins["L1_ffn_nb3"])
        tree_attention(nc, S, name + "_qkv", xn3, leaves, table)
        tree_routes(nc, S, name + "_rf", 1, 3, xn3, leaves_f, ins["L1_ffn_nwf"], ins["L1_ffn_nbf"])
        tree_output(nc, S, name + "_f", xn3, leaves_f, table)


def tree_hidden(v, step, rows, x, prod, h):
    step(v.tensor_tensor(prod[:, :, :], rows[:, W1:W1 + LW * D].rearrange("p (l d) -> p l d", d=D),
                         x.unsqueeze(1).broadcast_to([P, LW, D]), ALU.mult))
    step(v.tensor_reduce(h[:, :], prod[:, :, :], AX.X, ALU.add))
    return v.tensor_tensor(h[:, :], h[:, :], rows[:, B1:B1 + LW], ALU.add)


def tree_attention(nc, S, name, xn3, leaves, table):
    with phase(nc, name) as ph:
        lanes = range(LANES)
        N = 3 * LANES
        slots = [ph.sb(f"slot{m}", [P, ROW]) for m in range(N)]
        picks = [ph.sb(f"pick{m}", [P, 1], U32) for m in range(N)]
        prod = ph.sb("prod", [P, LW, D])
        h = [ph.sb(f"h{m}", [P, LW]) for m in range(N)]
        diag = [ph.sb(f"diag{k}", [P, LW, P]) for k in range(2)]
        qkv = [ph.sb(f"qkv{m}", [P, D]) for m in range(N)]
        xl = [ph.sb(f"xl{l}", [P, D]) for l in lanes]
        qT, kT, pr, pT = ([ph.sb(f"{n}{l}", [P, P]) for l in lanes] for n in ("qT", "kT", "pr", "pT"))
        st = [ph.sb(f"st{l}", [P, 4]) for l in lanes]
        ps = [ph.ps(f"ps{k}", [P, 512]) for k in range(8)]
        gathered = [ph.sem(f"gathered{m}") for m in range(N)]
        dve_step, pool_step, h_ready, diag_ready, out_mm, used = (
            ph.sem(n) for n in ("dve_step", "pool_step", "h_ready", "diag_ready", "out_mm", "used"))
        qk_turned, qkT_ready, s_mm, shifted, p_exp, p_turned, pT_ready, att_mm = (
            ph.sem(n) for n in ("qk_turned", "qkT_ready", "s_mm", "shifted", "p_exp", "p_turned", "pT_ready", "att_mm"))

        with nc.Block() as block:
            @block.gpsimd
            def _(g):
                leaf_gathers(g, Steps(g, pool_step), leaves, picks, slots, table, gathered, used, LANES)

            @block.vector
            def _(v):
                v.sem_inc(used, 1)
                step = Steps(v, dve_step)

                def evacuate(i, m):
                    v.wait_ge(out_mm, 1 + i * N + m + 1)
                    v.tensor_tensor(qkv[m][:, :], ps[m % 2][:, 0:D], slots[m][:, B2:B2 + D], ALU.add).then_inc(used, 1)

                with v.Fori(0, B // LANES) as i:
                    step.restart()
                    for l in lanes:
                        step(v.tensor_copy(xl[l][:, :], xn3[:, i * LANES + l, :]))
                    for m in range(N):
                        v.wait_ge(gathered[m], i * 16 + 16)
                        step(tree_hidden(v, step, slots[m], xl[m % LANES][:, :], prod, h[m]))
                        v.tensor_scalar(h[m][:, :], h[m][:, :], 0.0, None, ALU.max).then_inc(h_ready, 1)
                        if m:
                            evacuate(i, m - 1)
                    evacuate(i, N - 1)
                    for l in lanes:
                        v.wait_ge(qk_turned, i * LANES + l + 1)
                        v.tensor_copy(qT[l][:, :], ps[2 + l][:, 0:T])
                        v.tensor_copy(kT[l][:, :], ps[2 + l][:, T:2 * T]).then_inc(qkT_ready, 1)
                    for l in lanes:
                        v.wait_ge(s_mm, i * LANES + l + 1)
                        step(v.tensor_reduce(st[l][:, 0:1], ps[4 + l][:, 0:T], AX.X, ALU.max))
                        v.tensor_scalar(st[l][:, 1:2], st[l][:, 0:1], -float(D) ** -0.5, None, ALU.mult).then_inc(shifted, 1)
                    for l in lanes:
                        v.wait_ge(p_turned, i * LANES + l + 1)
                        v.tensor_copy(pT[l][:, :], ps[4 + l][:, T:2 * T]).then_inc(pT_ready, 1)
                    for l in lanes:
                        v.wait_ge(att_mm, i * LANES + l + 1)
                        step(v.reciprocal(st[l][:, 3:4], st[l][:, 2:3]))
                        step(v.scalar_tensor_tensor(out=xn3[:, i * LANES + l, :], in0=ps[6 + l][:, 0:D], scalar=st[l][:, 3:4],
                                                    in1=xl[l][:, :], op0=ALU.mult, op1=ALU.add))

            @block.scalar
            def _(a):
                with a.Fori(0, B // LANES) as i:
                    for m in range(N):
                        a.wait_ge(h_ready, i * N + m + 1)
                        if m >= 2:
                            a.wait_ge(out_mm, 1 + i * N + m - 1)
                        else:
                            a.wait_ge(out_mm, 1 + i * N)
                        for c in range(LW):
                            ins = a.activation(diag[m % 2][:, c, :], S.ident, ACT.Copy, scale=h[m][:, c:c + 1])
                        ins.then_inc(diag_ready, 1)
                    for l in lanes:
                        a.wait_ge(shifted, i * LANES + l + 1)
                        a.activation(pr[l][:, :], ps[4 + l][:, 0:T], ACT.Exp, bias=st[l][:, 1:2], scale=float(D) ** -0.5,
                                     accum_out=st[l][:, 2:3]).then_inc(p_exp, 1)

            @block.tensor
            def _(t):
                t.sem_inc(out_mm, 1)
                with t.Fori(0, B // LANES) as i:
                    for m in range(N):
                        t.wait_ge(diag_ready, i * N + m + 1)
                        if m >= 2:
                            t.wait_ge(used, 1 + i * N + m - 1)
                        else:
                            t.wait_ge(used, 1 + i * N)
                        for c in range(LW):
                            mm = t.matmul(ps[m % 2][:, 0:D], diag[m % 2][:, c, :], slots[m][:, W2 + c * D:W2 + (c + 1) * D],
                                          start=(c == 0), stop=(c == LW - 1))
                        mm.then_inc(out_mm, 1)
                    for l in lanes:
                        t.wait_ge(used, 1 + i * N + LANES + l + 1)
                        t.transpose(ps[2 + l][:, 0:T], qkv[l][:, :], S.ident)
                        t.transpose(ps[2 + l][:, T:2 * T], qkv[LANES + l][:, :], S.ident).then_inc(qk_turned, 1)
                    for l in lanes:
                        t.wait_ge(qkT_ready, i * LANES + l + 1)
                        t.matmul(ps[4 + l][:, 0:T], qT[l][:, :], kT[l][:, :], start=True, stop=True).then_inc(s_mm, 1)
                    for l in lanes:
                        t.wait_ge(p_exp, i * LANES + l + 1)
                        t.transpose(ps[4 + l][:, T:2 * T], pr[l][:, :], S.ident).then_inc(p_turned, 1)
                    for l in lanes:
                        t.wait_ge(pT_ready, i * LANES + l + 1)
                        t.matmul(ps[6 + l][:, 0:D], pT[l][:, :], qkv[2 * LANES + l][:, :], start=True,
                                 stop=True).then_inc(att_mm, 1)


def tree_output(nc, S, name, y, leaves, table):
    with phase(nc, name) as ph:
        N = 4
        slots = [ph.sb(f"slot{m}", [P, ROW]) for m in range(N)]
        picks = [ph.sb(f"pick{m}", [P, 1], U32) for m in range(N)]
        prod = ph.sb("prod", [P, LW, D])
        h = [ph.sb(f"h{m}", [P, LW]) for m in range(N)]
        diag = [ph.sb(f"diag{k}", [P, LW, P]) for k in range(2)]
        out = [ph.sb(f"out{k}", [P, D]) for k in range(2)]
        xl = [ph.sb(f"xl{m}", [P, D]) for m in range(N)]
        ps = [ph.ps(f"ps{k}", [P, 512]) for k in range(2)]
        gathered = [ph.sem(f"gathered{m}") for m in range(N)]
        dve_step, pool_step, h_ready, act_ready, diag_ready, out_mm, used = (
            ph.sem(n) for n in ("dve_step", "pool_step", "h_ready", "act_ready", "diag_ready", "out_mm", "used"))
        with nc.Block() as block:
            @block.gpsimd
            def _(g):
                leaf_gathers(g, Steps(g, pool_step), leaves, picks, slots, table, gathered, used, N)

            @block.vector
            def _(v):
                v.sem_inc(used, 1)
                step = Steps(v, dve_step)

                def add_up(i, m):
                    v.wait_ge(out_mm, 1 + i * N + m + 1)
                    step(v.tensor_tensor(out[m % 2][:, :], ps[m % 2][:, 0:D], slots[m][:, B2:B2 + D], ALU.add))
                    v.tensor_tensor(out[m % 2][:, :], out[m % 2][:, :], xl[m][:, :], ALU.add).then_inc(used, 1)
                    v.wait_ge(used, 1 + i * N + m + 1)
                    step(v.tensor_tensor(S.x[:, i * N + m, :], S.x[:, i * N + m, :], out[m % 2][:, :], ALU.add))
                    step(v.bn_stats(S.stats[:, i * N + m, :], S.x[:, i * N + m, :]))

                with v.Fori(0, B // N) as i:
                    step.restart()
                    for m in range(N):
                        step(v.tensor_copy(xl[m][:, :], y[:, i * N + m, :]))
                        v.wait_ge(gathered[m], i * 16 + 16)
                        tree_hidden(v, step, slots[m], xl[m][:, :], prod, h[m]).then_inc(h_ready, 1)
                        if m:
                            add_up(i, m - 1)
                    add_up(i, N - 1)

            @block.scalar
            def _(a):
                with a.Fori(0, B // N) as i:
                    for m in range(N):
                        a.wait_ge(h_ready, i * N + m + 1)
                        a.activation(h[m][:, :], h[m][:, :], ACT.Gelu).then_inc(act_ready, 1)
                        a.wait_ge(act_ready, i * N + m + 1)
                        a.wait_ge(out_mm, 1 + i * N + m - 1) if m >= 2 else a.wait_ge(out_mm, 1 + i * N)
                        for c in range(LW):
                            ins = a.activation(diag[m % 2][:, c, :], S.ident, ACT.Copy, scale=h[m][:, c:c + 1])
                        ins.then_inc(diag_ready, 1)

            @block.tensor
            def _(t):
                t.sem_inc(out_mm, 1)
                with t.Fori(0, B // N) as i:
                    for m in range(N):
                        t.wait_ge(diag_ready, i * N + m + 1)
                        t.wait_ge(used, 1 + i * N + m - 1) if m >= 2 else t.wait_ge(used, 1 + i * N)
                        for c in range(LW):
                            mm = t.matmul(ps[m % 2][:, 0:D], diag[m % 2][:, c, :], slots[m][:, W2 + c * D:W2 + (c + 1) * D],
                                          start=(c == 0), stop=(c == LW - 1))
                        mm.then_inc(out_mm, 1)


def wide_head_attention(nc, S, name, ins):
    HEADS, DH = 16, 64
    EPS = 1e-6
    NCH = HEADS * DH // P
    HPC = 8
    with phase(nc, name) as ph:
        lanes = range(LANES)
        wq = ph.sb("wq", [P, HEADS * DH])
        wkv = ph.sb("wkv", [P, 2, 2 * HEADS * DH])
        wout = ph.sb("wout", [P, NCH, D])
        nulls = ph.sb("nulls", [P, 2, DH])
        wnull = ph.sb("wnull", [P, HEADS])
        prod = ph.sb("prod", [P, HEADS, DH])
        scale_row, bias_row = ph.sb("scale_row", [P, D]), ph.sb("bias_row", [P, D])
        xn = [ph.sb(f"xn{l}", [P, D]) for l in lanes]
        xnT = [ph.sb(f"xnT{l}", [P, T]) for l in lanes]
        cT = [ph.sb(f"cT{l}", [P, 2, P]) for l in lanes]
        qT = [ph.sb(f"qT{l}", [P, NCH, T]) for l in lanes]
        kT = [ph.sb(f"kT{l}", [P, NCH, P]) for l in lanes]
        vals = [ph.sb(f"vals{l}", [P, HEADS, DH + 1]) for l in lanes]
        s0 = [ph.sb(f"s0{l}", [P, HEADS]) for l in lanes]
        p0 = [ph.sb(f"p0{l}", [P, HEADS]) for l in lanes]
        pnv = [ph.sb(f"pnv{l}", [P, HEADS, DH]) for l in lanes]
        probs = [ph.sb(f"probs{l}", [P, HEADS, P]) for l in lanes]
        probsT = [ph.sb(f"probsT{l}", [P, HEADS, P]) for l in lanes]
        mx = [ph.sb(f"mx{l}", [P, HEADS]) for l in lanes]
        rs = [ph.sb(f"rs{l}", [P, HEADS]) for l in lanes]
        osb = [ph.sb(f"osb{l}", [P, HEADS, DH]) for l in lanes]
        oT = [ph.sb(f"oT{l}", [P, NCH, T]) for l in lanes]
        st = [ph.sb(f"st{l}", [P, 6]) for l in lanes]
        mv = [ph.sb(f"mv{l}", [P, 2]) for l in lanes]
        rstd = [ph.sb(f"rstd{l}", [P, 1]) for l in lanes]
        res = [ph.sb(f"res{l}", [P, D]) for l in lanes]
        psA = [ph.ps(f"psA{l}", [P, 1024]) for l in lanes]
        psB = [ph.ps(f"psB{l}", [P, 1024]) for l in lanes]
        (dve_step, pool_step, stats_done, pow_ready, loaded, null_ready, ones_set, xn_ready, xn_turned, xnT_ready, cT_ready,
         q_mm, s0_ready, q_ready, k_mm, k_ready, v_mm, v_ready) = (ph.sem(n) for n in (
             "dve_step", "pool_step", "stats_done", "pow_ready", "loaded", "null_ready", "ones_set", "xn_ready", "xn_turned",
             "xnT_ready", "cT_ready", "q_mm", "s0_ready", "q_ready", "k_mm", "k_ready", "v_mm", "v_ready"))
        (scores_ready, shifted, exp_ready, turned, probsT_ready, p0_shift, p0_ready, pnv_ready, out_ready, o_ready, o_turned,
         oT_ready, proj_ready, var_ready, rstd_ready) = (ph.sem(n) for n in (
             "scores_ready", "shifted", "exp_ready", "turned", "probsT_ready", "p0_shift", "p0_ready", "pnv_ready",
             "out_ready", "o_ready", "o_turned", "oT_ready", "proj_ready", "var_ready", "rstd_ready"))

        def chunk_count(i, c, l):
            return i * (2 * LANES) + (c * LANES + l + 1)

        def out_parts(l):
            def view(x, n):
                return x.rearrange("p (h d) -> p h d", d=DH + 1) if n else None
            return [(slice(0, 7), view(psA[l][:, 0:7 * (DH + 1)], 7)),
                    (slice(7, 14), view(psA[l][:, 512:512 + 7 * (DH + 1)], 7)),
                    (slice(14, 16), view(psB[l][:, 0:2 * (DH + 1)], 2))]

        with nc.Block() as block:
            @block.sync
            def _(sp):
                sp.dma_start(wq[:, :], ins["L2_xattn_Wq"]).then_inc(loaded, 16)
                sp.dma_start(nulls[:, :, :], ins["L2_xattn_null_kv"].partition_broadcast(P)).then_inc(loaded, 16)
                sp.dma_start(wkv[:, :, :], ins["L2_xattn_Wkv"].rearrange("(s p) n -> p s n", p=P)).then_inc(loaded, 16)
                sp.dma_start(wout[:, :, :], ins["L2_xattn_Wout"].rearrange("(c p) n -> p c n", p=P)).then_inc(loaded, 16)
                sp.dma_start(scale_row[:, :], ins["L2_xattn_ln_scale"].partition_broadcast(P)).then_inc(loaded, 16)
                sp.dma_start(bias_row[:, :], ins["L2_xattn_ln_bias"].partition_broadcast(P)).then_inc(loaded, 16)

            @block.gpsimd
            def _(g):
                for l in lanes:
                    g.memset(vals[l][:, :, :], 1.0).then_inc(ones_set, 1)
                inverse_roots(g, S, stats_done, pow_ready)
                g.wait_ge(loaded, 96)
                with g.Fori(0, B // LANES) as i:
                    for l in lanes:
                        g.wait_ge(v_mm, 1 + i * LANES)
                        g.tensor_copy(cT[l][:, :, :], S.ctxT[:, :, bass.ds(i * LANES + l, 1), :]
                                      .rearrange("p s o k -> p (s o) k")).then_inc(cT_ready, 1)
                    for l in lanes:
                        g.wait_ge(p0_ready, i * LANES + l + 1)
                        g.tensor_tensor(pnv[l][:, :, :], nulls[:, 1, :].unsqueeze(1).broadcast_to([P, HEADS, DH]),
                                        p0[l][:, :].unsqueeze(2).broadcast_to([P, HEADS, DH]), ALU.mult).then_inc(pnv_ready, 1)
                    for l in lanes:
                        g.wait_ge(var_ready, i * LANES + l + 1)
                        g.tensor_tensor(rstd[l][:, :], mv[l][:, 1:2], S.mhalf[:, 0:1], ALU.pow).then_inc(rstd_ready, 1)

            @block.vector
            def _(v):
                step = Steps(v, dve_step)
                layer_norm_coefficients(v, step, S, stats_done, pow_ready)
                v.wait_ge(loaded, 96)
                step(v.tensor_tensor(prod[:, :, :], wq[:, :].rearrange("p (h d) -> p h d", d=DH),
                                     nulls[:, 0, :].unsqueeze(1).broadcast_to([P, HEADS, DH]), ALU.mult))
                v.tensor_reduce(wnull[:, :], prod[:, :, :], AX.X, ALU.add).then_inc(null_ready, 1)
                with v.Fori(0, B // LANES) as i:
                    step.restart()
                    for l in lanes:
                        b = i * LANES + l
                        v.tensor_scalar(xn[l][:, :], S.x[:, b, :], S.mean[:, bass.ds(b, 1)], S.rstd[:, bass.ds(b, 1)],
                                        ALU.subtract, ALU.mult).then_inc(xn_ready, 1)
                    for l in lanes:
                        v.wait_ge(q_mm, i * LANES + l + 1)
                        v.tensor_scalar(s0[l][:, :], psB[l][:, 512:512 + HEADS], DH ** -0.5, None,
                                        ALU.mult).then_inc(s0_ready, 1)
                    for l in lanes:
                        v.wait_ge(k_mm, i * LANES + l + 1)
                        v.tensor_copy(kT[l][:, :, :].rearrange("p c k -> p (c k)"), psB[l][:, :]).then_inc(k_ready, 1)
                    for c in range(2):
                        for l in lanes:
                            heads = slice(c * HPC, (c + 1) * HPC)
                            ps = psA[l][:, :].rearrange("p (s j k) -> p j s k", s=2, k=P)
                            v.wait_ge(scores_ready, chunk_count(i, c, l))
                            step(v.tensor_reduce(mx[l][:, heads].rearrange("p (j s) -> p j s", s=2), ps, AX.X, ALU.max))
                            step(v.tensor_tensor(mx[l][:, heads], mx[l][:, heads], s0[l][:, heads], ALU.max))
                            v.tensor_tensor(probs[l][:, heads, :].rearrange("p (j s) k -> p j s k", s=2), ps,
                                            mx[l][:, heads].rearrange("p (j s) -> p j s", s=2).unsqueeze(3)
                                            .broadcast_to([P, HPC // 2, 2, P]), ALU.subtract).then_inc(shifted, 1)
                            if c:
                                v.tensor_tensor(p0[l][:, :], s0[l][:, :], mx[l][:, :], ALU.subtract).then_inc(p0_shift, 1)
                    for l in lanes:
                        v.wait_ge(out_ready, i * LANES + l + 1)
                        v.wait_ge(pnv_ready, i * LANES + l + 1)
                        for heads, ps in out_parts(l):
                            n = heads.stop - heads.start
                            step(v.tensor_tensor(rs[l][:, heads], ps[:, :, DH], p0[l][:, heads], ALU.add))
                            step(v.tensor_tensor(osb[l][:, heads, :], ps[:, :, 0:DH], pnv[l][:, heads, :], ALU.add))
                        step(v.reciprocal(rs[l][:, :], rs[l][:, :]))
                        v.tensor_tensor(osb[l][:, :, :], osb[l][:, :, :],
                                        rs[l][:, :].unsqueeze(2).broadcast_to([P, HEADS, DH]), ALU.mult).then_inc(o_ready, 1)
                    for l in lanes:
                        v.wait_ge(proj_ready, i * LANES + l + 1)
                        step(v.tensor_copy(res[l][:, :], psB[l][:, 0:D]))
                        step(v.bn_stats(st[l][:, :], res[l][:, :]))
                        step(v.bn_aggr(mv[l][:, :], st[l][:, :]))
                        v.tensor_scalar(mv[l][:, 1:2], mv[l][:, 1:2], EPS, None, ALU.add).then_inc(var_ready, 1)
                    for l in lanes:
                        b = i * LANES + l
                        v.wait_ge(rstd_ready, b + 1)
                        step(v.tensor_scalar(res[l][:, :], res[l][:, :], mv[l][:, 0:1], rstd[l][:, 0:1], ALU.subtract, ALU.mult))
                        step(v.tensor_tensor(res[l][:, :], res[l][:, :], scale_row[:, :], ALU.mult))
                        step(v.tensor_tensor(res[l][:, :], res[l][:, :], bias_row[:, :], ALU.add))
                        step(v.tensor_tensor(S.x[:, b, :], S.x[:, b, :], res[l][:, :], ALU.add))
                        step(v.bn_stats(S.stats[:, b, :], S.x[:, b, :]))

            @block.scalar
            def _(a):
                a.wait_ge(ones_set, LANES)
                with a.Fori(0, B // LANES) as i:
                    for l in lanes:
                        a.wait_ge(xn_turned, i * LANES + l + 1)
                        a.activation(xnT[l][:, :], psB[l][:, 0:T], ACT.Copy).then_inc(xnT_ready, 1)
                    for l in lanes:
                        a.wait_ge(q_mm, i * LANES + l + 1)
                        a.activation(qT[l][:, :, :].rearrange("p c t -> p (c t)"), psA[l][:, :], ACT.Copy,
                                     scale=DH ** -0.5).then_inc(q_ready, 1)
                    for l in lanes:
                        a.wait_ge(v_mm, 1 + i * LANES + l + 1)
                        a.activation(vals[l][:, :, 0:DH], psA[l][:, :].rearrange("p (h d) -> p h d", d=DH),
                                     ACT.Copy).then_inc(v_ready, 1)
                    for c in range(2):
                        for l in lanes:
                            pr = probs[l][:, c * HPC:(c + 1) * HPC, :]
                            a.wait_ge(shifted, chunk_count(i, c, l))
                            a.activation(pr, pr, ACT.Exp).then_inc(exp_ready, 1)
                            if c:
                                a.wait_ge(p0_shift, i * LANES + l + 1)
                                a.activation(p0[l][:, :], p0[l][:, :], ACT.Exp).then_inc(p0_ready, 1)
                        for l in lanes:
                            a.wait_ge(turned, chunk_count(i, c, l))
                            a.activation(probsT[l][:, c * HPC:(c + 1) * HPC, :].rearrange("p j k -> p (j k)"),
                                         psB[l][:, :], ACT.Copy).then_inc(probsT_ready, 1)
                    for l in lanes:
                        a.wait_ge(o_turned, i * LANES + l + 1)
                        a.activation(oT[l][:, :, :].rearrange("p c t -> p (c t)"), psA[l][:, :], ACT.Copy).then_inc(oT_ready, 1)

            @block.tensor
            def _(t):
                t.sem_inc(v_mm, 1)
                t.wait_ge(loaded, 96)
                t.wait_ge(null_ready, 1)
                with t.Fori(0, B // LANES) as i:
                    for l in lanes:
                        t.wait_ge(xn_ready, i * LANES + l + 1)
                        t.transpose(psB[l][:, 0:T], xn[l][:, :], S.ident).then_inc(xn_turned, 1)
                    for l in lanes:
                        t.wait_ge(xnT_ready, i * LANES + l + 1)
                        t.matmul(psB[l][:, 512:512 + HEADS], xnT[l][:, :], wnull[:, :], start=True, stop=True)
                        for c in range(NCH):
                            mm = t.matmul(psA[l][:, c * T:(c + 1) * T], wq[:, c * P:(c + 1) * P], xnT[l][:, :],
                                          start=True, stop=True)
                        mm.then_inc(q_mm, 1)
                    for l in lanes:
                        b = i * LANES + l
                        t.wait_ge(s0_ready, b + 1)
                        t.wait_ge(cT_ready, b + 1)
                        for c in range(NCH):
                            for s in range(2):
                                mm = t.matmul(psB[l][:, c * P:(c + 1) * P], wkv[:, s, c * P:(c + 1) * P], cT[l][:, s, :],
                                              start=(s == 0), stop=(s == 1))
                        mm.then_inc(k_mm, 1)
                    for l in lanes:
                        t.wait_ge(q_ready, i * LANES + l + 1)
                        for n in range(2):
                            at = HEADS * DH + n * 512
                            for s in range(2):
                                mm = t.matmul(psA[l][:, n * 512:(n + 1) * 512], cT[l][:, s, :], wkv[:, s, at:at + 512],
                                              start=(s == 0), stop=(s == 1))
                        mm.then_inc(v_mm, 1)

                    def scores(c, l):
                        if c == 0:
                            t.wait_ge(v_ready, i * LANES + l + 1)
                            t.wait_ge(k_ready, i * LANES + l + 1)
                        else:
                            t.wait_ge(shifted, chunk_count(i, c - 1, l))
                        for j in range(HPC):
                            h = c * HPC + j
                            rows = slice(DH * (h % 2), DH * (h % 2) + DH)
                            at = 512 * (j % 2) + P * (j // 2)
                            mm = t.matmul(psA[l][:, at:at + P], qT[l][rows, h // 2, :], kT[l][rows, h // 2, :],
                                          start=True, stop=True)
                        mm.then_inc(scores_ready, 1)

                    for l in lanes:
                        scores(0, l)
                    for c in range(2):
                        if c == 0:
                            for l in lanes:
                                scores(1, l)
                        for l in lanes:
                            t.wait_ge(exp_ready, chunk_count(i, c, l))
                            if c:
                                t.wait_ge(probsT_ready, chunk_count(i, c - 1, l))
                            for j in range(HPC):
                                mm = t.transpose(psB[l][:, j * P:(j + 1) * P], probs[l][:, c * HPC + j, :], S.ident)
                            mm.then_inc(turned, 1)
                    for l in lanes:
                        t.wait_ge(probsT_ready, chunk_count(i, 1, l))
                        for heads, ps in out_parts(l):
                            for j, h in enumerate(range(heads.start, heads.stop)):
                                mm = t.matmul(ps[:, j, :], probsT[l][:, h, :], vals[l][:, h, :], start=True, stop=True)
                        mm.then_inc(out_ready, 1)
                    for l in lanes:
                        t.wait_ge(o_ready, i * LANES + l + 1)
                        for c in range(NCH):
                            mm = t.transpose(psA[l][:, c * T:(c + 1) * T],
                                             osb[l][:, 2 * c:2 * c + 2, :].rearrange("p h d -> p (h d)"), S.ident)
                        mm.then_inc(o_turned, 1)
                    for l in lanes:
                        t.wait_ge(oT_ready, i * LANES + l + 1)
                        for c in range(NCH):
                            mm = t.matmul(psB[l][:, 0:D], oT[l][:, c, :], wout[:, c, :], start=(c == 0), stop=(c == NCH - 1))
                        mm.then_inc(proj_ready, 1)


def normed_rows_and_logits(nc, S, ph, name, experts, w, w_dram, xT_all, logits):
    with phase(nc, name) as pn:
        lanes = range(LANES)
        xn = [pn.sb(f"xn{l}", [P, D]) for l in lanes]
        xT = [pn.sb(f"xT{l}", [P, T]) for l in lanes]
        ps = [pn.ps(f"ps{k}", [P, 512]) for k in range(4)]
        dve_step, stats_done, pow_ready, loaded, xn_ready, turned, xT_ready, xT_kept, logits_mm, logits_kept = (
            pn.sem(n) for n in ("dve_step", "stats_done", "pow_ready", "loaded", "xn_ready", "turned", "xT_ready", "xT_kept",
                                "logits_mm", "logits_kept"))
        with nc.Block() as block:
            @block.sync
            def _(sp):
                sp.dma_start(w[:, :], w_dram).then_inc(loaded, 16)

            @block.gpsimd
            def _(g):
                inverse_roots(g, S, stats_done, pow_ready)

            @block.vector
            def _(v):
                v.sem_inc(logits_kept, 1)
                v.sem_inc(xT_ready, 1)
                step = Steps(v, dve_step)
                layer_norm_coefficients(v, step, S, stats_done, pow_ready)
                with v.Fori(0, B // LANES) as i:
                    for l in lanes:
                        b = i * LANES + l
                        v.wait_ge(turned, 1 + i * LANES)
                        v.tensor_scalar(xn[l][:, :], S.x[:, b, :], S.mean[:, bass.ds(b, 1)], S.rstd[:, bass.ds(b, 1)],
                                        ALU.subtract, ALU.mult).then_inc(xn_ready, 1)
                    for l in lanes:
                        b = i * LANES + l
                        v.wait_ge(turned, 1 + b + 1)
                        v.wait_ge(logits_mm, 1 + i * LANES)
                        v.wait_ge(xT_kept, 1 + i * LANES)
                        v.tensor_copy(xT[l][:, :], ps[l][:, 0:T]).then_inc(xT_ready, 1)
                    for l in lanes:
                        b = i * LANES + l
                        v.wait_ge(logits_mm, 1 + b + 1)
                        v.tensor_copy(logits[:, b, :], ps[2 + l][:, 0:experts]).then_inc(logits_kept, 1)

            @block.scalar
            def _(a):
                a.sem_inc(xT_kept, 1)
                with a.Fori(0, B // LANES) as i:
                    for l in lanes:
                        b = i * LANES + l
                        a.wait_ge(xT_ready, 1 + b + 1)
                        a.activation(xT_all[:, b, :], xT[l][:, :], ACT.Copy).then_inc(xT_kept, 1)

            @block.tensor
            def _(t):
                t.sem_inc(logits_mm, 1)
                t.sem_inc(turned, 1)
                t.wait_ge(loaded, 16)
                with t.Fori(0, B // LANES) as i:
                    for l in lanes:
                        t.wait_ge(xn_ready, i * LANES + l + 1)
                        t.wait_ge(xT_ready, 1 + i * LANES)
                        t.transpose(ps[l][:, 0:T], xn[l][:, :], S.ident).then_inc(turned, 1)
                    for l in lanes:
                        t.wait_ge(xT_ready, 1 + i * LANES + l + 1)
                        t.wait_ge(logits_kept, 1 + i * LANES)
                        t.matmul(ps[2 + l][:, 0:experts], xT[l][:, :], w[:, :], start=True, stop=True).then_inc(logits_mm, 1)


def chosen(v, step, S, vals, n, count, above, ties, sel):
    mine = vals.unsqueeze(3).broadcast_to([P, B, n, n])
    other = vals.unsqueeze(2).broadcast_to([P, B, n, n])
    before = S.before16.rearrange("p (a b) -> p a b", b=16)[:, 0:n, 0:n]
    step(v.tensor_tensor(above, other, mine, ALU.is_gt))
    step(v.tensor_tensor(ties, other, mine, ALU.is_equal))
    step(v.tensor_tensor(ties, ties, before.unsqueeze(1).broadcast_to([P, B, n, n]), ALU.mult))
    step(v.tensor_tensor(above, above, ties, ALU.add))
    step(v.tensor_reduce(sel, above, AX.X, ALU.add))
    step(v.tensor_scalar(sel, sel, float(count), None, ALU.is_lt))


def grouped_mixture(nc, S, name, ins):
    E, F, GROUPS, TOP_GROUPS, TOP, SHARED, SCALE = 16, 128, 4, 2, 4, 2, 2.5
    ALL = E + SHARED
    PER = E // GROUPS
    G = 4
    with phase(nc, name) as ph:
        wr = ph.sb("wr", [P, E])
        gate, up, down = (ph.sb(n, [P, ALL, F]) for n in ("gate", "up", "down"))
        xT = ph.sb("xT", [P, B, T])
        mix = ph.sb("mix", [P, B, ALL])
        score = ph.sb("score", [P, B, E])
        weights_loaded = ph.sem("weights_loaded")
        with nc.Block() as block:
            @block.sync
            def _(sp):
                for dst, n in ((gate, "gate_w"), (up, "up_w"), (down, "down_w")):
                    sp.dma_start(dst[:, 0:E, :], ins["L2_ffn_" + n].rearrange("e i j -> i e j")).then_inc(weights_loaded, 16)
                for dst, n in ((gate, "sh_gate_w"), (up, "sh_up_w")):
                    sp.dma_start(dst[:, E:ALL, :], ins["L2_ffn_" + n].rearrange("i (e j) -> i e j", j=F)).then_inc(weights_loaded, 16)
                sp.dma_start(down[:, E:ALL, :], ins["L2_ffn_sh_down_w"].rearrange("(e i) j -> i e j", i=F)).then_inc(weights_loaded, 16)
        normed_rows_and_logits(nc, S, ph, name + "_n", E, wr, ins["L2_router_wT"], xT, score)

        with phase(nc, name + "_r") as pr:
            bias = pr.sb("bias", [P, E])
            biased, masked = pr.sb("biased", [P, B, E]), pr.sb("masked", [P, B, E])
            above, ties = pr.sb("above", [P, B, E, E]), pr.sb("ties", [P, B, E, E])
            hi, lo = pr.sb("hi", [P, B, GROUPS, 2]), pr.sb("lo", [P, B, GROUPS, 2])
            best, second, third = (pr.sb(n, [P, B, GROUPS]) for n in ("best", "second", "third"))
            total = pr.sb("total", [P, B])
            dve_step, bias_loaded, exp_done = pr.sem("dve_step"), pr.sem("bias_loaded"), pr.sem("exp_done")
            with nc.Block() as block:
                @block.sync
                def _(sp):
                    sp.dma_start(bias[:, :], ins["L2_ffn_bias"].partition_broadcast(P)).then_inc(bias_loaded, 16)

                @block.scalar
                def _(a):
                    a.activation(score[:, :, :], score[:, :, :], ACT.Exp, scale=-1.0).then_inc(exp_done, 1)

                @block.vector
                def _(v):
                    step = Steps(v, dve_step)
                    v.wait_ge(bias_loaded, 16)
                    v.wait_ge(exp_done, 1)
                    step(v.tensor_scalar(score[:, :, :], score[:, :, :], 1.0, None, ALU.add))
                    step(v.reciprocal(score[:, :, :], score[:, :, :]))
                    step(v.tensor_tensor(biased[:, :, :], score[:, :, :],
                                         bias[:, :].unsqueeze(1).broadcast_to([P, B, E]), ALU.add))
                    quad = biased[:, :, :].rearrange("p b (g two c) -> p (b g) two c", two=2, c=2)
                    h2, l2 = (x[:, :, :, :].rearrange("p b g c -> p (b g) c") for x in (hi, lo))
                    bst, sec, thr = (x[:, :, :].rearrange("p b g -> p (b g)") for x in (best, second, third))
                    step(v.tensor_tensor(h2, quad[:, :, 0, :], quad[:, :, 1, :], ALU.max))
                    step(v.tensor_tensor(l2, quad[:, :, 0, :], quad[:, :, 1, :], ALU.min))
                    step(v.tensor_tensor(bst, h2[:, :, 0], h2[:, :, 1], ALU.max))
                    step(v.tensor_tensor(sec, h2[:, :, 0], h2[:, :, 1], ALU.min))
                    step(v.tensor_tensor(thr, l2[:, :, 0], l2[:, :, 1], ALU.max))
                    step(v.tensor_tensor(sec, sec, thr, ALU.max))
                    step(v.tensor_tensor(bst, bst, sec, ALU.add))
                    chosen(v, step, S, best[:, :, :], GROUPS, TOP_GROUPS, above[:, :, 0:GROUPS, 0:GROUPS],
                           ties[:, :, 0:GROUPS, 0:GROUPS], second[:, :, :])
                    m = sec.unsqueeze(2).broadcast_to([P, B * GROUPS, PER])
                    mk, bs = (x[:, :, :].rearrange("p b (g c) -> p (b g) c", c=PER) for x in (masked, biased))
                    step(v.tensor_tensor(mk, bs, m, ALU.mult))
                    step(v.tensor_scalar(thr, sec, -1.0, None, ALU.add))
                    step(v.tensor_tensor(mk, mk, thr.unsqueeze(2).broadcast_to([P, B * GROUPS, PER]), ALU.add))
                    chosen(v, step, S, masked[:, :, :], E, TOP, above[:, :, :, :], ties[:, :, :, :], biased[:, :, :])
                    step(v.tensor_tensor(masked[:, :, :], score[:, :, :], biased[:, :, :], ALU.mult))
                    step(v.tensor_reduce(total[:, :], masked[:, :, :], AX.X, ALU.add))
                    step(v.tensor_scalar(total[:, :], total[:, :], 1e-20, None, ALU.add))
                    step(v.reciprocal(total[:, :], total[:, :]))
                    step(v.tensor_scalar(total[:, :], total[:, :], SCALE, None, ALU.mult))
                    step(v.memset(mix[:, :, :], 1.0))
                    step(v.tensor_tensor(mix[:, :, 0:E], masked[:, :, :], total[:, :].unsqueeze(2).broadcast_to([P, B, E]),
                                         ALU.mult))

        with phase(nc, name + "_e") as pe:
            sg = [pe.sb(f"sg{k}", [P, G * T]) for k in range(2)]
            act = [pe.sb(f"act{k}", [P, G * T]) for k in range(2)]
            ps_g = [pe.ps(f"ps_g{k}", [P, G * T]) for k in range(2)]
            ps_u = [pe.ps(f"ps_u{k}", [P, G * T]) for k in range(2)]
            ps_y = [pe.ps(f"ps_y{k}", [P, G, D]) for k in range(2)]
            dve_step, gu_ready, silu_ready, act_ready, y_ready, y_added = (
                pe.sem(n) for n in ("dve_step", "gu_ready", "silu_ready", "act_ready", "y_ready", "y_added"))
            with nc.Block() as block:
                @block.vector
                def _(v):
                    v.sem_inc(y_added, 1)
                    v.sem_inc(act_ready, 1)
                    step = Steps(v, dve_step)

                    def add_up(i, e):
                        v.wait_ge(y_ready, i * ALL + e + 1)
                        if e:
                            v.wait_ge(y_added, 1 + i * ALL + e)
                        for k in range(G):
                            x = S.x[:, i * G + k, :]
                            ins_ = v.scalar_tensor_tensor(out=x, in0=ps_y[e % 2][:, k, :], scalar=mix[:, i * G + k, e:e + 1],
                                                          in1=x, op0=ALU.mult, op1=ALU.add)
                        ins_.then_inc(y_added, 1)

                    with v.Fori(0, B // G) as i:
                        step.restart()
                        for e in range(ALL):
                            v.wait_ge(silu_ready, i * ALL + e + 1)
                            v.tensor_tensor(act[e % 2][:, :], sg[e % 2][:, :], ps_u[e % 2][:, :], ALU.mult).then_inc(act_ready, 1)
                            if e:
                                add_up(i, e - 1)
                        add_up(i, ALL - 1)
                        v.wait_ge(y_added, 1 + i * ALL + ALL)
                        for k in range(G):
                            step(v.bn_stats(S.stats[:, i * G + k, :], S.x[:, i * G + k, :]))

                @block.scalar
                def _(a):
                    with a.Fori(0, B // G) as i:
                        for e in range(ALL):
                            a.wait_ge(gu_ready, i * ALL + e + 1)
                            a.wait_ge(act_ready, 1 + i * ALL + e - 1) if e >= 2 else a.wait_ge(act_ready, 1 + i * ALL)
                            a.activation(sg[e % 2][:, :], ps_g[e % 2][:, :], ACT.Silu).then_inc(silu_ready, 1)

                @block.tensor
                def _(t):
                    t.wait_ge(weights_loaded, 96)

                    def project(i, e):
                        t.wait_ge(act_ready, 1 + i * ALL + e + 1)
                        t.wait_ge(y_added, 1 + i * ALL + e - 1) if e >= 2 else t.wait_ge(y_added, 1 + i * ALL)
                        for k in range(G):
                            mm = t.matmul(ps_y[e % 2][:, k, :], act[e % 2][:, k * T:(k + 1) * T], down[:, e, :],
                                          start=True, stop=True)
                        mm.then_inc(y_ready, 1)

                    with t.Fori(0, B // G) as i:
                        for e in range(ALL):
                            t.wait_ge(act_ready, 1 + i * ALL + e - 1) if e >= 2 else t.wait_ge(act_ready, 1 + i * ALL)
                            rows = xT[:, bass.ds(i * G, G), :].rearrange("p b t -> p (b t)")
                            t.matmul(ps_g[e % 2][:, :], gate[:, e, :], rows, start=True, stop=True)
                            t.matmul(ps_u[e % 2][:, :], up[:, e, :], rows, start=True, stop=True).then_inc(gu_ready, 1)
                            if e:
                                project(i, e - 1)
                        project(i, ALL - 1)


def top_two_mixture(nc, S, name, ins):
    E, HID, TOP = 8, 512, 2
    HC = HID // P
    G = 4
    with phase(nc, name) as ph:
        wr = ph.sb("wr", [P, E])
        w1 = ph.sb("w1", [P, E, HID])
        w2 = ph.sb("w2", [P, E, HC, D])
        b1 = ph.sb("b1", [P, E, HC])
        b2 = ph.sb("b2", [E, D])
        xT = ph.sb("xT", [P, B, T])
        mix = ph.sb("mix", [P, B, E])
        prob = ph.sb("prob", [P, B, E])
        weights_loaded = ph.sem("weights_loaded")
        with nc.Block() as block:
            @block.sync
            def _(sp):
                sp.dma_start(w1[:, :, :], ins["L3_w1T"].rearrange("e d h -> d e h")).then_inc(weights_loaded, 16)
                sp.dma_start(w2[:, :, :, :], ins["L3_w2T"].rearrange("e (c p) d -> p e c d", p=P)).then_inc(weights_loaded, 16)
                sp.dma_start(b1[:, :, :], ins["L3_b1T"]).then_inc(weights_loaded, 16)
                sp.dma_start(b2[:, :], ins["L3_ffn_b2"]).then_inc(weights_loaded, 16)
        normed_rows_and_logits(nc, S, ph, name + "_n", E, wr, ins["L3_gate_wT"], xT, prob)

        with phase(nc, name + "_r") as pr:
            lanes = range(LANES)
            above, ties = pr.sb("above", [P, B, E, E]), pr.sb("ties", [P, B, E, E])
            sel, top, total = pr.sb("sel", [P, B, E]), pr.sb("top", [P, B]), pr.sb("total", [P, B])
            m1 = [pr.sb(f"m1{l}", [P, E]) for l in lanes]
            mT = [pr.sb(f"mT{l}", [E, T]) for l in lanes]
            ps = [pr.ps(f"ps{k}", [P, 512]) for k in range(4)]
            dve_step, shift_done, exp_done, m_ready, m_turned, mT_ready, bias_ready = (
                pr.sem(n) for n in ("dve_step", "shift_done", "exp_done", "m_ready", "m_turned", "mT_ready", "bias_ready"))
            with nc.Block() as block:
                @block.scalar
                def _(a):
                    a.wait_ge(shift_done, 1)
                    a.activation(prob[:, :, :], prob[:, :, :], ACT.Exp).then_inc(exp_done, 1)

                @block.vector
                def _(v):
                    step = Steps(v, dve_step)
                    row = lambda x: x[:, :].unsqueeze(2).broadcast_to([P, B, E])
                    step(v.tensor_reduce(top[:, :], prob[:, :, :], AX.X, ALU.max))
                    v.tensor_tensor(prob[:, :, :], prob[:, :, :], row(top), ALU.subtract).then_inc(shift_done, 1)
                    v.wait_ge(exp_done, 1)
                    step(v.tensor_reduce(total[:, :], prob[:, :, :], AX.X, ALU.add))
                    step(v.reciprocal(total[:, :], total[:, :]))
                    step(v.tensor_tensor(prob[:, :, :], prob[:, :, :], row(total), ALU.mult))
                    chosen(v, step, S, prob[:, :, :], E, TOP, above[:, :, :, :], ties[:, :, :, :], sel[:, :, :])
                    step(v.tensor_tensor(prob[:, :, :], prob[:, :, :], sel[:, :, :], ALU.mult))
                    step(v.tensor_reduce(total[:, :], prob[:, :, :], AX.X, ALU.add))
                    step(v.reciprocal(total[:, :], total[:, :]))
                    step(v.tensor_tensor(mix[:, :, :], prob[:, :, :], row(total), ALU.mult))
                    with v.Fori(0, B // LANES) as i:
                        step.restart()
                        for l in lanes:
                            v.tensor_copy(m1[l][:, :], mix[:, i * LANES + l, :]).then_inc(m_ready, 1)
                        for l in lanes:
                            v.wait_ge(m_turned, i * LANES + l + 1)
                            v.tensor_copy(mT[l][:, :], ps[l][0:E, 0:T]).then_inc(mT_ready, 1)
                        for l in lanes:
                            v.wait_ge(bias_ready, i * LANES + l + 1)
                            step(v.tensor_tensor(S.x[:, i * LANES + l, :], S.x[:, i * LANES + l, :], ps[2 + l][:, 0:D], ALU.add))

                @block.tensor
                def _(t):
                    t.wait_ge(weights_loaded, 64)
                    with t.Fori(0, B // LANES) as i:
                        for l in lanes:
                            t.wait_ge(m_ready, i * LANES + l + 1)
                            t.transpose(ps[l][0:E, 0:T], m1[l][:, :], S.ident).then_inc(m_turned, 1)
                        for l in lanes:
                            t.wait_ge(mT_ready, i * LANES + l + 1)
                            t.matmul(ps[2 + l][:, 0:D], mT[l][:, :], b2[:, :], start=True, stop=True).then_inc(bias_ready, 1)

        with phase(nc, name + "_e") as pe:
            act = [pe.sb(f"act{k}", [P, HC, G * T]) for k in range(2)]
            ps_h = [pe.ps(f"ps_h{k}", [P, G * T]) for k in range(4)]
            ps_y = [pe.ps(f"ps_y{k}", [P, G, D]) for k in range(2)]
            h_ready, act_ready, y_ready, y_added = (pe.sem(n) for n in ("h_ready", "act_ready", "y_ready", "y_added"))
            with nc.Block() as block:
                @block.vector
                def _(v):
                    v.sem_inc(y_added, 1)
                    with v.Fori(0, B // G) as i:
                        for e in range(E):
                            v.wait_ge(y_ready, 1 + i * E + e + 1)
                            if e:
                                v.wait_ge(y_added, 1 + i * E + e)
                            for k in range(G):
                                x = S.x[:, i * G + k, :]
                                ins_ = v.scalar_tensor_tensor(out=x, in0=ps_y[e % 2][:, k, :], scalar=mix[:, i * G + k, e:e + 1],
                                                              in1=x, op0=ALU.mult, op1=ALU.add)
                            ins_.then_inc(y_added, 1)

                @block.scalar
                def _(a):
                    a.sem_inc(act_ready, 1)
                    with a.Fori(0, B // G) as i:
                        for e in range(E):
                            a.wait_ge(y_ready, 1 + i * E + e - 1) if e >= 2 else a.wait_ge(y_ready, 1 + i * E)
                            for c in range(HC):
                                a.wait_ge(h_ready, (i * E + e) * HC + c + 1)
                                a.activation(act[e % 2][:, c, :], ps_h[c][:, :], ACT.Relu, bias=b1[:, e, c:c + 1]).then_inc(act_ready, 1)

                @block.tensor
                def _(t):
                    t.sem_inc(y_ready, 1)
                    def project(i, e):
                        t.wait_ge(act_ready, 1 + (i * E + e + 1) * HC)
                        t.wait_ge(y_added, 1 + i * E + e - 1) if e >= 2 else t.wait_ge(y_added, 1 + i * E)
                        for k in range(G):
                            for c in range(HC):
                                mm = t.matmul(ps_y[e % 2][:, k, :], act[e % 2][:, c, k * T:(k + 1) * T], w2[:, e, c, :],
                                              start=(c == 0), stop=(c == HC - 1))
                        mm.then_inc(y_ready, 1)

                    with t.Fori(0, B // G) as i:
                        rows = xT[:, bass.ds(i * G, G), :].rearrange("p b t -> p (b t)")
                        for e in range(E):
                            for c in range(HC):
                                t.wait_ge(act_ready, 1 + (i * E + e - 1) * HC + c + 1) if e else t.wait_ge(act_ready, 1 + i * E * HC)
                                t.matmul(ps_h[c][:, :], w1[:, e, c * P:(c + 1) * P], rows, start=True, stop=True).then_inc(h_ready, 1)
                            if e:
                                project(i, e - 1)
                        project(i, E - 1)


def projected_attention(nc, S, name, ins):
    with phase(nc, name + "_w") as ph:
        wqkvT = ph.sb("wqkvT", [P, 3 * D])
        wprojT = ph.sb("wprojT", [P, D])
        b_proj = ph.sb("b_proj", [P, D])
        loaded = ph.sem("loaded")
        with nc.Block() as block:
            @block.sync
            def _(sp):
                sp.dma_start(wqkvT[:, :], ins["L3_w_qkvT"]).then_inc(loaded, 16)
                sp.dma_start(wprojT[:, :], ins["L3_w_projT"]).then_inc(loaded, 16)
                sp.dma_start(b_proj[:, :], ins["L3_xattn_b_proj"].partition_broadcast(P)).then_inc(loaded, 16)
                sp.wait_ge(loaded, 48)
        small_head_attention(nc, S, name, True, weights={
            "wqT": wqkvT[:, 0:D], "wkT": wqkvT[:, D:2 * D], "wvT": wqkvT[:, 2 * D:3 * D],
            "wprojT": wprojT[:, :], "b_proj": b_proj[:, :]})


def build(nc, ins, out):
    at, width = constant_offsets()
    with ExitStack() as ctx:
        def sb(name, shape, dt=F32):
            return ctx.enter_context(nc.sbuf_tensor(name, shape, dt))
        S = Shared()
        S.x = sb("x", [P, B, D])
        S.ctx = sb("ctx", [P, B, CTX])
        S.ctxT = sb("ctxT", [P, 2, B, P])
        S.stats = sb("stats", [P, B, 6])
        S.mean, S.dif, S.var, S.rstd, S.mhalf = (sb(n, [P, B]) for n in ("mean", "dif", "var", "rstd", "mhalf"))
        consts = sb("consts", [P, width])

        def const(name):
            return consts[:, at[name][0]:at[name][1]]
        S.ident, S.iota_row, S.iota_col, S.upto, S.ones = (const(n) for n in ("ident", "iota_row", "iota_col", "upto", "ones"))
        S.headmask, S.cos, S.sin, S.sameexpert = (const(n) for n in ("headmask", "cos", "sin", "sameexpert"))
        S.expertmask, S.decay, S.before16 = (const(n) for n in ("expertmask", "decay", "before16"))
        S.iota256 = consts[:, at["iota_row"][0]:at["iota_row2"][1]]
        load_inputs(nc, S, ins, consts)
        all_stages(nc, S, ins)
        with phase(nc, "store") as ph:
            stored = ph.sem("stored")
            with nc.Block() as block:
                @block.sync
                def _(sp):
                    sp.dma_start(out.rearrange("b t d -> t b d"), S.x[:, :, :]).then_inc(stored, 16)
                    sp.wait_ge(stored, 16)


def load_inputs(nc, S, ins, consts):
    with phase(nc, "load") as ph:
        x_loaded, rest_loaded, step_sem, half_set = (ph.sem(n) for n in ("x_loaded", "rest_loaded", "dve_step", "half_set"))
        with nc.Block() as block:
            @block.sync
            def _(sp):
                sp.dma_start(S.x[:, :, :], ins["x"].rearrange("b t d -> t b d")).then_inc(x_loaded, 16)
                sp.dma_start(consts[:, :], ins["consts"]).then_inc(rest_loaded, 16)
                sp.dma_start(S.ctxT[:, :, :, :], ins["ctxT"].rearrange("s p b k -> p s b k")).then_inc(rest_loaded, 16)
                sp.dma_start(S.ctx[:, :, :], ins["ctx"].rearrange("b t d -> t b d")).then_inc(rest_loaded, 16)
                sp.wait_ge(rest_loaded, 48)

            @block.vector
            def _(v):
                v.memset(S.mhalf[:, :], -0.5).then_inc(half_set, 1)
                v.wait_ge(x_loaded, 16)
                v.wait_ge(half_set, 1)
                step = Steps(v, step_sem)
                with v.Fori(0, B) as b:
                    step.restart()
                    step(v.bn_stats(S.stats[:, b, :], S.x[:, b, :]))


def all_stages(nc, S, ins):
    stages = [
        lambda: small_head_attention(nc, S, "L0x", False, seq_len=ins["seq_len"], bias=ins["L0_xattn_b"]),
        lambda: expert_choice_attention(nc, S, "L0f", ins),
        lambda: patch_depool(nc, S, "L1x", ins),
        lambda: routed_trees(nc, S, "L1f", ins),
        lambda: wide_head_attention(nc, S, "L2x", ins),
        lambda: grouped_mixture(nc, S, "L2f", ins),
        lambda: projected_attention(nc, S, "L3x", ins),
        lambda: top_two_mixture(nc, S, "L3f", ins),
    ]
    for stage in stages:
        stage()


def lay_out(inputs):
    c = np.ascontiguousarray
    g = {k: np.asarray(v) for k, v in inputs.items()}
    f = {}
    f["x"] = c(g["x"])
    f["ctx"] = c(g["ctx_2048"])
    f["ctxT"] = c(g["ctx_2048"].transpose(2, 0, 1).reshape(2, P, B, T))
    f["seq_len"] = c(g["itok_Bx1_68_817"].reshape(B))
    f["L0_xattn_b"] = c(g["L0_xattn_b"])
    f["L0_ffn_WrT"] = c(g["L0_ffn_Wr"].T)
    f["L0_ffn_Wqkv"] = c(g["L0_ffn_Wqkv"])
    half = np.r_[ROPE_HALF:ROPE_N, 0:ROPE_HALF]
    f["L0_ffn_Wswap"] = c(np.stack([g["L0_ffn_Wqkv"][:, :, half], g["L0_ffn_Wqkv"][:, :, D + half]], 2))
    f["L0_ffn_Wo"] = c(g["L0_ffn_Wo"])
    f["L1_W_inT"] = c(g["L1_xattn_W_in"].T)
    for n in ("L1_xattn_b_in", "L1_xattn_g_res", "L1_xattn_g_init"):
        f[n] = c(g[n])
    f["patch_lensT"] = c(g["mask_BxS2_if0"].T)
    f["L1_ffn_nw3"] = c(np.concatenate([g[f"L1_ffn_{n}_nw"] for n in "qkv"]).T)
    f["L1_ffn_nb3"] = c(np.concatenate([g[f"L1_ffn_{n}_nb"] for n in "qkv"]))
    f["L1_ffn_nwf"] = c(g["L1_ffn_f_nw"].T)
    f["L1_ffn_nbf"] = c(g["L1_ffn_f_nb"])
    f["leaf_table"] = c(np.concatenate([np.concatenate([
        g[f"L1_ffn_{n}_w1"].transpose(0, 2, 1).reshape(LEAVES, LW * D), g[f"L1_ffn_{n}_b1"],
        g[f"L1_ffn_{n}_w2"].reshape(LEAVES, LW * D), g[f"L1_ffn_{n}_b2"]], 1) for n in "qkvf"]))
    for n in ("L2_xattn_Wq", "L2_xattn_Wkv", "L2_xattn_Wout", "L2_xattn_null_kv", "L2_xattn_ln_scale", "L2_xattn_ln_bias",
              "L2_ffn_bias", "L2_ffn_gate_w", "L2_ffn_up_w", "L2_ffn_down_w", "L2_ffn_sh_gate_w", "L2_ffn_sh_up_w",
              "L2_ffn_sh_down_w", "L3_xattn_b_proj", "L3_ffn_b2"):
        f[n] = c(g[n])
    f["L2_router_wT"] = c(g["L2_ffn_router_w"].T)
    f["L3_w_qkvT"] = c(g["L3_xattn_w_qkv"].T)
    f["L3_w_projT"] = c(g["L3_xattn_w_proj"].T)
    f["L3_gate_wT"] = c(g["L3_ffn_gate_w"].T)
    f["L3_w1T"] = c(g["L3_ffn_w1"].transpose(0, 2, 1))
    f["L3_w2T"] = c(g["L3_ffn_w2"].transpose(0, 2, 1))
    f["L3_b1T"] = c(g["L3_ffn_b1"].reshape(8, 4, P).transpose(2, 0, 1))
    f["consts"] = c(np.concatenate([np.asarray(a, np.float32) for a in constant_columns().values()], 1))
    return f


def kernel(**inputs):
    import concourse.bacc as bacc
    from concourse.bass_utils import run_bass_kernel_spmd

    nc = bacc.Bacc("TRN2", target_bir_lowering=False, num_devices=1)
    arrays, ins = {}, {}
    for name, a in lay_out(inputs).items():
        arrays[f"in_{name}"] = a
        ins[name] = nc.dram_tensor(f"in_{name}", a.shape, mybir.dt.from_np(a.dtype), kind="ExternalInput").ap()
    out = nc.dram_tensor("out_0", (B, T, D), F32, kind="ExternalOutput").ap()
    build(nc, ins, out)
    r = run_bass_kernel_spmd(nc, [arrays], core_ids=[0])
    return r.results[0]["out_0"]
```

```python
from contextlib import ExitStack, contextmanager

import numpy as np

import concourse.bass as bass
from concourse import mybir

F32 = mybir.dt.float32
I32 = mybir.dt.int32
U32 = mybir.dt.uint32
ALU = mybir.AluOpType
ACT = mybir.ActivationFunctionType
AX = mybir.AxisListType

P = 128
B = 16
T = 128
D = 128
CTX = 256
LANES = 2
LN_EPS = 1e-5
NEG = -1e30

ROPE_HALF, ROPE_N, ROPE_BASE = 32, 64, 10000.0
E0, K0 = 8, 16
NODES, LEAVES, LW = 255, 256, 16
LOGP = -0.001


def constant_columns():
    p = np.arange(P)[:, None]
    c = np.arange(P)[None, :]
    f = np.float32
    inv = (1.0 / np.power(f(ROPE_BASE), np.arange(ROPE_HALF, dtype=f) * f(2.0) / f(ROPE_N))).astype(f)
    ang = (np.arange(T, dtype=f)[:, None] * inv).astype(f)
    sin, cos = np.sin(ang), np.cos(ang)
    dt = -np.log(-np.expm1(LOGP))
    power = np.maximum(c - p, 0)
    pair = np.arange(16)
    return {
        "ident": (p == c),
        "iota_row": np.broadcast_to(c, (P, P)),
        "iota_row2": np.broadcast_to(c + P, (P, P)),
        "iota_col": p,
        "upto": (p <= c),
        "ones": np.ones((P, P)),
        "headmask": (p // 8 == np.arange(16)[None, :]),
        "cos": np.concatenate([cos, cos], 1),
        "sin": np.concatenate([-sin, sin], 1),
        "sameexpert": (p // K0 == c // K0),
        "expertmask": (p // K0 == np.arange(E0)[None, :]),
        "decay": np.where(c >= p, np.exp(-dt * power), 0.0),
        "pairhead": (np.arange(16)[None, None, :] == 2 * np.arange(8)[None, :, None] + p[:, :, None] // 64).reshape(P, P),
        "before16": np.broadcast_to((pair[None, :] < pair[:, None]).reshape(1, 256), (P, 256)),
    }


def constant_offsets():
    at, n = {}, 0
    for name, a in constant_columns().items():
        at[name] = (n, n + a.shape[1])
        n += a.shape[1]
    return at, n


class Phase:

    def __init__(self, nc, name):
        self.nc, self.name, self.ctx, self.sems = nc, name, ExitStack(), []

    def sb(self, name, shape, dt=F32):
        return self.ctx.enter_context(self.nc.sbuf_tensor(f"{self.name}_{name}", shape, dt))

    def ps(self, name, shape):
        return self.ctx.enter_context(self.nc.psum_tensor(f"{self.name}_{name}", shape, F32))

    def sem(self, name):
        s = self.nc.alloc_semaphore(f"{self.name}_{name}")
        self.sems.append(s)
        return s

    def close(self):
        self.nc.clear_and_free_semaphores(self.sems)
        self.nc.all_engine_barrier()
        self.ctx.close()


@contextmanager
def phase(nc, name):
    ph = Phase(nc, name)
    yield ph
    ph.close()


class Steps:

    def __init__(self, eng, sem):
        self.eng, self.sem, self.n = eng, sem, 0

    def __call__(self, ins):
        self.n += 1
        ins.then_inc(self.sem, 1)
        self.eng.wait_ge(self.sem, self.n)

    def restart(self):
        self.eng.sem_clear(self.sem)
        self.n = 0


class Shared:
    pass


def layer_norm_coefficients(v, step, S, stats_done, pow_ready):
    me, mo = S.stats[:, :, 1], S.stats[:, :, 4]
    ve, vo = S.stats[:, :, 2], S.stats[:, :, 5]
    step(v.tensor_tensor(S.mean[:, :], me, mo, ALU.add))
    step(v.tensor_tensor(S.dif[:, :], me, mo, ALU.subtract))
    step(v.tensor_scalar(S.mean[:, :], S.mean[:, :], 0.5, None, ALU.mult))
    step(v.tensor_tensor(S.var[:, :], ve, vo, ALU.add))
    step(v.scalar_tensor_tensor(out=S.dif[:, :], in0=S.dif[:, :], scalar=0.25, in1=S.dif[:, :],
                                op0=ALU.mult, op1=ALU.mult))
    step(v.scalar_tensor_tensor(out=S.var[:, :], in0=S.var[:, :], scalar=1.0 / D, in1=S.dif[:, :],
                                op0=ALU.mult, op1=ALU.add))
    v.tensor_scalar(S.var[:, :], S.var[:, :], LN_EPS, None, ALU.add).then_inc(stats_done, 1)
    v.wait_ge(pow_ready, 1)


def inverse_roots(g, S, stats_done, pow_ready):
    g.wait_ge(stats_done, 1)
    g.tensor_tensor(S.rstd[:, :], S.var[:, :], S.mhalf[:, :], ALU.pow).then_inc(pow_ready, 1)


def skewed(eng, first, second, body_starts=None):
    def both(j, l, j_before):
        for new, old in zip(first, second):
            new(j, l)
            old(j_before, 1 - l)

    for new in first:
        new(0, 0)
    with eng.Fori(0, B // LANES - 1) as i:
        if body_starts:
            body_starts()
        both(i, 1, i)
        both(i + 1, 0, i)
    if body_starts:
        body_starts()
    both(B // LANES - 1, 1, B // LANES - 1)
    for old in second:
        old(B // LANES - 1, 1)


def normalized(v, step, S, xn_all):
    step(v.tensor_tensor(xn_all[:, :, :], S.x[:, :, :], S.mean[:, :].unsqueeze(2).broadcast_to([P, B, D]), ALU.subtract))
    return v.tensor_tensor(xn_all[:, :, :], xn_all[:, :, :], S.rstd[:, :].unsqueeze(2).broadcast_to([P, B, D]), ALU.mult)


def nothing(j, l):
    pass


def small_head_attention(nc, S, name, own_keys, seq_len=None, bias=None, weights=None):
    HEADS, DH = 16, 8
    SETS = 2 if own_keys else 1
    HPC = 512 // (SETS * P)
    CHUNKS = HEADS // HPC
    with phase(nc, name) as ph:
        lanes = range(LANES)
        xn_all = ph.sb("xn_all", [P, B, D])
        xn = [ph.sb(f"xn{l}", [P, D]) for l in lanes]
        res = [ph.sb(f"res{l}", [P, D]) for l in lanes]
        xnT = [ph.sb(f"xnT{l}", [P, T]) for l in lanes]
        qT = [ph.sb(f"qT{l}", [P, T]) for l in lanes]
        qmask = [ph.sb(f"qmask{l}", [P, HEADS, T]) for l in lanes]
        keys = [ph.sb(f"keys{l}", [P, SETS, P]) for l in lanes]
        probs = [ph.sb(f"probs{l}", [P, HEADS, SETS, P]) for l in lanes]
        probsT = [ph.sb(f"probsT{l}", [P, HEADS, SETS, P]) for l in lanes]
        vals = [ph.sb(f"vals{l}", [P, SETS, HEADS, DH + 1]) for l in lanes]
        mx = [ph.sb(f"mx{l}", [P, HEADS]) for l in lanes]
        rs = [ph.sb(f"rs{l}", [P, HEADS]) for l in lanes]
        osb = [ph.sb(f"osb{l}", [P, HEADS, DH]) for l in lanes]
        psA = [ph.ps(f"psA{l}", [P, 1024]) for l in lanes]
        psB = [ph.ps(f"psB{l}", [P, 512]) for l in lanes]
        psO = [ph.ps(f"psO{l}", [P, 512]) for l in lanes]

        dve_step = ph.sem("dve_step")
        stats_done, pow_ready, vals_ready, normed = (ph.sem(n) for n in ("stats_done", "pow_ready", "vals_ready", "normed"))
        (xn_ready, xnT_ready, q_ready, keys_ready, scores_ready, shifted, exp_ready, turned, probsT_ready, out_ready) = (
            [ph.sem(f"{n}{l}") for l in lanes] for n in (
                "xn_ready", "xnT_ready", "q_ready", "keys_ready", "scores_ready", "shifted", "exp_ready", "turned",
                "probsT_ready", "out_ready"))
        if own_keys:
            xnT_sb_ready, qkv_ready, o_sb_ready, oT_ready, oT_sb_ready, proj_ready = (
                [ph.sem(f"{n}{l}") for l in lanes] for n in (
                    "xnT_sb_ready", "qkv_ready", "o_sb_ready", "oT_ready", "oT_sb_ready", "proj_ready"))
            oT = [ph.sb(f"oT{l}", [P, P]) for l in lanes]
        else:
            len_i = ph.sb("len_i", [P, B], I32)
            len_f = ph.sb("len_f", [P, B])
            bias_row = ph.sb("bias_row", [P, P])
            bias_row_b = [ph.sb(f"bias_row_b{l}", [P, P]) for l in lanes]
            len_loaded = ph.sem("len_loaded")

        def bank(c):
            return slice(c % 2 * 512, c % 2 * 512 + 512)

        with nc.Block() as block:
            if not own_keys:
                @block.sync
                def _(sp):
                    sp.dma_start(len_i[:, :], seq_len.partition_broadcast(P)).then_inc(len_loaded, 16)
                    sp.dma_start(bias_row[:, :], bias.partition_broadcast(P)).then_inc(len_loaded, 16)

            @block.gpsimd
            def _(g):
                for l in lanes:
                    g.memset(vals[l][:, :, :, :], 1.0).then_inc(vals_ready, 1)
                inverse_roots(g, S, stats_done, pow_ready)
                g.wait_ge(normed, 1)

                def rows(j, l):
                    g.wait_ge(xnT_ready[l], 1 + j)
                    g.tensor_copy(xn[l][:, :], xn_all[:, j * LANES + l, :]).then_inc(xn_ready[l], 1)

                def keys_and_queries(j, l):
                    g.wait_ge(scores_ready[l], 1 + j * CHUNKS)
                    g.tensor_copy(keys[l][:, 0, :], S.ctxT[:, 0, j * LANES + l, :])
                    g.wait_ge(q_ready[l], j + 1)
                    for h in range(0, HEADS, 4):
                        g.tensor_tensor(qmask[l][:, h:h + 4, :], qT[l][:, :].unsqueeze(1).broadcast_to([P, 4, T]),
                                        S.headmask[:, h:h + 4].unsqueeze(2).broadcast_to([P, 4, T]),
                                        ALU.mult).then_inc(keys_ready[l], 1)
                skewed(g, [rows, keys_and_queries], [nothing, nothing])

            @block.vector
            def _(v):
                step = Steps(v, dve_step)
                layer_norm_coefficients(v, step, S, stats_done, pow_ready)
                if not own_keys:
                    v.wait_ge(len_loaded, 32)
                    step(v.tensor_copy(len_f[:, :], len_i[:, :]))

                normalized(v, step, S, xn_all).then_inc(normed, 1)

                def bias_added(j, l):
                    b = j * LANES + l
                    if not own_keys:
                        step(v.tensor_scalar(bias_row_b[l][:, :], S.iota_row, len_f[:, bass.ds(b, 1)], -1e12,
                                             ALU.is_ge, ALU.mult))
                        step(v.tensor_tensor(bias_row_b[l][:, :], bias_row_b[l][:, :], bias_row[:, :], ALU.add))

                def shift(c):
                    def stage(j, l):
                        heads = slice(c * HPC, (c + 1) * HPC)
                        pr = probs[l][:, heads, :, :]
                        ps = psA[l][:, bank(c)].rearrange("p (j s k) -> p j s k", s=SETS, j=HPC)
                        v.wait_ge(scores_ready[l], 1 + j * CHUNKS + c + 1)
                        if own_keys:
                            step(v.tensor_reduce(mx[l][:, heads], ps, AX.XY, ALU.max))
                            v.tensor_tensor(pr, ps, mx[l][:, heads].unsqueeze(2).unsqueeze(3)
                                            .broadcast_to([P, HPC, SETS, P]), ALU.subtract).then_inc(shifted[l], 1)
                        else:
                            step(v.tensor_tensor(pr[:, :, 0, :], ps[:, :, 0, :],
                                                 bias_row_b[l][:, :].unsqueeze(1).broadcast_to([P, HPC, P]), ALU.add))
                            step(v.tensor_reduce(mx[l][:, heads], pr, AX.XY, ALU.max))
                            v.tensor_scalar(mx[l][:, heads], mx[l][:, heads], -1.0, None, ALU.mult).then_inc(shifted[l], 1)
                    return stage

                def divided(j, l):
                    b = j * LANES + l
                    ov = psO[l][:, 0:HEADS * (DH + 1)].rearrange("p (h d) -> p h d", d=DH + 1)
                    v.wait_ge(out_ready[l], 1 + j + 1)
                    step(v.reciprocal(rs[l][:, :], ov[:, :, DH]))
                    ins = v.tensor_tensor(osb[l][:, :, :], ov[:, :, 0:DH],
                                          rs[l][:, :].unsqueeze(2).broadcast_to([P, HEADS, DH]), ALU.mult)
                    if own_keys:
                        ins.then_inc(o_sb_ready[l], 1)
                    else:
                        step(ins)
                        step(v.tensor_tensor(S.x[:, b, :], S.x[:, b, :],
                                             osb[l][:, :, :].rearrange("p h d -> p (h d)"), ALU.add))
                        step(v.bn_stats(S.stats[:, b, :], S.x[:, b, :]))

                def added(j, l):
                    b = j * LANES + l
                    v.wait_ge(proj_ready[l], j + 1)
                    step(v.tensor_tensor(res[l][:, :], psO[l][:, 0:D], weights["b_proj"], ALU.add))
                    step(v.tensor_tensor(S.x[:, b, :], S.x[:, b, :], res[l][:, :], ALU.add))
                    step(v.bn_stats(S.stats[:, b, :], S.x[:, b, :]))

                if own_keys:
                    skewed(v, [nothing] * 3 + [shift(c) for c in range(5)],
                           [shift(c) for c in range(5, 8)] + [nothing] * 2 + [divided, nothing, added], step.restart)
                else:
                    skewed(v, [bias_added, nothing] + [shift(c) for c in range(3)],
                           [shift(3), nothing, nothing, nothing, divided], step.restart)

            @block.scalar
            def _(a):
                a.wait_ge(vals_ready, 2)

                def turned_x(j, l):
                    b = j * LANES + l
                    a.wait_ge(out_ready[l], 1 + j)
                    a.activation(vals[l][:, 0, :, 0:DH],
                                 S.ctx[:, bass.ds(b, 1), P:2 * P].rearrange("p o (h d) -> p (o h) d", d=DH), ACT.Copy)
                    a.wait_ge(xnT_ready[l], 1 + j + 1)
                    if not own_keys:
                        a.activation(qT[l][:, :], psB[l][:, 0:T], ACT.Copy, scale=DH ** -0.5).then_inc(q_ready[l], 1)
                    else:
                        a.activation(xnT[l][:, :], psB[l][:, 0:T], ACT.Copy).then_inc(xnT_sb_ready[l], 1)

                def qkv(j, l):
                    a.wait_ge(qkv_ready[l], j + 1)
                    a.activation(keys[l][:, 1, :], psA[l][:, T:2 * T], ACT.Copy)
                    a.activation(qT[l][:, :], psA[l][:, 0:T], ACT.Copy, scale=DH ** -0.5)
                    a.activation(vals[l][:, 1, :, 0:DH],
                                 psA[l][:, 2 * T:3 * T].rearrange("p (h d) -> p h d", d=DH), ACT.Copy).then_inc(q_ready[l], 1)

                def exp_and_turned(c):
                    def stage(j, l):
                        if 2 <= c <= CHUNKS + 1:
                            a.wait_ge(turned[l], j * CHUNKS + c - 1)
                            a.activation(probsT[l][:, (c - 2) * HPC:(c - 1) * HPC, :, :].rearrange("p j s k -> p (j s k)"),
                                         psB[l][:, :], ACT.Copy).then_inc(probsT_ready[l], 1)
                        if c < CHUNKS:
                            pr = probs[l][:, c * HPC:(c + 1) * HPC, :, :]
                            a.wait_ge(shifted[l], j * CHUNKS + c + 1)
                            if own_keys:
                                a.activation(pr, pr, ACT.Exp).then_inc(exp_ready[l], 1)
                            else:
                                for h in range(c * HPC, (c + 1) * HPC):
                                    row = probs[l][:, h, 0, :]
                                    ins = a.activation(row, row, ACT.Exp, bias=mx[l][:, h:h + 1])
                                ins.then_inc(exp_ready[l], 1)
                    return stage

                def turned_o(j, l):
                    a.wait_ge(oT_ready[l], j + 1)
                    a.activation(oT[l][:, :], psB[l][:, 0:T], ACT.Copy).then_inc(oT_sb_ready[l], 1)

                if own_keys:
                    skewed(a, [turned_x, qkv, nothing] + [exp_and_turned(c) for c in range(5)],
                           [exp_and_turned(c) for c in range(5, 10)] + [nothing, turned_o, nothing])
                else:
                    skewed(a, [turned_x, nothing] + [exp_and_turned(c) for c in range(3)],
                           [exp_and_turned(c) for c in range(3, 6)] + [nothing, nothing])

            @block.tensor
            def _(t):
                for l in lanes:
                    t.sem_inc(xnT_ready[l], 1)
                    t.sem_inc(out_ready[l], 1)
                    t.sem_inc(scores_ready[l], 1)

                def turn_x(j, l):
                    t.wait_ge(xn_ready[l], j + 1)
                    t.transpose(psB[l][:, 0:T], xn[l][:, :], S.ident).then_inc(xnT_ready[l], 1)

                def qkv(j, l):
                    t.wait_ge(xnT_sb_ready[l], j + 1)
                    t.matmul(psA[l][:, 0:T], weights["wqT"], xnT[l][:, :], start=True, stop=True)
                    t.matmul(psA[l][:, T:2 * T], weights["wkT"], xnT[l][:, :], start=True, stop=True)
                    t.matmul(psA[l][:, 2 * T:3 * T], xnT[l][:, :], weights["wvT"], start=True,
                             stop=True).then_inc(qkv_ready[l], 1)

                def chunk(c):
                    def stage(j, l):
                        if c < CHUNKS:
                            t.wait_ge(keys_ready[l], j * 4 + c * HPC // 4 + 1)
                            if c > 1:
                                t.wait_ge(shifted[l], j * CHUNKS + c - 1)
                            for k in range(HPC):
                                mm = t.matmul(psA[l][:, bank(c)].rearrange("p (j n) -> p j n", j=HPC)[:, k, :],
                                              qmask[l][:, c * HPC + k, :], keys[l][:, :, :].rearrange("p s k -> p (s k)"),
                                              start=True, stop=True)
                            mm.then_inc(scores_ready[l], 1)
                        if 2 <= c <= CHUNKS + 1:
                            t.wait_ge(exp_ready[l], j * CHUNKS + c - 1)
                            if c > 2:
                                t.wait_ge(probsT_ready[l], j * CHUNKS + c - 2)
                            for n in range(4):
                                h, s = (c - 2) * HPC + n // SETS, n % SETS
                                mm = t.transpose(psB[l][:, n * P:(n + 1) * P], probs[l][:, h, s, :], S.ident)
                            mm.then_inc(turned[l], 1)
                        if c >= 3:
                            if c == CHUNKS + 2:
                                t.wait_ge(probsT_ready[l], j * CHUNKS + CHUNKS)
                            for h in range((c - 3) * HPC, (c - 2) * HPC):
                                for s in range(SETS):
                                    mm = t.matmul(psO[l][:, h * (DH + 1):(h + 1) * (DH + 1)], probsT[l][:, h, s, :],
                                                  vals[l][:, s, h, :], start=(s == 0), stop=(s == SETS - 1))
                            if c == CHUNKS + 2:
                                mm.then_inc(out_ready[l], 1)
                    return stage

                def turn_o(j, l):
                    t.wait_ge(o_sb_ready[l], j + 1)
                    t.transpose(psB[l][:, 0:T], osb[l][:, :, :].rearrange("p h d -> p (h d)"),
                                S.ident).then_inc(oT_ready[l], 1)

                def project(j, l):
                    t.wait_ge(oT_sb_ready[l], j + 1)
                    t.matmul(psO[l][:, 0:D], oT[l][:, :], weights["wprojT"], start=True,
                             stop=True).then_inc(proj_ready[l], 1)

                if own_keys:
                    skewed(t, [turn_x, qkv, nothing] + [chunk(c) for c in range(5)],
                           [chunk(c) for c in range(5, 11)] + [turn_o, project])
                else:
                    skewed(t, [turn_x, nothing] + [chunk(c) for c in range(3)], [chunk(c) for c in range(3, 7)] + [nothing])


def expert_choice_attention(nc, S, name, ins):
    W3 = 3 * D
    G = B * E0 * K0
    with phase(nc, name) as ph:
        lanes = range(LANES)
        wr = ph.sb("wr", [P, E0])
        wqkv = ph.sb("wqkv", [P, E0, W3])
        wswap = ph.sb("wswap", [P, E0, 2, ROPE_N])
        wo = ph.sb("wo", [P, E0, D])
        n1 = ph.sb("n1", [P, B, D])
        gates = ph.sb("gates", [P, B, 1 + E0])
        gatesT = ph.sb("gatesT", [P, T])
        left = ph.sb("left", [P, T])
        top = ph.sb("top", [P, K0])
        top_i = ph.sb("top_i", [P, K0], U32)
        top_f = ph.sb("top_f", [P, K0])
        spread = ph.sb("spread", [P, G])
        taken = ph.sb("taken", [P, G])
        pick = [ph.sb(f"pick{l}", [P, P]) for l in lanes]
        pickT = [ph.sb(f"pickT{l}", [P, P]) for l in lanes]
        xn = [ph.sb(f"xn{l}", [P, D]) for l in lanes]
        cols = ph.sb("cols", [P, B, 1 + E0])
        gathT = ph.sb("gathT", [P, E0, B, K0])
        cosg = ph.sb("cosg", [ROPE_N, E0, B, K0])
        sing = ph.sb("sing", [ROPE_N, E0, B, K0])
        QT = ph.sb("QT", [P, E0, B, K0])
        KT = ph.sb("KT", [P, E0, B, K0])
        VT = ph.sb("VT", [P, E0, B, K0])
        QS = ph.sb("QS", [ROPE_N, E0, B, K0])
        KS = ph.sb("KS", [ROPE_N, E0, B, K0])
        AVT = ph.sb("AVT", [P, E0, B, K0])
        OUTT = ph.sb("OUTT", [P, E0, B, K0])
        q1 = [ph.sb(f"q1{l}", [P, P]) for l in lanes]
        v1 = [ph.sb(f"v1{l}", [P, P]) for l in lanes]
        vv = [ph.sb(f"vv{l}", [P, P]) for l in lanes]
        sc = [ph.sb(f"sc{l}", [P, P]) for l in lanes]
        mk = [ph.sb(f"mk{l}", [P, P]) for l in lanes]
        pT = [ph.sb(f"pT{l}", [P, P]) for l in lanes]
        st = [ph.sb(f"st{l}", [P, 4]) for l in lanes]
        ps = [ph.ps(f"ps{n}", [P, 512]) for n in range(8)]

        dve_step, act_step = ph.sem("dve_step"), ph.sem("act_step")
        stats_done, pow_ready, w_loaded = ph.sem("stats_done"), ph.sem("pow_ready"), ph.sem("w_loaded")
        xn_ready, xnT_ready, xnT_sb, logits_ready = (ph.sem(n) for n in ("xn_ready", "xnT_ready", "xnT_sb", "logits_ready"))
        logits_sb, gates_ready, gatesT_ready = ph.sem("logits_sb"), ph.sem("gates_ready"), ph.sem("gatesT_ready")
        spread_ready, taken_ready = ph.sem("spread_ready"), ph.sem("taken_ready")

        def stage_block(fn):
            with nc.Block() as block:
                fn(block)

        with nc.Block() as block:
            @block.sync
            def _(sp):
                sp.dma_start(wr[:, :], ins["L0_ffn_WrT"]).then_inc(w_loaded, 16)
                sp.dma_start(wqkv[:, :, :], ins["L0_ffn_Wqkv"].rearrange("e i j -> i e j")).then_inc(w_loaded, 16)
                sp.dma_start(wswap[:, :, :, :], ins["L0_ffn_Wswap"].rearrange("e i n j -> i e n j")).then_inc(w_loaded, 16)
                sp.dma_start(wo[:, :, :], ins["L0_ffn_Wo"].rearrange("e i j -> i e j")).then_inc(w_loaded, 16)

            @block.gpsimd
            def _(g):
                inverse_roots(g, S, stats_done, pow_ready)

            @block.vector
            def _(v):
                step = Steps(v, dve_step)
                layer_norm_coefficients(v, step, S, stats_done, pow_ready)
                step(v.tensor_copy(gates[:, :, 0], S.iota_col.broadcast_to([P, B])))
                with v.Fori(0, B // LANES) as i:
                    step.restart()
                    for l in lanes:
                        b = i * LANES + l
                        step(v.tensor_scalar(xn[l][:, :], S.x[:, b, :], S.mean[:, bass.ds(b, 1)],
                                             S.rstd[:, bass.ds(b, 1)], ALU.subtract, ALU.mult))
                        v.tensor_copy(n1[:, b, :], xn[l][:, :]).then_inc(xn_ready, 1)
                    for l in lanes:
                        b = i * LANES + l
                        v.wait_ge(xnT_ready, b + 1)
                        v.tensor_copy(pT[l][:, :], ps[l][:, 0:T]).then_inc(xnT_sb, 1)
                    for l in lanes:
                        b = i * LANES + l
                        v.wait_ge(logits_ready, b + 1)
                        v.tensor_copy(gates[:, b, 1:1 + E0], ps[2 + l][:, 0:E0]).then_inc(logits_sb, 1)
                v.wait_ge(gates_ready, 1)
                gv = gates[:, :, 1:1 + E0]
                step(v.tensor_scalar(gv, gv, 1.0, None, ALU.add))
                step(v.reciprocal(gv, gv))
                v.tensor_copy(left[:, :].rearrange("p (b e) -> p b e", e=E0), gv).then_inc(gates_ready, 1)
                v.wait_ge(gatesT_ready, 1)
                step(v.tensor_copy(gatesT[:, :], ps[4][:, 0:T]))
                step(v.max(top[:, 0:8], gatesT[:, :]))
                step(v.max_index(out=top_i[:, 0:8], in_max=top[:, 0:8], in_values=gatesT[:, :]))
                step(v.match_replace(out=left[:, :], in_to_replace=top[:, 0:8], in_values=gatesT[:, :], imm_value=-1.0))
                step(v.max(top[:, 8:16], left[:, :]))
                step(v.max_index(out=top_i[:, 8:16], in_max=top[:, 8:16], in_values=left[:, :]))
                step(v.tensor_copy(top_f[:, :], top_i[:, :]))
                v.tensor_tensor(spread[:, :].rearrange("p (c k) -> p c k", k=K0),
                                top_f[:, :].unsqueeze(1).broadcast_to([P, P, K0]),
                                S.ident.unsqueeze(2).broadcast_to([P, P, K0]), ALU.mult).then_inc(spread_ready, 1)
                for n in range(4):
                    v.wait_ge(taken_ready, n + 1)
                    step(v.tensor_copy(taken[:, n * 512:(n + 1) * 512], ps[4 + n][:, :]))

            @block.scalar
            def _(a):
                a.wait_ge(logits_sb, B)
                gv = gates[:, :, 1:1 + E0]
                a.activation(gv, gv, ACT.Exp, scale=-1.0).then_inc(gates_ready, 1)

            @block.tensor
            def _(t):
                t.wait_ge(w_loaded, 64)
                with t.Fori(0, B // LANES) as i:
                    for l in lanes:
                        t.wait_ge(xn_ready, i * LANES + l + 1)
                        t.transpose(ps[l][:, 0:T], xn[l][:, :], S.ident).then_inc(xnT_ready, 1)
                    for l in lanes:
                        t.wait_ge(xnT_sb, i * LANES + l + 1)
                        t.matmul(ps[2 + l][:, 0:E0], pT[l][:, :], wr[:, :], start=True, stop=True).then_inc(logits_ready, 1)
                t.wait_ge(gates_ready, 2)
                t.transpose(ps[4][:, 0:T], left[:, :], S.ident).then_inc(gatesT_ready, 1)
                t.wait_ge(spread_ready, 1)
                for n in range(4):
                    t.matmul(ps[4 + n][:, :], S.ones, spread[:, n * 512:(n + 1) * 512], start=True,
                             stop=True).then_inc(taken_ready, 1)

        pick_ready, gath_ready, gath_free = ph.sem("pick_ready"), ph.sem("gath_ready"), ph.sem("gath_free")
        qkv_mm, qkv_sb, rope_done = ph.sem("qkv_mm"), ph.sem("qkv_sb"), ph.sem("rope_done")
        dve_step2 = ph.sem("dve_step2")
        with nc.Block() as block:
            @block.vector
            def _(v):
                v.sem_inc(gath_free, 1)
                step = Steps(v, dve_step2)
                with v.Fori(0, B // LANES) as i:
                    step.restart()
                    for l in lanes:
                        b = i * LANES + l
                        step(v.tensor_copy(xn[l][:, :], n1[:, b, :]))
                        v.tensor_scalar(pick[l][:, :], taken[:, bass.ds(b * P, P)], S.iota_col, None,
                                        ALU.is_equal).then_inc(pick_ready, 1)
                    for l in lanes:
                        b = i * LANES + l
                        v.wait_ge(gath_ready, b + 1)
                        step(v.tensor_copy(cols[:, b, :], ps[4 * l][:, 0:1 + E0]))
                        step(v.tensor_copy(gathT[:, :, b, :], ps[4 * l + 1][:, 0:P].rearrange("p (e k) -> p e k", k=K0)))
                        step(v.tensor_copy(cosg[:, :, b, :], ps[4 * l + 2][0:ROPE_N, 0:P].rearrange("p (e k) -> p e k", k=K0)))
                        v.tensor_copy(sing[:, :, b, :], ps[4 * l + 3][0:ROPE_N, 0:P]
                                      .rearrange("p (e k) -> p e k", k=K0)).then_inc(gath_free, 1)
                step = Steps(v, dve_step2)
                step.restart()
                v.wait_ge(qkv_sb, 2 * E0)
                for x, xs in ((QT, QS), (KT, KS)):
                    r = x[0:ROPE_N, :, :, :]
                    step(v.tensor_tensor(r, r, cosg[:, :, :, :], ALU.mult))
                    step(v.tensor_tensor(xs[:, :, :, :], xs[:, :, :, :], sing[:, :, :, :], ALU.mult))
                    step(v.tensor_tensor(r, r, xs[:, :, :, :], ALU.add))

            @block.scalar
            def _(a):
                for e in range(E0):
                    p4 = ps[4 * (e % 2):4 * (e % 2) + 4]
                    a.wait_ge(qkv_mm, 2 * e + 1)
                    a.activation(QT[:, e, :, :].rearrange("p b k -> p (b k)"), p4[0][:, 0:256], ACT.Copy)
                    a.activation(KT[:, e, :, :].rearrange("p b k -> p (b k)"), p4[0][:, 256:512], ACT.Copy)
                    a.activation(VT[:, e, :, :].rearrange("p b k -> p (b k)"), p4[1][:, 0:256], ACT.Copy).then_inc(qkv_sb, 1)
                    a.wait_ge(qkv_mm, 2 * e + 2)
                    a.activation(QS[:, e, :, :].rearrange("p b k -> p (b k)"), p4[2][0:ROPE_N, 0:256], ACT.Copy)
                    a.activation(KS[:, e, :, :].rearrange("p b k -> p (b k)"), p4[2][0:ROPE_N, 256:512],
                                 ACT.Copy).then_inc(qkv_sb, 1)

            @block.tensor
            def _(t):
                with t.Fori(0, B // LANES) as i:
                    for l in lanes:
                        b = i * LANES + l
                        t.wait_ge(pick_ready, b + 1)
                        t.wait_ge(gath_free, 1 + i * LANES)
                        t.matmul(ps[4 * l][:, 0:1 + E0], pick[l][:, :], gates[:, b, :], start=True, stop=True)
                        t.matmul(ps[4 * l + 1][:, 0:P], xn[l][:, :], pick[l][:, :], start=True, stop=True)
                        t.matmul(ps[4 * l + 2][0:ROPE_N, 0:P], S.cos, pick[l][:, :], start=True, stop=True)
                        t.matmul(ps[4 * l + 3][0:ROPE_N, 0:P], S.sin, pick[l][:, :], start=True,
                                 stop=True).then_inc(gath_ready, 1)
                t.wait_ge(gath_free, 1 + B)
                for e in range(E0):
                    p4 = ps[4 * (e % 2):4 * (e % 2) + 4]
                    if e >= 2:
                        t.wait_ge(qkv_sb, 2 * (e - 1))
                    rows = gathT[:, e, :, :].rearrange("p b k -> p (b k)")
                    t.matmul(p4[0][:, 0:256], wqkv[:, e, 0:D], rows, start=True, stop=True)
                    t.matmul(p4[0][:, 256:512], wqkv[:, e, D:2 * D], rows, start=True, stop=True)
                    t.matmul(p4[1][:, 0:256], wqkv[:, e, 2 * D:3 * D], rows, start=True, stop=True).then_inc(qkv_mm, 1)
                    t.matmul(p4[2][0:ROPE_N, 0:256], wswap[:, e, 0, :], rows, start=True, stop=True)
                    t.matmul(p4[2][0:ROPE_N, 256:512], wswap[:, e, 1, :], rows, start=True, stop=True).then_inc(qkv_mm, 1)

        q1_ready, s_ready, p_shift, p_exp, p_ready, p_turned, pT_ready, av_ready, av_sb = (
            ph.sem(n) for n in ("q1_ready", "s_ready", "p_shift", "p_exp", "p_ready", "p_turned", "pT_ready", "av_ready", "av_sb"))
        v_turned, vv_ready, out_mm, out_sb = ph.sem("v_turned"), ph.sem("vv_ready"), ph.sem("out_mm"), ph.sem("out_sb")
        o1_ready, o_turned, o2_ready, scat_ready = (ph.sem(n) for n in ("o1_ready", "o_turned", "o2_ready", "scat_ready"))
        dve_step3 = ph.sem("dve_step3")
        with nc.Block() as block:
            def rows_of(X, b):
                return X[:, :, b, :]

            @block.vector
            def _(v):
                step = Steps(v, dve_step3)
                with v.Fori(0, B // LANES) as i:
                    step.restart()
                    for l in lanes:
                        b = i * LANES + l
                        step(v.tensor_copy(v1[l][:, :].rearrange("p (e k) -> p e k", k=K0), rows_of(VT, b)))
                        v.tensor_copy(q1[l][:, :].rearrange("p (e k) -> p e k", k=K0), rows_of(QT, b)).then_inc(q1_ready, 1)
                        step(v.scalar_tensor_tensor(out=mk[l][:, :], in0=taken[:, bass.ds(b * P, P)],
                                                    scalar=cols[:, b, 0:1], in1=S.sameexpert,
                                                    op0=ALU.is_le, op1=ALU.mult))
                        step(v.tensor_scalar(mk[l][:, :], mk[l][:, :], -1.0, -NEG, ALU.add, ALU.mult))
                        step(v.tensor_tensor(pick[l][:, 0:E0], cols[:, b, 1:1 + E0], S.expertmask, ALU.mult))
                        step(v.tensor_reduce(st[l][:, 3:4], pick[l][:, 0:E0], AX.X, ALU.add))
                    for l in lanes:
                        b = i * LANES + l
                        v.wait_ge(s_ready, b + 1)
                        step(v.scalar_tensor_tensor(out=sc[l][:, :], in0=ps[l][:, 0:P], scalar=float(D) ** -0.5,
                                                    in1=mk[l][:, :], op0=ALU.mult, op1=ALU.add))
                        step(v.tensor_reduce(st[l][:, 0:1], sc[l][:, :], AX.X, ALU.max))
                        v.tensor_scalar(st[l][:, 1:2], st[l][:, 0:1], -1.0, None, ALU.mult).then_inc(p_shift, 1)
                        v.wait_ge(v_turned, b + 1)
                        v.tensor_copy(vv[l][:, :], ps[4 + l][:, 0:P]).then_inc(vv_ready, 1)
                    for l in lanes:
                        b = i * LANES + l
                        v.wait_ge(p_exp, b + 1)
                        step(v.reciprocal(st[l][:, 0:1], st[l][:, 2:3]))
                        v.tensor_scalar(sc[l][:, :], sc[l][:, :], st[l][:, 0:1], st[l][:, 3:4],
                                        ALU.mult, ALU.mult).then_inc(p_ready, 1)
                    for l in lanes:
                        b = i * LANES + l
                        v.wait_ge(p_turned, b + 1)
                        v.tensor_copy(pT[l][:, :], ps[2 + l][:, 0:P]).then_inc(pT_ready, 1)
                    for l in lanes:
                        b = i * LANES + l
                        v.wait_ge(av_ready, b + 1)
                        v.tensor_copy(rows_of(AVT, b), ps[6 + l][:, 0:P].rearrange("p (e k) -> p e k", k=K0)).then_inc(av_sb, 1)
                step.restart()
                for e in range(E0):
                    v.wait_ge(out_mm, e + 1)
                    v.tensor_copy(OUTT[:, e, :, :].rearrange("p b k -> p (b k)"), ps[e][:, 0:256]).then_inc(out_sb, 1)
                v.wait_ge(out_sb, E0)
                with v.Fori(0, B // LANES) as i:
                    step.restart()
                    for l in lanes:
                        b = i * LANES + l
                        step(v.tensor_copy(v1[l][:, :].rearrange("p (e k) -> p e k", k=K0), rows_of(OUTT, b)))
                        v.tensor_scalar(pickT[l][:, :], S.iota_row, cols[:, b, 0:1], None, ALU.is_equal).then_inc(o1_ready, 1)
                    for l in lanes:
                        b = i * LANES + l
                        v.wait_ge(o_turned, b + 1)
                        v.tensor_copy(vv[l][:, :], ps[l][:, 0:P]).then_inc(o2_ready, 1)
                    for l in lanes:
                        b = i * LANES + l
                        v.wait_ge(scat_ready, b + 1)
                        step(v.tensor_tensor(S.x[:, b, :], S.x[:, b, :], ps[2 + l][:, 0:D], ALU.add))
                        step(v.bn_stats(S.stats[:, b, :], S.x[:, b, :]))

            @block.scalar
            def _(a):
                with a.Fori(0, B // LANES) as i:
                    for l in lanes:
                        b = i * LANES + l
                        a.wait_ge(p_shift, b + 1)
                        a.activation(sc[l][:, :], sc[l][:, :], ACT.Exp, bias=st[l][:, 1:2],
                                     accum_out=st[l][:, 2:3]).then_inc(p_exp, 1)

            @block.tensor
            def _(t):
                with t.Fori(0, B // LANES) as i:
                    for l in lanes:
                        b = i * LANES + l
                        t.wait_ge(q1_ready, b + 1)
                        t.matmul(ps[l][:, 0:P], q1[l][:, :], rows_of(KT, b), start=True, stop=True).then_inc(s_ready, 1)
                        t.transpose(ps[4 + l][:, 0:P], v1[l][:, :], S.ident).then_inc(v_turned, 1)
                    for l in lanes:
                        t.wait_ge(p_ready, i * LANES + l + 1)
                        t.transpose(ps[2 + l][:, 0:P], sc[l][:, :], S.ident).then_inc(p_turned, 1)
                    for l in lanes:
                        t.wait_ge(pT_ready, i * LANES + l + 1)
                        t.wait_ge(vv_ready, i * LANES + l + 1)
                        t.matmul(ps[6 + l][:, 0:P], vv[l][:, :], pT[l][:, :], start=True, stop=True).then_inc(av_ready, 1)
                t.wait_ge(av_sb, B)
                for e in range(E0):
                    t.matmul(ps[e][:, 0:256], wo[:, e, :], AVT[:, e, :, :].rearrange("p b k -> p (b k)"),
                             start=True, stop=True).then_inc(out_mm, 1)
                t.wait_ge(out_sb, E0)
                with t.Fori(0, B // LANES) as i:
                    for l in lanes:
                        t.wait_ge(o1_ready, i * LANES + l + 1)
                        t.transpose(ps[l][:, 0:P], v1[l][:, :], S.ident).then_inc(o_turned, 1)
                    for l in lanes:
                        t.wait_ge(o2_ready, i * LANES + l + 1)
                        t.matmul(ps[2 + l][:, 0:D], pickT[l][:, :], vv[l][:, :], start=True, stop=True).then_inc(scat_ready, 1)


def patch_depool(nc, S, name, ins):
    RMS_EPS = 1e-5
    dt = float(-np.log(-np.expm1(LOGP)))
    with phase(nc, name) as ph:
        lanes = range(LANES)
        w_in = ph.sb("w_in", [P, D])
        b_in, g_res, g_init = ph.sb("b_in", [P, D]), ph.sb("g_res", [P, D]), ph.sb("g_init", [P, D])
        len_i = ph.sb("len_i", [P, B], I32)
        len_f = ph.sb("len_f", [P, B])
        ends = ph.sb("ends", [P, B])
        ends_neg = ph.sb("ends_neg", [P, B])
        squares = ph.sb("squares", [P, B, CTX])
        ctx_ms = ph.sb("ctx_ms", [P, B])
        ctx_rms = ph.sb("ctx_rms", [P, B])
        xn = [ph.sb(f"xn{l}", [P, D]) for l in lanes]
        xsq = [ph.sb(f"xsq{l}", [P, D]) for l in lanes]
        hT = [ph.sb(f"hT{l}", [P, T]) for l in lanes]
        ms = [ph.sb(f"ms{l}", [P, 2]) for l in lanes]
        hit = [ph.sb(f"hit{l}", [P, T]) for l in lanes]
        marked = [ph.sb(f"marked{l}", [P, P]) for l in lanes]
        mark = [ph.sb(f"mark{l}", [P, 1]) for l in lanes]
        plug = [ph.sb(f"plug{l}", [P, T]) for l in lanes]
        u = [ph.sb(f"u{l}", [P, D]) for l in lanes]
        s = [ph.sb(f"s{l}", [P, D]) for l in lanes]
        ps = [ph.ps(f"ps{n}", [P, 512]) for n in range(8)]
        dve_step, act_step, stats_done, pow_ready, loaded, lens_mm, sq_done, ctx_pow, ms_ready, rms_ready = (
            ph.sem(n) for n in ("dve_step", "act_step", "stats_done", "pow_ready", "loaded", "lens_mm", "sq_done",
                                "ctx_pow", "ms_ready", "rms_ready"))
        hit_ready, mark_ready, marked_ready, plug_mm, plug_ready, u_ready, s_mm, s_ready, h_ready, h_turned, hT_ready, sum_ready = (
            ph.sem(n) for n in ("hit_ready", "mark_ready", "marked_ready", "plug_mm", "plug_ready", "u_ready", "s_mm",
                                "s_ready", "h_ready", "h_turned", "hT_ready", "sum_ready"))
        lens_ready, ctx_ms_ready = ph.sem("lens_ready"), ph.sem("ctx_ms_ready")
        with nc.Block() as block:
            @block.sync
            def _(sp):
                sp.dma_start(w_in[:, :], ins["L1_W_inT"]).then_inc(loaded, 16)
                sp.dma_start(b_in[:, :], ins["L1_xattn_b_in"].partition_broadcast(P)).then_inc(loaded, 16)
                sp.dma_start(g_res[:, :], ins["L1_xattn_g_res"].partition_broadcast(P)).then_inc(loaded, 16)
                sp.dma_start(g_init[:, :], ins["L1_xattn_g_init"][0:D].partition_broadcast(P)).then_inc(loaded, 16)
                sp.dma_start(len_i[:, :], ins["patch_lensT"]).then_inc(loaded, 16)

            @block.gpsimd
            def _(g):
                inverse_roots(g, S, stats_done, pow_ready)
                g.wait_ge(ctx_ms_ready, 1)
                g.tensor_tensor(ctx_rms[:, :], ctx_ms[:, :], S.mhalf[:, :], ALU.pow).then_inc(ctx_pow, 1)
                with g.Fori(0, B // LANES) as i:
                    for l in lanes:
                        g.wait_ge(ms_ready, i * LANES + l + 1)
                        g.tensor_tensor(ms[l][:, 1:2], ms[l][:, 0:1], S.mhalf[:, 0:1], ALU.pow).then_inc(rms_ready, 1)

            @block.scalar
            def _(a):
                a.activation(squares[:, :, :], S.ctx[:, :, :], ACT.Square).then_inc(sq_done, 1)

            @block.vector
            def _(v):
                step = Steps(v, dve_step)
                layer_norm_coefficients(v, step, S, stats_done, pow_ready)
                v.wait_ge(sq_done, 1)
                step(v.tensor_reduce(ctx_ms[:, :], squares[:, :, :], AX.X, ALU.add))
                v.tensor_scalar(ctx_ms[:, :], ctx_ms[:, :], 1.0 / CTX, RMS_EPS, ALU.mult, ALU.add).then_inc(ctx_ms_ready, 1)
                v.wait_ge(loaded, 80)
                v.tensor_copy(len_f[:, :], len_i[:, :]).then_inc(lens_ready, 1)
                v.wait_ge(lens_mm, 1)
                step(v.tensor_scalar(ends[:, :], ps[0][:, 0:B], -1.0, None, ALU.add))
                step(v.tensor_scalar(ends_neg[:, :], ends[:, :], 0.0, float(T), ALU.is_lt, ALU.mult))
                step(v.tensor_tensor(ends[:, :], ends[:, :], ends_neg[:, :], ALU.add))
                v.wait_ge(ctx_pow, 1)
                with v.Fori(0, B // LANES) as i:
                    step.restart()
                    for l in lanes:
                        b = i * LANES + l
                        v.tensor_scalar(hit[l][:, :], S.iota_row, ends[:, bass.ds(b, 1)], None, ALU.is_equal).then_inc(hit_ready, 1)
                        step(v.tensor_scalar(xn[l][:, :], S.x[:, b, :], S.mean[:, bass.ds(b, 1)],
                                             S.rstd[:, bass.ds(b, 1)], ALU.subtract, ALU.mult))
                        step(v.tensor_tensor(xsq[l][:, :], xn[l][:, :], xn[l][:, :], ALU.mult))
                        step(v.tensor_reduce(ms[l][:, 0:1], xsq[l][:, :], AX.X, ALU.add))
                        v.tensor_scalar(ms[l][:, 0:1], ms[l][:, 0:1], 1.0 / D, RMS_EPS, ALU.mult, ALU.add).then_inc(ms_ready, 1)
                        step(v.tensor_scalar(u[l][:, :], S.ctx[:, b, 0:D], ctx_rms[:, bass.ds(b, 1)], 1.0 / dt,
                                             ALU.mult, ALU.mult))
                        v.scalar_tensor_tensor(out=u[l][:, :], in0=u[l][:, :], scalar=float(dt * np.exp(LOGP)),
                                               in1=g_init[:, :], op0=ALU.mult, op1=ALU.mult).then_inc(u_ready, 1)
                    for l in lanes:
                        b = i * LANES + l
                        v.wait_ge(rms_ready, b + 1)
                        v.scalar_tensor_tensor(out=xsq[l][:, :], in0=xn[l][:, :], scalar=ms[l][:, 1:2],
                                               in1=g_res[:, :], op0=ALU.mult, op1=ALU.mult).then_inc(h_ready, 1)
                        v.wait_ge(mark_ready, b + 1)
                        step(v.tensor_scalar(mark[l][:, :], ps[l][:, 0:1], 1.0, None, ALU.min))
                        v.tensor_scalar(marked[l][:, :], S.ones, mark[l][:, 0:1], None, ALU.mult).then_inc(marked_ready, 1)
                        v.wait_ge(s_mm, b + 1)
                        v.tensor_copy(s[l][:, :], ps[6 + l][:, 0:D]).then_inc(s_ready, 1)
                    for l in lanes:
                        b = i * LANES + l
                        v.wait_ge(h_turned, b + 1)
                        v.tensor_copy(hT[l][:, :], ps[4 + l][:, 0:T]).then_inc(hT_ready, 1)
                        v.wait_ge(plug_mm, b + 1)
                        step(v.tensor_scalar(plug[l][:, :], ps[2 + l][:, 0:T], -1.0, 0.0, ALU.add, ALU.max))
                        v.tensor_scalar(plug[l][:, :], plug[l][:, :], S.iota_col, None, ALU.is_equal).then_inc(plug_ready, 1)
                        step(v.tensor_tensor(xn[l][:, :], S.x[:, b, :], b_in[:, :], ALU.add))
                    for l in lanes:
                        b = i * LANES + l
                        v.wait_ge(sum_ready, b + 1)
                        step(v.tensor_tensor(S.x[:, b, :], xn[l][:, :], ps[l][:, 0:D], ALU.add))
                        step(v.bn_stats(S.stats[:, b, :], S.x[:, b, :]))

            @block.tensor
            def _(t):
                t.wait_ge(lens_ready, 1)
                t.matmul(ps[0][:, 0:B], S.upto, len_f[:, :], start=True, stop=True).then_inc(lens_mm, 1)
                with t.Fori(0, B // LANES) as i:
                    for l in lanes:
                        b = i * LANES + l
                        t.wait_ge(hit_ready, b + 1)
                        t.matmul(ps[l][:, 0:1], hit[l][:, :], S.ones[:, 0:1], start=True, stop=True).then_inc(mark_ready, 1)
                        t.wait_ge(u_ready, b + 1)
                        t.matmul(ps[6 + l][:, 0:D], S.decay, u[l][:, :], start=True, stop=True).then_inc(s_mm, 1)
                    for l in lanes:
                        b = i * LANES + l
                        t.wait_ge(h_ready, b + 1)
                        t.transpose(ps[4 + l][:, 0:T], xsq[l][:, :], S.ident).then_inc(h_turned, 1)
                        t.wait_ge(marked_ready, b + 1)
                        t.matmul(ps[2 + l][:, 0:T], marked[l][:, :], S.upto, start=True, stop=True).then_inc(plug_mm, 1)
                    for l in lanes:
                        b = i * LANES + l
                        t.wait_ge(hT_ready, b + 1)
                        t.wait_ge(plug_ready, b + 1)
                        t.wait_ge(s_ready, b + 1)
                        t.matmul(ps[l][:, 0:D], hT[l][:, :], w_in[:, :], start=True, stop=False)
                        t.matmul(ps[l][:, 0:D], plug[l][:, :], s[l][:, :], start=False, stop=True).then_inc(sum_ready, 1)


ROW = LW * D + LW + LW * D + D
W1, B1, W2, B2 = 0, LW * D, LW * D + LW, LW * D + LW + LW * D
DEPTH = 8


def tree_routes(nc, S, name, nets, first_net, stream, leaves, node_w, node_b):
    G = 4
    with phase(nc, name) as ph:
        w = ph.sb("w", [P, nets * NODES])
        nb = ph.sb("nb", [P, nets * NODES])
        xn = [ph.sb(f"xn{k}", [P, D]) for k in range(G)]
        xT = [ph.sb(f"xT{k}", [P, T]) for k in range(G)]
        right = ph.sb("right", [P, G, nets, NODES])
        path = [ph.sb(f"path{k}", [P, G * nets, LEAVES]) for k in range(2)]
        leaf_f = ph.sb("leaf_f", [P, G, nets])
        ps = [ph.ps(f"ps{k}", [P, 1024]) for k in range(G)]
        dve_step, loaded, x_ready, turned, xT_ready, logits_ready = (
            ph.sem(n) for n in ("dve_step", "loaded", "x_ready", "turned", "xT_ready", "logits_ready"))
        with nc.Block() as block:
            @block.sync
            def _(sp):
                sp.dma_start(w[:, :], node_w).then_inc(loaded, 16)
                sp.dma_start(nb[:, :], node_b.partition_broadcast(P)).then_inc(loaded, 16)

            @block.vector
            def _(v):
                step = Steps(v, dve_step)
                v.wait_ge(loaded, 32)
                step(v.tensor_scalar(nb[:, :], nb[:, :], -1.0, None, ALU.mult))
                rt = right[:, :, :, :].rearrange("p k n c -> p (k n) c")

                def rows(i):
                    for k in range(G):
                        v.tensor_copy(xn[k][:, :], stream[:, i * G + k, :]).then_inc(x_ready, 1)

                def turned_rows(i):
                    for k in range(G):
                        v.wait_ge(turned, i * G + k + 1)
                        v.tensor_copy(xT[k][:, :], ps[k][:, 0:T]).then_inc(xT_ready, 1)

                def decisions(i):
                    for k in range(G):
                        v.wait_ge(logits_ready, i * G + k + 1)
                        for n0 in range(0, nets, 2):
                            m = min(2, nets - n0)
                            at = 512 * (n0 // 2)
                            ins = v.tensor_tensor(right[:, k, n0:n0 + m, :].rearrange("p n c -> p (n c)"),
                                                  ps[k][:, at:at + m * NODES],
                                                  nb[:, n0 * NODES:(n0 + m) * NODES], ALU.is_gt)
                    step(ins)

                def walk(levels):
                    for level in levels:
                        width = 2 ** level
                        a, b = path[(level + 1) % 2], path[level % 2]
                        pair = b[:, :, 0:2 * width].rearrange("p g (c two) -> p g c two", two=2)
                        step(v.tensor_tensor(pair[:, :, :, 1], a[:, :, 0:width], rt[:, :, width - 1:2 * width - 1], ALU.mult))
                        step(v.tensor_tensor(pair[:, :, :, 0], a[:, :, 0:width], pair[:, :, :, 1], ALU.subtract))

                def first_level():
                    step(v.tensor_scalar(path[0][:, :, 0:1], rt[:, :, 0:1], -1.0, 1.0, ALU.mult, ALU.add))
                    step(v.tensor_copy(path[0][:, :, 1:2], rt[:, :, 0:1]))

                def leaf(i):
                    last, width = path[(DEPTH - 2) % 2], LEAVES // 2
                    go = rt[:, :, width - 1:2 * width - 1]
                    twice = S.iota256.rearrange("p (c two) -> p c two", two=2)[:, :, 0]
                    step(v.tensor_tensor(go, go, twice.unsqueeze(1).broadcast_to([P, G * nets, width]), ALU.add))
                    step(v.tensor_tensor(go, go, last[:, :, 0:width], ALU.mult))
                    step(v.tensor_reduce(leaf_f[:, :, :].rearrange("p k n -> p (k n)"), go, AX.X, ALU.add))
                    for n in range(nets):
                        ins = v.tensor_scalar(leaf_f[:, :, n], leaf_f[:, :, n], float(LEAVES * (first_net + n)), None, ALU.add)
                    step(ins)
                    step(v.tensor_copy(leaves[:, bass.ds(i * G, G), :] if not isinstance(i, int)
                                       else leaves[:, i * G:(i + 1) * G, :], leaf_f[:, :, :]))

                rows(0)
                turned_rows(0)
                decisions(0)
                with v.Fori(0, B // G - 1) as i:
                    step.restart()
                    rows(i + 1)
                    first_level()
                    walk(range(1, 4))
                    turned_rows(i + 1)
                    walk(range(4, DEPTH - 1))
                    leaf(i)
                    decisions(i + 1)
                step.restart()
                first_level()
                walk(range(1, DEPTH - 1))
                leaf(B // G - 1)

            @block.tensor
            def _(t):
                t.wait_ge(loaded, 32)
                with t.Fori(0, B // G) as i:
                    for k in range(G):
                        t.wait_ge(x_ready, i * G + k + 1)
                        t.transpose(ps[k][:, 0:T], xn[k][:, :], S.ident).then_inc(turned, 1)
                    for k in range(G):
                        t.wait_ge(xT_ready, i * G + k + 1)
                        for n0 in range(0, nets, 2):
                            m = min(2, nets - n0)
                            at = 512 * (n0 // 2)
                            mm = t.matmul(ps[k][:, at:at + m * NODES], xT[k][:, :],
                                          w[:, n0 * NODES:(n0 + m) * NODES], start=True, stop=True)
                        mm.then_inc(logits_ready, 1)


def leaf_gathers(g, step, leaves, picks, slots, table, gathered, used, slot_of):
    n = len(slots)
    per = n // slot_of

    def gather(i, m):
        k, net = m % slot_of, m // slot_of
        step(g.tensor_copy(picks[m][:, :], leaves[:, i * slot_of + k, net:net + 1]))
        g.indirect_dma_start(out=slots[m][:, :], out_offset=None, in_=table,
                             in_offset=bass.IndirectOffsetOnAxis(ap=picks[m][:, 0:1], axis=0)).then_inc(gathered[m], 16)
    for m in range(n):
        gather(0, m)
    with g.Fori(0, B // slot_of - 1) as i:
        step.restart()
        for m in range(n):
            g.wait_ge(used, 1 + i * n + m + 1)
            gather(i + 1, m)


def routed_trees(nc, S, name, ins):
    with phase(nc, name) as ph:
        xn3 = ph.sb("xn3", [P, B, D])
        leaves = ph.sb("leaves", [P, B, 3], U32)
        leaves_f = ph.sb("leaves_f", [P, B, 1], U32)
        table = ins["leaf_table"]

        with phase(nc, name + "_norm") as pn:
            stats = pn.sb("stats", [P, B, 6])
            mu, dif, var = pn.sb("mu", [P, B]), pn.sb("dif", [P, B]), pn.sb("var", [P, B])
            half = pn.sb("half", [P, B])
            dve_step, stats_done, pow_ready, var_ready, sd_ready, den_ready, inv_ready = (
                pn.sem(n) for n in ("dve_step", "stats_done", "pow_ready", "var_ready", "sd_ready", "den_ready", "inv_ready"))
            with nc.Block() as block:
                @block.gpsimd
                def _(g):
                    g.memset(half[:, :], 0.5).then_inc(sd_ready, 1)
                    inverse_roots(g, S, stats_done, pow_ready)
                    g.wait_ge(sd_ready, 1)
                    g.wait_ge(var_ready, 1)
                    g.tensor_tensor(var[:, :], var[:, :], half[:, :], ALU.pow).then_inc(sd_ready, 1)
                    g.wait_ge(den_ready, 1)
                    g.tensor_tensor(var[:, :], var[:, :], S.mhalf[:, :], ALU.pow).then_inc(inv_ready, 1)

                @block.vector
                def _(v):
                    step = Steps(v, dve_step)
                    layer_norm_coefficients(v, step, S, stats_done, pow_ready)
                    step(normalized(v, step, S, xn3))
                    for b in range(B):
                        ins = v.bn_stats(stats[:, b, :], xn3[:, b, :])
                    step(ins)
                    step(v.tensor_tensor(mu[:, :], stats[:, :, 1], stats[:, :, 4], ALU.add))
                    step(v.tensor_tensor(dif[:, :], stats[:, :, 1], stats[:, :, 4], ALU.subtract))
                    step(v.tensor_scalar(mu[:, :], mu[:, :], 0.5, None, ALU.mult))
                    step(v.tensor_tensor(var[:, :], stats[:, :, 2], stats[:, :, 5], ALU.add))
                    step(v.scalar_tensor_tensor(out=dif[:, :], in0=dif[:, :], scalar=0.25 * D, in1=dif[:, :],
                                                op0=ALU.mult, op1=ALU.mult))
                    step(v.tensor_tensor(var[:, :], var[:, :], dif[:, :], ALU.add))
                    v.tensor_scalar(var[:, :], var[:, :], 1.0 / (D - 1), None, ALU.mult).then_inc(var_ready, 1)
                    v.wait_ge(sd_ready, 2)
                    v.tensor_scalar(var[:, :], var[:, :], 1e-5, None, ALU.add).then_inc(den_ready, 1)
                    v.wait_ge(inv_ready, 1)
                    step(v.tensor_tensor(xn3[:, :, :], xn3[:, :, :], mu[:, :].unsqueeze(2).broadcast_to([P, B, D]), ALU.subtract))
                    step(v.tensor_tensor(xn3[:, :, :], xn3[:, :, :], var[:, :].unsqueeze(2).broadcast_to([P, B, D]), ALU.mult))

        tree_routes(nc, S, name + "_r3", 3, 0, xn3, leaves, ins["L1_ffn_nw3"], ins["L1_ffn_nb3"])
        tree_attention(nc, S, name + "_qkv", xn3, leaves, table)
        tree_routes(nc, S, name + "_rf", 1, 3, xn3, leaves_f, ins["L1_ffn_nwf"], ins["L1_ffn_nbf"])
        tree_output(nc, S, name + "_f", xn3, leaves_f, table)


def row_of(stream, b):
    rows = stream[:, b:b + 1, :] if isinstance(b, int) else stream[:, bass.ds(b, 1), :]
    return rows.broadcast_to([P, LW, D])


def tree_hidden(v, step, rows, x, prod, h):
    step(v.tensor_tensor(prod[:, :, :], rows[:, W1:W1 + LW * D].rearrange("p (l d) -> p l d", d=D),
                         x, ALU.mult))
    step(v.tensor_reduce(h[:, :], prod[:, :, :], AX.X, ALU.add))
    return v.tensor_tensor(h[:, :], h[:, :], rows[:, B1:B1 + LW], ALU.add)


def tree_attention(nc, S, name, xn3, leaves, table):
    with phase(nc, name) as ph:
        lanes = range(LANES)
        N = 3 * LANES
        slots = [ph.sb(f"slot{m}", [P, ROW]) for m in range(N)]
        picks = [ph.sb(f"pick{m}", [P, 1], U32) for m in range(N)]
        prod = ph.sb("prod", [P, LW, D])
        h = [ph.sb(f"h{m}", [P, LW]) for m in range(N)]
        diag = [ph.sb(f"diag{k}", [P, LW, P]) for k in range(2)]
        qkv = [ph.sb(f"qkv{m}", [P, D]) for m in range(N)]
        qT, kT, pr, pT = ([ph.sb(f"{n}{l}", [P, P]) for l in lanes] for n in ("qT", "kT", "pr", "pT"))
        st = [ph.sb(f"st{l}", [P, 4]) for l in lanes]
        ps = [ph.ps(f"ps{k}", [P, 512]) for k in range(8)]
        gathered = [ph.sem(f"gathered{m}") for m in range(N)]
        dve_step, pool_step, h_ready, diag_ready, out_mm, used = (
            ph.sem(n) for n in ("dve_step", "pool_step", "h_ready", "diag_ready", "out_mm", "used"))
        qk_turned, qkT_ready, s_mm, shifted, p_exp, p_turned, pT_ready, att_mm = (
            ph.sem(n) for n in ("qk_turned", "qkT_ready", "s_mm", "shifted", "p_exp", "p_turned", "pT_ready", "att_mm"))

        with nc.Block() as block:
            @block.gpsimd
            def _(g):
                leaf_gathers(g, Steps(g, pool_step), leaves, picks, slots, table, gathered, used, LANES)

            @block.vector
            def _(v):
                v.sem_inc(used, 1)
                step = Steps(v, dve_step)

                def evacuate(i, m):
                    v.wait_ge(out_mm, 1 + i * N + m + 1)
                    v.tensor_tensor(qkv[m][:, :], ps[m % 2][:, 0:D], slots[m][:, B2:B2 + D], ALU.add).then_inc(used, 1)

                def hidden(i, m):
                    v.wait_ge(gathered[m], i * 16 + 16)
                    step(tree_hidden(v, step, slots[m], row_of(xn3, i * LANES + m % LANES), prod, h[m]))
                    v.tensor_scalar(h[m][:, :], h[m][:, :], 0.0, None, ALU.max).then_inc(h_ready, 1)

                def attend(i, k):
                    for l in lanes:
                        if k == 0:
                            v.wait_ge(qk_turned, i * LANES + l + 1)
                            v.tensor_copy(qT[l][:, :], ps[2 + l][:, 0:T])
                            v.tensor_copy(kT[l][:, :], ps[2 + l][:, T:2 * T]).then_inc(qkT_ready, 1)
                        elif k == 1:
                            v.wait_ge(s_mm, i * LANES + l + 1)
                            step(v.tensor_reduce(st[l][:, 0:1], ps[4 + l][:, 0:T], AX.X, ALU.max))
                            v.tensor_scalar(st[l][:, 1:2], st[l][:, 0:1], -float(D) ** -0.5, None, ALU.mult).then_inc(shifted, 1)
                        elif k == 2:
                            v.wait_ge(p_turned, i * LANES + l + 1)
                            v.tensor_copy(pT[l][:, :], ps[4 + l][:, T:2 * T]).then_inc(pT_ready, 1)
                        else:
                            b = i * LANES + l
                            v.wait_ge(att_mm, b + 1)
                            step(v.reciprocal(st[l][:, 3:4], st[l][:, 2:3]))
                            step(v.scalar_tensor_tensor(out=xn3[:, b, :], in0=ps[6 + l][:, 0:D], scalar=st[l][:, 3:4],
                                                        in1=xn3[:, b, :], op0=ALU.mult, op1=ALU.add))

                def iteration(i, before):
                    for m in range(N):
                        hidden(i, m)
                        if m >= 2:
                            if before is not None:
                                attend(before, m - 2)
                            evacuate(i, m - 2)
                        elif before is not None:
                            evacuate(before, N - 2 + m)

                iteration(0, None)
                with v.Fori(0, B // LANES - 1) as i:
                    step.restart()
                    iteration(i + 1, i)
                step.restart()
                evacuate(B // LANES - 1, N - 2)
                evacuate(B // LANES - 1, N - 1)
                for k in range(4):
                    attend(B // LANES - 1, k)

            @block.scalar
            def _(a):
                def exps(i):
                    for l in lanes:
                        a.wait_ge(shifted, i * LANES + l + 1)
                        a.activation(pr[l][:, :], ps[4 + l][:, 0:T], ACT.Exp, bias=st[l][:, 1:2], scale=float(D) ** -0.5,
                                     accum_out=st[l][:, 2:3]).then_inc(p_exp, 1)

                def iteration(i, before):
                    for m in range(N):
                        a.wait_ge(h_ready, i * N + m + 1)
                        a.wait_ge(out_mm, 1 if before is None and m < 2 else i * N + m)
                        for c in range(LW):
                            ins = a.activation(diag[m % 2][:, c, :], S.ident, ACT.Copy, scale=h[m][:, c:c + 1])
                        ins.then_inc(diag_ready, 1)
                        if m == 3 and before is not None:
                            exps(before)

                iteration(0, None)
                with a.Fori(0, B // LANES - 1) as i:
                    iteration(i + 1, i)
                exps(B // LANES - 1)

            @block.tensor
            def _(t):
                t.sem_inc(out_mm, 1)
                def attend(i, k):
                    for l in lanes:
                        if k == 0:
                            t.wait_ge(used, 1 + i * N + N)
                            t.transpose(ps[2 + l][:, 0:T], qkv[l][:, :], S.ident)
                            t.transpose(ps[2 + l][:, T:2 * T], qkv[LANES + l][:, :], S.ident).then_inc(qk_turned, 1)
                        elif k == 1:
                            t.wait_ge(qkT_ready, i * LANES + l + 1)
                            t.matmul(ps[4 + l][:, 0:T], qT[l][:, :], kT[l][:, :], start=True, stop=True).then_inc(s_mm, 1)
                        elif k == 2:
                            t.wait_ge(p_exp, i * LANES + l + 1)
                            t.transpose(ps[4 + l][:, T:2 * T], pr[l][:, :], S.ident).then_inc(p_turned, 1)
                        else:
                            t.wait_ge(pT_ready, i * LANES + l + 1)
                            t.matmul(ps[6 + l][:, 0:D], pT[l][:, :], qkv[2 * LANES + l][:, :], start=True,
                                     stop=True).then_inc(att_mm, 1)

                def iteration(i, before):
                    for m in range(N):
                        if before is not None and m >= 2:
                            attend(before, m - 2)
                        t.wait_ge(diag_ready, i * N + m + 1)
                        t.wait_ge(used, 1 if before is None and m < 2 else i * N + m)
                        for c in range(LW):
                            mm = t.matmul(ps[m % 2][:, 0:D], diag[m % 2][:, c, :], slots[m][:, W2 + c * D:W2 + (c + 1) * D],
                                          start=(c == 0), stop=(c == LW - 1))
                        mm.then_inc(out_mm, 1)

                iteration(0, None)
                with t.Fori(0, B // LANES - 1) as i:
                    iteration(i + 1, i)
                for k in range(4):
                    attend(B // LANES - 1, k)


def tree_output(nc, S, name, y, leaves, table):
    with phase(nc, name) as ph:
        N = 4
        slots = [ph.sb(f"slot{m}", [P, ROW]) for m in range(N)]
        picks = [ph.sb(f"pick{m}", [P, 1], U32) for m in range(N)]
        prod = ph.sb("prod", [P, LW, D])
        h = [ph.sb(f"h{m}", [P, LW]) for m in range(N)]
        diag = [ph.sb(f"diag{k}", [P, LW, P]) for k in range(2)]
        out = [ph.sb(f"out{k}", [P, D]) for k in range(2)]
        ps = [ph.ps(f"ps{k}", [P, 512]) for k in range(2)]
        gathered = [ph.sem(f"gathered{m}") for m in range(N)]
        dve_step, pool_step, h_ready, act_ready, diag_ready, out_mm, used = (
            ph.sem(n) for n in ("dve_step", "pool_step", "h_ready", "act_ready", "diag_ready", "out_mm", "used"))
        with nc.Block() as block:
            @block.gpsimd
            def _(g):
                leaf_gathers(g, Steps(g, pool_step), leaves, picks, slots, table, gathered, used, N)

            @block.vector
            def _(v):
                v.sem_inc(used, 1)
                step = Steps(v, dve_step)

                def add_up(i, m):
                    v.wait_ge(out_mm, 1 + i * N + m + 1)
                    v.tensor_tensor(out[m % 2][:, :], ps[m % 2][:, 0:D], slots[m][:, B2:B2 + D], ALU.add).then_inc(used, 1)
                    v.wait_ge(used, 1 + i * N + m + 1)
                    step(v.tensor_tensor(out[m % 2][:, :], out[m % 2][:, :], y[:, i * N + m, :], ALU.add))
                    step(v.tensor_tensor(S.x[:, i * N + m, :], S.x[:, i * N + m, :], out[m % 2][:, :], ALU.add))
                    step(v.bn_stats(S.stats[:, i * N + m, :], S.x[:, i * N + m, :]))

                def hidden(i, m):
                    v.wait_ge(gathered[m], i * 16 + 16)
                    tree_hidden(v, step, slots[m], row_of(y, i * N + m), prod, h[m]).then_inc(h_ready, 1)

                for m in range(N):
                    hidden(0, m)
                    if m >= 2:
                        add_up(0, m - 2)
                with v.Fori(0, B // N - 1) as i:
                    step.restart()
                    for m in range(N):
                        hidden(i + 1, m)
                        if m >= 2:
                            add_up(i + 1, m - 2)
                        else:
                            add_up(i, N - 2 + m)
                step.restart()
                add_up(B // N - 1, N - 2)
                add_up(B // N - 1, N - 1)

            @block.scalar
            def _(a):
                def iteration(i, first):
                    for m in range(N):
                        a.wait_ge(h_ready, i * N + m + 1)
                        a.activation(h[m][:, :], h[m][:, :], ACT.Gelu).then_inc(act_ready, 1)
                        a.wait_ge(act_ready, i * N + m + 1)
                        a.wait_ge(out_mm, 1 if first and m < 2 else i * N + m)
                        for c in range(LW):
                            ins = a.activation(diag[m % 2][:, c, :], S.ident, ACT.Copy, scale=h[m][:, c:c + 1])
                        ins.then_inc(diag_ready, 1)

                iteration(0, True)
                with a.Fori(0, B // N - 1) as i:
                    iteration(i + 1, False)

            @block.tensor
            def _(t):
                t.sem_inc(out_mm, 1)
                def iteration(i, first):
                    for m in range(N):
                        t.wait_ge(diag_ready, i * N + m + 1)
                        t.wait_ge(used, 1 if first and m < 2 else i * N + m)
                        for c in range(LW):
                            mm = t.matmul(ps[m % 2][:, 0:D], diag[m % 2][:, c, :], slots[m][:, W2 + c * D:W2 + (c + 1) * D],
                                          start=(c == 0), stop=(c == LW - 1))
                        mm.then_inc(out_mm, 1)

                iteration(0, True)
                with t.Fori(0, B // N - 1) as i:
                    iteration(i + 1, False)


def wide_head_attention(nc, S, name, ins):
    HEADS, DH = 16, 64
    EPS = 1e-6
    NCH = HEADS * DH // P
    HPC = 4
    CHUNKS = HEADS // HPC
    scale = DH ** -0.5
    with phase(nc, name) as ph:
        lanes = range(LANES)
        wq = ph.sb("wq", [P, HEADS * DH])
        wkv = ph.sb("wkv", [P, 2, 2 * HEADS * DH])
        wout = ph.sb("wout", [P, NCH, D])
        null_key = ph.sb("null_key", [P, DH])
        null_value = ph.sb("null_value", [P, 1])
        value_cols = ph.sb("value_cols", [P, NCH, HEADS])
        wnull = ph.sb("wnull", [P, HEADS])
        null_out = ph.sb("null_out", [P, D])
        prod = ph.sb("prod", [P, HEADS, DH])
        scale_row, bias_row = ph.sb("scale_row", [P, D]), ph.sb("bias_row", [P, D])
        xn_all = ph.sb("xn_all", [P, B, D])
        xn = [ph.sb(f"xn{l}", [P, D]) for l in lanes]
        xnT = [ph.sb(f"xnT{l}", [P, T]) for l in lanes]
        cT = [ph.sb(f"cT{l}", [P, 2, P]) for l in lanes]
        qT = [ph.sb(f"qT{l}", [P, NCH, T]) for l in lanes]
        keys = [ph.sb(f"keys{l}", [P, NCH, 2, P]) for l in lanes]
        vals = [ph.sb(f"vals{l}", [P, NCH, 2 * P]) for l in lanes]
        probs = [ph.sb(f"probs{l}", [P, HEADS, P]) for l in lanes]
        probsT = [ph.sb(f"probsT{l}", [P, HEADS, P]) for l in lanes]
        s0, p0, mx, neg, sums = ([ph.sb(f"{n}{l}", [P, HEADS]) for l in lanes] for n in ("s0", "p0", "mx", "neg", "sums"))
        p0T = [ph.sb(f"p0T{l}", [P, T]) for l in lanes]
        oT = [ph.sb(f"oT{l}", [P, NCH, T]) for l in lanes]
        st = [ph.sb(f"st{l}", [P, 6]) for l in lanes]
        mv = [ph.sb(f"mv{l}", [P, 2]) for l in lanes]
        rstd = [ph.sb(f"rstd{l}", [P, 1]) for l in lanes]
        res = [ph.sb(f"res{l}", [P, D]) for l in lanes]
        psA = [ph.ps(f"psA{l}", [P, 1024]) for l in lanes]
        psB = [ph.ps(f"psB{l}", [P, 512]) for l in lanes]
        psO = [ph.ps(f"psO{l}", [P, 512]) for l in lanes]
        dve_step, stats_done, pow_ready, loaded, null_ready, zeros_set, null_mm, null_out_ready, normed = (ph.sem(n) for n in (
            "dve_step", "stats_done", "pow_ready", "loaded", "null_ready", "zeros_set", "null_mm", "null_out_ready", "normed"))
        (xn_ready, xn_turned, xnT_ready, cT_ready, s0_mm, q_mm, q_ready, k_mm, k_low_ready, k_high_ready, v_mm, v_ready) = (
            [ph.sem(f"{n}{l}") for l in lanes] for n in (
                "xn_ready", "xn_turned", "xnT_ready", "cT_ready", "s0_mm", "q_mm", "q_ready", "k_mm", "k_low_ready",
                "k_high_ready", "v_mm", "v_ready"))
        (scores_ready, maxed, exp_ready, normed_ready, turned, probsT_ready, out_mm, oT_ready, p0_turned, p0T_ready,
         res_ready, proj_ready, var_ready, rstd_ready) = ([ph.sem(f"{n}{l}") for l in lanes] for n in (
             "scores_ready", "maxed", "exp_ready", "normed_ready", "turned", "probsT_ready", "out_mm", "oT_ready",
             "p0_turned", "p0T_ready", "res_ready", "proj_ready", "var_ready", "rstd_ready"))

        def bank(c):
            return slice(c % 2 * 512, c % 2 * 512 + 512)

        with nc.Block() as block:
            @block.sync
            def _(sp):
                sp.dma_start(wq[:, :], ins["L2_xattn_Wq"]).then_inc(loaded, 16)
                sp.dma_start(null_key[:, :], ins["L2_null_key"].partition_broadcast(P)).then_inc(loaded, 16)
                sp.dma_start(null_value[:, :], ins["L2_null_values"]).then_inc(loaded, 16)
                sp.dma_start(wkv[:, :, :], ins["L2_xattn_Wkv"].rearrange("(s p) n -> p s n", p=P)).then_inc(loaded, 16)
                sp.dma_start(wout[:, :, :], ins["L2_xattn_Wout"].rearrange("(c p) n -> p c n", p=P)).then_inc(loaded, 16)
                sp.dma_start(scale_row[:, :], ins["L2_xattn_ln_scale"].partition_broadcast(P)).then_inc(loaded, 16)
                sp.dma_start(bias_row[:, :], ins["L2_xattn_ln_bias"].partition_broadcast(P)).then_inc(loaded, 16)

            @block.gpsimd
            def _(g):
                inverse_roots(g, S, stats_done, pow_ready)
                for l in lanes:
                    g.memset(keys[l][:, :, :, :], 0.0).then_inc(zeros_set, 1)
                    g.memset(vals[l][:, :, :], 0.0).then_inc(zeros_set, 1)

                def rows(j, l):
                    g.wait_ge(xn_turned[l], 1 + j)
                    g.tensor_copy(xn[l][:, :], xn_all[:, j * LANES + l, :]).then_inc(xn_ready[l], 1)

                def context(j, l):
                    g.wait_ge(v_mm[l], 1 + 2 * j)
                    b = j * LANES + l
                    g.tensor_copy(cT[l][:, :, :], S.ctxT[:, :, bass.ds(b, 1), :]
                                  .rearrange("p s o k -> p (s o) k")).then_inc(cT_ready[l], 1)

                def root(j, l):
                    g.wait_ge(var_ready[l], j + 1)
                    g.tensor_tensor(rstd[l][:, :], mv[l][:, 1:2], S.mhalf[:, 0:1], ALU.pow).then_inc(rstd_ready[l], 1)
                g.wait_ge(normed, 1)
                skewed(g, [rows, context], [nothing, root])

            @block.vector
            def _(v):
                step = Steps(v, dve_step)
                layer_norm_coefficients(v, step, S, stats_done, pow_ready)
                normalized(v, step, S, xn_all).then_inc(normed, 1)
                v.wait_ge(loaded, 112)
                step(v.tensor_tensor(prod[:, :, :], wq[:, :].rearrange("p (h d) -> p h d", d=DH),
                                     null_key[:, :].unsqueeze(1).broadcast_to([P, HEADS, DH]), ALU.mult))
                v.tensor_reduce(wnull[:, :], prod[:, :, :], AX.X, ALU.add).then_inc(null_ready, 1)
                v.tensor_scalar(value_cols[:, :, :].rearrange("p c h -> p (c h)"), S.pairhead, null_value[:, 0:1], None,
                                ALU.mult).then_inc(null_ready, 1)
                v.wait_ge(null_mm, 1)
                v.tensor_copy(null_out[0:HEADS, :], psB[0][0:HEADS, 0:D]).then_inc(null_out_ready, 1)
                v.wait_ge(zeros_set, 4)

                def null_scores(j, l):
                    v.wait_ge(s0_mm[l], j + 1)
                    step(v.tensor_scalar(s0[l][:, :], psO[l][:, 0:HEADS], scale, None, ALU.mult))

                def low_keys(j, l):
                    for n in range(2):
                        v.wait_ge(k_mm[l], 2 * j + n + 1)
                        v.tensor_copy(keys[l][0:DH, 4 * n:4 * n + 4, 0, :],
                                      psA[l][0:DH, bank(n)].rearrange("p (c k) -> p c k", k=P)).then_inc(k_low_ready[l], 1)

                def maximum(c, j, l):
                    heads = slice(c * HPC, (c + 1) * HPC)
                    v.wait_ge(scores_ready[l], j * CHUNKS + c + 1)
                    step(v.tensor_reduce(mx[l][:, heads], psA[l][:, bank(c)].rearrange("p (j k) -> p j k", k=P), AX.X, ALU.max))
                    step(v.tensor_tensor(mx[l][:, heads], mx[l][:, heads], s0[l][:, heads], ALU.max))
                    v.tensor_scalar(neg[l][:, heads], mx[l][:, heads], -1.0, None, ALU.mult)
                    v.tensor_tensor(p0[l][:, heads], s0[l][:, heads], mx[l][:, heads], ALU.subtract).then_inc(maxed[l], 1)

                def divide(c, j, l):
                    heads = slice(c * HPC, (c + 1) * HPC)
                    v.wait_ge(exp_ready[l], j * CHUNKS + c + 1)
                    step(v.tensor_tensor(sums[l][:, heads], sums[l][:, heads], p0[l][:, heads], ALU.add))
                    step(v.reciprocal(sums[l][:, heads], sums[l][:, heads]))
                    v.tensor_tensor(p0[l][:, heads], p0[l][:, heads], sums[l][:, heads], ALU.mult)
                    v.tensor_tensor(probs[l][:, heads, :], probs[l][:, heads, :],
                                    sums[l][:, heads].unsqueeze(2).broadcast_to([P, HPC, P]), ALU.mult).then_inc(normed_ready[l], 1)

                def turned_out(n, j, l):
                    v.wait_ge(out_mm[l], 2 * j + n + 1)
                    v.tensor_copy(oT[l][:, 4 * n:4 * n + 4, :].rearrange("p c t -> p (c t)"), psO[l][:, :]).then_inc(oT_ready[l], 1)

                def chunk(c):
                    def stage(j, l):
                        if c:
                            divide(c - 1, j, l)
                        maximum(c, j, l)
                    return stage

                def last_division(j, l):
                    divide(CHUNKS - 1, j, l)

                def first_outputs(j, l):
                    turned_out(0, j, l)

                def last_outputs(j, l):
                    turned_out(1, j, l)

                def statistics(j, l):
                    v.wait_ge(proj_ready[l], j + 1)
                    v.tensor_copy(res[l][:, :], psO[l][:, 0:D]).then_inc(res_ready[l], 1)
                    v.wait_ge(res_ready[l], 1 + j + 1)
                    step(v.bn_stats(st[l][:, :], res[l][:, :]))
                    step(v.bn_aggr(mv[l][:, :], st[l][:, :]))
                    v.tensor_scalar(mv[l][:, 1:2], mv[l][:, 1:2], EPS, None, ALU.add).then_inc(var_ready[l], 1)

                def added(j, l):
                    b = j * LANES + l
                    v.wait_ge(rstd_ready[l], j + 1)
                    step(v.tensor_scalar(res[l][:, :], res[l][:, :], mv[l][:, 0:1], rstd[l][:, 0:1], ALU.subtract, ALU.mult))
                    step(v.tensor_tensor(res[l][:, :], res[l][:, :], scale_row[:, :], ALU.mult))
                    step(v.tensor_tensor(res[l][:, :], res[l][:, :], bias_row[:, :], ALU.add))
                    step(v.tensor_tensor(S.x[:, b, :], S.x[:, b, :], res[l][:, :], ALU.add))
                    step(v.bn_stats(S.stats[:, b, :], S.x[:, b, :]))

                for l in lanes:
                    v.sem_inc(res_ready[l], 1)
                skewed(v, [nothing, null_scores, low_keys, chunk(0), nothing, chunk(1), nothing],
                       [chunk(2), chunk(3), last_division, first_outputs, last_outputs, statistics, added], step.restart)

            @block.scalar
            def _(a):
                a.wait_ge(zeros_set, 4)

                def turned_x(j, l):
                    a.wait_ge(xn_turned[l], 1 + j + 1)
                    a.activation(xnT[l][:, :], psB[l][:, 0:T], ACT.Copy).then_inc(xnT_ready[l], 1)

                def queries(j, l):
                    for n in range(2):
                        a.wait_ge(q_mm[l], 2 * j + n + 1)
                        a.activation(qT[l][:, 4 * n:4 * n + 4, :].rearrange("p c t -> p (c t)"), psA[l][:, bank(n)], ACT.Copy,
                                     scale=scale).then_inc(q_ready[l], 1)

                def high_keys(j, l):
                    for n in range(2):
                        a.wait_ge(k_mm[l], 2 * j + n + 1)
                        a.activation(keys[l][DH:P, 4 * n:4 * n + 4, 1, :],
                                     psA[l][DH:P, bank(n)].rearrange("p (c k) -> p c k", k=P),
                                     ACT.Copy).then_inc(k_high_ready[l], 1)

                def values(n):
                    def stage(j, l):
                        a.wait_ge(v_mm[l], 1 + 2 * j + n + 1)
                        pairs = psO[l][:, :].rearrange("p (c d) -> p c d", d=2 * DH)
                        a.activation(vals[l][:, 4 * n:4 * n + 4, 0:DH], pairs[:, :, 0:DH], ACT.Copy)
                        a.activation(vals[l][:, 4 * n:4 * n + 4, 2 * P - DH:2 * P], pairs[:, :, DH:2 * DH],
                                     ACT.Copy).then_inc(v_ready[l], 1)
                    return stage

                def chunk(c):
                    def stage(j, l):
                        if c >= 2:
                            a.wait_ge(turned[l], j * CHUNKS + c - 1)
                            a.activation(probsT[l][:, (c - 2) * HPC:(c - 1) * HPC, :].rearrange("p j k -> p (j k)"),
                                         psB[l][:, :], ACT.Copy).then_inc(probsT_ready[l], 1)
                        if c < CHUNKS:
                            a.wait_ge(maxed[l], j * CHUNKS + c + 1)
                            for h in range(c * HPC, (c + 1) * HPC):
                                at = c % 2 * 512 + h % HPC * P
                                a.activation(probs[l][:, h, :], psA[l][:, at:at + P], ACT.Exp, bias=neg[l][:, h:h + 1],
                                             accum_out=sums[l][:, h:h + 1])
                            p0c = p0[l][:, c * HPC:(c + 1) * HPC]
                            a.activation(p0c, p0c, ACT.Exp).then_inc(exp_ready[l], 1)
                    return stage

                def null_turned(j, l):
                    a.wait_ge(p0_turned[l], j + 1)
                    a.activation(p0T[l][0:HEADS, :], psB[l][0:HEADS, 0:T], ACT.Copy).then_inc(p0T_ready[l], 1)

                skewed(a, [turned_x, queries, high_keys, chunk(0), values(0), chunk(1), values(1)],
                       [chunk(2), chunk(3), chunk(4), chunk(5), null_turned, nothing, nothing])

            @block.tensor
            def _(t):
                for l in lanes:
                    t.sem_inc(xn_turned[l], 1)
                    t.sem_inc(v_mm[l], 1)
                t.wait_ge(null_ready, 2)
                for c in range(NCH):
                    mm = t.matmul(psB[0][0:HEADS, 0:D], value_cols[:, c, :], wout[:, c, :], start=(c == 0), stop=(c == NCH - 1))
                mm.then_inc(null_mm, 1)
                t.wait_ge(null_out_ready, 1)

                def turn_x(j, l):
                    t.wait_ge(xn_ready[l], j + 1)
                    t.transpose(psB[l][:, 0:T], xn[l][:, :], S.ident).then_inc(xn_turned[l], 1)

                def queries(j, l):
                    t.wait_ge(xnT_ready[l], j + 1)
                    t.wait_ge(res_ready[l], 1 + j)
                    t.matmul(psO[l][:, 0:HEADS], xnT[l][:, :], wnull[:, :], start=True, stop=True).then_inc(s0_mm[l], 1)
                    for n in range(2):
                        for c in range(4 * n, 4 * n + 4):
                            mm = t.matmul(psA[l][:, c * T:(c + 1) * T], wq[:, c * P:(c + 1) * P], xnT[l][:, :],
                                          start=True, stop=True)
                        mm.then_inc(q_mm[l], 1)

                def new_keys(j, l):
                    t.wait_ge(cT_ready[l], j + 1)
                    for n in range(2):
                        t.wait_ge(q_ready[l], 2 * j + n + 1)
                        for c in range(4 * n, 4 * n + 4):
                            for s in range(2):
                                mm = t.matmul(psA[l][:, c * P:(c + 1) * P], wkv[:, s, c * P:(c + 1) * P], cT[l][:, s, :],
                                              start=(s == 0), stop=(s == 1))
                        mm.then_inc(k_mm[l], 1)

                def values(n):
                    def stage(j, l):
                        if n:
                            t.wait_ge(v_ready[l], 2 * j + 1)
                        at = HEADS * DH + n * 512
                        for s in range(2):
                            mm = t.matmul(psO[l][:, :], cT[l][:, s, :], wkv[:, s, at:at + 512], start=(s == 0), stop=(s == 1))
                        mm.then_inc(v_mm[l], 1)
                    return stage

                def chunk(c):
                    def stage(j, l):
                        if c < CHUNKS:
                            if c < 2:
                                t.wait_ge(k_low_ready[l], 2 * j + 2)
                                t.wait_ge(k_high_ready[l], 2 * j + 2)
                            else:
                                t.wait_ge(exp_ready[l], j * CHUNKS + c - 1)
                            for k in range(2):
                                at = c % 2 * 512 + k * 2 * P
                                mm = t.matmul(psA[l][:, at:at + 2 * P], qT[l][:, 2 * c + k, :],
                                              keys[l][:, 2 * c + k, :, :].rearrange("p s k -> p (s k)"), start=True, stop=True)
                            mm.then_inc(scores_ready[l], 1)
                        if 2 <= c <= CHUNKS + 1:
                            t.wait_ge(normed_ready[l], j * CHUNKS + c - 1)
                            if c > 2:
                                t.wait_ge(probsT_ready[l], j * CHUNKS + c - 2)
                            for k in range(HPC):
                                mm = t.transpose(psB[l][:, k * P:(k + 1) * P], probs[l][:, (c - 2) * HPC + k, :], S.ident)
                            mm.then_inc(turned[l], 1)
                        if c >= 3:
                            if c == 3:
                                t.wait_ge(v_ready[l], 2 * j + 2)
                            if c == CHUNKS + 2:
                                t.wait_ge(probsT_ready[l], j * CHUNKS + CHUNKS)
                            if c == 5:
                                t.wait_ge(oT_ready[l], 2 * j + 1)
                            for pair in (2 * (c - 3), 2 * (c - 3) + 1):
                                for k in range(2):
                                    mm = t.matmul(psO[l][:, pair % 4 * T:pair % 4 * T + T], vals[l][:, pair, k * P:(k + 1) * P],
                                                  probsT[l][:, 2 * pair + k, :], start=(k == 0), stop=(k == 1))
                            if c % 2 == 0:
                                mm.then_inc(out_mm[l], 1)
                    return stage

                def turn_null(j, l):
                    t.transpose(psB[l][0:HEADS, 0:T], p0[l][:, :], S.ident).then_inc(p0_turned[l], 1)

                def project(j, l):
                    t.wait_ge(oT_ready[l], 2 * j + 2)
                    t.wait_ge(p0T_ready[l], j + 1)
                    for c in range(NCH):
                        t.matmul(psO[l][:, 0:D], oT[l][:, c, :], wout[:, c, :], start=(c == 0), stop=False)
                    t.matmul(psO[l][:, 0:D], p0T[l][0:HEADS, :], null_out[0:HEADS, :], start=False,
                             stop=True).then_inc(proj_ready[l], 1)

                def last_chunk(j, l):
                    chunk(CHUNKS + 2)(j, l)
                    turn_null(j, l)
                skewed(t, [turn_x, queries, new_keys, chunk(0), values(0), chunk(1), values(1)],
                       [chunk(2), chunk(3), chunk(4), chunk(5), last_chunk, project, nothing])


def normed_rows_and_logits(nc, S, ph, name, experts, w, w_dram, xT_all, logits):
    with phase(nc, name) as pn:
        lanes = range(LANES)
        xn = [pn.sb(f"xn{l}", [P, D]) for l in lanes]
        xT = [pn.sb(f"xT{l}", [P, T]) for l in lanes]
        ps = [pn.ps(f"ps{k}", [P, 512]) for k in range(4)]
        dve_step, stats_done, pow_ready, loaded, xn_ready, turned, xT_ready, xT_kept, logits_mm, logits_kept = (
            pn.sem(n) for n in ("dve_step", "stats_done", "pow_ready", "loaded", "xn_ready", "turned", "xT_ready", "xT_kept",
                                "logits_mm", "logits_kept"))
        with nc.Block() as block:
            @block.sync
            def _(sp):
                sp.dma_start(w[:, :], w_dram).then_inc(loaded, 16)

            @block.gpsimd
            def _(g):
                inverse_roots(g, S, stats_done, pow_ready)

            @block.vector
            def _(v):
                v.sem_inc(logits_kept, 1)
                v.sem_inc(xT_ready, 1)
                step = Steps(v, dve_step)
                layer_norm_coefficients(v, step, S, stats_done, pow_ready)
                with v.Fori(0, B // LANES) as i:
                    for l in lanes:
                        b = i * LANES + l
                        v.wait_ge(turned, 1 + i * LANES)
                        v.tensor_scalar(xn[l][:, :], S.x[:, b, :], S.mean[:, bass.ds(b, 1)], S.rstd[:, bass.ds(b, 1)],
                                        ALU.subtract, ALU.mult).then_inc(xn_ready, 1)
                    for l in lanes:
                        b = i * LANES + l
                        v.wait_ge(turned, 1 + b + 1)
                        v.wait_ge(logits_mm, 1 + i * LANES)
                        v.wait_ge(xT_kept, 1 + i * LANES)
                        v.tensor_copy(xT[l][:, :], ps[l][:, 0:T]).then_inc(xT_ready, 1)
                    for l in lanes:
                        b = i * LANES + l
                        v.wait_ge(logits_mm, 1 + b + 1)
                        v.tensor_copy(logits[:, b, :], ps[2 + l][:, 0:experts]).then_inc(logits_kept, 1)

            @block.scalar
            def _(a):
                a.sem_inc(xT_kept, 1)
                with a.Fori(0, B // LANES) as i:
                    for l in lanes:
                        b = i * LANES + l
                        a.wait_ge(xT_ready, 1 + b + 1)
                        a.activation(xT_all[:, b, :], xT[l][:, :], ACT.Copy).then_inc(xT_kept, 1)

            @block.tensor
            def _(t):
                t.sem_inc(logits_mm, 1)
                t.sem_inc(turned, 1)
                t.wait_ge(loaded, 16)
                with t.Fori(0, B // LANES) as i:
                    for l in lanes:
                        t.wait_ge(xn_ready, i * LANES + l + 1)
                        t.wait_ge(xT_ready, 1 + i * LANES)
                        t.transpose(ps[l][:, 0:T], xn[l][:, :], S.ident).then_inc(turned, 1)
                    for l in lanes:
                        t.wait_ge(xT_ready, 1 + i * LANES + l + 1)
                        t.wait_ge(logits_kept, 1 + i * LANES)
                        t.matmul(ps[2 + l][:, 0:experts], xT[l][:, :], w[:, :], start=True, stop=True).then_inc(logits_mm, 1)


def chosen(v, step, S, vals, n, count, above, ties, sel):
    mine = vals.unsqueeze(3).broadcast_to([P, B, n, n])
    other = vals.unsqueeze(2).broadcast_to([P, B, n, n])
    before = S.before16.rearrange("p (a b) -> p a b", b=16)[:, 0:n, 0:n]
    step(v.tensor_tensor(above, other, mine, ALU.is_gt))
    step(v.tensor_tensor(ties, other, mine, ALU.is_equal))
    step(v.tensor_tensor(ties, ties, before.unsqueeze(1).broadcast_to([P, B, n, n]), ALU.mult))
    step(v.tensor_tensor(above, above, ties, ALU.add))
    step(v.tensor_reduce(sel, above, AX.X, ALU.add))
    step(v.tensor_scalar(sel, sel, float(count), None, ALU.is_lt))


def grouped_mixture(nc, S, name, ins):
    E, F, GROUPS, TOP_GROUPS, TOP, SHARED, SCALE = 16, 128, 4, 2, 4, 2, 2.5
    ALL = E + SHARED
    PER = E // GROUPS
    G = 4
    with phase(nc, name) as ph:
        wr = ph.sb("wr", [P, E])
        gate, up, down = (ph.sb(n, [P, ALL, F]) for n in ("gate", "up", "down"))
        xT = ph.sb("xT", [P, B, T])
        mix = ph.sb("mix", [P, B, ALL])
        score = ph.sb("score", [P, B, E])
        weights_loaded = ph.sem("weights_loaded")
        with nc.Block() as block:
            @block.sync
            def _(sp):
                for dst, n in ((gate, "gate_w"), (up, "up_w"), (down, "down_w")):
                    sp.dma_start(dst[:, 0:E, :], ins["L2_ffn_" + n].rearrange("e i j -> i e j")).then_inc(weights_loaded, 16)
                for dst, n in ((gate, "sh_gate_w"), (up, "sh_up_w")):
                    sp.dma_start(dst[:, E:ALL, :], ins["L2_ffn_" + n].rearrange("i (e j) -> i e j", j=F)).then_inc(weights_loaded, 16)
                sp.dma_start(down[:, E:ALL, :], ins["L2_ffn_sh_down_w"].rearrange("(e i) j -> i e j", i=F)).then_inc(weights_loaded, 16)
        normed_rows_and_logits(nc, S, ph, name + "_n", E, wr, ins["L2_router_wT"], xT, score)

        with phase(nc, name + "_r") as pr:
            bias = pr.sb("bias", [P, E])
            biased, masked = pr.sb("biased", [P, B, E]), pr.sb("masked", [P, B, E])
            above, ties = pr.sb("above", [P, B, E, E]), pr.sb("ties", [P, B, E, E])
            hi, lo = pr.sb("hi", [P, B, GROUPS, 2]), pr.sb("lo", [P, B, GROUPS, 2])
            best, second, third = (pr.sb(n, [P, B, GROUPS]) for n in ("best", "second", "third"))
            total = pr.sb("total", [P, B])
            dve_step, bias_loaded, exp_done = pr.sem("dve_step"), pr.sem("bias_loaded"), pr.sem("exp_done")
            with nc.Block() as block:
                @block.sync
                def _(sp):
                    sp.dma_start(bias[:, :], ins["L2_ffn_bias"].partition_broadcast(P)).then_inc(bias_loaded, 16)

                @block.scalar
                def _(a):
                    a.activation(score[:, :, :], score[:, :, :], ACT.Exp, scale=-1.0).then_inc(exp_done, 1)

                @block.vector
                def _(v):
                    step = Steps(v, dve_step)
                    v.wait_ge(bias_loaded, 16)
                    v.wait_ge(exp_done, 1)
                    step(v.tensor_scalar(score[:, :, :], score[:, :, :], 1.0, None, ALU.add))
                    step(v.reciprocal(score[:, :, :], score[:, :, :]))
                    step(v.tensor_tensor(biased[:, :, :], score[:, :, :],
                                         bias[:, :].unsqueeze(1).broadcast_to([P, B, E]), ALU.add))
                    quad = biased[:, :, :].rearrange("p b (g two c) -> p (b g) two c", two=2, c=2)
                    h2, l2 = (x[:, :, :, :].rearrange("p b g c -> p (b g) c") for x in (hi, lo))
                    bst, sec, thr = (x[:, :, :].rearrange("p b g -> p (b g)") for x in (best, second, third))
                    step(v.tensor_tensor(h2, quad[:, :, 0, :], quad[:, :, 1, :], ALU.max))
                    step(v.tensor_tensor(l2, quad[:, :, 0, :], quad[:, :, 1, :], ALU.min))
                    step(v.tensor_tensor(bst, h2[:, :, 0], h2[:, :, 1], ALU.max))
                    step(v.tensor_tensor(sec, h2[:, :, 0], h2[:, :, 1], ALU.min))
                    step(v.tensor_tensor(thr, l2[:, :, 0], l2[:, :, 1], ALU.max))
                    step(v.tensor_tensor(sec, sec, thr, ALU.max))
                    step(v.tensor_tensor(bst, bst, sec, ALU.add))
                    chosen(v, step, S, best[:, :, :], GROUPS, TOP_GROUPS, above[:, :, 0:GROUPS, 0:GROUPS],
                           ties[:, :, 0:GROUPS, 0:GROUPS], second[:, :, :])
                    m = sec.unsqueeze(2).broadcast_to([P, B * GROUPS, PER])
                    mk, bs = (x[:, :, :].rearrange("p b (g c) -> p (b g) c", c=PER) for x in (masked, biased))
                    step(v.tensor_tensor(mk, bs, m, ALU.mult))
                    step(v.tensor_scalar(thr, sec, -1.0, None, ALU.add))
                    step(v.tensor_tensor(mk, mk, thr.unsqueeze(2).broadcast_to([P, B * GROUPS, PER]), ALU.add))
                    chosen(v, step, S, masked[:, :, :], E, TOP, above[:, :, :, :], ties[:, :, :, :], biased[:, :, :])
                    step(v.tensor_tensor(masked[:, :, :], score[:, :, :], biased[:, :, :], ALU.mult))
                    step(v.tensor_reduce(total[:, :], masked[:, :, :], AX.X, ALU.add))
                    step(v.tensor_scalar(total[:, :], total[:, :], 1e-20, None, ALU.add))
                    step(v.reciprocal(total[:, :], total[:, :]))
                    step(v.tensor_scalar(total[:, :], total[:, :], SCALE, None, ALU.mult))
                    step(v.memset(mix[:, :, :], 1.0))
                    step(v.tensor_tensor(mix[:, :, 0:E], masked[:, :, :], total[:, :].unsqueeze(2).broadcast_to([P, B, E]),
                                         ALU.mult))

        with phase(nc, name + "_e") as pe:
            sg = [pe.sb(f"sg{k}", [P, G * T]) for k in range(2)]
            act = [pe.sb(f"act{k}", [P, G * T]) for k in range(2)]
            ps_g = [pe.ps(f"ps_g{k}", [P, G * T]) for k in range(2)]
            ps_u = [pe.ps(f"ps_u{k}", [P, G * T]) for k in range(2)]
            ps_y = [pe.ps(f"ps_y{k}", [P, G, D]) for k in range(2)]
            dve_step, gu_ready, silu_ready, act_ready, y_ready, y_added = (
                pe.sem(n) for n in ("dve_step", "gu_ready", "silu_ready", "act_ready", "y_ready", "y_added"))
            with nc.Block() as block:
                @block.vector
                def _(v):
                    v.sem_inc(y_added, 1)
                    v.sem_inc(act_ready, 1)
                    step = Steps(v, dve_step)

                    def add_up(i, e):
                        v.wait_ge(y_ready, i * ALL + e + 1)
                        if e:
                            v.wait_ge(y_added, 1 + i * ALL + e)
                        for k in range(G):
                            x = S.x[:, i * G + k, :]
                            ins_ = v.scalar_tensor_tensor(out=x, in0=ps_y[e % 2][:, k, :], scalar=mix[:, i * G + k, e:e + 1],
                                                          in1=x, op0=ALU.mult, op1=ALU.add)
                        ins_.then_inc(y_added, 1)

                    with v.Fori(0, B // G) as i:
                        step.restart()
                        for e in range(ALL):
                            v.wait_ge(silu_ready, i * ALL + e + 1)
                            v.tensor_tensor(act[e % 2][:, :], sg[e % 2][:, :], ps_u[e % 2][:, :], ALU.mult).then_inc(act_ready, 1)
                            if e:
                                add_up(i, e - 1)
                        add_up(i, ALL - 1)
                        v.wait_ge(y_added, 1 + i * ALL + ALL)
                        for k in range(G):
                            step(v.bn_stats(S.stats[:, i * G + k, :], S.x[:, i * G + k, :]))

                @block.scalar
                def _(a):
                    with a.Fori(0, B // G) as i:
                        for e in range(ALL):
                            a.wait_ge(gu_ready, i * ALL + e + 1)
                            a.wait_ge(act_ready, 1 + i * ALL + e - 1) if e >= 2 else a.wait_ge(act_ready, 1 + i * ALL)
                            a.activation(sg[e % 2][:, :], ps_g[e % 2][:, :], ACT.Silu).then_inc(silu_ready, 1)

                @block.tensor
                def _(t):
                    t.wait_ge(weights_loaded, 96)

                    def project(i, e):
                        t.wait_ge(act_ready, 1 + i * ALL + e + 1)
                        t.wait_ge(y_added, 1 + i * ALL + e - 1) if e >= 2 else t.wait_ge(y_added, 1 + i * ALL)
                        for k in range(G):
                            mm = t.matmul(ps_y[e % 2][:, k, :], act[e % 2][:, k * T:(k + 1) * T], down[:, e, :],
                                          start=True, stop=True)
                        mm.then_inc(y_ready, 1)

                    with t.Fori(0, B // G) as i:
                        for e in range(ALL):
                            t.wait_ge(act_ready, 1 + i * ALL + e - 1) if e >= 2 else t.wait_ge(act_ready, 1 + i * ALL)
                            rows = xT[:, bass.ds(i * G, G), :].rearrange("p b t -> p (b t)")
                            t.matmul(ps_g[e % 2][:, :], gate[:, e, :], rows, start=True, stop=True)
                            t.matmul(ps_u[e % 2][:, :], up[:, e, :], rows, start=True, stop=True).then_inc(gu_ready, 1)
                            if e:
                                project(i, e - 1)
                        project(i, ALL - 1)


def top_two_mixture(nc, S, name, ins):
    E, HID, TOP = 8, 512, 2
    HC = HID // P
    G = 4
    with phase(nc, name) as ph:
        wr = ph.sb("wr", [P, E])
        w1 = ph.sb("w1", [P, E, HID])
        w2 = ph.sb("w2", [P, E, HC, D])
        b1 = ph.sb("b1", [P, E, HC])
        b2 = ph.sb("b2", [E, D])
        xT = ph.sb("xT", [P, B, T])
        mix = ph.sb("mix", [P, B, E])
        prob = ph.sb("prob", [P, B, E])
        weights_loaded = ph.sem("weights_loaded")
        with nc.Block() as block:
            @block.sync
            def _(sp):
                sp.dma_start(w1[:, :, :], ins["L3_w1T"].rearrange("e d h -> d e h")).then_inc(weights_loaded, 16)
                sp.dma_start(w2[:, :, :, :], ins["L3_w2T"].rearrange("e (c p) d -> p e c d", p=P)).then_inc(weights_loaded, 16)
                sp.dma_start(b1[:, :, :], ins["L3_b1T"]).then_inc(weights_loaded, 16)
                sp.dma_start(b2[:, :], ins["L3_ffn_b2"]).then_inc(weights_loaded, 16)
        normed_rows_and_logits(nc, S, ph, name + "_n", E, wr, ins["L3_gate_wT"], xT, prob)

        with phase(nc, name + "_r") as pr:
            lanes = range(LANES)
            above, ties = pr.sb("above", [P, B, E, E]), pr.sb("ties", [P, B, E, E])
            sel, top, total = pr.sb("sel", [P, B, E]), pr.sb("top", [P, B]), pr.sb("total", [P, B])
            m1 = [pr.sb(f"m1{l}", [P, E]) for l in lanes]
            mT = [pr.sb(f"mT{l}", [E, T]) for l in lanes]
            ps = [pr.ps(f"ps{k}", [P, 512]) for k in range(4)]
            dve_step, shift_done, exp_done, m_ready, m_turned, mT_ready, bias_ready = (
                pr.sem(n) for n in ("dve_step", "shift_done", "exp_done", "m_ready", "m_turned", "mT_ready", "bias_ready"))
            with nc.Block() as block:
                @block.scalar
                def _(a):
                    a.wait_ge(shift_done, 1)
                    a.activation(prob[:, :, :], prob[:, :, :], ACT.Exp).then_inc(exp_done, 1)

                @block.vector
                def _(v):
                    step = Steps(v, dve_step)
                    row = lambda x: x[:, :].unsqueeze(2).broadcast_to([P, B, E])
                    step(v.tensor_reduce(top[:, :], prob[:, :, :], AX.X, ALU.max))
                    v.tensor_tensor(prob[:, :, :], prob[:, :, :], row(top), ALU.subtract).then_inc(shift_done, 1)
                    v.wait_ge(exp_done, 1)
                    step(v.tensor_reduce(total[:, :], prob[:, :, :], AX.X, ALU.add))
                    step(v.reciprocal(total[:, :], total[:, :]))
                    step(v.tensor_tensor(prob[:, :, :], prob[:, :, :], row(total), ALU.mult))
                    chosen(v, step, S, prob[:, :, :], E, TOP, above[:, :, :, :], ties[:, :, :, :], sel[:, :, :])
                    step(v.tensor_tensor(prob[:, :, :], prob[:, :, :], sel[:, :, :], ALU.mult))
                    step(v.tensor_reduce(total[:, :], prob[:, :, :], AX.X, ALU.add))
                    step(v.reciprocal(total[:, :], total[:, :]))
                    step(v.tensor_tensor(mix[:, :, :], prob[:, :, :], row(total), ALU.mult))
                    with v.Fori(0, B // LANES) as i:
                        step.restart()
                        for l in lanes:
                            v.tensor_copy(m1[l][:, :], mix[:, i * LANES + l, :]).then_inc(m_ready, 1)
                        for l in lanes:
                            v.wait_ge(m_turned, i * LANES + l + 1)
                            v.tensor_copy(mT[l][:, :], ps[l][0:E, 0:T]).then_inc(mT_ready, 1)
                        for l in lanes:
                            v.wait_ge(bias_ready, i * LANES + l + 1)
                            step(v.tensor_tensor(S.x[:, i * LANES + l, :], S.x[:, i * LANES + l, :], ps[2 + l][:, 0:D], ALU.add))

                @block.tensor
                def _(t):
                    t.wait_ge(weights_loaded, 64)
                    with t.Fori(0, B // LANES) as i:
                        for l in lanes:
                            t.wait_ge(m_ready, i * LANES + l + 1)
                            t.transpose(ps[l][0:E, 0:T], m1[l][:, :], S.ident).then_inc(m_turned, 1)
                        for l in lanes:
                            t.wait_ge(mT_ready, i * LANES + l + 1)
                            t.matmul(ps[2 + l][:, 0:D], mT[l][:, :], b2[:, :], start=True, stop=True).then_inc(bias_ready, 1)

        with phase(nc, name + "_e") as pe:
            act = [pe.sb(f"act{k}", [P, HC, G * T]) for k in range(2)]
            ps_h = [pe.ps(f"ps_h{k}", [P, G * T]) for k in range(4)]
            ps_y = [pe.ps(f"ps_y{k}", [P, G, D]) for k in range(2)]
            h_ready, act_ready, y_ready, y_added = (pe.sem(n) for n in ("h_ready", "act_ready", "y_ready", "y_added"))
            with nc.Block() as block:
                @block.vector
                def _(v):
                    v.sem_inc(y_added, 1)
                    with v.Fori(0, B // G) as i:
                        for e in range(E):
                            v.wait_ge(y_ready, 1 + i * E + e + 1)
                            if e:
                                v.wait_ge(y_added, 1 + i * E + e)
                            for k in range(G):
                                x = S.x[:, i * G + k, :]
                                ins_ = v.scalar_tensor_tensor(out=x, in0=ps_y[e % 2][:, k, :], scalar=mix[:, i * G + k, e:e + 1],
                                                              in1=x, op0=ALU.mult, op1=ALU.add)
                            ins_.then_inc(y_added, 1)

                @block.scalar
                def _(a):
                    a.sem_inc(act_ready, 1)
                    with a.Fori(0, B // G) as i:
                        for e in range(E):
                            a.wait_ge(y_ready, 1 + i * E + e - 1) if e >= 2 else a.wait_ge(y_ready, 1 + i * E)
                            for c in range(HC):
                                a.wait_ge(h_ready, (i * E + e) * HC + c + 1)
                                a.activation(act[e % 2][:, c, :], ps_h[c][:, :], ACT.Relu, bias=b1[:, e, c:c + 1]).then_inc(act_ready, 1)

                @block.tensor
                def _(t):
                    t.sem_inc(y_ready, 1)
                    def project(i, e):
                        t.wait_ge(act_ready, 1 + (i * E + e + 1) * HC)
                        t.wait_ge(y_added, 1 + i * E + e - 1) if e >= 2 else t.wait_ge(y_added, 1 + i * E)
                        for k in range(G):
                            for c in range(HC):
                                mm = t.matmul(ps_y[e % 2][:, k, :], act[e % 2][:, c, k * T:(k + 1) * T], w2[:, e, c, :],
                                              start=(c == 0), stop=(c == HC - 1))
                        mm.then_inc(y_ready, 1)

                    with t.Fori(0, B // G) as i:
                        rows = xT[:, bass.ds(i * G, G), :].rearrange("p b t -> p (b t)")
                        for e in range(E):
                            for c in range(HC):
                                t.wait_ge(act_ready, 1 + (i * E + e - 1) * HC + c + 1) if e else t.wait_ge(act_ready, 1 + i * E * HC)
                                t.matmul(ps_h[c][:, :], w1[:, e, c * P:(c + 1) * P], rows, start=True, stop=True).then_inc(h_ready, 1)
                            if e:
                                project(i, e - 1)
                        project(i, E - 1)


def projected_attention(nc, S, name, ins):
    with phase(nc, name + "_w") as ph:
        wqkvT = ph.sb("wqkvT", [P, 3 * D])
        wprojT = ph.sb("wprojT", [P, D])
        b_proj = ph.sb("b_proj", [P, D])
        loaded = ph.sem("loaded")
        with nc.Block() as block:
            @block.sync
            def _(sp):
                sp.dma_start(wqkvT[:, :], ins["L3_w_qkvT"]).then_inc(loaded, 16)
                sp.dma_start(wprojT[:, :], ins["L3_w_projT"]).then_inc(loaded, 16)
                sp.dma_start(b_proj[:, :], ins["L3_xattn_b_proj"].partition_broadcast(P)).then_inc(loaded, 16)
                sp.wait_ge(loaded, 48)
        small_head_attention(nc, S, name, True, weights={
            "wqT": wqkvT[:, 0:D], "wkT": wqkvT[:, D:2 * D], "wvT": wqkvT[:, 2 * D:3 * D],
            "wprojT": wprojT[:, :], "b_proj": b_proj[:, :]})


def build(nc, ins, out):
    at, width = constant_offsets()
    with ExitStack() as ctx:
        def sb(name, shape, dt=F32):
            return ctx.enter_context(nc.sbuf_tensor(name, shape, dt))
        S = Shared()
        S.x = sb("x", [P, B, D])
        S.ctx = sb("ctx", [P, B, CTX])
        S.ctxT = sb("ctxT", [P, 2, B, P])
        S.stats = sb("stats", [P, B, 6])
        S.mean, S.dif, S.var, S.rstd, S.mhalf = (sb(n, [P, B]) for n in ("mean", "dif", "var", "rstd", "mhalf"))
        consts = sb("consts", [P, width])

        def const(name):
            return consts[:, at[name][0]:at[name][1]]
        S.ident, S.iota_row, S.iota_col, S.upto, S.ones = (const(n) for n in ("ident", "iota_row", "iota_col", "upto", "ones"))
        S.headmask, S.cos, S.sin, S.sameexpert = (const(n) for n in ("headmask", "cos", "sin", "sameexpert"))
        S.expertmask, S.decay, S.before16, S.pairhead = (const(n) for n in ("expertmask", "decay", "before16", "pairhead"))
        S.iota256 = consts[:, at["iota_row"][0]:at["iota_row2"][1]]
        load_inputs(nc, S, ins, consts)
        all_stages(nc, S, ins)
        with phase(nc, "store") as ph:
            stored = ph.sem("stored")
            with nc.Block() as block:
                @block.sync
                def _(sp):
                    sp.dma_start(out.rearrange("b t d -> t b d"), S.x[:, :, :]).then_inc(stored, 16)
                    sp.wait_ge(stored, 16)


def load_inputs(nc, S, ins, consts):
    with phase(nc, "load") as ph:
        x_loaded, rest_loaded, step_sem, half_set = (ph.sem(n) for n in ("x_loaded", "rest_loaded", "dve_step", "half_set"))
        with nc.Block() as block:
            @block.sync
            def _(sp):
                sp.dma_start(S.x[:, :, :], ins["x"].rearrange("b t d -> t b d")).then_inc(x_loaded, 16)
                sp.dma_start(consts[:, :], ins["consts"]).then_inc(rest_loaded, 16)
                sp.dma_start(S.ctxT[:, :, :, :], ins["ctxT"].rearrange("s p b k -> p s b k")).then_inc(rest_loaded, 16)
                sp.dma_start(S.ctx[:, :, :], ins["ctx"].rearrange("b t d -> t b d")).then_inc(rest_loaded, 16)
                sp.wait_ge(rest_loaded, 48)

            @block.vector
            def _(v):
                v.memset(S.mhalf[:, :], -0.5).then_inc(half_set, 1)
                v.wait_ge(x_loaded, 16)
                v.wait_ge(half_set, 1)
                step = Steps(v, step_sem)
                with v.Fori(0, B) as b:
                    step.restart()
                    step(v.bn_stats(S.stats[:, b, :], S.x[:, b, :]))


def all_stages(nc, S, ins):
    stages = [
        lambda: small_head_attention(nc, S, "L0x", False, seq_len=ins["seq_len"], bias=ins["L0_xattn_b"]),
        lambda: expert_choice_attention(nc, S, "L0f", ins),
        lambda: patch_depool(nc, S, "L1x", ins),
        lambda: routed_trees(nc, S, "L1f", ins),
        lambda: wide_head_attention(nc, S, "L2x", ins),
        lambda: grouped_mixture(nc, S, "L2f", ins),
        lambda: projected_attention(nc, S, "L3x", ins),
        lambda: top_two_mixture(nc, S, "L3f", ins),
    ]
    for stage in stages:
        stage()


def lay_out(inputs):
    c = np.ascontiguousarray
    g = {k: np.asarray(v) for k, v in inputs.items()}
    f = {}
    f["x"] = c(g["x"])
    f["ctx"] = c(g["ctx_2048"])
    f["ctxT"] = c(g["ctx_2048"].transpose(2, 0, 1).reshape(2, P, B, T))
    f["seq_len"] = c(g["itok_Bx1_68_817"].reshape(B))
    f["L0_xattn_b"] = c(g["L0_xattn_b"])
    f["L0_ffn_WrT"] = c(g["L0_ffn_Wr"].T)
    f["L0_ffn_Wqkv"] = c(g["L0_ffn_Wqkv"])
    half = np.r_[ROPE_HALF:ROPE_N, 0:ROPE_HALF]
    f["L0_ffn_Wswap"] = c(np.stack([g["L0_ffn_Wqkv"][:, :, half], g["L0_ffn_Wqkv"][:, :, D + half]], 2))
    f["L0_ffn_Wo"] = c(g["L0_ffn_Wo"])
    f["L1_W_inT"] = c(g["L1_xattn_W_in"].T)
    for n in ("L1_xattn_b_in", "L1_xattn_g_res", "L1_xattn_g_init"):
        f[n] = c(g[n])
    f["patch_lensT"] = c(g["mask_BxS2_if0"].T)
    f["L1_ffn_nw3"] = c(np.concatenate([g[f"L1_ffn_{n}_nw"] for n in "qkv"]).T)
    f["L1_ffn_nb3"] = c(np.concatenate([g[f"L1_ffn_{n}_nb"] for n in "qkv"]))
    f["L1_ffn_nwf"] = c(g["L1_ffn_f_nw"].T)
    f["L1_ffn_nbf"] = c(g["L1_ffn_f_nb"])
    f["leaf_table"] = c(np.concatenate([np.concatenate([
        g[f"L1_ffn_{n}_w1"].transpose(0, 2, 1).reshape(LEAVES, LW * D), g[f"L1_ffn_{n}_b1"],
        g[f"L1_ffn_{n}_w2"].reshape(LEAVES, LW * D), g[f"L1_ffn_{n}_b2"]], 1) for n in "qkvf"]))
    for n in ("L2_xattn_Wq", "L2_xattn_Wkv", "L2_xattn_Wout", "L2_xattn_ln_scale", "L2_xattn_ln_bias",
              "L2_ffn_bias", "L2_ffn_gate_w", "L2_ffn_up_w", "L2_ffn_down_w", "L2_ffn_sh_gate_w", "L2_ffn_sh_up_w",
              "L2_ffn_sh_down_w", "L3_xattn_b_proj", "L3_ffn_b2"):
        f[n] = c(g[n])
    f["L2_null_key"] = c(g["L2_xattn_null_kv"][0])
    f["L2_null_values"] = c(np.concatenate([g["L2_xattn_null_kv"][1]] * 2)[:, None])
    f["L2_router_wT"] = c(g["L2_ffn_router_w"].T)
    f["L3_w_qkvT"] = c(g["L3_xattn_w_qkv"].T)
    f["L3_w_projT"] = c(g["L3_xattn_w_proj"].T)
    f["L3_gate_wT"] = c(g["L3_ffn_gate_w"].T)
    f["L3_w1T"] = c(g["L3_ffn_w1"].transpose(0, 2, 1))
    f["L3_w2T"] = c(g["L3_ffn_w2"].transpose(0, 2, 1))
    f["L3_b1T"] = c(g["L3_ffn_b1"].reshape(8, 4, P).transpose(2, 0, 1))
    f["consts"] = c(np.concatenate([np.asarray(a, np.float32) for a in constant_columns().values()], 1))
    return f


def kernel(**inputs):
    import concourse.bacc as bacc
    from concourse.bass_utils import run_bass_kernel_spmd

    nc = bacc.Bacc("TRN2", target_bir_lowering=False, num_devices=1)
    arrays, ins = {}, {}
    for name, a in lay_out(inputs).items():
        arrays[f"in_{name}"] = a
        ins[name] = nc.dram_tensor(f"in_{name}", a.shape, mybir.dt.from_np(a.dtype), kind="ExternalInput").ap()
    out = nc.dram_tensor("out_0", (B, T, D), F32, kind="ExternalOutput").ap()
    build(nc, ins, out)
    r = run_bass_kernel_spmd(nc, [arrays], core_ids=[0])
    return r.results[0]["out_0"]
```

```python
from contextlib import ExitStack, contextmanager

import numpy as np

import concourse.bass as bass
from concourse import mybir

F32 = mybir.dt.float32
I32 = mybir.dt.int32
U32 = mybir.dt.uint32
ALU = mybir.AluOpType
ACT = mybir.ActivationFunctionType
AX = mybir.AxisListType

P = 128
B = 16
T = 128
D = 128
CTX = 256
LANES = 2
LN_EPS = 1e-5
NEG = -1e30

ROPE_HALF, ROPE_N, ROPE_BASE = 32, 64, 10000.0
E0, K0 = 8, 16
NODES, LEAVES, LW = 255, 256, 16
LOGP = -0.001


def constant_columns():
    p = np.arange(P)[:, None]
    c = np.arange(P)[None, :]
    f = np.float32
    inv = (1.0 / np.power(f(ROPE_BASE), np.arange(ROPE_HALF, dtype=f) * f(2.0) / f(ROPE_N))).astype(f)
    ang = (np.arange(T, dtype=f)[:, None] * inv).astype(f)
    sin, cos = np.sin(ang), np.cos(ang)
    dt = -np.log(-np.expm1(LOGP))
    power = np.maximum(c - p, 0)
    return {
        "ident": (p == c),
        "iota_row": np.broadcast_to(c, (P, P)),
        "iota_row2": np.broadcast_to(c + P, (P, P)),
        "iota_col": p,
        "upto": (p <= c),
        "ones": np.ones((P, P)),
        "headmask": (p // 8 == np.arange(16)[None, :]),
        "cos": np.concatenate([cos, cos], 1),
        "sin": np.concatenate([-sin, sin], 1),
        "sameexpert": (p // K0 == c // K0),
        "expertmask": (p // K0 == np.arange(E0)[None, :]),
        "decay": np.where(c >= p, np.exp(-dt * power), 0.0),
        "pairhead": (np.arange(16)[None, None, :] == 2 * np.arange(8)[None, :, None] + p[:, :, None] // 64).reshape(P, P),
    }


def constant_offsets():
    at, n = {}, 0
    for name, a in constant_columns().items():
        at[name] = (n, n + a.shape[1])
        n += a.shape[1]
    return at, n


class Phase:

    def __init__(self, nc, name):
        self.nc, self.name, self.ctx, self.sems = nc, name, ExitStack(), []

    def sb(self, name, shape, dt=F32):
        return self.ctx.enter_context(self.nc.sbuf_tensor(f"{self.name}_{name}", shape, dt))

    def ps(self, name, shape):
        return self.ctx.enter_context(self.nc.psum_tensor(f"{self.name}_{name}", shape, F32))

    def sem(self, name):
        s = self.nc.alloc_semaphore(f"{self.name}_{name}")
        self.sems.append(s)
        return s

    def close(self):
        self.nc.clear_and_free_semaphores(self.sems)
        self.nc.all_engine_barrier()
        self.ctx.close()


@contextmanager
def phase(nc, name):
    ph = Phase(nc, name)
    yield ph
    ph.close()


class Steps:

    def __init__(self, eng, sem):
        self.eng, self.sem, self.n = eng, sem, 0

    def __call__(self, ins):
        self.n += 1
        ins.then_inc(self.sem, 1)
        self.eng.wait_ge(self.sem, self.n)

    def restart(self):
        self.eng.sem_clear(self.sem)
        self.n = 0


class Shared:
    pass


def layer_norm_coefficients(v, step, S, stats_done, pow_ready):
    me, mo = S.stats[:, :, 1], S.stats[:, :, 4]
    ve, vo = S.stats[:, :, 2], S.stats[:, :, 5]
    step(v.tensor_tensor(S.mean[:, :], me, mo, ALU.add))
    step(v.tensor_tensor(S.dif[:, :], me, mo, ALU.subtract))
    step(v.tensor_scalar(S.mean[:, :], S.mean[:, :], 0.5, None, ALU.mult))
    step(v.tensor_tensor(S.var[:, :], ve, vo, ALU.add))
    step(v.scalar_tensor_tensor(out=S.dif[:, :], in0=S.dif[:, :], scalar=0.25, in1=S.dif[:, :],
                                op0=ALU.mult, op1=ALU.mult))
    step(v.scalar_tensor_tensor(out=S.var[:, :], in0=S.var[:, :], scalar=1.0 / D, in1=S.dif[:, :],
                                op0=ALU.mult, op1=ALU.add))
    v.tensor_scalar(S.var[:, :], S.var[:, :], LN_EPS, None, ALU.add).then_inc(stats_done, 1)


def inverse_roots(g, S, stats_done, pow_ready):
    g.wait_ge(stats_done, 1)
    g.tensor_tensor(S.rstd[:, :], S.var[:, :], S.mhalf[:, :], ALU.pow).then_inc(pow_ready, 1)


def skewed(eng, first, second, body_starts=None):
    def both(j, l, j_before):
        for new, old in zip(first, second):
            new(j, l)
            old(j_before, 1 - l)

    for new in first:
        new(0, 0)
    with eng.Fori(0, B // LANES - 1) as i:
        if body_starts:
            body_starts()
        both(i, 1, i)
        both(i + 1, 0, i)
    if body_starts:
        body_starts()
    both(B // LANES - 1, 1, B // LANES - 1)
    for old in second:
        old(B // LANES - 1, 1)


def normalized(v, step, S, xn_all, pow_ready, normed, parts):
    shape = [P, B // parts, D]
    for n in range(parts):
        part = slice(n * B // parts, (n + 1) * B // parts)
        ins = v.tensor_tensor(xn_all[:, part, :], S.x[:, part, :], S.mean[:, part].unsqueeze(2).broadcast_to(shape), ALU.subtract)
    step(ins)
    v.wait_ge(pow_ready, 1)
    for n in range(parts):
        part = slice(n * B // parts, (n + 1) * B // parts)
        v.tensor_tensor(xn_all[:, part, :], xn_all[:, part, :], S.rstd[:, part].unsqueeze(2).broadcast_to(shape),
                        ALU.mult).then_inc(normed, 1)


def all_statistics(v, step, S):
    for b in range(B):
        ins = v.bn_stats(S.stats[:, b, :], S.x[:, b, :])
    step(ins)


def nothing(j, l):
    pass


def small_head_attention(nc, S, name, own_keys, seq_len=None, bias=None, weights=None, context=None, contextT=None):
    HEADS, DH = 16, 8
    SETS = 2 if own_keys else 1
    HPC = 512 // (SETS * P)
    CHUNKS = HEADS // HPC
    with phase(nc, name) as ph:
        lanes = range(LANES)
        xn_all = ph.sb("xn_all", [P, B, D])
        xn = [ph.sb(f"xn{l}", [P, D]) for l in lanes]
        xnT = [ph.sb(f"xnT{l}", [P, T]) for l in lanes]
        qT = [ph.sb(f"qT{l}", [P, T]) for l in lanes]
        qmask = [ph.sb(f"qmask{l}", [P, HEADS, T]) for l in lanes]
        keys = [ph.sb(f"keys{l}", [P, SETS, P]) for l in lanes]
        probs = [ph.sb(f"probs{l}", [P, HEADS, SETS, P]) for l in lanes]
        probsT = [ph.sb(f"probsT{l}", [P, HEADS, SETS, P]) for l in lanes]
        vals = [ph.sb(f"vals{l}", [P, SETS, HEADS, DH + 1]) for l in lanes]
        mx = [ph.sb(f"mx{l}", [P, HEADS]) for l in lanes]
        rs = [ph.sb(f"rs{l}", [P, HEADS]) for l in lanes]
        osb = [ph.sb(f"osb{l}", [P, HEADS, DH]) for l in lanes]
        psA = [ph.ps(f"psA{l}", [P, 1024]) for l in lanes]
        psB = [ph.ps(f"psB{l}", [P, 512]) for l in lanes]
        psO = [ph.ps(f"psO{l}", [P, 512]) for l in lanes]

        dve_step = ph.sem("dve_step")
        stats_done, pow_ready, vals_ready, normed = (ph.sem(n) for n in ("stats_done", "pow_ready", "vals_ready", "normed"))
        (xn_ready, xnT_ready, q_ready, keys_ready, scores_ready, shifted, exp_ready, turned, probsT_ready, out_ready) = (
            [ph.sem(f"{n}{l}") for l in lanes] for n in (
                "xn_ready", "xnT_ready", "q_ready", "keys_ready", "scores_ready", "shifted", "exp_ready", "turned",
                "probsT_ready", "out_ready"))
        if own_keys:
            bank_free = shifted
            xnT_sb_ready, qkv_ready, o_sb_ready, oT_ready, oT_sb_ready, proj_ready = (
                [ph.sem(f"{n}{l}") for l in lanes] for n in (
                    "xnT_sb_ready", "qkv_ready", "o_sb_ready", "oT_ready", "oT_sb_ready", "proj_ready"))
            oT = [ph.sb(f"oT{l}", [P, P]) for l in lanes]
            res = [ph.sb(f"res{l}", [P, D]) for l in lanes]
        else:
            len_i = ph.sb("len_i", [P, B], I32)
            len_f = ph.sb("len_f", [P, B])
            bias_row = ph.sb("bias_row", [P, P])
            bias_row_b = [ph.sb(f"bias_row_b{l}", [P, P]) for l in lanes]
            bank_free = [ph.sem(f"bank_free{l}") for l in lanes]
            len_loaded, half_loaded, context_loaded = (ph.sem(n) for n in ("len_loaded", "half_loaded", "context_loaded"))

        def bank(c):
            return slice(c % 2 * 512, c % 2 * 512 + 512)

        with nc.Block() as block:
            if not own_keys:
                @block.sync
                def _(sp):
                    sp.dma_start(len_i[:, :], seq_len.partition_broadcast(P)).then_inc(len_loaded, 16)
                    sp.dma_start(bias_row[:, :], bias.partition_broadcast(P)).then_inc(len_loaded, 16)
                    sp.dma_start(S.ctxT[:, 0, :, :], contextT[0]).then_inc(half_loaded, 16)
                    sp.dma_start(S.ctx[:, :, P:CTX], context[:, :, P:CTX].rearrange("b t d -> t b d")).then_inc(half_loaded, 16)
                    sp.dma_start(S.ctx[:, :, 0:P], context[:, :, 0:P].rearrange("b t d -> t b d")).then_inc(context_loaded, 16)
                    sp.dma_start(S.ctxT[:, 1, :, :], contextT[1]).then_inc(context_loaded, 16)
                    sp.wait_ge(context_loaded, 32)

            @block.gpsimd
            def _(g):
                for l in lanes:
                    g.memset(vals[l][:, :, :, :], 1.0).then_inc(vals_ready, 1)
                inverse_roots(g, S, stats_done, pow_ready)

                def rows(j, l):
                    g.wait_ge(xnT_ready[l], 1 + j)
                    g.tensor_copy(xn[l][:, :], xn_all[:, j * LANES + l, :]).then_inc(xn_ready[l], 1)

                def next_rows(j, l):
                    if not isinstance(j, int):
                        rows(j + 1, l)

                def keys_and_queries(j, l):
                    g.wait_ge(scores_ready[l], 1 + j * CHUNKS)
                    g.tensor_copy(keys[l][:, 0, :], S.ctxT[:, 0, j * LANES + l, :])
                    g.wait_ge(q_ready[l], j + 1)
                    for h in range(0, HEADS, 4):
                        g.tensor_tensor(qmask[l][:, h:h + 4, :], qT[l][:, :].unsqueeze(1).broadcast_to([P, 4, T]),
                                        S.headmask[:, h:h + 4].unsqueeze(2).broadcast_to([P, 4, T]),
                                        ALU.mult).then_inc(keys_ready[l], 1)
                g.wait_ge(normed, 1)
                for l in lanes:
                    rows(0, l)
                g.wait_ge(normed, 4)
                if not own_keys:
                    g.wait_ge(half_loaded, 32)
                skewed(g, [keys_and_queries], [next_rows])

            @block.vector
            def _(v):
                step = Steps(v, dve_step)
                layer_norm_coefficients(v, step, S, stats_done, pow_ready)
                if not own_keys:
                    v.wait_ge(len_loaded, 32)
                    step(v.tensor_copy(len_f[:, :], len_i[:, :]))

                normalized(v, step, S, xn_all, pow_ready, normed, 4)

                def bias_added(j, l):
                    b = j * LANES + l
                    if not own_keys:
                        step(v.tensor_scalar(bias_row_b[l][:, :], S.iota_row, len_f[:, bass.ds(b, 1)], -1e12,
                                             ALU.is_ge, ALU.mult))
                        step(v.tensor_tensor(bias_row_b[l][:, :], bias_row_b[l][:, :], bias_row[:, :], ALU.add))

                def shift(c):
                    def stage(j, l):
                        heads = slice(c * HPC, (c + 1) * HPC)
                        pr = probs[l][:, heads, :, :]
                        ps = psA[l][:, bank(c)].rearrange("p (j s k) -> p j s k", s=SETS, j=HPC)
                        v.wait_ge(scores_ready[l], 1 + j * CHUNKS + c + 1)
                        if own_keys:
                            step(v.tensor_reduce(mx[l][:, heads], ps, AX.XY, ALU.max))
                            v.tensor_tensor(pr, ps, mx[l][:, heads].unsqueeze(2).unsqueeze(3)
                                            .broadcast_to([P, HPC, SETS, P]), ALU.subtract).then_inc(shifted[l], 1)
                        else:
                            step(v.tensor_tensor(pr[:, :, 0, :], ps[:, :, 0, :],
                                                 bias_row_b[l][:, :].unsqueeze(1).broadcast_to([P, HPC, P]), ALU.add))
                            v.sem_inc(bank_free[l], 1)
                            step(v.tensor_reduce(mx[l][:, heads], pr, AX.XY, ALU.max))
                            v.tensor_scalar(mx[l][:, heads], mx[l][:, heads], -1.0, None, ALU.mult).then_inc(shifted[l], 1)
                    return stage

                def divided(j, l):
                    b = j * LANES + l
                    ov = psO[l][:, 0:HEADS * (DH + 1)].rearrange("p (h d) -> p h d", d=DH + 1)
                    v.wait_ge(out_ready[l], 1 + j + 1)
                    step(v.reciprocal(rs[l][:, :], ov[:, :, DH]))
                    ins = v.tensor_tensor(osb[l][:, :, :], ov[:, :, 0:DH],
                                          rs[l][:, :].unsqueeze(2).broadcast_to([P, HEADS, DH]), ALU.mult)
                    if own_keys:
                        ins.then_inc(o_sb_ready[l], 1)
                    else:
                        step(ins)
                        step(v.tensor_tensor(S.x[:, b, :], S.x[:, b, :],
                                             osb[l][:, :, :].rearrange("p h d -> p (h d)"), ALU.add))
                        v.bn_stats(S.stats[:, b, :], S.x[:, b, :])

                def added(j, l):
                    b = j * LANES + l
                    v.wait_ge(proj_ready[l], j + 1)
                    step(v.tensor_tensor(res[l][:, :], psO[l][:, 0:D], weights["b_proj"], ALU.add))
                    step(v.tensor_tensor(S.x[:, b, :], S.x[:, b, :], res[l][:, :], ALU.add))
                    v.bn_stats(S.stats[:, b, :], S.x[:, b, :])

                if own_keys:
                    skewed(v, [nothing] * 3 + [shift(c) for c in range(5)],
                           [shift(c) for c in range(5, 8)] + [nothing] * 2 + [divided, nothing, added], step.restart)
                else:
                    skewed(v, [nothing, bias_added] + [shift(c) for c in range(3)],
                           [shift(3), nothing, nothing, nothing, divided], step.restart)

            @block.scalar
            def _(a):
                a.wait_ge(vals_ready, 2)
                if not own_keys:
                    a.wait_ge(half_loaded, 32)

                def turned_x(j, l):
                    b = j * LANES + l
                    a.wait_ge(out_ready[l], 1 + j)
                    a.activation(vals[l][:, 0, :, 0:DH],
                                 S.ctx[:, bass.ds(b, 1), P:2 * P].rearrange("p o (h d) -> p (o h) d", d=DH), ACT.Copy)
                    a.wait_ge(xnT_ready[l], 1 + j + 1)
                    if not own_keys:
                        a.activation(qT[l][:, :], psB[l][:, 0:T], ACT.Copy, scale=DH ** -0.5).then_inc(q_ready[l], 1)
                    else:
                        a.activation(xnT[l][:, :], psB[l][:, 0:T], ACT.Copy).then_inc(xnT_sb_ready[l], 1)

                def qkv(j, l):
                    a.wait_ge(qkv_ready[l], j + 1)
                    a.activation(keys[l][:, 1, :], psA[l][:, T:2 * T], ACT.Copy)
                    a.activation(qT[l][:, :], psA[l][:, 0:T], ACT.Copy, scale=DH ** -0.5)
                    a.activation(vals[l][:, 1, :, 0:DH],
                                 psA[l][:, 2 * T:3 * T].rearrange("p (h d) -> p h d", d=DH), ACT.Copy).then_inc(q_ready[l], 1)

                def exp_and_turned(c):
                    def stage(j, l):
                        if 2 <= c <= CHUNKS + 1:
                            a.wait_ge(turned[l], j * CHUNKS + c - 1)
                            a.activation(probsT[l][:, (c - 2) * HPC:(c - 1) * HPC, :, :].rearrange("p j s k -> p (j s k)"),
                                         psB[l][:, :], ACT.Copy).then_inc(probsT_ready[l], 1)
                        if c < CHUNKS:
                            pr = probs[l][:, c * HPC:(c + 1) * HPC, :, :]
                            a.wait_ge(shifted[l], j * CHUNKS + c + 1)
                            if own_keys:
                                a.activation(pr, pr, ACT.Exp).then_inc(exp_ready[l], 1)
                            else:
                                for h in range(c * HPC, (c + 1) * HPC):
                                    row = probs[l][:, h, 0, :]
                                    ins = a.activation(row, row, ACT.Exp, bias=mx[l][:, h:h + 1])
                                ins.then_inc(exp_ready[l], 1)
                    return stage

                def turned_o(j, l):
                    a.wait_ge(oT_ready[l], j + 1)
                    a.activation(oT[l][:, :], psB[l][:, 0:T], ACT.Copy).then_inc(oT_sb_ready[l], 1)

                if own_keys:
                    skewed(a, [turned_x, qkv, nothing] + [exp_and_turned(c) for c in range(5)],
                           [exp_and_turned(c) for c in range(5, 10)] + [nothing, turned_o, nothing])
                else:
                    skewed(a, [turned_x, nothing] + [exp_and_turned(c) for c in range(3)],
                           [exp_and_turned(c) for c in range(3, 6)] + [nothing, nothing])

            @block.tensor
            def _(t):
                for l in lanes:
                    t.sem_inc(xnT_ready[l], 1)
                    t.sem_inc(out_ready[l], 1)
                    t.sem_inc(scores_ready[l], 1)

                def turn_x(j, l):
                    t.wait_ge(xn_ready[l], j + 1)
                    t.transpose(psB[l][:, 0:T], xn[l][:, :], S.ident).then_inc(xnT_ready[l], 1)

                def qkv(j, l):
                    t.wait_ge(xnT_sb_ready[l], j + 1)
                    t.matmul(psA[l][:, 0:T], weights["wqT"], xnT[l][:, :], start=True, stop=True)
                    t.matmul(psA[l][:, T:2 * T], weights["wkT"], xnT[l][:, :], start=True, stop=True)
                    t.matmul(psA[l][:, 2 * T:3 * T], xnT[l][:, :], weights["wvT"], start=True,
                             stop=True).then_inc(qkv_ready[l], 1)

                def chunk(c):
                    def stage(j, l):
                        if c < CHUNKS:
                            t.wait_ge(keys_ready[l], j * 4 + c * HPC // 4 + 1)
                            if c > 1:
                                t.wait_ge(bank_free[l], j * CHUNKS + c - 1)
                            for k in range(HPC):
                                mm = t.matmul(psA[l][:, bank(c)].rearrange("p (j n) -> p j n", j=HPC)[:, k, :],
                                              qmask[l][:, c * HPC + k, :], keys[l][:, :, :].rearrange("p s k -> p (s k)"),
                                              start=True, stop=True)
                            mm.then_inc(scores_ready[l], 1)
                        if 2 <= c <= CHUNKS + 1:
                            t.wait_ge(exp_ready[l], j * CHUNKS + c - 1)
                            if c > 2:
                                t.wait_ge(probsT_ready[l], j * CHUNKS + c - 2)
                            for n in range(4):
                                h, s = (c - 2) * HPC + n // SETS, n % SETS
                                mm = t.transpose(psB[l][:, n * P:(n + 1) * P], probs[l][:, h, s, :], S.ident)
                            mm.then_inc(turned[l], 1)
                        if c >= 3:
                            if c == CHUNKS + 2:
                                t.wait_ge(probsT_ready[l], j * CHUNKS + CHUNKS)
                            for h in range((c - 3) * HPC, (c - 2) * HPC):
                                for s in range(SETS):
                                    mm = t.matmul(psO[l][:, h * (DH + 1):(h + 1) * (DH + 1)], probsT[l][:, h, s, :],
                                                  vals[l][:, s, h, :], start=(s == 0), stop=(s == SETS - 1))
                            if c == CHUNKS + 2:
                                mm.then_inc(out_ready[l], 1)
                    return stage

                def turn_o(j, l):
                    t.wait_ge(o_sb_ready[l], j + 1)
                    t.transpose(psB[l][:, 0:T], osb[l][:, :, :].rearrange("p h d -> p (h d)"),
                                S.ident).then_inc(oT_ready[l], 1)

                def project(j, l):
                    t.wait_ge(oT_sb_ready[l], j + 1)
                    t.matmul(psO[l][:, 0:D], oT[l][:, :], weights["wprojT"], start=True,
                             stop=True).then_inc(proj_ready[l], 1)

                if own_keys:
                    skewed(t, [turn_x, qkv, nothing] + [chunk(c) for c in range(5)],
                           [chunk(c) for c in range(5, 11)] + [turn_o, project])
                else:
                    skewed(t, [turn_x, nothing] + [chunk(c) for c in range(3)], [chunk(c) for c in range(3, 7)] + [nothing])


def expert_choice_attention(nc, S, name, ins):
    W3 = 3 * D
    WIDE = 4
    G = B * E0 * K0
    with phase(nc, name) as ph:
        lanes = range(WIDE)
        wr = ph.sb("wr", [P, E0])
        wqkv = ph.sb("wqkv", [P, E0, W3])
        wswap = ph.sb("wswap", [P, E0, 2, ROPE_N])
        wo = ph.sb("wo", [P, E0, D])
        n1 = ph.sb("n1", [P, B, D])
        gates = ph.sb("gates", [P, B, 1 + E0])
        gatesT = ph.sb("gatesT", [P, T])
        left = ph.sb("left", [P, T])
        top = ph.sb("top", [P, K0])
        top_i = ph.sb("top_i", [P, K0], U32)
        top_f = ph.sb("top_f", [P, K0])
        spread = ph.sb("spread", [P, G])
        taken = ph.sb("taken", [P, G])
        pick = [ph.sb(f"pick{l}", [P, P]) for l in lanes]
        pickT = [ph.sb(f"pickT{l}", [P, P]) for l in lanes]
        xn = [ph.sb(f"xn{l}", [P, D]) for l in lanes]
        cols = ph.sb("cols", [P, B, 1 + E0])
        gathT = ph.sb("gathT", [P, E0, B, K0])
        cosg = ph.sb("cosg", [ROPE_N, E0, B, K0])
        sing = ph.sb("sing", [ROPE_N, E0, B, K0])
        QT = ph.sb("QT", [P, E0, B, K0])
        KT = ph.sb("KT", [P, E0, B, K0])
        VT = ph.sb("VT", [P, E0, B, K0])
        QS = ph.sb("QS", [ROPE_N, E0, B, K0])
        KS = ph.sb("KS", [ROPE_N, E0, B, K0])
        AVT = ph.sb("AVT", [P, E0, B, K0])
        OUTT = ph.sb("OUTT", [P, E0, B, K0])
        q1 = [ph.sb(f"q1{l}", [P, P]) for l in lanes]
        v1 = [ph.sb(f"v1{l}", [P, P]) for l in lanes]
        vv = [ph.sb(f"vv{l}", [P, P]) for l in lanes]
        sc = [ph.sb(f"sc{l}", [P, P]) for l in lanes]
        masks = ph.sb("masks", [P, B, P])
        own, own_gate = ph.sb("own", [P, B, E0]), ph.sb("own_gate", [P, B])
        pT = [ph.sb(f"pT{l}", [P, P]) for l in lanes]
        st = [ph.sb(f"st{l}", [P, 4]) for l in lanes]
        ps = [ph.ps(f"ps{n}", [P, 512]) for n in range(8)]

        dve_step = ph.sem("dve_step")
        stats_done, pow_ready, w_loaded = ph.sem("stats_done"), ph.sem("pow_ready"), ph.sem("w_loaded")
        xn_ready, xnT_ready, xnT_sb, logits_ready = (ph.sem(n) for n in ("xn_ready", "xnT_ready", "xnT_sb", "logits_ready"))
        logits_sb, gates_ready, gatesT_ready = ph.sem("logits_sb"), ph.sem("gates_ready"), ph.sem("gatesT_ready")
        spread_ready, taken_ready, normed = (ph.sem(n) for n in ("spread_ready", "taken_ready", "normed"))

        with nc.Block() as block:
            @block.sync
            def _(sp):
                sp.dma_start(wr[:, :], ins["L0_ffn_WrT"]).then_inc(w_loaded, 16)
                sp.dma_start(wqkv[:, :, :], ins["L0_ffn_Wqkv"].rearrange("e i j -> i e j")).then_inc(w_loaded, 16)
                sp.dma_start(wswap[:, :, :, :], ins["L0_ffn_Wswap"].rearrange("e i n j -> i e n j")).then_inc(w_loaded, 16)
                sp.dma_start(wo[:, :, :], ins["L0_ffn_Wo"].rearrange("e i j -> i e j")).then_inc(w_loaded, 16)

            @block.gpsimd
            def _(g):
                inverse_roots(g, S, stats_done, pow_ready)

            @block.vector
            def _(v):
                step = Steps(v, dve_step)
                layer_norm_coefficients(v, step, S, stats_done, pow_ready)
                step(v.tensor_copy(gates[:, :, 0], S.iota_col.broadcast_to([P, B])))
                normalized(v, step, S, n1, pow_ready, normed, 1)
                v.wait_ge(normed, 1)
                with v.Fori(0, B // WIDE) as i:
                    step.restart()
                    for l in lanes:
                        b = i * WIDE + l
                        v.tensor_copy(xn[l][:, :], n1[:, b, :]).then_inc(xn_ready, 1)
                    for l in lanes:
                        b = i * WIDE + l
                        v.wait_ge(xnT_ready, b + 1)
                        v.tensor_copy(pT[l][:, :], ps[2 * l][:, 0:T]).then_inc(xnT_sb, 1)
                    for l in lanes:
                        b = i * WIDE + l
                        v.wait_ge(logits_ready, b + 1)
                        v.tensor_copy(gates[:, b, 1:1 + E0], ps[2 * l + 1][:, 0:E0]).then_inc(logits_sb, 1)
                v.wait_ge(gates_ready, 1)
                gv = gates[:, :, 1:1 + E0]
                step(v.tensor_scalar(gv, gv, 1.0, None, ALU.add))
                step(v.reciprocal(gv, gv))
                v.tensor_copy(left[:, :].rearrange("p (b e) -> p b e", e=E0), gv).then_inc(gates_ready, 1)
                v.wait_ge(gatesT_ready, 1)
                step(v.tensor_copy(gatesT[:, :], ps[4][:, 0:T]))
                step(v.max(top[:, 0:8], gatesT[:, :]))
                step(v.max_index(out=top_i[:, 0:8], in_max=top[:, 0:8], in_values=gatesT[:, :]))
                step(v.match_replace(out=left[:, :], in_to_replace=top[:, 0:8], in_values=gatesT[:, :], imm_value=-1.0))
                step(v.max(top[:, 8:16], left[:, :]))
                step(v.max_index(out=top_i[:, 8:16], in_max=top[:, 8:16], in_values=left[:, :]))
                step(v.tensor_copy(top_f[:, :], top_i[:, :]))
                v.tensor_tensor(spread[:, :].rearrange("p (c k) -> p c k", k=K0),
                                top_f[:, :].unsqueeze(1).broadcast_to([P, P, K0]),
                                S.ident.unsqueeze(2).broadcast_to([P, P, K0]), ALU.mult).then_inc(spread_ready, 1)
                for n in range(4):
                    v.wait_ge(taken_ready, n + 1)
                    step(v.tensor_copy(taken[:, n * 512:(n + 1) * 512], ps[4 + n][:, :]))

            @block.scalar
            def _(a):
                a.wait_ge(logits_sb, B)
                gv = gates[:, :, 1:1 + E0]
                a.activation(gv, gv, ACT.Exp, scale=-1.0).then_inc(gates_ready, 1)

            @block.tensor
            def _(t):
                t.wait_ge(w_loaded, 64)
                with t.Fori(0, B // WIDE) as i:
                    for l in lanes:
                        t.wait_ge(xn_ready, i * WIDE + l + 1)
                        t.transpose(ps[2 * l][:, 0:T], xn[l][:, :], S.ident).then_inc(xnT_ready, 1)
                    for l in lanes:
                        t.wait_ge(xnT_sb, i * WIDE + l + 1)
                        t.matmul(ps[2 * l + 1][:, 0:E0], pT[l][:, :], wr[:, :], start=True, stop=True).then_inc(logits_ready, 1)
                t.wait_ge(gates_ready, 2)
                t.transpose(ps[4][:, 0:T], left[:, :], S.ident).then_inc(gatesT_ready, 1)
                t.wait_ge(spread_ready, 1)
                for n in range(4):
                    t.matmul(ps[4 + n][:, :], S.ones, spread[:, n * 512:(n + 1) * 512], start=True,
                             stop=True).then_inc(taken_ready, 1)

        pick_ready, gath_ready, gath_free = ph.sem("pick_ready"), ph.sem("gath_ready"), ph.sem("gath_free")
        qkv_mm, qkv_sb = ph.sem("qkv_mm"), ph.sem("qkv_sb")
        dve_step2 = ph.sem("dve_step2")
        with nc.Block() as block:
            @block.vector
            def _(v):
                v.sem_inc(gath_free, 1)
                step = Steps(v, dve_step2)
                with v.Fori(0, B // WIDE) as i:
                    step.restart()
                    for l in lanes:
                        b = i * WIDE + l
                        step(v.tensor_copy(xn[l][:, :], n1[:, b, :]))
                        v.tensor_scalar(pick[l][:, :], taken[:, bass.ds(b * P, P)], S.iota_col, None,
                                        ALU.is_equal).then_inc(pick_ready, 1)
                    for l in lanes:
                        b = i * WIDE + l
                        v.wait_ge(gath_ready, b + 1)
                        v.tensor_copy(cols[:, b, :], ps[2 * l][:, P:P + 1 + E0])
                        v.tensor_copy(gathT[:, :, b, :], ps[2 * l][:, 0:P].rearrange("p (e k) -> p e k", k=K0))
                        v.tensor_copy(cosg[:, :, b, :], ps[2 * l + 1][0:ROPE_N, 0:P].rearrange("p (e k) -> p e k", k=K0))
                        v.tensor_copy(sing[:, :, b, :], ps[2 * l + 1][0:ROPE_N, P:2 * P]
                                      .rearrange("p (e k) -> p e k", k=K0)).then_inc(gath_free, 1)
                step = Steps(v, dve_step2)
                step.restart()
                v.wait_ge(qkv_sb, 2 * E0)
                for x, xs in ((QT, QS), (KT, KS)):
                    r = x[0:ROPE_N, :, :, :]
                    step(v.tensor_tensor(r, r, cosg[:, :, :, :], ALU.mult))
                    step(v.tensor_tensor(xs[:, :, :, :], xs[:, :, :, :], sing[:, :, :, :], ALU.mult))
                    step(v.tensor_tensor(r, r, xs[:, :, :, :], ALU.add))

            @block.scalar
            def _(a):
                for e in range(E0):
                    p4 = ps[4 * (e % 2):4 * (e % 2) + 4]
                    a.wait_ge(qkv_mm, 2 * e + 1)
                    a.activation(QT[:, e, :, :].rearrange("p b k -> p (b k)"), p4[0][:, 0:256], ACT.Copy)
                    a.activation(KT[:, e, :, :].rearrange("p b k -> p (b k)"), p4[0][:, 256:512], ACT.Copy)
                    a.activation(VT[:, e, :, :].rearrange("p b k -> p (b k)"), p4[1][:, 0:256], ACT.Copy).then_inc(qkv_sb, 1)
                    a.wait_ge(qkv_mm, 2 * e + 2)
                    a.activation(QS[:, e, :, :].rearrange("p b k -> p (b k)"), p4[2][0:ROPE_N, 0:256], ACT.Copy)
                    a.activation(KS[:, e, :, :].rearrange("p b k -> p (b k)"), p4[2][0:ROPE_N, 256:512],
                                 ACT.Copy).then_inc(qkv_sb, 1)

            @block.tensor
            def _(t):
                with t.Fori(0, B // WIDE) as i:
                    for l in lanes:
                        b = i * WIDE + l
                        t.wait_ge(pick_ready, b + 1)
                        t.wait_ge(gath_free, 1 + i * WIDE)
                        t.matmul(ps[2 * l][:, P:P + 1 + E0], pick[l][:, :], gates[:, b, :], start=True, stop=True)
                        t.matmul(ps[2 * l][:, 0:P], xn[l][:, :], pick[l][:, :], start=True, stop=True)
                        t.matmul(ps[2 * l + 1][0:ROPE_N, 0:P], S.cos, pick[l][:, :], start=True, stop=True)
                        t.matmul(ps[2 * l + 1][0:ROPE_N, P:2 * P], S.sin, pick[l][:, :], start=True,
                                 stop=True).then_inc(gath_ready, 1)
                t.wait_ge(gath_free, 1 + B)
                for e in range(E0):
                    p4 = ps[4 * (e % 2):4 * (e % 2) + 4]
                    if e >= 2:
                        t.wait_ge(qkv_sb, 2 * (e - 1))
                    rows = gathT[:, e, :, :].rearrange("p b k -> p (b k)")
                    t.matmul(p4[0][:, 0:256], wqkv[:, e, 0:D], rows, start=True, stop=True)
                    t.matmul(p4[0][:, 256:512], wqkv[:, e, D:2 * D], rows, start=True, stop=True)
                    t.matmul(p4[1][:, 0:256], wqkv[:, e, 2 * D:3 * D], rows, start=True, stop=True).then_inc(qkv_mm, 1)
                    t.matmul(p4[2][0:ROPE_N, 0:256], wswap[:, e, 0, :], rows, start=True, stop=True)
                    t.matmul(p4[2][0:ROPE_N, 256:512], wswap[:, e, 1, :], rows, start=True, stop=True).then_inc(qkv_mm, 1)

        q1_ready, s_ready, p_shift, p_exp, p_ready, p_turned, pT_ready, av_ready, av_sb = (
            ph.sem(n) for n in ("q1_ready", "s_ready", "p_shift", "p_exp", "p_ready", "p_turned", "pT_ready", "av_ready", "av_sb"))
        v_turned, vv_ready, out_mm, out_sb = ph.sem("v_turned"), ph.sem("vv_ready"), ph.sem("out_mm"), ph.sem("out_sb")
        o1_ready, o_turned, o2_ready, scat_ready = (ph.sem(n) for n in ("o1_ready", "o_turned", "o2_ready", "scat_ready"))
        dve_step3, o0_ready = ph.sem("dve_step3"), ph.sem("o0_ready")
        with nc.Block() as block:
            def rows_of(X, b):
                return X[:, :, b, :]

            @block.vector
            def _(v):
                step = Steps(v, dve_step3)
                step(v.tensor_tensor(masks[:, :, :], taken[:, :].rearrange("p (b t) -> p b t", b=B),
                                     cols[:, :, 0:1].broadcast_to([P, B, P]), ALU.is_le))
                step(v.tensor_tensor(masks[:, :, :], masks[:, :, :], S.sameexpert.unsqueeze(1).broadcast_to([P, B, P]), ALU.mult))
                step(v.tensor_scalar(masks[:, :, :], masks[:, :, :], -1.0, -NEG, ALU.add, ALU.mult))
                step(v.tensor_tensor(own[:, :, :], cols[:, :, 1:1 + E0], S.expertmask.unsqueeze(1).broadcast_to([P, B, E0]), ALU.mult))
                step(v.tensor_reduce(own_gate[:, :], own[:, :, :], AX.X, ALU.add))
                with v.Fori(0, B // WIDE) as i:
                    step.restart()
                    for l in lanes:
                        b = i * WIDE + l
                        v.wait_ge(s_ready, b + 1)
                        step(v.scalar_tensor_tensor(out=sc[l][:, :], in0=ps[2 * l][:, 0:P], scalar=float(D) ** -0.5,
                                                    in1=masks[:, b, :], op0=ALU.mult, op1=ALU.add))
                        step(v.tensor_reduce(st[l][:, 0:1], sc[l][:, :], AX.X, ALU.max))
                        v.tensor_scalar(st[l][:, 1:2], st[l][:, 0:1], -1.0, None, ALU.mult).then_inc(p_shift, 1)
                    for l in lanes:
                        b = i * WIDE + l
                        v.wait_ge(p_exp, b + 1)
                        step(v.reciprocal(st[l][:, 0:1], st[l][:, 2:3]))
                        v.tensor_scalar(sc[l][:, :], sc[l][:, :], st[l][:, 0:1], own_gate[:, bass.ds(b, 1)],
                                        ALU.mult, ALU.mult).then_inc(p_ready, 1)
                step.restart()
                with v.Fori(0, B // WIDE) as i:
                    step.restart()
                    for l in lanes:
                        b = i * WIDE + l
                        v.tensor_scalar(pickT[l][:, :], S.iota_row, cols[:, b, 0:1], None, ALU.is_equal).then_inc(o1_ready, 1)
                    for l in lanes:
                        b = i * WIDE + l
                        v.wait_ge(scat_ready, b + 1)
                        step(v.tensor_tensor(S.x[:, b, :], S.x[:, b, :], ps[2 * l + 1][:, 0:D], ALU.add))
                        v.bn_stats(S.stats[:, b, :], S.x[:, b, :])

            @block.gpsimd
            def _(g):
                with g.Fori(0, B // WIDE) as i:
                    for l in lanes:
                        b = i * WIDE + l
                        g.wait_ge(v_turned, 1 + i * WIDE)
                        g.tensor_copy(v1[l][:, :].rearrange("p (e k) -> p e k", k=K0), rows_of(VT, b))
                        g.tensor_copy(q1[l][:, :].rearrange("p (e k) -> p e k", k=K0), rows_of(QT, b)).then_inc(q1_ready, 1)
                g.wait_ge(out_sb, E0)
                with g.Fori(0, B // WIDE) as i:
                    for l in lanes:
                        b = i * WIDE + l
                        g.wait_ge(o_turned, 1 + i * WIDE)
                        g.tensor_copy(v1[l][:, :].rearrange("p (e k) -> p e k", k=K0), rows_of(OUTT, b)).then_inc(o0_ready, 1)

            @block.scalar
            def _(a):
                a.sem_inc(av_sb, 1)
                with a.Fori(0, B // WIDE) as i:
                    for l in lanes:
                        b = i * WIDE + l
                        a.wait_ge(v_turned, 1 + b + 1)
                        a.activation(vv[l][:, :], ps[2 * l + 1][:, 0:P], ACT.Copy).then_inc(vv_ready, 1)
                    for l in lanes:
                        b = i * WIDE + l
                        a.wait_ge(p_shift, b + 1)
                        a.activation(sc[l][:, :], sc[l][:, :], ACT.Exp, bias=st[l][:, 1:2],
                                     accum_out=st[l][:, 2:3]).then_inc(p_exp, 1)
                    for l in lanes:
                        b = i * WIDE + l
                        a.wait_ge(p_turned, b + 1)
                        a.activation(pT[l][:, :], ps[2 * l][:, 0:P], ACT.Copy).then_inc(pT_ready, 1)
                    for l in lanes:
                        b = i * WIDE + l
                        a.wait_ge(av_ready, b + 1)
                        a.activation(rows_of(AVT, b), ps[2 * l][:, 0:P].rearrange("p (e k) -> p e k", k=K0),
                                     ACT.Copy).then_inc(av_sb, 1)
                for e in range(E0):
                    a.wait_ge(out_mm, e + 1)
                    a.activation(OUTT[:, e, :, :].rearrange("p b k -> p (b k)"), ps[e][:, 0:256], ACT.Copy).then_inc(out_sb, 1)
                with a.Fori(0, B // WIDE) as i:
                    for l in lanes:
                        b = i * WIDE + l
                        a.wait_ge(o_turned, 1 + b + 1)
                        a.activation(vv[l][:, :], ps[2 * l][:, 0:P], ACT.Copy).then_inc(o2_ready, 1)

            @block.tensor
            def _(t):
                t.sem_inc(v_turned, 1)
                t.sem_inc(o_turned, 1)
                with t.Fori(0, B // WIDE) as i:
                    t.wait_ge(av_sb, 1 + i * WIDE)
                    for l in lanes:
                        b = i * WIDE + l
                        t.wait_ge(q1_ready, b + 1)
                        t.matmul(ps[2 * l][:, 0:P], q1[l][:, :], rows_of(KT, b), start=True, stop=True).then_inc(s_ready, 1)
                        t.transpose(ps[2 * l + 1][:, 0:P], v1[l][:, :], S.ident).then_inc(v_turned, 1)
                    for l in lanes:
                        t.wait_ge(p_ready, i * WIDE + l + 1)
                        t.transpose(ps[2 * l][:, 0:P], sc[l][:, :], S.ident).then_inc(p_turned, 1)
                    for l in lanes:
                        t.wait_ge(pT_ready, i * WIDE + l + 1)
                        t.wait_ge(vv_ready, i * WIDE + l + 1)
                        t.matmul(ps[2 * l][:, 0:P], vv[l][:, :], pT[l][:, :], start=True, stop=True).then_inc(av_ready, 1)
                t.wait_ge(av_sb, 1 + B)
                for e in range(E0):
                    t.matmul(ps[e][:, 0:256], wo[:, e, :], AVT[:, e, :, :].rearrange("p b k -> p (b k)"),
                             start=True, stop=True).then_inc(out_mm, 1)
                t.wait_ge(out_sb, E0)
                with t.Fori(0, B // WIDE) as i:
                    for l in lanes:
                        t.wait_ge(o0_ready, i * WIDE + l + 1)
                        t.transpose(ps[2 * l][:, 0:P], v1[l][:, :], S.ident).then_inc(o_turned, 1)
                    for l in lanes:
                        t.wait_ge(o1_ready, i * WIDE + l + 1)
                        t.wait_ge(o2_ready, i * WIDE + l + 1)
                        t.matmul(ps[2 * l + 1][:, 0:D], pickT[l][:, :], vv[l][:, :], start=True, stop=True).then_inc(scat_ready, 1)


def patch_depool(nc, S, name, ins):
    RMS_EPS = 1e-5
    dt = float(-np.log(-np.expm1(LOGP)))
    WIDE = 4
    with phase(nc, name) as ph:
        lanes = range(WIDE)
        w_in = ph.sb("w_in", [P, D])
        b_in, g_res, g_init = ph.sb("b_in", [P, D]), ph.sb("g_res", [P, D]), ph.sb("g_init", [P, D])
        len_i = ph.sb("len_i", [P, B], I32)
        len_f = ph.sb("len_f", [P, B])
        ends = ph.sb("ends", [P, B])
        ends_neg = ph.sb("ends_neg", [P, B])
        squares = ph.sb("squares", [P, B, CTX])
        ctx_ms = ph.sb("ctx_ms", [P, B])
        ctx_rms = ph.sb("ctx_rms", [P, B])
        xn_all = ph.sb("xn_all", [P, B, D])
        xsq = ph.sb("xsq", [P, B, D])
        xb = ph.sb("xb", [P, B, D])
        ms, rms = ph.sb("ms", [P, B]), ph.sb("rms", [P, B])
        u_all = ph.sb("u_all", [P, B, D])
        h = [ph.sb(f"h{l}", [P, D]) for l in lanes]
        hT = [ph.sb(f"hT{l}", [P, T]) for l in lanes]
        hit = [ph.sb(f"hit{l}", [P, T]) for l in lanes]
        marked = [ph.sb(f"marked{l}", [P, P]) for l in lanes]
        mark = [ph.sb(f"mark{l}", [P, 1]) for l in lanes]
        plug = [ph.sb(f"plug{l}", [P, T]) for l in lanes]
        s = [ph.sb(f"s{l}", [P, D]) for l in lanes]
        psA, psB = ([ph.ps(f"{n}{l}", [P, 512]) for l in lanes] for n in ("psA", "psB"))
        dve_step, stats_done, pow_ready, loaded, lens_mm, sq_done, ctx_pow, ms_ready, rms_ready = (
            ph.sem(n) for n in ("dve_step", "stats_done", "pow_ready", "loaded", "lens_mm", "sq_done",
                                "ctx_pow", "ms_ready", "rms_ready"))
        hit_ready, mark_ready, marked_ready, plug_mm, plug_ready, u_ready, s_mm, s_ready, h_ready, h_turned, hT_ready, sum_ready = (
            ph.sem(n) for n in ("hit_ready", "mark_ready", "marked_ready", "plug_mm", "plug_ready", "u_ready", "s_mm",
                                "s_ready", "h_ready", "h_turned", "hT_ready", "sum_ready"))
        xn_done, xsq_ready, batch_ready = (ph.sem(n) for n in ("xn_done", "xsq_ready", "batch_ready"))
        lens_ready, ctx_ms_ready = ph.sem("lens_ready"), ph.sem("ctx_ms_ready")
        with nc.Block() as block:
            @block.sync
            def _(sp):
                sp.dma_start(w_in[:, :], ins["L1_W_inT"]).then_inc(loaded, 16)
                sp.dma_start(b_in[:, :], ins["L1_xattn_b_in"].partition_broadcast(P)).then_inc(loaded, 16)
                sp.dma_start(g_res[:, :], ins["L1_xattn_g_res"].partition_broadcast(P)).then_inc(loaded, 16)
                sp.dma_start(g_init[:, :], ins["L1_xattn_g_init"][0:D].partition_broadcast(P)).then_inc(loaded, 16)
                sp.dma_start(len_i[:, :], ins["patch_lensT"]).then_inc(loaded, 16)

            @block.gpsimd
            def _(g):
                inverse_roots(g, S, stats_done, pow_ready)
                g.wait_ge(ctx_ms_ready, 1)
                g.tensor_tensor(ctx_rms[:, :], ctx_ms[:, :], S.mhalf[:, :], ALU.pow).then_inc(ctx_pow, 1)
                g.wait_ge(ms_ready, 1)
                g.tensor_tensor(rms[:, :], ms[:, :], S.mhalf[:, :], ALU.pow).then_inc(rms_ready, 1)
                g.wait_ge(ctx_pow, 1)
                g.tensor_tensor(u_all[:, :, :], S.ctx[:, :, 0:D], ctx_rms[:, :].unsqueeze(2).broadcast_to([P, B, D]),
                                ALU.mult).then_inc(u_ready, 1)

            @block.scalar
            def _(a):
                for b in range(B):
                    ins = a.activation(squares[:, b, :], S.ctx[:, b, :], ACT.Square, accum_out=ctx_ms[:, b:b + 1])
                ins.then_inc(sq_done, 1)
                a.wait_ge(xn_done, 1)
                for b in range(B):
                    ins = a.activation(xsq[:, b, :], xn_all[:, b, :], ACT.Square, accum_out=ms[:, b:b + 1])
                ins.then_inc(xsq_ready, 1)
                with a.Fori(0, B // WIDE) as i:
                    for l in lanes:
                        a.wait_ge(s_mm, i * WIDE + l + 1)
                        a.activation(s[l][:, :], psB[l][:, 0:D], ACT.Copy,
                                     scale=float(1.0 / dt * (dt * np.exp(LOGP)))).then_inc(s_ready, 1)
                    for l in lanes:
                        a.wait_ge(h_turned, i * WIDE + l + 1)
                        a.activation(hT[l][:, :], psB[l][:, 0:T], ACT.Copy).then_inc(hT_ready, 1)

            @block.vector
            def _(v):
                step = Steps(v, dve_step)
                layer_norm_coefficients(v, step, S, stats_done, pow_ready)
                normalized(v, step, S, xn_all, pow_ready, xn_done, 1)
                v.wait_ge(sq_done, 1)
                v.tensor_scalar(ctx_ms[:, :], ctx_ms[:, :], 1.0 / CTX, RMS_EPS, ALU.mult, ALU.add).then_inc(ctx_ms_ready, 1)
                v.wait_ge(loaded, 80)
                v.tensor_copy(len_f[:, :], len_i[:, :]).then_inc(lens_ready, 1)
                v.wait_ge(lens_mm, 1)
                step(v.tensor_scalar(ends[:, :], psA[0][:, 0:B], -1.0, None, ALU.add))
                step(v.tensor_scalar(ends_neg[:, :], ends[:, :], 0.0, float(T), ALU.is_lt, ALU.mult))
                step(v.tensor_tensor(ends[:, :], ends[:, :], ends_neg[:, :], ALU.add))
                v.wait_ge(xsq_ready, 1)
                v.tensor_scalar(ms[:, :], ms[:, :], 1.0 / D, RMS_EPS, ALU.mult, ALU.add).then_inc(ms_ready, 1)
                v.wait_ge(rms_ready, 1)
                step(v.tensor_tensor(xn_all[:, :, :], xn_all[:, :, :], rms[:, :].unsqueeze(2).broadcast_to([P, B, D]), ALU.mult))
                step(v.tensor_tensor(xn_all[:, :, :], xn_all[:, :, :], g_res[:, :].unsqueeze(1).broadcast_to([P, B, D]), ALU.mult))
                step(v.tensor_tensor(xb[:, :, :], S.x[:, :, :], b_in[:, :].unsqueeze(1).broadcast_to([P, B, D]), ALU.add))
                v.wait_ge(u_ready, 1)
                v.tensor_tensor(u_all[:, :, :], u_all[:, :, :], g_init[:, :].unsqueeze(1).broadcast_to([P, B, D]),
                                ALU.mult).then_inc(batch_ready, 1)
                with v.Fori(0, B // WIDE) as i:
                    step.restart()
                    for l in lanes:
                        b = i * WIDE + l
                        v.tensor_scalar(hit[l][:, :], S.iota_row, ends[:, bass.ds(b, 1)], None, ALU.is_equal).then_inc(hit_ready, 1)
                        v.tensor_copy(h[l][:, :], xn_all[:, b, :]).then_inc(h_ready, 1)
                    for l in lanes:
                        b = i * WIDE + l
                        v.wait_ge(mark_ready, b + 1)
                        step(v.tensor_scalar(mark[l][:, :], psA[l][:, 0:1], 1.0, None, ALU.min))
                        v.tensor_scalar(marked[l][:, :], S.ones, mark[l][:, 0:1], None, ALU.mult).then_inc(marked_ready, 1)
                    for l in lanes:
                        b = i * WIDE + l
                        v.wait_ge(plug_mm, b + 1)
                        step(v.tensor_scalar(plug[l][:, :], psA[l][:, 0:T], -1.0, 0.0, ALU.add, ALU.max))
                        v.tensor_scalar(plug[l][:, :], plug[l][:, :], S.iota_col, None, ALU.is_equal).then_inc(plug_ready, 1)
                    for l in lanes:
                        b = i * WIDE + l
                        v.wait_ge(sum_ready, b + 1)
                        step(v.tensor_tensor(S.x[:, b, :], xb[:, b, :], psA[l][:, 0:D], ALU.add))
                        v.bn_stats(S.stats[:, b, :], S.x[:, b, :])

            @block.tensor
            def _(t):
                t.wait_ge(lens_ready, 1)
                t.matmul(psA[0][:, 0:B], S.upto, len_f[:, :], start=True, stop=True).then_inc(lens_mm, 1)
                t.wait_ge(batch_ready, 1)
                with t.Fori(0, B // WIDE) as i:
                    for l in lanes:
                        b = i * WIDE + l
                        t.wait_ge(hit_ready, b + 1)
                        t.wait_ge(h_ready, b + 1)
                        t.matmul(psB[l][:, 0:D], S.decay, u_all[:, b, :], start=True, stop=True).then_inc(s_mm, 1)
                        t.matmul(psA[l][:, 0:1], hit[l][:, :], S.ones[:, 0:1], start=True, stop=True).then_inc(mark_ready, 1)
                    for l in lanes:
                        b = i * WIDE + l
                        t.wait_ge(s_ready, b + 1)
                        t.transpose(psB[l][:, 0:T], h[l][:, :], S.ident).then_inc(h_turned, 1)
                        t.wait_ge(marked_ready, b + 1)
                        t.matmul(psA[l][:, 0:T], marked[l][:, :], S.upto, start=True, stop=True).then_inc(plug_mm, 1)
                    for l in lanes:
                        b = i * WIDE + l
                        t.wait_ge(hT_ready, b + 1)
                        t.wait_ge(plug_ready, b + 1)
                        t.matmul(psA[l][:, 0:D], hT[l][:, :], w_in[:, :], start=True, stop=False)
                        t.matmul(psA[l][:, 0:D], plug[l][:, :], s[l][:, :], start=False, stop=True).then_inc(sum_ready, 1)


ROW = LW * D + LW + LW * D + D
W1, B1, W2, B2 = 0, LW * D, LW * D + LW, LW * D + LW + LW * D
DEPTH = 8


def tree_routes(nc, S, name, nets, first_net, stream, leaves, node_w, node_b, gathers):
    G = 4
    with phase(nc, name) as ph:
        w = ph.sb("w", [P, nets * NODES])
        nb = ph.sb("nb", [P, nets * NODES])
        xn = [ph.sb(f"xn{k}", [P, D]) for k in range(G)]
        xT = [ph.sb(f"xT{k}", [P, T]) for k in range(G)]
        right = ph.sb("right", [P, G, nets, NODES])
        path = [ph.sb(f"path{k}", [P, G * nets, LEAVES]) for k in range(2)]
        leaf_f = ph.sb("leaf_f", [P, G, nets])
        ps = [ph.ps(f"ps{k}", [P, 1024]) for k in range(G)]
        dve_step, pool_step, loaded, x_ready, turned, xT_ready, logits_ready, leaves_ready = (
            ph.sem(n) for n in ("dve_step", "pool_step", "loaded", "x_ready", "turned", "xT_ready", "logits_ready",
                                "leaves_ready"))
        with nc.Block() as block:
            @block.sync
            def _(sp):
                sp.dma_start(w[:, :], node_w).then_inc(loaded, 16)
                sp.dma_start(nb[:, :], node_b.partition_broadcast(P)).then_inc(loaded, 16)

            @block.gpsimd
            def _(g):
                g.wait_ge(leaves_ready, 1)
                gathers.first(g, Steps(g, pool_step))

            @block.vector
            def _(v):
                step = Steps(v, dve_step)
                v.wait_ge(loaded, 32)
                step(v.tensor_scalar(nb[:, :], nb[:, :], -1.0, None, ALU.mult))
                rt = right[:, :, :, :].rearrange("p k n c -> p (k n) c")

                def rows(i):
                    for k in range(G):
                        v.tensor_copy(xn[k][:, :], stream[:, i * G + k, :]).then_inc(x_ready, 1)

                def turned_rows(i):
                    for k in range(G):
                        v.wait_ge(turned, i * G + k + 1)
                        v.tensor_copy(xT[k][:, :], ps[k][:, 0:T]).then_inc(xT_ready, 1)

                def decisions(i):
                    for k in range(G):
                        v.wait_ge(logits_ready, i * G + k + 1)
                        for n0 in range(0, nets, 2):
                            m = min(2, nets - n0)
                            at = 512 * (n0 // 2)
                            ins = v.tensor_tensor(right[:, k, n0:n0 + m, :].rearrange("p n c -> p (n c)"),
                                                  ps[k][:, at:at + m * NODES],
                                                  nb[:, n0 * NODES:(n0 + m) * NODES], ALU.is_gt)
                    step(ins)

                def walk(levels):
                    for level in levels:
                        width = 2 ** level
                        a, b = path[(level + 1) % 2], path[level % 2]
                        pair = b[:, :, 0:2 * width].rearrange("p g (c two) -> p g c two", two=2)
                        step(v.tensor_tensor(pair[:, :, :, 1], a[:, :, 0:width], rt[:, :, width - 1:2 * width - 1], ALU.mult))
                        step(v.tensor_tensor(pair[:, :, :, 0], a[:, :, 0:width], pair[:, :, :, 1], ALU.subtract))

                def first_level():
                    step(v.tensor_scalar(path[0][:, :, 0:1], rt[:, :, 0:1], -1.0, 1.0, ALU.mult, ALU.add))
                    step(v.tensor_copy(path[0][:, :, 1:2], rt[:, :, 0:1]))

                def leaf(i):
                    last, width = path[(DEPTH - 2) % 2], LEAVES // 2
                    go = rt[:, :, width - 1:2 * width - 1]
                    twice = S.iota256.rearrange("p (c two) -> p c two", two=2)[:, :, 0]
                    step(v.tensor_tensor(go, go, twice.unsqueeze(1).broadcast_to([P, G * nets, width]), ALU.add))
                    step(v.tensor_tensor(go, go, last[:, :, 0:width], ALU.mult))
                    step(v.tensor_reduce(leaf_f[:, :, :].rearrange("p k n -> p (k n)"), go, AX.X, ALU.add))
                    for n in range(nets):
                        ins = v.tensor_scalar(leaf_f[:, :, n], leaf_f[:, :, n], float(LEAVES * (first_net + n)), None, ALU.add)
                    step(ins)
                    step(v.tensor_copy(leaves[:, bass.ds(i * G, G), :] if not isinstance(i, int)
                                       else leaves[:, i * G:(i + 1) * G, :], leaf_f[:, :, :]))
                    v.sem_inc(leaves_ready, 1)

                rows(0)
                turned_rows(0)
                decisions(0)
                with v.Fori(0, B // G - 1) as i:
                    step.restart()
                    rows(i + 1)
                    first_level()
                    walk(range(1, 4))
                    turned_rows(i + 1)
                    walk(range(4, DEPTH - 1))
                    leaf(i)
                    decisions(i + 1)
                step.restart()
                first_level()
                walk(range(1, DEPTH - 1))
                leaf(B // G - 1)

            @block.tensor
            def _(t):
                t.wait_ge(loaded, 32)
                with t.Fori(0, B // G) as i:
                    for k in range(G):
                        t.wait_ge(x_ready, i * G + k + 1)
                        t.transpose(ps[k][:, 0:T], xn[k][:, :], S.ident).then_inc(turned, 1)
                    for k in range(G):
                        t.wait_ge(xT_ready, i * G + k + 1)
                        for n0 in range(0, nets, 2):
                            m = min(2, nets - n0)
                            at = 512 * (n0 // 2)
                            mm = t.matmul(ps[k][:, at:at + m * NODES], xT[k][:, :],
                                          w[:, n0 * NODES:(n0 + m) * NODES], start=True, stop=True)
                        mm.then_inc(logits_ready, 1)


class LeafGathers:

    def __init__(self, ph, name, leaves, slots, picks, table, samples):
        self.leaves, self.slots, self.picks, self.table, self.samples = leaves, slots, picks, table, samples
        self.gathered = [ph.sem(f"{name}_gathered{m}") for m in range(len(slots))]

    def gather(self, g, step, i, m):
        k, net = m % self.samples, m // self.samples
        step(g.tensor_copy(self.picks[m][:, :], self.leaves[:, i * self.samples + k, net:net + 1]))
        g.indirect_dma_start(out=self.slots[m][:, :], out_offset=None, in_=self.table,
                             in_offset=bass.IndirectOffsetOnAxis(ap=self.picks[m][:, 0:1], axis=0)
                             ).then_inc(self.gathered[m], 16)

    def first(self, g, step):
        for m in range(len(self.slots)):
            self.gather(g, step, 0, m)

    def others(self, g, step, used):
        n = len(self.slots)
        with g.Fori(0, B // self.samples - 1) as i:
            step.restart()
            for m in range(n):
                g.wait_ge(used, 1 + i * n + m + 1)
                self.gather(g, step, i + 1, m)


def routed_trees(nc, S, name, ins):
    with phase(nc, name) as ph:
        xn3 = ph.sb("xn3", [P, B, D])
        leaves = ph.sb("leaves", [P, B, 3], U32)
        leaves_f = ph.sb("leaves_f", [P, B, 1], U32)
        table = ins["leaf_table"]

        with phase(nc, name + "_norm") as pn:
            stats = pn.sb("stats", [P, B, 6])
            mu, dif, var = pn.sb("mu", [P, B]), pn.sb("dif", [P, B]), pn.sb("var", [P, B])
            half = pn.sb("half", [P, B])
            xn_done, dve_step, stats_done, pow_ready, var_ready, sd_ready, den_ready, inv_ready = (
                pn.sem(n) for n in ("xn_done", "dve_step", "stats_done", "pow_ready", "var_ready", "sd_ready", "den_ready", "inv_ready"))
            with nc.Block() as block:
                @block.gpsimd
                def _(g):
                    g.memset(half[:, :], 0.5).then_inc(sd_ready, 1)
                    inverse_roots(g, S, stats_done, pow_ready)
                    g.wait_ge(sd_ready, 1)
                    g.wait_ge(var_ready, 1)
                    g.tensor_tensor(var[:, :], var[:, :], half[:, :], ALU.pow).then_inc(sd_ready, 1)
                    g.wait_ge(den_ready, 1)
                    g.tensor_tensor(var[:, :], var[:, :], S.mhalf[:, :], ALU.pow).then_inc(inv_ready, 1)

                @block.vector
                def _(v):
                    step = Steps(v, dve_step)
                    layer_norm_coefficients(v, step, S, stats_done, pow_ready)
                    normalized(v, step, S, xn3, pow_ready, xn_done, 1)
                    v.wait_ge(xn_done, 1)
                    for b in range(B):
                        ins = v.bn_stats(stats[:, b, :], xn3[:, b, :])
                    step(ins)
                    step(v.tensor_tensor(mu[:, :], stats[:, :, 1], stats[:, :, 4], ALU.add))
                    step(v.tensor_tensor(dif[:, :], stats[:, :, 1], stats[:, :, 4], ALU.subtract))
                    step(v.tensor_scalar(mu[:, :], mu[:, :], 0.5, None, ALU.mult))
                    step(v.tensor_tensor(var[:, :], stats[:, :, 2], stats[:, :, 5], ALU.add))
                    step(v.scalar_tensor_tensor(out=dif[:, :], in0=dif[:, :], scalar=0.25 * D, in1=dif[:, :],
                                                op0=ALU.mult, op1=ALU.mult))
                    step(v.tensor_tensor(var[:, :], var[:, :], dif[:, :], ALU.add))
                    v.tensor_scalar(var[:, :], var[:, :], 1.0 / (D - 1), None, ALU.mult).then_inc(var_ready, 1)
                    v.wait_ge(sd_ready, 2)
                    v.tensor_scalar(var[:, :], var[:, :], 1e-5, None, ALU.add).then_inc(den_ready, 1)
                    v.wait_ge(inv_ready, 1)
                    step(v.tensor_tensor(xn3[:, :, :], xn3[:, :, :], mu[:, :].unsqueeze(2).broadcast_to([P, B, D]), ALU.subtract))
                    step(v.tensor_tensor(xn3[:, :, :], xn3[:, :, :], var[:, :].unsqueeze(2).broadcast_to([P, B, D]), ALU.mult))

        slots = [ph.sb(f"slot{m}", [P, ROW]) for m in range(3 * LANES)]
        picks = [ph.sb(f"pick{m}", [P, 1], U32) for m in range(3 * LANES)]
        gathers = LeafGathers(ph, "qkv", leaves, slots, picks, table, LANES)
        gathers_f = LeafGathers(ph, "f", leaves_f, slots[0:4], picks[0:4], table, 4)
        tree_routes(nc, S, name + "_r3", 3, 0, xn3, leaves, ins["L1_ffn_nw3"], ins["L1_ffn_nb3"], gathers)
        tree_attention(nc, S, name + "_qkv", xn3, gathers)
        tree_routes(nc, S, name + "_rf", 1, 3, xn3, leaves_f, ins["L1_ffn_nwf"], ins["L1_ffn_nbf"], gathers_f)
        tree_output(nc, S, name + "_f", xn3, gathers_f)


def row_of(stream, b):
    rows = stream[:, b:b + 1, :] if isinstance(b, int) else stream[:, bass.ds(b, 1), :]
    return rows.broadcast_to([P, LW, D])


def tree_hidden(v, step, rows, x, prod, h):
    step(v.tensor_tensor(prod[:, :, :], rows[:, W1:W1 + LW * D].rearrange("p (l d) -> p l d", d=D),
                         x, ALU.mult))
    step(v.tensor_reduce(h[:, :], prod[:, :, :], AX.X, ALU.add))
    return v.tensor_tensor(h[:, :], h[:, :], rows[:, B1:B1 + LW], ALU.add)


def tree_attention(nc, S, name, xn3, gathers):
    with phase(nc, name) as ph:
        lanes = range(LANES)
        N = 3 * LANES
        slots, gathered = gathers.slots, gathers.gathered
        prod = ph.sb("prod", [P, LW, D])
        h = [ph.sb(f"h{m}", [P, LW]) for m in range(N)]
        diag = [ph.sb(f"diag{k}", [P, LW, P]) for k in range(2)]
        qkv = [ph.sb(f"qkv{m}", [P, D]) for m in range(N)]
        qT, kT, pr, pT = ([ph.sb(f"{n}{l}", [P, P]) for l in lanes] for n in ("qT", "kT", "pr", "pT"))
        st = [ph.sb(f"st{l}", [P, 4]) for l in lanes]
        ps = [ph.ps(f"ps{k}", [P, 512]) for k in range(8)]
        dve_step, pool_step, h_ready, diag_ready, out_mm, used = (
            ph.sem(n) for n in ("dve_step", "pool_step", "h_ready", "diag_ready", "out_mm", "used"))
        qk_turned, qkT_ready, s_mm, shifted, p_exp, p_turned, pT_ready, att_mm = (
            ph.sem(n) for n in ("qk_turned", "qkT_ready", "s_mm", "shifted", "p_exp", "p_turned", "pT_ready", "att_mm"))

        with nc.Block() as block:
            @block.gpsimd
            def _(g):
                gathers.others(g, Steps(g, pool_step), used)

            @block.vector
            def _(v):
                v.sem_inc(used, 1)
                step = Steps(v, dve_step)

                def evacuate(i, m):
                    v.wait_ge(out_mm, 1 + i * N + m + 1)
                    v.tensor_tensor(qkv[m][:, :], ps[m % 2][:, 0:D], slots[m][:, B2:B2 + D], ALU.add).then_inc(used, 1)

                def hidden(i, m):
                    v.wait_ge(gathered[m], i * 16 + 16)
                    step(tree_hidden(v, step, slots[m], row_of(xn3, i * LANES + m % LANES), prod, h[m]))
                    v.tensor_scalar(h[m][:, :], h[m][:, :], 0.0, None, ALU.max).then_inc(h_ready, 1)

                def attend(i, k):
                    for l in lanes:
                        if k == 0:
                            v.wait_ge(qk_turned, i * LANES + l + 1)
                            v.tensor_copy(qT[l][:, :], ps[2 + l][:, 0:T])
                            v.tensor_copy(kT[l][:, :], ps[2 + l][:, T:2 * T]).then_inc(qkT_ready, 1)
                        elif k == 1:
                            v.wait_ge(s_mm, i * LANES + l + 1)
                            step(v.tensor_reduce(st[l][:, 0:1], ps[4 + l][:, 0:T], AX.X, ALU.max))
                            v.tensor_scalar(st[l][:, 1:2], st[l][:, 0:1], -float(D) ** -0.5, None, ALU.mult).then_inc(shifted, 1)
                        elif k == 2:
                            v.wait_ge(p_turned, i * LANES + l + 1)
                            v.tensor_copy(pT[l][:, :], ps[4 + l][:, T:2 * T]).then_inc(pT_ready, 1)
                        else:
                            b = i * LANES + l
                            v.wait_ge(att_mm, b + 1)
                            step(v.reciprocal(st[l][:, 3:4], st[l][:, 2:3]))
                            step(v.scalar_tensor_tensor(out=xn3[:, b, :], in0=ps[6 + l][:, 0:D], scalar=st[l][:, 3:4],
                                                        in1=xn3[:, b, :], op0=ALU.mult, op1=ALU.add))

                def iteration(i, before):
                    for m in range(N):
                        hidden(i, m)
                        if m >= 2:
                            if before is not None:
                                attend(before, m - 2)
                            evacuate(i, m - 2)
                        elif before is not None:
                            evacuate(before, N - 2 + m)

                iteration(0, None)
                with v.Fori(0, B // LANES - 1) as i:
                    step.restart()
                    iteration(i + 1, i)
                step.restart()
                evacuate(B // LANES - 1, N - 2)
                evacuate(B // LANES - 1, N - 1)
                for k in range(4):
                    attend(B // LANES - 1, k)

            @block.scalar
            def _(a):
                def exps(i):
                    for l in lanes:
                        a.wait_ge(shifted, i * LANES + l + 1)
                        a.activation(pr[l][:, :], ps[4 + l][:, 0:T], ACT.Exp, bias=st[l][:, 1:2], scale=float(D) ** -0.5,
                                     accum_out=st[l][:, 2:3]).then_inc(p_exp, 1)

                def iteration(i, before):
                    for m in range(N):
                        if m == 3 and before is not None:
                            exps(before)
                        a.wait_ge(h_ready, i * N + m + 1)
                        a.wait_ge(out_mm, 1 if before is None and m < 2 else i * N + m)
                        for c in range(LW):
                            ins = a.activation(diag[m % 2][:, c, :], S.ident, ACT.Copy, scale=h[m][:, c:c + 1])
                            if c % 4 == 3:
                                ins.then_inc(diag_ready, 1)

                iteration(0, None)
                with a.Fori(0, B // LANES - 1) as i:
                    iteration(i + 1, i)
                exps(B // LANES - 1)

            @block.tensor
            def _(t):
                t.sem_inc(out_mm, 1)
                def attend(i, k):
                    for l in lanes:
                        if k == 0:
                            t.wait_ge(used, 1 + i * N + N)
                            t.transpose(ps[2 + l][:, 0:T], qkv[l][:, :], S.ident)
                            t.transpose(ps[2 + l][:, T:2 * T], qkv[LANES + l][:, :], S.ident).then_inc(qk_turned, 1)
                        elif k == 1:
                            t.wait_ge(qkT_ready, i * LANES + l + 1)
                            t.matmul(ps[4 + l][:, 0:T], qT[l][:, :], kT[l][:, :], start=True, stop=True).then_inc(s_mm, 1)
                        elif k == 2:
                            t.wait_ge(p_exp, i * LANES + l + 1)
                            t.transpose(ps[4 + l][:, T:2 * T], pr[l][:, :], S.ident).then_inc(p_turned, 1)
                        else:
                            t.wait_ge(pT_ready, i * LANES + l + 1)
                            t.matmul(ps[6 + l][:, 0:D], pT[l][:, :], qkv[2 * LANES + l][:, :], start=True,
                                     stop=True).then_inc(att_mm, 1)

                def iteration(i, before):
                    for m in range(N):
                        if before is not None and 1 <= m <= 4:
                            attend(before, m - 1)
                        t.wait_ge(used, 1 if before is None and m < 2 else i * N + m)
                        for c in range(LW):
                            if c % 4 == 0:
                                t.wait_ge(diag_ready, (i * N + m) * (LW // 4) + c // 4 + 1)
                            mm = t.matmul(ps[m % 2][:, 0:D], diag[m % 2][:, c, :], slots[m][:, W2 + c * D:W2 + (c + 1) * D],
                                          start=(c == 0), stop=(c == LW - 1))
                        mm.then_inc(out_mm, 1)

                iteration(0, None)
                with t.Fori(0, B // LANES - 1) as i:
                    iteration(i + 1, i)
                for k in range(4):
                    attend(B // LANES - 1, k)


def tree_output(nc, S, name, y, gathers):
    with phase(nc, name) as ph:
        N = 4
        slots, gathered = gathers.slots, gathers.gathered
        prod = ph.sb("prod", [P, LW, D])
        h = [ph.sb(f"h{m}", [P, LW]) for m in range(N)]
        diag = [ph.sb(f"diag{k}", [P, LW, P]) for k in range(2)]
        out = [ph.sb(f"out{k}", [P, D]) for k in range(2)]
        ps = [ph.ps(f"ps{k}", [P, 512]) for k in range(2)]
        dve_step, pool_step, h_ready, act_ready, diag_ready, out_mm, used = (
            ph.sem(n) for n in ("dve_step", "pool_step", "h_ready", "act_ready", "diag_ready", "out_mm", "used"))
        with nc.Block() as block:
            @block.gpsimd
            def _(g):
                gathers.others(g, Steps(g, pool_step), used)

            @block.vector
            def _(v):
                v.sem_inc(used, 1)
                step = Steps(v, dve_step)

                def free_slot(i, m):
                    v.wait_ge(out_mm, 1 + i * N + m + 1)
                    v.tensor_tensor(out[m % 2][:, :], ps[m % 2][:, 0:D], slots[m][:, B2:B2 + D], ALU.add).then_inc(used, 1)

                def add_up(i, m):
                    v.wait_ge(used, 1 + i * N + m + 1)
                    step(v.tensor_tensor(out[m % 2][:, :], out[m % 2][:, :], y[:, i * N + m, :], ALU.add))
                    step(v.tensor_tensor(S.x[:, i * N + m, :], S.x[:, i * N + m, :], out[m % 2][:, :], ALU.add))

                def hidden(i, m):
                    v.wait_ge(gathered[m], i * 16 + 16)
                    tree_hidden(v, step, slots[m], row_of(y, i * N + m), prod, h[m]).then_inc(h_ready, 1)

                for m in range(N):
                    hidden(0, m)
                    if m >= 2:
                        add_up(0, m - 2)
                    if m:
                        free_slot(0, m - 1)
                with v.Fori(0, B // N - 1) as i:
                    step.restart()
                    for m in range(N):
                        hidden(i + 1, m)
                        if m >= 2:
                            add_up(i + 1, m - 2)
                        else:
                            add_up(i, N - 2 + m)
                        if m:
                            free_slot(i + 1, m - 1)
                        else:
                            free_slot(i, N - 1)
                step.restart()
                add_up(B // N - 1, N - 2)
                free_slot(B // N - 1, N - 1)
                add_up(B // N - 1, N - 1)
                all_statistics(v, step, S)

            @block.scalar
            def _(a):
                def iteration(i, first):
                    for m in range(N):
                        a.wait_ge(h_ready, i * N + m + 1)
                        a.activation(h[m][:, :], h[m][:, :], ACT.Gelu).then_inc(act_ready, 1)
                        a.wait_ge(act_ready, i * N + m + 1)
                        a.wait_ge(out_mm, 1 if first and m < 2 else i * N + m)
                        for c in range(LW):
                            ins = a.activation(diag[m % 2][:, c, :], S.ident, ACT.Copy, scale=h[m][:, c:c + 1])
                            if c % 4 == 3:
                                ins.then_inc(diag_ready, 1)

                iteration(0, True)
                with a.Fori(0, B // N - 1) as i:
                    iteration(i + 1, False)

            @block.tensor
            def _(t):
                t.sem_inc(out_mm, 1)
                def iteration(i, first):
                    for m in range(N):
                        t.wait_ge(used, 1 if first and m < 2 else i * N + m)
                        for c in range(LW):
                            if c % 4 == 0:
                                t.wait_ge(diag_ready, (i * N + m) * (LW // 4) + c // 4 + 1)
                            mm = t.matmul(ps[m % 2][:, 0:D], diag[m % 2][:, c, :], slots[m][:, W2 + c * D:W2 + (c + 1) * D],
                                          start=(c == 0), stop=(c == LW - 1))
                        mm.then_inc(out_mm, 1)

                iteration(0, True)
                with t.Fori(0, B // N - 1) as i:
                    iteration(i + 1, False)


def wide_head_attention(nc, S, name, ins):
    HEADS, DH = 16, 64
    EPS = 1e-6
    NCH = HEADS * DH // P
    HPC = 4
    CHUNKS = HEADS // HPC
    scale = DH ** -0.5
    with phase(nc, name) as ph:
        lanes = range(LANES)
        wq = ph.sb("wq", [P, HEADS * DH])
        wkv = ph.sb("wkv", [P, 2, 2 * HEADS * DH])
        wout = ph.sb("wout", [P, NCH, D])
        null_key = ph.sb("null_key", [P, DH])
        null_value = ph.sb("null_value", [P, 1])
        value_cols = ph.sb("value_cols", [P, NCH, HEADS])
        wnull = ph.sb("wnull", [P, HEADS])
        null_out = ph.sb("null_out", [P, D])
        prod = ph.sb("prod", [P, HEADS, DH])
        scale_row, bias_row = ph.sb("scale_row", [P, D]), ph.sb("bias_row", [P, D])
        xn_all = ph.sb("xn_all", [P, B, D])
        xn = [ph.sb(f"xn{l}", [P, D]) for l in lanes]
        xnT = [ph.sb(f"xnT{l}", [P, T]) for l in lanes]
        cT = [ph.sb(f"cT{l}", [P, 2, P]) for l in lanes]
        qT = [ph.sb(f"qT{l}", [P, NCH, T]) for l in lanes]
        keys = [ph.sb(f"keys{l}", [P, NCH, 2, P]) for l in lanes]
        vals = [ph.sb(f"vals{l}", [P, NCH, 2 * P]) for l in lanes]
        probs = [ph.sb(f"probs{l}", [P, HEADS, P]) for l in lanes]
        probsT = [ph.sb(f"probsT{l}", [P, HEADS, P]) for l in lanes]
        s0, p0, mx, neg, sums = ([ph.sb(f"{n}{l}", [P, HEADS]) for l in lanes] for n in ("s0", "p0", "mx", "neg", "sums"))
        p0T = [ph.sb(f"p0T{l}", [P, T]) for l in lanes]
        oT = [ph.sb(f"oT{l}", [P, NCH, T]) for l in lanes]
        st = [ph.sb(f"st{l}", [P, 6]) for l in lanes]
        mv = [ph.sb(f"mv{l}", [P, 2]) for l in lanes]
        rstd = [ph.sb(f"rstd{l}", [P, 1]) for l in lanes]
        res = [ph.sb(f"res{l}", [P, D]) for l in lanes]
        psA = [ph.ps(f"psA{l}", [P, 1024]) for l in lanes]
        psB = [ph.ps(f"psB{l}", [P, 512]) for l in lanes]
        psO = [ph.ps(f"psO{l}", [P, 512]) for l in lanes]
        dve_step, stats_done, pow_ready, loaded, null_ready, zeros_set, null_mm, null_out_ready, normed = (ph.sem(n) for n in (
            "dve_step", "stats_done", "pow_ready", "loaded", "null_ready", "zeros_set", "null_mm", "null_out_ready", "normed"))
        (xn_ready, xn_turned, xnT_ready, cT_ready, s0_mm, q_mm, q_ready, k_mm, k_low_ready, k_high_ready, v_mm, v_ready) = (
            [ph.sem(f"{n}{l}") for l in lanes] for n in (
                "xn_ready", "xn_turned", "xnT_ready", "cT_ready", "s0_mm", "q_mm", "q_ready", "k_mm", "k_low_ready",
                "k_high_ready", "v_mm", "v_ready"))
        (scores_ready, maxed, exp_ready, normed_ready, turned, probsT_ready, out_mm, oT_ready, p0_turned, p0T_ready,
         res_ready, proj_ready, var_ready, rstd_ready) = ([ph.sem(f"{n}{l}") for l in lanes] for n in (
             "scores_ready", "maxed", "exp_ready", "normed_ready", "turned", "probsT_ready", "out_mm", "oT_ready",
             "p0_turned", "p0T_ready", "res_ready", "proj_ready", "var_ready", "rstd_ready"))

        def bank(c):
            return slice(c % 2 * 512, c % 2 * 512 + 512)

        with nc.Block() as block:
            @block.sync
            def _(sp):
                sp.dma_start(wq[:, :], ins["L2_xattn_Wq"]).then_inc(loaded, 16)
                sp.dma_start(null_key[:, :], ins["L2_null_key"].partition_broadcast(P)).then_inc(loaded, 16)
                sp.dma_start(null_value[:, :], ins["L2_null_values"]).then_inc(loaded, 16)
                sp.dma_start(wkv[:, :, :], ins["L2_xattn_Wkv"].rearrange("(s p) n -> p s n", p=P)).then_inc(loaded, 16)
                sp.dma_start(wout[:, :, :], ins["L2_xattn_Wout"].rearrange("(c p) n -> p c n", p=P)).then_inc(loaded, 16)
                sp.dma_start(scale_row[:, :], ins["L2_xattn_ln_scale"].partition_broadcast(P)).then_inc(loaded, 16)
                sp.dma_start(bias_row[:, :], ins["L2_xattn_ln_bias"].partition_broadcast(P)).then_inc(loaded, 16)

            @block.gpsimd
            def _(g):
                inverse_roots(g, S, stats_done, pow_ready)
                for l in lanes:
                    g.memset(keys[l][:, :, :, :], 0.0).then_inc(zeros_set, 1)
                    g.memset(vals[l][:, :, :], 0.0).then_inc(zeros_set, 1)

                def rows(j, l):
                    g.wait_ge(xn_turned[l], 1 + j)
                    g.tensor_copy(xn[l][:, :], xn_all[:, j * LANES + l, :]).then_inc(xn_ready[l], 1)

                def next_rows(j, l):
                    if not isinstance(j, int):
                        rows(j + 1, l)

                def context(j, l):
                    g.wait_ge(v_mm[l], 1 + 2 * j)
                    b = j * LANES + l
                    g.tensor_copy(cT[l][:, :, :], S.ctxT[:, :, bass.ds(b, 1), :]
                                  .rearrange("p s o k -> p (s o) k")).then_inc(cT_ready[l], 1)

                def root(j, l):
                    g.wait_ge(var_ready[l], j + 1)
                    g.tensor_tensor(rstd[l][:, :], mv[l][:, 1:2], S.mhalf[:, 0:1], ALU.pow).then_inc(rstd_ready[l], 1)
                g.wait_ge(normed, 1)
                for l in lanes:
                    rows(0, l)
                g.wait_ge(normed, 4)
                skewed(g, [context, nothing], [next_rows, root])

            @block.vector
            def _(v):
                step = Steps(v, dve_step)
                layer_norm_coefficients(v, step, S, stats_done, pow_ready)
                normalized(v, step, S, xn_all, pow_ready, normed, 4)
                v.wait_ge(loaded, 112)
                step(v.tensor_tensor(prod[:, :, :], wq[:, :].rearrange("p (h d) -> p h d", d=DH),
                                     null_key[:, :].unsqueeze(1).broadcast_to([P, HEADS, DH]), ALU.mult))
                v.tensor_reduce(wnull[:, :], prod[:, :, :], AX.X, ALU.add).then_inc(null_ready, 1)
                v.tensor_scalar(value_cols[:, :, :].rearrange("p c h -> p (c h)"), S.pairhead, null_value[:, 0:1], None,
                                ALU.mult).then_inc(null_ready, 1)
                v.wait_ge(null_mm, 1)
                v.tensor_copy(null_out[0:HEADS, :], psB[0][0:HEADS, 0:D]).then_inc(null_out_ready, 1)
                v.wait_ge(zeros_set, 4)

                def null_scores(j, l):
                    v.wait_ge(s0_mm[l], j + 1)
                    step(v.tensor_scalar(s0[l][:, :], psO[l][:, 0:HEADS], scale, None, ALU.mult))

                def low_keys(j, l):
                    for n in range(2):
                        v.wait_ge(k_mm[l], 2 * j + n + 1)
                        v.tensor_copy(keys[l][0:DH, 4 * n:4 * n + 4, 0, :],
                                      psA[l][0:DH, bank(n)].rearrange("p (c k) -> p c k", k=P)).then_inc(k_low_ready[l], 1)

                def maximum(c, j, l):
                    heads = slice(c * HPC, (c + 1) * HPC)
                    v.wait_ge(scores_ready[l], j * CHUNKS + c + 1)
                    step(v.tensor_reduce(mx[l][:, heads], psA[l][:, bank(c)].rearrange("p (j k) -> p j k", k=P), AX.X, ALU.max))
                    step(v.tensor_tensor(mx[l][:, heads], mx[l][:, heads], s0[l][:, heads], ALU.max))
                    v.tensor_scalar(neg[l][:, heads], mx[l][:, heads], -1.0, None, ALU.mult)
                    v.tensor_tensor(p0[l][:, heads], s0[l][:, heads], mx[l][:, heads], ALU.subtract).then_inc(maxed[l], 1)

                def divide(c, j, l):
                    heads = slice(c * HPC, (c + 1) * HPC)
                    v.wait_ge(exp_ready[l], j * CHUNKS + c + 1)
                    step(v.tensor_tensor(sums[l][:, heads], sums[l][:, heads], p0[l][:, heads], ALU.add))
                    step(v.reciprocal(sums[l][:, heads], sums[l][:, heads]))
                    v.tensor_tensor(p0[l][:, heads], p0[l][:, heads], sums[l][:, heads], ALU.mult)
                    v.tensor_tensor(probs[l][:, heads, :], probs[l][:, heads, :],
                                    sums[l][:, heads].unsqueeze(2).broadcast_to([P, HPC, P]), ALU.mult).then_inc(normed_ready[l], 1)

                def turned_out(n, j, l):
                    v.wait_ge(out_mm[l], 2 * j + n + 1)
                    v.tensor_copy(oT[l][:, 4 * n:4 * n + 4, :].rearrange("p c t -> p (c t)"), psO[l][:, :]).then_inc(oT_ready[l], 1)

                def chunk(c):
                    def stage(j, l):
                        if c:
                            divide(c - 1, j, l)
                        maximum(c, j, l)
                    return stage

                def last_division(j, l):
                    divide(CHUNKS - 1, j, l)
                    turned_out(0, j, l)

                def last_outputs(j, l):
                    turned_out(1, j, l)

                def statistics(j, l):
                    v.wait_ge(proj_ready[l], j + 1)
                    v.tensor_copy(res[l][:, :], psO[l][:, 0:D]).then_inc(res_ready[l], 1)
                    v.wait_ge(res_ready[l], 1 + j + 1)
                    step(v.bn_stats(st[l][:, :], res[l][:, :]))
                    step(v.bn_aggr(mv[l][:, :], st[l][:, :]))
                    v.tensor_scalar(mv[l][:, 1:2], mv[l][:, 1:2], EPS, None, ALU.add).then_inc(var_ready[l], 1)

                def added(j, l):
                    b = j * LANES + l
                    v.wait_ge(rstd_ready[l], j + 1)
                    step(v.tensor_scalar(res[l][:, :], res[l][:, :], mv[l][:, 0:1], rstd[l][:, 0:1], ALU.subtract, ALU.mult))
                    step(v.tensor_tensor(res[l][:, :], res[l][:, :], scale_row[:, :], ALU.mult))
                    step(v.tensor_tensor(res[l][:, :], res[l][:, :], bias_row[:, :], ALU.add))
                    step(v.tensor_tensor(S.x[:, b, :], S.x[:, b, :], res[l][:, :], ALU.add))

                for l in lanes:
                    v.sem_inc(res_ready[l], 1)
                skewed(v, [nothing, null_scores, low_keys, chunk(0), nothing, chunk(1), nothing],
                       [chunk(2), chunk(3), last_division, nothing, last_outputs, statistics, added], step.restart)
                all_statistics(v, step, S)

            @block.scalar
            def _(a):
                a.wait_ge(zeros_set, 4)

                def turned_x(j, l):
                    a.wait_ge(xn_turned[l], 1 + j + 1)
                    a.activation(xnT[l][:, :], psB[l][:, 0:T], ACT.Copy).then_inc(xnT_ready[l], 1)

                def queries(j, l):
                    for n in range(2):
                        a.wait_ge(q_mm[l], 2 * j + n + 1)
                        a.activation(qT[l][:, 4 * n:4 * n + 4, :].rearrange("p c t -> p (c t)"), psA[l][:, bank(n)], ACT.Copy,
                                     scale=scale).then_inc(q_ready[l], 1)

                def high_keys(j, l):
                    for n in range(2):
                        a.wait_ge(k_mm[l], 2 * j + n + 1)
                        a.activation(keys[l][DH:P, 4 * n:4 * n + 4, 1, :],
                                     psA[l][DH:P, bank(n)].rearrange("p (c k) -> p c k", k=P),
                                     ACT.Copy).then_inc(k_high_ready[l], 1)

                def values(n):
                    def stage(j, l):
                        a.wait_ge(v_mm[l], 1 + 2 * j + n + 1)
                        pairs = psO[l][:, :].rearrange("p (c d) -> p c d", d=2 * DH)
                        a.activation(vals[l][:, 4 * n:4 * n + 4, 0:DH], pairs[:, :, 0:DH], ACT.Copy)
                        a.activation(vals[l][:, 4 * n:4 * n + 4, 2 * P - DH:2 * P], pairs[:, :, DH:2 * DH],
                                     ACT.Copy).then_inc(v_ready[l], 1)
                    return stage

                def chunk(c):
                    def stage(j, l):
                        if c >= 2:
                            a.wait_ge(turned[l], j * CHUNKS + c - 1)
                            a.activation(probsT[l][:, (c - 2) * HPC:(c - 1) * HPC, :].rearrange("p j k -> p (j k)"),
                                         psB[l][:, :], ACT.Copy).then_inc(probsT_ready[l], 1)
                        if c < CHUNKS:
                            a.wait_ge(maxed[l], j * CHUNKS + c + 1)
                            for h in range(c * HPC, (c + 1) * HPC):
                                at = c % 2 * 512 + h % HPC * P
                                a.activation(probs[l][:, h, :], psA[l][:, at:at + P], ACT.Exp, bias=neg[l][:, h:h + 1],
                                             accum_out=sums[l][:, h:h + 1])
                            p0c = p0[l][:, c * HPC:(c + 1) * HPC]
                            a.activation(p0c, p0c, ACT.Exp).then_inc(exp_ready[l], 1)
                    return stage

                def null_turned(j, l):
                    a.wait_ge(p0_turned[l], j + 1)
                    a.activation(p0T[l][0:HEADS, :], psB[l][0:HEADS, 0:T], ACT.Copy).then_inc(p0T_ready[l], 1)

                skewed(a, [turned_x, queries, high_keys, chunk(0), values(0), chunk(1), values(1)],
                       [chunk(2), chunk(3), chunk(4), chunk(5), null_turned, nothing, nothing])

            @block.tensor
            def _(t):
                for l in lanes:
                    t.sem_inc(xn_turned[l], 1)
                    t.sem_inc(v_mm[l], 1)
                t.wait_ge(null_ready, 2)
                for c in range(NCH):
                    mm = t.matmul(psB[0][0:HEADS, 0:D], value_cols[:, c, :], wout[:, c, :], start=(c == 0), stop=(c == NCH - 1))
                mm.then_inc(null_mm, 1)
                t.wait_ge(null_out_ready, 1)

                def turn_x(j, l):
                    t.wait_ge(xn_ready[l], j + 1)
                    t.transpose(psB[l][:, 0:T], xn[l][:, :], S.ident).then_inc(xn_turned[l], 1)

                def queries(j, l):
                    t.wait_ge(xnT_ready[l], j + 1)
                    t.wait_ge(res_ready[l], 1 + j)
                    t.matmul(psO[l][:, 0:HEADS], xnT[l][:, :], wnull[:, :], start=True, stop=True).then_inc(s0_mm[l], 1)
                    for n in range(2):
                        for c in range(4 * n, 4 * n + 4):
                            mm = t.matmul(psA[l][:, c * T:(c + 1) * T], wq[:, c * P:(c + 1) * P], xnT[l][:, :],
                                          start=True, stop=True)
                        mm.then_inc(q_mm[l], 1)

                def new_keys(j, l):
                    t.wait_ge(cT_ready[l], j + 1)
                    for n in range(2):
                        t.wait_ge(q_ready[l], 2 * j + n + 1)
                        for c in range(4 * n, 4 * n + 4):
                            for s in range(2):
                                mm = t.matmul(psA[l][:, c * P:(c + 1) * P], wkv[:, s, c * P:(c + 1) * P], cT[l][:, s, :],
                                              start=(s == 0), stop=(s == 1))
                        mm.then_inc(k_mm[l], 1)

                def values(n):
                    def stage(j, l):
                        if n:
                            t.wait_ge(v_ready[l], 2 * j + 1)
                        at = HEADS * DH + n * 512
                        for s in range(2):
                            mm = t.matmul(psO[l][:, :], cT[l][:, s, :], wkv[:, s, at:at + 512], start=(s == 0), stop=(s == 1))
                        mm.then_inc(v_mm[l], 1)
                    return stage

                def chunk(c):
                    def stage(j, l):
                        if c < CHUNKS:
                            if c < 2:
                                t.wait_ge(k_low_ready[l], 2 * j + 2)
                                t.wait_ge(k_high_ready[l], 2 * j + 2)
                            else:
                                t.wait_ge(exp_ready[l], j * CHUNKS + c - 1)
                            for k in range(2):
                                at = c % 2 * 512 + k * 2 * P
                                mm = t.matmul(psA[l][:, at:at + 2 * P], qT[l][:, 2 * c + k, :],
                                              keys[l][:, 2 * c + k, :, :].rearrange("p s k -> p (s k)"), start=True, stop=True)
                            mm.then_inc(scores_ready[l], 1)
                        if 2 <= c <= CHUNKS + 1:
                            t.wait_ge(normed_ready[l], j * CHUNKS + c - 1)
                            if c > 2:
                                t.wait_ge(probsT_ready[l], j * CHUNKS + c - 2)
                            for k in range(HPC):
                                mm = t.transpose(psB[l][:, k * P:(k + 1) * P], probs[l][:, (c - 2) * HPC + k, :], S.ident)
                            mm.then_inc(turned[l], 1)
                        if c >= 3:
                            if c == 3:
                                t.wait_ge(v_ready[l], 2 * j + 2)
                            if c == CHUNKS + 2:
                                t.wait_ge(probsT_ready[l], j * CHUNKS + CHUNKS)
                            if c == 5:
                                t.wait_ge(oT_ready[l], 2 * j + 1)
                            for pair in (2 * (c - 3), 2 * (c - 3) + 1):
                                for k in range(2):
                                    mm = t.matmul(psO[l][:, pair % 4 * T:pair % 4 * T + T], vals[l][:, pair, k * P:(k + 1) * P],
                                                  probsT[l][:, 2 * pair + k, :], start=(k == 0), stop=(k == 1))
                            if c % 2 == 0:
                                mm.then_inc(out_mm[l], 1)
                    return stage

                def turn_null(j, l):
                    t.transpose(psB[l][0:HEADS, 0:T], p0[l][:, :], S.ident).then_inc(p0_turned[l], 1)

                def project(j, l):
                    t.wait_ge(oT_ready[l], 2 * j + 2)
                    t.wait_ge(p0T_ready[l], j + 1)
                    for c in range(NCH):
                        t.matmul(psO[l][:, 0:D], oT[l][:, c, :], wout[:, c, :], start=(c == 0), stop=False)
                    t.matmul(psO[l][:, 0:D], p0T[l][0:HEADS, :], null_out[0:HEADS, :], start=False,
                             stop=True).then_inc(proj_ready[l], 1)

                def last_chunk(j, l):
                    chunk(CHUNKS + 2)(j, l)
                    turn_null(j, l)
                skewed(t, [turn_x, queries, new_keys, chunk(0), values(0), chunk(1), values(1)],
                       [chunk(2), chunk(3), chunk(4), chunk(5), last_chunk, project, nothing])


def normed_rows_and_logits(nc, S, ph, name, experts, w, w_dram, xT_all, logits):
    WIDE = 4
    with phase(nc, name) as pn:
        lanes = range(WIDE)
        xn_all = pn.sb("xn_all", [P, B, D])
        xn = [pn.sb(f"xn{l}", [P, D]) for l in lanes]
        xT = [pn.sb(f"xT{l}", [P, T]) for l in lanes]
        ps = [pn.ps(f"ps{k}", [P, 512]) for k in range(2 * WIDE)]
        normed, dve_step, stats_done, pow_ready, loaded, xn_ready, turned, xT_ready, xT_kept, logits_mm, logits_kept = (
            pn.sem(n) for n in ("normed", "dve_step", "stats_done", "pow_ready", "loaded", "xn_ready", "turned", "xT_ready", "xT_kept",
                                "logits_mm", "logits_kept"))
        with nc.Block() as block:
            @block.sync
            def _(sp):
                sp.dma_start(w[:, :], w_dram).then_inc(loaded, 16)

            @block.gpsimd
            def _(g):
                inverse_roots(g, S, stats_done, pow_ready)
                g.wait_ge(normed, 1)
                with g.Fori(0, B // WIDE) as i:
                    for l in lanes:
                        g.wait_ge(turned, 1 + i * WIDE)
                        g.tensor_copy(xn[l][:, :], xn_all[:, i * WIDE + l, :]).then_inc(xn_ready, 1)

            @block.vector
            def _(v):
                v.sem_inc(logits_kept, 1)
                v.sem_inc(xT_ready, 1)
                step = Steps(v, dve_step)
                layer_norm_coefficients(v, step, S, stats_done, pow_ready)
                normalized(v, step, S, xn_all, pow_ready, normed, 1)
                with v.Fori(0, B // WIDE) as i:
                    for l in lanes:
                        b = i * WIDE + l
                        v.wait_ge(turned, 1 + b + 1)
                        v.wait_ge(logits_mm, 1 + i * WIDE)
                        v.wait_ge(xT_kept, 1 + i * WIDE)
                        v.tensor_copy(xT[l][:, :], ps[2 * l][:, 0:T]).then_inc(xT_ready, 1)
                    for l in lanes:
                        b = i * WIDE + l
                        v.wait_ge(logits_mm, 1 + b + 1)
                        v.tensor_copy(logits[:, b, :], ps[2 * l + 1][:, 0:experts]).then_inc(logits_kept, 1)

            @block.scalar
            def _(a):
                a.sem_inc(xT_kept, 1)
                with a.Fori(0, B // WIDE) as i:
                    for l in lanes:
                        b = i * WIDE + l
                        a.wait_ge(xT_ready, 1 + b + 1)
                        a.activation(xT_all[:, b, :], xT[l][:, :], ACT.Copy).then_inc(xT_kept, 1)

            @block.tensor
            def _(t):
                t.sem_inc(logits_mm, 1)
                t.sem_inc(turned, 1)
                t.wait_ge(loaded, 16)
                with t.Fori(0, B // WIDE) as i:
                    for l in lanes:
                        t.wait_ge(xn_ready, i * WIDE + l + 1)
                        t.wait_ge(xT_ready, 1 + i * WIDE)
                        t.transpose(ps[2 * l][:, 0:T], xn[l][:, :], S.ident).then_inc(turned, 1)
                    for l in lanes:
                        t.wait_ge(xT_ready, 1 + i * WIDE + l + 1)
                        t.wait_ge(logits_kept, 1 + i * WIDE)
                        t.matmul(ps[2 * l + 1][:, 0:experts], xT[l][:, :], w[:, :], start=True, stop=True).then_inc(logits_mm, 1)


def chosen(v, step, vals, n, count, above, sel):
    for e in range(n):
        mine = vals[:, :, e:e + 1]
        if e:
            v.tensor_tensor(above[:, :, e, 0:e], vals[:, :, 0:e], mine.broadcast_to([P, B, e]), ALU.is_ge)
        ins = v.tensor_tensor(above[:, :, e, e:n], vals[:, :, e:n], mine.broadcast_to([P, B, n - e]), ALU.is_gt)
    step(ins)
    step(v.tensor_reduce(sel, above, AX.X, ALU.add))
    step(v.tensor_scalar(sel, sel, float(count), None, ALU.is_lt))


def grouped_mixture(nc, S, name, ins):
    E, F, GROUPS, TOP_GROUPS, TOP, SHARED, SCALE = 16, 128, 4, 2, 4, 2, 2.5
    ALL = E + SHARED
    PER = E // GROUPS
    G = 4
    with phase(nc, name) as ph:
        wr = ph.sb("wr", [P, E])
        gate, up, down = (ph.sb(n, [P, ALL, F]) for n in ("gate", "up", "down"))
        xT = ph.sb("xT", [P, B, T])
        mix = ph.sb("mix", [P, B, ALL])
        score = ph.sb("score", [P, B, E])
        weights_loaded = ph.sem("weights_loaded")
        with nc.Block() as block:
            @block.sync
            def _(sp):
                for dst, n in ((gate, "gate_w"), (up, "up_w"), (down, "down_w")):
                    sp.dma_start(dst[:, 0:E, :], ins["L2_ffn_" + n].rearrange("e i j -> i e j")).then_inc(weights_loaded, 16)
                for dst, n in ((gate, "sh_gate_w"), (up, "sh_up_w")):
                    sp.dma_start(dst[:, E:ALL, :], ins["L2_ffn_" + n].rearrange("i (e j) -> i e j", j=F)).then_inc(weights_loaded, 16)
                sp.dma_start(down[:, E:ALL, :], ins["L2_ffn_sh_down_w"].rearrange("(e i) j -> i e j", i=F)).then_inc(weights_loaded, 16)
        normed_rows_and_logits(nc, S, ph, name + "_n", E, wr, ins["L2_router_wT"], xT, score)

        with phase(nc, name + "_r") as pr:
            bias = pr.sb("bias", [P, E])
            biased, masked = pr.sb("biased", [P, B, E]), pr.sb("masked", [P, B, E])
            above = pr.sb("above", [P, B, E, E])
            hi, lo = pr.sb("hi", [P, B, GROUPS, 2]), pr.sb("lo", [P, B, GROUPS, 2])
            best, second, third = (pr.sb(n, [P, B, GROUPS]) for n in ("best", "second", "third"))
            total = pr.sb("total", [P, B])
            dve_step, bias_loaded, exp_done = pr.sem("dve_step"), pr.sem("bias_loaded"), pr.sem("exp_done")
            with nc.Block() as block:
                @block.sync
                def _(sp):
                    sp.dma_start(bias[:, :], ins["L2_ffn_bias"].partition_broadcast(P)).then_inc(bias_loaded, 16)

                @block.scalar
                def _(a):
                    a.activation(score[:, :, :], score[:, :, :], ACT.Exp, scale=-1.0).then_inc(exp_done, 1)

                @block.vector
                def _(v):
                    step = Steps(v, dve_step)
                    v.wait_ge(bias_loaded, 16)
                    v.wait_ge(exp_done, 1)
                    step(v.tensor_scalar(score[:, :, :], score[:, :, :], 1.0, None, ALU.add))
                    step(v.reciprocal(score[:, :, :], score[:, :, :]))
                    step(v.tensor_tensor(biased[:, :, :], score[:, :, :],
                                         bias[:, :].unsqueeze(1).broadcast_to([P, B, E]), ALU.add))
                    quad = biased[:, :, :].rearrange("p b (g two c) -> p (b g) two c", two=2, c=2)
                    h2, l2 = (x[:, :, :, :].rearrange("p b g c -> p (b g) c") for x in (hi, lo))
                    bst, sec, thr = (x[:, :, :].rearrange("p b g -> p (b g)") for x in (best, second, third))
                    step(v.tensor_tensor(h2, quad[:, :, 0, :], quad[:, :, 1, :], ALU.max))
                    step(v.tensor_tensor(l2, quad[:, :, 0, :], quad[:, :, 1, :], ALU.min))
                    step(v.tensor_tensor(bst, h2[:, :, 0], h2[:, :, 1], ALU.max))
                    step(v.tensor_tensor(sec, h2[:, :, 0], h2[:, :, 1], ALU.min))
                    step(v.tensor_tensor(thr, l2[:, :, 0], l2[:, :, 1], ALU.max))
                    step(v.tensor_tensor(sec, sec, thr, ALU.max))
                    step(v.tensor_tensor(bst, bst, sec, ALU.add))
                    chosen(v, step, best[:, :, :], GROUPS, TOP_GROUPS, above[:, :, 0:GROUPS, 0:GROUPS], second[:, :, :])
                    m = sec.unsqueeze(2).broadcast_to([P, B * GROUPS, PER])
                    mk, bs = (x[:, :, :].rearrange("p b (g c) -> p (b g) c", c=PER) for x in (masked, biased))
                    step(v.tensor_tensor(mk, bs, m, ALU.mult))
                    step(v.tensor_scalar(thr, sec, -1.0, None, ALU.add))
                    step(v.tensor_tensor(mk, mk, thr.unsqueeze(2).broadcast_to([P, B * GROUPS, PER]), ALU.add))
                    chosen(v, step, masked[:, :, :], E, TOP, above[:, :, :, :], biased[:, :, :])
                    step(v.tensor_tensor(masked[:, :, :], score[:, :, :], biased[:, :, :], ALU.mult))
                    step(v.tensor_reduce(total[:, :], masked[:, :, :], AX.X, ALU.add))
                    step(v.tensor_scalar(total[:, :], total[:, :], 1e-20, None, ALU.add))
                    step(v.reciprocal(total[:, :], total[:, :]))
                    step(v.tensor_scalar(total[:, :], total[:, :], SCALE, None, ALU.mult))
                    step(v.memset(mix[:, :, :], 1.0))
                    step(v.tensor_tensor(mix[:, :, 0:E], masked[:, :, :], total[:, :].unsqueeze(2).broadcast_to([P, B, E]),
                                         ALU.mult))

        with phase(nc, name + "_e") as pe:
            sg = [pe.sb(f"sg{k}", [P, G * T]) for k in range(2)]
            act = [pe.sb(f"act{k}", [P, G * T]) for k in range(2)]
            ps_g = [pe.ps(f"ps_g{k}", [P, G * T]) for k in range(2)]
            ps_u = [pe.ps(f"ps_u{k}", [P, G * T]) for k in range(2)]
            ps_y = [pe.ps(f"ps_y{k}", [P, G, D]) for k in range(2)]
            dve_step, gu_ready, silu_ready, act_ready, y_ready, y_added = (
                pe.sem(n) for n in ("dve_step", "gu_ready", "silu_ready", "act_ready", "y_ready", "y_added"))
            with nc.Block() as block:
                @block.vector
                def _(v):
                    v.sem_inc(y_added, 1)
                    v.sem_inc(act_ready, 1)
                    step = Steps(v, dve_step)

                    def add_up(i, e):
                        v.wait_ge(y_ready, i * ALL + e + 1)
                        if e:
                            v.wait_ge(y_added, 1 + i * ALL + e)
                        for k in range(G):
                            x = S.x[:, i * G + k, :]
                            ins_ = v.scalar_tensor_tensor(out=x, in0=ps_y[e % 2][:, k, :], scalar=mix[:, i * G + k, e:e + 1],
                                                          in1=x, op0=ALU.mult, op1=ALU.add)
                        ins_.then_inc(y_added, 1)

                    with v.Fori(0, B // G) as i:
                        step.restart()
                        for e in range(ALL):
                            v.wait_ge(silu_ready, i * ALL + e + 1)
                            v.tensor_tensor(act[e % 2][:, :], sg[e % 2][:, :], ps_u[e % 2][:, :], ALU.mult).then_inc(act_ready, 1)
                            if e:
                                add_up(i, e - 1)
                        add_up(i, ALL - 1)
                        v.wait_ge(y_added, 1 + i * ALL + ALL)
                        for k in range(G):
                            step(v.bn_stats(S.stats[:, i * G + k, :], S.x[:, i * G + k, :]))

                @block.scalar
                def _(a):
                    with a.Fori(0, B // G) as i:
                        for e in range(ALL):
                            a.wait_ge(gu_ready, i * ALL + e + 1)
                            a.wait_ge(act_ready, 1 + i * ALL + e - 1) if e >= 2 else a.wait_ge(act_ready, 1 + i * ALL)
                            a.activation(sg[e % 2][:, :], ps_g[e % 2][:, :], ACT.Silu).then_inc(silu_ready, 1)

                @block.tensor
                def _(t):
                    t.wait_ge(weights_loaded, 96)

                    def project(i, e):
                        t.wait_ge(act_ready, 1 + i * ALL + e + 1)
                        t.wait_ge(y_added, 1 + i * ALL + e - 1) if e >= 2 else t.wait_ge(y_added, 1 + i * ALL)
                        for k in range(G):
                            mm = t.matmul(ps_y[e % 2][:, k, :], act[e % 2][:, k * T:(k + 1) * T], down[:, e, :],
                                          start=True, stop=True)
                        mm.then_inc(y_ready, 1)

                    with t.Fori(0, B // G) as i:
                        for e in range(ALL):
                            t.wait_ge(act_ready, 1 + i * ALL + e - 1) if e >= 2 else t.wait_ge(act_ready, 1 + i * ALL)
                            rows = xT[:, bass.ds(i * G, G), :].rearrange("p b t -> p (b t)")
                            t.matmul(ps_g[e % 2][:, :], gate[:, e, :], rows, start=True, stop=True)
                            t.matmul(ps_u[e % 2][:, :], up[:, e, :], rows, start=True, stop=True).then_inc(gu_ready, 1)
                            if e:
                                project(i, e - 1)
                        project(i, ALL - 1)


def top_two_mixture(nc, S, name, ins):
    E, HID, TOP = 8, 512, 2
    HC = HID // P
    G = 4
    with phase(nc, name) as ph:
        wr = ph.sb("wr", [P, E])
        w1 = ph.sb("w1", [P, E, HID])
        w2 = ph.sb("w2", [P, E, HC, D])
        b1 = ph.sb("b1", [P, E, HC])
        b2 = ph.sb("b2", [E, D])
        xT = ph.sb("xT", [P, B, T])
        mix = ph.sb("mix", [P, B, E])
        prob = ph.sb("prob", [P, B, E])
        weights_loaded = ph.sem("weights_loaded")
        with nc.Block() as block:
            @block.sync
            def _(sp):
                sp.dma_start(w1[:, :, :], ins["L3_w1T"].rearrange("e d h -> d e h")).then_inc(weights_loaded, 16)
                sp.dma_start(w2[:, :, :, :], ins["L3_w2T"].rearrange("e (c p) d -> p e c d", p=P)).then_inc(weights_loaded, 16)
                sp.dma_start(b1[:, :, :], ins["L3_b1T"]).then_inc(weights_loaded, 16)
                sp.dma_start(b2[:, :], ins["L3_ffn_b2"]).then_inc(weights_loaded, 16)
        normed_rows_and_logits(nc, S, ph, name + "_n", E, wr, ins["L3_gate_wT"], xT, prob)

        with phase(nc, name + "_r") as pr:
            WIDE = 4
            lanes = range(WIDE)
            above = pr.sb("above", [P, B, E, E])
            sel, top, total = pr.sb("sel", [P, B, E]), pr.sb("top", [P, B]), pr.sb("total", [P, B])
            m1 = [pr.sb(f"m1{l}", [P, E]) for l in lanes]
            mT = [pr.sb(f"mT{l}", [E, T]) for l in lanes]
            ps = [pr.ps(f"ps{k}", [P, 512]) for k in range(2 * WIDE)]
            dve_step, shift_done, exp_done, m_ready, m_turned, mT_ready, bias_ready = (
                pr.sem(n) for n in ("dve_step", "shift_done", "exp_done", "m_ready", "m_turned", "mT_ready", "bias_ready"))
            with nc.Block() as block:
                @block.scalar
                def _(a):
                    a.wait_ge(shift_done, 1)
                    a.activation(prob[:, :, :], prob[:, :, :], ACT.Exp).then_inc(exp_done, 1)

                @block.vector
                def _(v):
                    step = Steps(v, dve_step)
                    row = lambda x: x[:, :].unsqueeze(2).broadcast_to([P, B, E])
                    step(v.tensor_reduce(top[:, :], prob[:, :, :], AX.X, ALU.max))
                    v.tensor_tensor(prob[:, :, :], prob[:, :, :], row(top), ALU.subtract).then_inc(shift_done, 1)
                    v.wait_ge(exp_done, 1)
                    step(v.tensor_reduce(total[:, :], prob[:, :, :], AX.X, ALU.add))
                    step(v.reciprocal(total[:, :], total[:, :]))
                    step(v.tensor_tensor(prob[:, :, :], prob[:, :, :], row(total), ALU.mult))
                    chosen(v, step, prob[:, :, :], E, TOP, above[:, :, :, :], sel[:, :, :])
                    step(v.tensor_tensor(prob[:, :, :], prob[:, :, :], sel[:, :, :], ALU.mult))
                    step(v.tensor_reduce(total[:, :], prob[:, :, :], AX.X, ALU.add))
                    step(v.reciprocal(total[:, :], total[:, :]))
                    step(v.tensor_tensor(mix[:, :, :], prob[:, :, :], row(total), ALU.mult))
                    with v.Fori(0, B // WIDE) as i:
                        step.restart()
                        for l in lanes:
                            v.tensor_copy(m1[l][:, :], mix[:, i * WIDE + l, :]).then_inc(m_ready, 1)
                        for l in lanes:
                            v.wait_ge(m_turned, i * WIDE + l + 1)
                            v.tensor_copy(mT[l][:, :], ps[2 * l][0:E, 0:T]).then_inc(mT_ready, 1)
                        for l in lanes:
                            v.wait_ge(bias_ready, i * WIDE + l + 1)
                            step(v.tensor_tensor(S.x[:, i * WIDE + l, :], S.x[:, i * WIDE + l, :], ps[2 * l + 1][:, 0:D], ALU.add))

                @block.tensor
                def _(t):
                    t.wait_ge(weights_loaded, 64)
                    with t.Fori(0, B // WIDE) as i:
                        for l in lanes:
                            t.wait_ge(m_ready, i * WIDE + l + 1)
                            t.transpose(ps[2 * l][0:E, 0:T], m1[l][:, :], S.ident).then_inc(m_turned, 1)
                        for l in lanes:
                            t.wait_ge(mT_ready, i * WIDE + l + 1)
                            t.matmul(ps[2 * l + 1][:, 0:D], mT[l][:, :], b2[:, :], start=True, stop=True).then_inc(bias_ready, 1)

        with phase(nc, name + "_e") as pe:
            act = [pe.sb(f"act{k}", [P, HC, G * T]) for k in range(2)]
            ps_h = [pe.ps(f"ps_h{k}", [P, G * T]) for k in range(4)]
            ps_y = [pe.ps(f"ps_y{k}", [P, G, D]) for k in range(2)]
            h_ready, act_ready, y_ready, y_added = (pe.sem(n) for n in ("h_ready", "act_ready", "y_ready", "y_added"))
            with nc.Block() as block:
                @block.vector
                def _(v):
                    v.sem_inc(y_added, 1)
                    with v.Fori(0, B // G) as i:
                        for e in range(E):
                            v.wait_ge(y_ready, 1 + i * E + e + 1)
                            if e:
                                v.wait_ge(y_added, 1 + i * E + e)
                            for k in range(G):
                                x = S.x[:, i * G + k, :]
                                ins_ = v.scalar_tensor_tensor(out=x, in0=ps_y[e % 2][:, k, :], scalar=mix[:, i * G + k, e:e + 1],
                                                              in1=x, op0=ALU.mult, op1=ALU.add)
                            ins_.then_inc(y_added, 1)

                @block.scalar
                def _(a):
                    a.sem_inc(act_ready, 1)
                    with a.Fori(0, B // G) as i:
                        for e in range(E):
                            a.wait_ge(y_ready, 1 + i * E + e - 1) if e >= 2 else a.wait_ge(y_ready, 1 + i * E)
                            for c in range(HC):
                                a.wait_ge(h_ready, (i * E + e) * HC + c + 1)
                                a.activation(act[e % 2][:, c, :], ps_h[c][:, :], ACT.Relu, bias=b1[:, e, c:c + 1]).then_inc(act_ready, 1)

                @block.tensor
                def _(t):
                    t.sem_inc(y_ready, 1)
                    def project(i, e):
                        t.wait_ge(act_ready, 1 + (i * E + e + 1) * HC)
                        t.wait_ge(y_added, 1 + i * E + e - 1) if e >= 2 else t.wait_ge(y_added, 1 + i * E)
                        for k in range(G):
                            for c in range(HC):
                                mm = t.matmul(ps_y[e % 2][:, k, :], act[e % 2][:, c, k * T:(k + 1) * T], w2[:, e, c, :],
                                              start=(c == 0), stop=(c == HC - 1))
                        mm.then_inc(y_ready, 1)

                    with t.Fori(0, B // G) as i:
                        rows = xT[:, bass.ds(i * G, G), :].rearrange("p b t -> p (b t)")
                        for e in range(E):
                            for c in range(HC):
                                t.wait_ge(act_ready, 1 + (i * E + e - 1) * HC + c + 1) if e else t.wait_ge(act_ready, 1 + i * E * HC)
                                t.matmul(ps_h[c][:, :], w1[:, e, c * P:(c + 1) * P], rows, start=True, stop=True).then_inc(h_ready, 1)
                            if e:
                                project(i, e - 1)
                        project(i, E - 1)


def projected_attention(nc, S, name, ins):
    with phase(nc, name + "_w") as ph:
        wqkvT = ph.sb("wqkvT", [P, 3 * D])
        wprojT = ph.sb("wprojT", [P, D])
        b_proj = ph.sb("b_proj", [P, D])
        loaded = ph.sem("loaded")
        with nc.Block() as block:
            @block.sync
            def _(sp):
                sp.dma_start(wqkvT[:, :], ins["L3_w_qkvT"]).then_inc(loaded, 16)
                sp.dma_start(wprojT[:, :], ins["L3_w_projT"]).then_inc(loaded, 16)
                sp.dma_start(b_proj[:, :], ins["L3_xattn_b_proj"].partition_broadcast(P)).then_inc(loaded, 16)
                sp.wait_ge(loaded, 48)
        small_head_attention(nc, S, name, True, weights={
            "wqT": wqkvT[:, 0:D], "wkT": wqkvT[:, D:2 * D], "wvT": wqkvT[:, 2 * D:3 * D],
            "wprojT": wprojT[:, :], "b_proj": b_proj[:, :]})


def build(nc, ins, out):
    at, width = constant_offsets()
    with ExitStack() as ctx:
        def sb(name, shape, dt=F32):
            return ctx.enter_context(nc.sbuf_tensor(name, shape, dt))
        S = Shared()
        S.x = sb("x", [P, B, D])
        S.ctx = sb("ctx", [P, B, CTX])
        S.ctxT = sb("ctxT", [P, 2, B, P])
        S.stats = sb("stats", [P, B, 6])
        S.mean, S.dif, S.var, S.rstd, S.mhalf = (sb(n, [P, B]) for n in ("mean", "dif", "var", "rstd", "mhalf"))
        consts = sb("consts", [P, width])

        def const(name):
            return consts[:, at[name][0]:at[name][1]]
        S.ident, S.iota_row, S.iota_col, S.upto, S.ones = (const(n) for n in ("ident", "iota_row", "iota_col", "upto", "ones"))
        S.headmask, S.cos, S.sin, S.sameexpert = (const(n) for n in ("headmask", "cos", "sin", "sameexpert"))
        S.expertmask, S.decay, S.pairhead = (const(n) for n in ("expertmask", "decay", "pairhead"))
        S.iota256 = consts[:, at["iota_row"][0]:at["iota_row2"][1]]
        load_inputs(nc, S, ins, consts)
        all_stages(nc, S, ins)
        with phase(nc, "store") as ph:
            stored = ph.sem("stored")
            with nc.Block() as block:
                @block.sync
                def _(sp):
                    sp.dma_start(out.rearrange("b t d -> t b d"), S.x[:, :, :]).then_inc(stored, 16)
                    sp.wait_ge(stored, 16)


def load_inputs(nc, S, ins, consts):
    with phase(nc, "load") as ph:
        x_loaded, rest_loaded, step_sem, half_set = (ph.sem(n) for n in ("x_loaded", "rest_loaded", "dve_step", "half_set"))
        with nc.Block() as block:
            @block.sync
            def _(sp):
                sp.dma_start(S.x[:, :, :], ins["x"].rearrange("b t d -> t b d")).then_inc(x_loaded, 16)
                sp.dma_start(consts[:, :], ins["consts"]).then_inc(rest_loaded, 16)
                sp.wait_ge(rest_loaded, 16)

            @block.vector
            def _(v):
                v.memset(S.mhalf[:, :], -0.5).then_inc(half_set, 1)
                v.wait_ge(x_loaded, 16)
                v.wait_ge(half_set, 1)
                all_statistics(v, Steps(v, step_sem), S)


def all_stages(nc, S, ins):
    stages = [
        lambda: small_head_attention(nc, S, "L0x", False, seq_len=ins["seq_len"], bias=ins["L0_xattn_b"],
                                     context=ins["ctx"], contextT=ins["ctxT"]),
        lambda: expert_choice_attention(nc, S, "L0f", ins),
        lambda: patch_depool(nc, S, "L1x", ins),
        lambda: routed_trees(nc, S, "L1f", ins),
        lambda: wide_head_attention(nc, S, "L2x", ins),
        lambda: grouped_mixture(nc, S, "L2f", ins),
        lambda: projected_attention(nc, S, "L3x", ins),
        lambda: top_two_mixture(nc, S, "L3f", ins),
    ]
    for stage in stages:
        stage()


def lay_out(inputs):
    c = np.ascontiguousarray
    g = {k: np.asarray(v) for k, v in inputs.items()}
    f = {}
    f["x"] = c(g["x"])
    f["ctx"] = c(g["ctx_2048"])
    f["ctxT"] = c(g["ctx_2048"].transpose(2, 0, 1).reshape(2, P, B, T))
    f["seq_len"] = c(g["itok_Bx1_68_817"].reshape(B))
    f["L0_xattn_b"] = c(g["L0_xattn_b"])
    f["L0_ffn_WrT"] = c(g["L0_ffn_Wr"].T)
    f["L0_ffn_Wqkv"] = c(g["L0_ffn_Wqkv"])
    half = np.r_[ROPE_HALF:ROPE_N, 0:ROPE_HALF]
    f["L0_ffn_Wswap"] = c(np.stack([g["L0_ffn_Wqkv"][:, :, half], g["L0_ffn_Wqkv"][:, :, D + half]], 2))
    f["L0_ffn_Wo"] = c(g["L0_ffn_Wo"])
    f["L1_W_inT"] = c(g["L1_xattn_W_in"].T)
    for n in ("L1_xattn_b_in", "L1_xattn_g_res", "L1_xattn_g_init"):
        f[n] = c(g[n])
    f["patch_lensT"] = c(g["mask_BxS2_if0"].T)
    f["L1_ffn_nw3"] = c(np.concatenate([g[f"L1_ffn_{n}_nw"] for n in "qkv"]).T)
    f["L1_ffn_nb3"] = c(np.concatenate([g[f"L1_ffn_{n}_nb"] for n in "qkv"]))
    f["L1_ffn_nwf"] = c(g["L1_ffn_f_nw"].T)
    f["L1_ffn_nbf"] = c(g["L1_ffn_f_nb"])
    f["leaf_table"] = c(np.concatenate([np.concatenate([
        g[f"L1_ffn_{n}_w1"].transpose(0, 2, 1).reshape(LEAVES, LW * D), g[f"L1_ffn_{n}_b1"],
        g[f"L1_ffn_{n}_w2"].reshape(LEAVES, LW * D), g[f"L1_ffn_{n}_b2"]], 1) for n in "qkvf"]))
    for n in ("L2_xattn_Wq", "L2_xattn_Wkv", "L2_xattn_Wout", "L2_xattn_ln_scale", "L2_xattn_ln_bias",
              "L2_ffn_bias", "L2_ffn_gate_w", "L2_ffn_up_w", "L2_ffn_down_w", "L2_ffn_sh_gate_w", "L2_ffn_sh_up_w",
              "L2_ffn_sh_down_w", "L3_xattn_b_proj", "L3_ffn_b2"):
        f[n] = c(g[n])
    f["L2_null_key"] = c(g["L2_xattn_null_kv"][0])
    f["L2_null_values"] = c(np.concatenate([g["L2_xattn_null_kv"][1]] * 2)[:, None])
    f["L2_router_wT"] = c(g["L2_ffn_router_w"].T)
    f["L3_w_qkvT"] = c(g["L3_xattn_w_qkv"].T)
    f["L3_w_projT"] = c(g["L3_xattn_w_proj"].T)
    f["L3_gate_wT"] = c(g["L3_ffn_gate_w"].T)
    f["L3_w1T"] = c(g["L3_ffn_w1"].transpose(0, 2, 1))
    f["L3_w2T"] = c(g["L3_ffn_w2"].transpose(0, 2, 1))
    f["L3_b1T"] = c(g["L3_ffn_b1"].reshape(8, 4, P).transpose(2, 0, 1))
    f["consts"] = c(np.concatenate([np.asarray(a, np.float32) for a in constant_columns().values()], 1))
    return f


def kernel(**inputs):
    import concourse.bacc as bacc
    from concourse.bass_utils import run_bass_kernel_spmd

    nc = bacc.Bacc("TRN2", target_bir_lowering=False, num_devices=1)
    arrays, ins = {}, {}
    for name, a in lay_out(inputs).items():
        arrays[f"in_{name}"] = a
        ins[name] = nc.dram_tensor(f"in_{name}", a.shape, mybir.dt.from_np(a.dtype), kind="ExternalInput").ap()
    out = nc.dram_tensor("out_0", (B, T, D), F32, kind="ExternalOutput").ap()
    build(nc, ins, out)
    r = run_bass_kernel_spmd(nc, [arrays], core_ids=[0])
    return r.results[0]["out_0"]
```
